# Optimizing a Trainium2 kernel written in Bass

```python
import numpy as np
import jax
import jax.numpy as jnp

def _softmax(x, axis=-1):
    return jax.nn.softmax(x, axis=axis)

def _gelu(x):
    return jax.nn.gelu(x, approximate=True)

def _silu(x):
    return jax.nn.silu(x)

def _sigmoid(x):
    return jax.nn.sigmoid(x)

def _layernorm(x, axis=-1, eps=1e-05):
    m = jnp.mean(x, axis=axis, keepdims=True)
    v = jnp.var(x, axis=axis, keepdims=True)
    return (x - m) / jnp.sqrt(v + eps)

def _scatter_add(tgt, idx, src, axis=0):
    return tgt.at[idx].add(src)

def _segment_sum(src, seg, n):
    return jax.ops.segment_sum(src, seg, n)
kernel_name = 'mk_gps_d2_gnn_r16_07cff4'

def setup_inputs(seed: int=0):
    np.random.seed(seed)
    _w = jnp.asarray

    def _rec_inputs():
        import jax
        import jax.numpy as jnp
        _gk = jax.random.key(seed)
        x = -0.0003713 + 1 * jax.random.normal(jax.random.fold_in(_gk, 1), (3125, 256), jnp.float32)
        src = jax.random.randint(jax.random.fold_in(_gk, 2), (50000,), 0, 3125, jnp.int32)
        dst = jax.random.randint(jax.random.fold_in(_gk, 3), (50000,), 0, 3125, jnp.int32)
        _o = jnp.argsort(dst, stable=True)
        src = src[_o]
        dst = dst[_o]
        return (x, src, dst)
    x, src, dst = _rec_inputs()

    def _L0_gnn_setup():
        import jax, jax.numpy as jnp
        import numpy as np
        N, IN_CH, HEADS, OUT_CH, E = (3125, 256, 4, 64, 50000)
        key = jax.random.key(seed)
        k1, k2, k3, k4, k5 = jax.random.split(key, 5)
        x = jax.random.normal(k1, (N, IN_CH), dtype=jnp.float32)
        edge_index = jax.random.randint(k2, (2, E), 0, N, dtype=jnp.int64)
        bw = float(np.sqrt(6.0 / (IN_CH + HEADS * OUT_CH)))
        ba = float(np.sqrt(6.0 / (HEADS + OUT_CH)))
        weight = jax.random.uniform(k3, (IN_CH, HEADS * OUT_CH), jnp.float32, -bw, bw)
        attn_l = jax.random.uniform(k4, (HEADS, OUT_CH), jnp.float32, -ba, ba)
        attn_r = jax.random.uniform(k5, (HEADS, OUT_CH), jnp.float32, -ba, ba)
        return {'x': x, 'edge_index': edge_index, 'weight': weight, 'attn_l': attn_l, 'attn_r': attn_r}
    _L0_gnn_all = _L0_gnn_setup()
    _L0_gnn_in = {k: v for k, v in _L0_gnn_all.items() if k in ('weight', 'attn_l', 'attn_r')}
    del _L0_gnn_all

    def _L0_mix_setup():
        import jax, jax.numpy as jnp
        import numpy as np
        C_CURV = 1.0
        MIN_NORM = 1e-15
        BALL_EPS = 1e-05
        ATT_EPS = 1e-15
        DIM = 32

        def _norm(x):
            return jnp.clip(jnp.linalg.norm(x, axis=-1, keepdims=True), MIN_NORM)

        def proj(x, c):
            maxnorm = (1.0 - BALL_EPS) / jnp.sqrt(c)
            n = _norm(x)
            return jnp.where(n > maxnorm, x / n * maxnorm, x)

        def expmap0(u, c):
            sc = jnp.sqrt(c)
            n = _norm(u)
            return jnp.tanh(sc * n) * u / (sc * n)

        def logmap0(p, c):
            sc = jnp.sqrt(c)
            n = _norm(p)
            return jnp.arctanh(jnp.clip(sc * n, -1.0 + 1e-07, 1.0 - 1e-07)) * p / (sc * n)

        def mobius_add(x, y, c):
            x2 = jnp.sum(x * x, -1, keepdims=True)
            y2 = jnp.sum(y * y, -1, keepdims=True)
            xy = jnp.sum(x * y, -1, keepdims=True)
            num = (1 + 2 * c * xy + c * y2) * x + (1 - c * x2) * y
            den = 1 + 2 * c * xy + c * c * x2 * y2
            return num / jnp.clip(den, MIN_NORM)

        def conv1d(x, w, pad, groups=1):
            return jax.lax.conv_general_dilated(x, w, (1,), [(pad, pad)], dimension_numbers=('NCH', 'OIH', 'NCH'), feature_group_count=groups)

        def batchnorm(x, gamma, beta):
            mean = jnp.mean(x, axis=(0, 2), keepdims=True)
            var = jnp.var(x, axis=(0, 2), keepdims=True)
            xn = (x - mean) * jax.lax.rsqrt(var + 1e-05)
            return gamma[None, :, None] * xn + beta[None, :, None]

        def _reference_tuple_inner(x, w_qkv, bn_gamma, bn_beta, w_dw, w_pw, w_res, b_res):
            c = C_CURV
            h = logmap0(proj(x, c), c)
            h = jnp.transpose(h, (1, 2, 0))
            h = conv1d(h, w_qkv, pad=2)
            h = batchnorm(h, bn_gamma, bn_beta)
            h = jax.nn.relu(jnp.transpose(h, (2, 0, 1)))
            qkv = proj(expmap0(h, c), c)
            t = jnp.transpose(logmap0(proj(qkv, c), c), (1, 2, 0))
            s = conv1d(t, w_dw, pad=2, groups=t.shape[1])
            s = conv1d(s, w_pw, pad=0, groups=t.shape[1] // DIM)
            cat = jnp.concatenate([t, s], axis=1)
            ai = proj(expmap0(jnp.transpose(cat, (2, 0, 1)), c), c)
            t2 = logmap0(proj(ai, c), c)
            L, N, C2 = t2.shape
            g = C2 // (3 * DIM)
            qkv3 = jnp.transpose(t2, (1, 2, 0)).reshape(N, g, 3 * DIM, L)
            q, k, v = jnp.split(qkv3, 3, axis=2)
            q = jax.nn.relu(q)
            k = jax.nn.relu(k)
            vk = jnp.einsum('ngdl,ngel->ngde', v, k)
            out = jnp.einsum('ngde,ngdl->ngdl', vk, q)
            out = out / (jnp.sum(v, -1, keepdims=True) + ATT_EPS)
            out = jnp.transpose(out.reshape(N, g * DIM, L), (2, 0, 1))
            fx_h = proj(expmap0(out, c), c)
            ft = jnp.transpose(logmap0(proj(fx_h, c), c), (1, 2, 0))
            ft = conv1d(ft, w_res, pad=0) + b_res[None, :, None]
            fx = proj(expmap0(jnp.transpose(ft, (2, 0, 1)), c), c)
            residual = mobius_add(fx, x, c)
            return (fx, residual)
        key = jax.random.key(seed)
        ks = jax.random.split(key, 6)
        L, N, C, TD = (128, 16, 256, 256)
        x = jax.random.normal(ks[0], (L, N, C), jnp.float32) * 0.05
        w_qkv = jax.random.normal(ks[1], (3 * TD, C, 5), jnp.float32) / np.sqrt(C * 5)
        bn_gamma = jnp.ones((3 * TD,), jnp.float32)
        bn_beta = jnp.zeros((3 * TD,), jnp.float32)
        w_dw = jax.random.normal(ks[2], (3 * TD, 1, 5), jnp.float32) / np.sqrt(5.0)
        w_pw = jax.random.normal(ks[3], (3 * TD, DIM, 1), jnp.float32) / np.sqrt(DIM)
        w_res = jax.random.normal(ks[4], (C, 2 * TD, 1), jnp.float32) / np.sqrt(2 * TD)
        b_res = jnp.zeros((C,), jnp.float32)
        return {'x': x, 'w_qkv': w_qkv, 'bn_gamma': bn_gamma, 'bn_beta': bn_beta, 'w_dw': w_dw, 'w_pw': w_pw, 'w_res': w_res, 'b_res': b_res}
    _L0_mix_all = _L0_mix_setup()
    _L0_mix_in = {k: v for k, v in _L0_mix_all.items() if k in ('w_qkv', 'bn_gamma', 'bn_beta', 'w_dw', 'w_pw', 'w_res', 'b_res')}
    del _L0_mix_all

    def _L0_ffn_setup():
        import jax, jax.numpy as jnp
        import numpy as np
        B, N, D = (16, 256, 256)
        NUM_EXPERTS, TOP_K, HEADS = (4, 2, 4)
        N_EDGES = 65536
        LN_EPS = 1e-05

        def _layernorm(x, g, b):
            mu = x.mean(-1, keepdims=True)
            var = ((x - mu) ** 2).mean(-1, keepdims=True)
            return (x - mu) * jax.lax.rsqrt(var + LN_EPS) * g + b

        def _forward(x, edge_index, W_gat, att_src, att_dst, b_gat, ln_gamma, ln_beta, W1, b1, W2, b2):
            Bc, Nc, Dc = x.shape
            M = Bc * Nc
            x_flat = x.reshape(M, Dc)
            h = (x_flat @ W_gat).reshape(M, HEADS, NUM_EXPERTS)
            loops = jnp.arange(M, dtype=edge_index.dtype)
            src = jnp.concatenate([edge_index[0], loops])
            dst = jnp.concatenate([edge_index[1], loops])
            a_src = (h * att_src).sum(-1)
            a_dst = (h * att_dst).sum(-1)
            e = jax.nn.leaky_relu(a_src[src] + a_dst[dst], negative_slope=0.2)
            e_max = jax.ops.segment_max(e, dst, num_segments=M)
            ee = jnp.exp(e - e_max[dst])
            denom = jax.ops.segment_sum(ee, dst, num_segments=M)
            alpha = ee / (denom[dst] + 1e-16)
            msg = h[src] * alpha[:, :, None]
            agg = jax.ops.segment_sum(msg, dst, num_segments=M).reshape(M, HEADS * NUM_EXPERTS) + b_gat
            scores = _layernorm(agg, ln_gamma, ln_beta).reshape(M, HEADS, NUM_EXPERTS).mean(1)
            scores = scores.reshape(Bc, Nc, NUM_EXPERTS)
            topk_s, topk_i = jax.lax.top_k(scores, TOP_K)
            w = jax.nn.softmax(topk_s, axis=-1)
            out = jnp.zeros_like(x)
            for ei in range(NUM_EXPERTS):
                g = jnp.where(topk_i == ei, w, 0.0).sum(-1)
                hh = jax.nn.gelu(x @ W1[ei] + b1[ei], approximate=False)
                out = out + g[..., None] * (hh @ W2[ei] + b2[ei])
            return out
        key = jax.random.key(seed)
        ks = jax.random.split(key, 8)
        s = 0.05
        return {'x': jax.random.normal(ks[0], (B, N, D), jnp.float32), 'W_gat': jax.random.normal(ks[1], (D, HEADS * NUM_EXPERTS), jnp.float32) * s, 'att_src': jax.random.normal(ks[2], (HEADS, NUM_EXPERTS), jnp.float32) * s, 'att_dst': jax.random.normal(ks[3], (HEADS, NUM_EXPERTS), jnp.float32) * s, 'b_gat': jnp.zeros((HEADS * NUM_EXPERTS,), jnp.float32), 'ln_gamma': jnp.ones((HEADS * NUM_EXPERTS,), jnp.float32), 'ln_beta': jnp.zeros((HEADS * NUM_EXPERTS,), jnp.float32), 'W1': jax.random.normal(ks[4], (NUM_EXPERTS, D, 2 * D), jnp.float32) * s, 'b1': jnp.zeros((NUM_EXPERTS, 2 * D), jnp.float32), 'W2': jax.random.normal(ks[5], (NUM_EXPERTS, 2 * D, D), jnp.float32) * s, 'b2': jnp.zeros((NUM_EXPERTS, D), jnp.float32), 'edge_index': jax.random.randint(ks[6], (2, N_EDGES), 0, B * N, jnp.int32)}
    _L0_ffn_all = _L0_ffn_setup()
    _L0_ffn_in = {k: v for k, v in _L0_ffn_all.items() if k in ('W_gat', 'att_src', 'att_dst', 'b_gat', 'ln_gamma', 'ln_beta', 'W1', 'b1', 'W2', 'b2', 'edge_index')}
    del _L0_ffn_all

    def _L1_gnn_setup():
        import jax, jax.numpy as jnp
        import numpy as np
        N_NODES = 3125
        IN_DIM = 256
        OUT_DIM = 128
        NUM_HEADS = 2
        N_EDGES = 50000

        def _gat_forward(x, edge_index, W_w, W_b, a):
            N = x.shape[0]
            H, D = (NUM_HEADS, OUT_DIM)
            Wh = (x @ W_w + W_b).reshape(N, H, D)
            src, dst = (edge_index[0], edge_index[1])
            a_src, a_dst = (a[:D], a[D:])
            s = jnp.einsum('nhd,d->nh', Wh, a_src)
            t = jnp.einsum('nhd,d->nh', Wh, a_dst)
            e = jax.nn.leaky_relu(s[src] + t[dst], negative_slope=0.2)
            m = jax.ops.segment_max(e, src, num_segments=N)
            ex = jnp.exp(e - m[src])
            denom = jax.ops.segment_sum(ex, src, num_segments=N)
            alpha = ex / denom[src]
            agg = jax.ops.segment_sum(alpha[:, :, None] * Wh[dst], src, num_segments=N)
            deg = jax.ops.segment_sum(jnp.ones_like(src, dtype=Wh.dtype), src, num_segments=N)
            h_prime = jnp.where(deg[:, None, None] > 0, agg, Wh)
            return h_prime.reshape(N, H * D)
        key = jax.random.key(seed)
        k1, k2, k3, k4, k5 = jax.random.split(key, 5)
        x = jax.random.normal(k1, (N_NODES, IN_DIM), dtype=jnp.float32)
        edge_index = jax.random.randint(k2, (2, N_EDGES), 0, N_NODES, dtype=jnp.int64)
        fan = IN_DIM + OUT_DIM * NUM_HEADS
        W_w = jax.random.uniform(k3, (IN_DIM, OUT_DIM * NUM_HEADS), dtype=jnp.float32, minval=-np.sqrt(6.0 / fan), maxval=np.sqrt(6.0 / fan))
        W_b = jnp.zeros((OUT_DIM * NUM_HEADS,), dtype=jnp.float32)
        fa = 1 + 2 * OUT_DIM
        a = jax.random.uniform(k4, (2 * OUT_DIM,), dtype=jnp.float32, minval=-np.sqrt(6.0 / fa), maxval=np.sqrt(6.0 / fa))
        return {'x': x, 'edge_index': edge_index, 'W_w': W_w, 'W_b': W_b, 'a': a}
    _L1_gnn_all = _L1_gnn_setup()
    _L1_gnn_in = {k: v for k, v in _L1_gnn_all.items() if k in ('W_w', 'W_b', 'a')}
    del _L1_gnn_all

    def _L1_mix_setup():
        import jax, jax.numpy as jnp
        import numpy as np
        D_MODEL = 256
        NHEAD = 8
        D_HEAD = D_MODEL // NHEAD
        DIM_FF = 1024
        B, L = (4, 1024)
        LN_EPS = 1e-05

        def _layernorm(x, g, b):
            mu = jnp.mean(x, axis=-1, keepdims=True)
            var = jnp.mean((x - mu) ** 2, axis=-1, keepdims=True)
            return (x - mu) * jax.lax.rsqrt(var + LN_EPS) * g + b

        def _phi(x):
            return jnp.where(x > 0, x + 1.0, jnp.exp(x))
        key = jax.random.key(seed)
        ks = jax.random.split(key, 16)
        s_in = 1.0 / np.sqrt(D_MODEL)
        s_ff = 1.0 / np.sqrt(DIM_FF)
        inp = {'x': jax.random.normal(ks[0], (B, L, D_MODEL), dtype=jnp.float32), 'Wq': jax.random.normal(ks[1], (D_MODEL, D_MODEL), dtype=jnp.float32) * s_in, 'bq': jnp.zeros((D_MODEL,), jnp.float32), 'Wk': jax.random.normal(ks[2], (D_MODEL, D_MODEL), dtype=jnp.float32) * s_in, 'bk': jnp.zeros((D_MODEL,), jnp.float32), 'Wv': jax.random.normal(ks[3], (D_MODEL, D_MODEL), dtype=jnp.float32) * s_in, 'bv': jnp.zeros((D_MODEL,), jnp.float32), 'Wo': jax.random.normal(ks[4], (D_MODEL, D_MODEL), dtype=jnp.float32) * s_in, 'bo': jnp.zeros((D_MODEL,), jnp.float32), 'W1': jax.random.normal(ks[5], (D_MODEL, DIM_FF), dtype=jnp.float32) * s_in, 'b1': jnp.zeros((DIM_FF,), jnp.float32), 'W2': jax.random.normal(ks[6], (DIM_FF, D_MODEL), dtype=jnp.float32) * s_ff, 'b2': jnp.zeros((D_MODEL,), jnp.float32), 'ln1_g': jnp.ones((D_MODEL,), jnp.float32), 'ln1_b': jnp.zeros((D_MODEL,), jnp.float32), 'ln2_g': jnp.ones((D_MODEL,), jnp.float32), 'ln2_b': jnp.zeros((D_MODEL,), jnp.float32)}
        return inp
    _L1_mix_all = _L1_mix_setup()
    _L1_mix_in = {k: v for k, v in _L1_mix_all.items() if k in ('Wq', 'bq', 'Wk', 'bk', 'Wv', 'bv', 'Wo', 'bo', 'W1', 'b1', 'W2', 'b2', 'ln1_g', 'ln1_b', 'ln2_g', 'ln2_b')}
    del _L1_mix_all

    def _L1_ffn_setup():
        import jax, jax.numpy as jnp
        import numpy as np
        B, S, D, F, E, K = (8, 128, 256, 1024, 8, 2)
        key = jax.random.key(seed)
        ks = jax.random.split(key, 10)
        s = 0.02
        return {'x': jax.random.normal(ks[0], (B, S, D), dtype=jnp.float32), 'Wr': jax.random.normal(ks[1], (D, E), dtype=jnp.float32) * s, 'W1s': jax.random.normal(ks[2], (D, F), dtype=jnp.float32) * s, 'b1s': jnp.zeros((F,), dtype=jnp.float32), 'W2s': jax.random.normal(ks[3], (F, D), dtype=jnp.float32) * s, 'b2s': jnp.zeros((D,), dtype=jnp.float32), 'W1p': jax.random.normal(ks[4], (E, D, F), dtype=jnp.float32) * s, 'b1p': jnp.zeros((E, F), dtype=jnp.float32), 'W2p': jax.random.normal(ks[5], (E, F, D), dtype=jnp.float32) * s, 'b2p': jnp.zeros((E, D), dtype=jnp.float32)}
    _L1_ffn_all = _L1_ffn_setup()
    _L1_ffn_in = {k: v for k, v in _L1_ffn_all.items() if k in ('Wr', 'W1s', 'b1s', 'W2s', 'b2s', 'W1p', 'b1p', 'W2p', 'b2p')}
    del _L1_ffn_all
    return {'x': x, 'src': src, 'dst': dst, 'L0_gnn_weight': _L0_gnn_in['weight'], 'L0_gnn_attn_l': _L0_gnn_in['attn_l'], 'L0_gnn_attn_r': _L0_gnn_in['attn_r'], 'L0_mix_w_qkv': _L0_mix_in['w_qkv'], 'L0_mix_bn_gamma': _L0_mix_in['bn_gamma'], 'L0_mix_bn_beta': _L0_mix_in['bn_beta'], 'L0_mix_w_dw': _L0_mix_in['w_dw'], 'L0_mix_w_pw': _L0_mix_in['w_pw'], 'L0_mix_w_res': _L0_mix_in['w_res'], 'L0_mix_b_res': _L0_mix_in['b_res'], 'L0_ffn_W_gat': _L0_ffn_in['W_gat'], 'L0_ffn_att_src': _L0_ffn_in['att_src'], 'L0_ffn_att_dst': _L0_ffn_in['att_dst'], 'L0_ffn_b_gat': _L0_ffn_in['b_gat'], 'L0_ffn_ln_gamma': _L0_ffn_in['ln_gamma'], 'L0_ffn_ln_beta': _L0_ffn_in['ln_beta'], 'L0_ffn_W1': _L0_ffn_in['W1'], 'L0_ffn_b1': _L0_ffn_in['b1'], 'L0_ffn_W2': _L0_ffn_in['W2'], 'L0_ffn_b2': _L0_ffn_in['b2'], 'L0_ffn_edge_index': _L0_ffn_in['edge_index'], 'L1_gnn_W_w': _L1_gnn_in['W_w'], 'L1_gnn_W_b': _L1_gnn_in['W_b'], 'L1_gnn_a': _L1_gnn_in['a'], 'L1_mix_Wq': _L1_mix_in['Wq'], 'L1_mix_bq': _L1_mix_in['bq'], 'L1_mix_Wk': _L1_mix_in['Wk'], 'L1_mix_bk': _L1_mix_in['bk'], 'L1_mix_Wv': _L1_mix_in['Wv'], 'L1_mix_bv': _L1_mix_in['bv'], 'L1_mix_Wo': _L1_mix_in['Wo'], 'L1_mix_bo': _L1_mix_in['bo'], 'L1_mix_W1': _L1_mix_in['W1'], 'L1_mix_b1': _L1_mix_in['b1'], 'L1_mix_W2': _L1_mix_in['W2'], 'L1_mix_b2': _L1_mix_in['b2'], 'L1_mix_ln1_g': _L1_mix_in['ln1_g'], 'L1_mix_ln1_b': _L1_mix_in['ln1_b'], 'L1_mix_ln2_g': _L1_mix_in['ln2_g'], 'L1_mix_ln2_b': _L1_mix_in['ln2_b'], 'L1_ffn_Wr': _L1_ffn_in['Wr'], 'L1_ffn_W1s': _L1_ffn_in['W1s'], 'L1_ffn_b1s': _L1_ffn_in['b1s'], 'L1_ffn_W2s': _L1_ffn_in['W2s'], 'L1_ffn_b2s': _L1_ffn_in['b2s'], 'L1_ffn_W1p': _L1_ffn_in['W1p'], 'L1_ffn_b1p': _L1_ffn_in['b1p'], 'L1_ffn_W2p': _L1_ffn_in['W2p'], 'L1_ffn_b2p': _L1_ffn_in['b2p']}

def reference(x, src, dst, L0_gnn_weight, L0_gnn_attn_l, L0_gnn_attn_r, L0_mix_w_qkv, L0_mix_bn_gamma, L0_mix_bn_beta, L0_mix_w_dw, L0_mix_w_pw, L0_mix_w_res, L0_mix_b_res, L0_ffn_W_gat, L0_ffn_att_src, L0_ffn_att_dst, L0_ffn_b_gat, L0_ffn_ln_gamma, L0_ffn_ln_beta, L0_ffn_W1, L0_ffn_b1, L0_ffn_W2, L0_ffn_b2, L0_ffn_edge_index, L1_gnn_W_w, L1_gnn_W_b, L1_gnn_a, L1_mix_Wq, L1_mix_bq, L1_mix_Wk, L1_mix_bk, L1_mix_Wv, L1_mix_bv, L1_mix_Wo, L1_mix_bo, L1_mix_W1, L1_mix_b1, L1_mix_W2, L1_mix_b2, L1_mix_ln1_g, L1_mix_ln1_b, L1_mix_ln2_g, L1_mix_ln2_b, L1_ffn_Wr, L1_ffn_W1s, L1_ffn_b1s, L1_ffn_W2s, L1_ffn_b2s, L1_ffn_W1p, L1_ffn_b1p, L1_ffn_W2p, L1_ffn_b2p):
    import jax
    import jax.numpy as jnp

    def _L0_gnn_ref(x, edge_index, weight, attn_l, attn_r):
        import jax, jax.numpy as jnp
        import numpy as np
        N, IN_CH, HEADS, OUT_CH, E = (3125, 256, 4, 64, 50000)
        heads, out_ch = attn_l.shape
        n = x.shape[0]
        xt = jnp.matmul(x, weight).reshape(-1, heads, out_ch)
        row, col = (edge_index[0], edge_index[1])
        alpha_l = jnp.einsum('ehd,hd->eh', xt[row], attn_l)
        alpha_r = jnp.einsum('ehd,hd->eh', xt[col], attn_r)
        alpha = jax.nn.softmax(jax.nn.leaky_relu(alpha_l + alpha_r, 0.01), axis=1)
        tmp = jnp.einsum('nh,nhd->nd', alpha[:n], xt[col[:n]])
        out = jnp.broadcast_to(tmp[:, None, :], (n, heads, out_ch))
        return out.reshape(n, heads * out_ch)

    def _L0_mix_ref(x, w_qkv, bn_gamma, bn_beta, w_dw, w_pw, w_res, b_res):
        import jax, jax.numpy as jnp
        import numpy as np
        C_CURV = 1.0
        MIN_NORM = 1e-15
        BALL_EPS = 1e-05
        ATT_EPS = 1e-15
        DIM = 32

        def _norm(x):
            return jnp.clip(jnp.linalg.norm(x, axis=-1, keepdims=True), MIN_NORM)

        def proj(x, c):
            maxnorm = (1.0 - BALL_EPS) / jnp.sqrt(c)
            n = _norm(x)
            return jnp.where(n > maxnorm, x / n * maxnorm, x)

        def expmap0(u, c):
            sc = jnp.sqrt(c)
            n = _norm(u)
            return jnp.tanh(sc * n) * u / (sc * n)

        def logmap0(p, c):
            sc = jnp.sqrt(c)
            n = _norm(p)
            return jnp.arctanh(jnp.clip(sc * n, -1.0 + 1e-07, 1.0 - 1e-07)) * p / (sc * n)

        def mobius_add(x, y, c):
            x2 = jnp.sum(x * x, -1, keepdims=True)
            y2 = jnp.sum(y * y, -1, keepdims=True)
            xy = jnp.sum(x * y, -1, keepdims=True)
            num = (1 + 2 * c * xy + c * y2) * x + (1 - c * x2) * y
            den = 1 + 2 * c * xy + c * c * x2 * y2
            return num / jnp.clip(den, MIN_NORM)

        def conv1d(x, w, pad, groups=1):
            return jax.lax.conv_general_dilated(x, w, (1,), [(pad, pad)], dimension_numbers=('NCH', 'OIH', 'NCH'), feature_group_count=groups)

        def batchnorm(x, gamma, beta):
            mean = jnp.mean(x, axis=(0, 2), keepdims=True)
            var = jnp.var(x, axis=(0, 2), keepdims=True)
            xn = (x - mean) * jax.lax.rsqrt(var + 1e-05)
            return gamma[None, :, None] * xn + beta[None, :, None]

        def _reference_tuple_inner(x, w_qkv, bn_gamma, bn_beta, w_dw, w_pw, w_res, b_res):
            c = C_CURV
            h = logmap0(proj(x, c), c)
            h = jnp.transpose(h, (1, 2, 0))
            h = conv1d(h, w_qkv, pad=2)
            h = batchnorm(h, bn_gamma, bn_beta)
            h = jax.nn.relu(jnp.transpose(h, (2, 0, 1)))
            qkv = proj(expmap0(h, c), c)
            t = jnp.transpose(logmap0(proj(qkv, c), c), (1, 2, 0))
            s = conv1d(t, w_dw, pad=2, groups=t.shape[1])
            s = conv1d(s, w_pw, pad=0, groups=t.shape[1] // DIM)
            cat = jnp.concatenate([t, s], axis=1)
            ai = proj(expmap0(jnp.transpose(cat, (2, 0, 1)), c), c)
            t2 = logmap0(proj(ai, c), c)
            L, N, C2 = t2.shape
            g = C2 // (3 * DIM)
            qkv3 = jnp.transpose(t2, (1, 2, 0)).reshape(N, g, 3 * DIM, L)
            q, k, v = jnp.split(qkv3, 3, axis=2)
            q = jax.nn.relu(q)
            k = jax.nn.relu(k)
            vk = jnp.einsum('ngdl,ngel->ngde', v, k)
            out = jnp.einsum('ngde,ngdl->ngdl', vk, q)
            out = out / (jnp.sum(v, -1, keepdims=True) + ATT_EPS)
            out = jnp.transpose(out.reshape(N, g * DIM, L), (2, 0, 1))
            fx_h = proj(expmap0(out, c), c)
            ft = jnp.transpose(logmap0(proj(fx_h, c), c), (1, 2, 0))
            ft = conv1d(ft, w_res, pad=0) + b_res[None, :, None]
            fx = proj(expmap0(jnp.transpose(ft, (2, 0, 1)), c), c)
            residual = mobius_add(fx, x, c)
            return (fx, residual)
        return _reference_tuple_inner(x, w_qkv, bn_gamma, bn_beta, w_dw, w_pw, w_res, b_res)[0]

    def _L0_ffn_ref(x, W_gat, att_src, att_dst, b_gat, ln_gamma, ln_beta, W1, b1, W2, b2, edge_index):
        import jax, jax.numpy as jnp
        import numpy as np
        B, N, D = (16, 256, 256)
        NUM_EXPERTS, TOP_K, HEADS = (4, 2, 4)
        N_EDGES = 65536
        LN_EPS = 1e-05

        def _layernorm(x, g, b):
            mu = x.mean(-1, keepdims=True)
            var = ((x - mu) ** 2).mean(-1, keepdims=True)
            return (x - mu) * jax.lax.rsqrt(var + LN_EPS) * g + b

        def _forward(x, edge_index, W_gat, att_src, att_dst, b_gat, ln_gamma, ln_beta, W1, b1, W2, b2):
            Bc, Nc, Dc = x.shape
            M = Bc * Nc
            x_flat = x.reshape(M, Dc)
            h = (x_flat @ W_gat).reshape(M, HEADS, NUM_EXPERTS)
            loops = jnp.arange(M, dtype=edge_index.dtype)
            src = jnp.concatenate([edge_index[0], loops])
            dst = jnp.concatenate([edge_index[1], loops])
            a_src = (h * att_src).sum(-1)
            a_dst = (h * att_dst).sum(-1)
            e = jax.nn.leaky_relu(a_src[src] + a_dst[dst], negative_slope=0.2)
            e_max = jax.ops.segment_max(e, dst, num_segments=M)
            ee = jnp.exp(e - e_max[dst])
            denom = jax.ops.segment_sum(ee, dst, num_segments=M)
            alpha = ee / (denom[dst] + 1e-16)
            msg = h[src] * alpha[:, :, None]
            agg = jax.ops.segment_sum(msg, dst, num_segments=M).reshape(M, HEADS * NUM_EXPERTS) + b_gat
            scores = _layernorm(agg, ln_gamma, ln_beta).reshape(M, HEADS, NUM_EXPERTS).mean(1)
            scores = scores.reshape(Bc, Nc, NUM_EXPERTS)
            topk_s, topk_i = jax.lax.top_k(scores, TOP_K)
            w = jax.nn.softmax(topk_s, axis=-1)
            out = jnp.zeros_like(x)
            for ei in range(NUM_EXPERTS):
                g = jnp.where(topk_i == ei, w, 0.0).sum(-1)
                hh = jax.nn.gelu(x @ W1[ei] + b1[ei], approximate=False)
                out = out + g[..., None] * (hh @ W2[ei] + b2[ei])
            return out
        return _forward(x, edge_index, W_gat, att_src, att_dst, b_gat, ln_gamma, ln_beta, W1, b1, W2, b2)

    def _L1_gnn_ref(x, edge_index, W_w, W_b, a):
        import jax, jax.numpy as jnp
        import numpy as np
        N_NODES = 3125
        IN_DIM = 256
        OUT_DIM = 128
        NUM_HEADS = 2
        N_EDGES = 50000

        def _gat_forward(x, edge_index, W_w, W_b, a):
            N = x.shape[0]
            H, D = (NUM_HEADS, OUT_DIM)
            Wh = (x @ W_w + W_b).reshape(N, H, D)
            src, dst = (edge_index[0], edge_index[1])
            a_src, a_dst = (a[:D], a[D:])
            s = jnp.einsum('nhd,d->nh', Wh, a_src)
            t = jnp.einsum('nhd,d->nh', Wh, a_dst)
            e = jax.nn.leaky_relu(s[src] + t[dst], negative_slope=0.2)
            m = jax.ops.segment_max(e, src, num_segments=N)
            ex = jnp.exp(e - m[src])
            denom = jax.ops.segment_sum(ex, src, num_segments=N)
            alpha = ex / denom[src]
            agg = jax.ops.segment_sum(alpha[:, :, None] * Wh[dst], src, num_segments=N)
            deg = jax.ops.segment_sum(jnp.ones_like(src, dtype=Wh.dtype), src, num_segments=N)
            h_prime = jnp.where(deg[:, None, None] > 0, agg, Wh)
            return h_prime.reshape(N, H * D)
        return _gat_forward(x, edge_index, W_w, W_b, a)

    def _L1_mix_ref(x, Wq, bq, Wk, bk, Wv, bv, Wo, bo, W1, b1, W2, b2, ln1_g, ln1_b, ln2_g, ln2_b):
        import jax, jax.numpy as jnp
        import numpy as np
        D_MODEL = 256
        NHEAD = 8
        D_HEAD = D_MODEL // NHEAD
        DIM_FF = 1024
        B, L = (4, 1024)
        LN_EPS = 1e-05

        def _layernorm(x, g, b):
            mu = jnp.mean(x, axis=-1, keepdims=True)
            var = jnp.mean((x - mu) ** 2, axis=-1, keepdims=True)
            return (x - mu) * jax.lax.rsqrt(var + LN_EPS) * g + b

        def _phi(x):
            return jnp.where(x > 0, x + 1.0, jnp.exp(x))
        Bq, Lq, _ = x.shape
        q = (x @ Wq + bq).reshape(Bq, Lq, NHEAD, D_HEAD)
        k = (x @ Wk + bk).reshape(Bq, Lq, NHEAD, D_HEAD)
        v = (x @ Wv + bv).reshape(Bq, Lq, NHEAD, D_HEAD)
        q_phi = _phi(q)
        k_phi = _phi(k)
        kv = jnp.einsum('blhd,blhe->bhde', k_phi, v)
        k_sum = k_phi.sum(axis=1)
        z = 1.0 / (jnp.einsum('blhd,bhd->blh', q_phi, k_sum) + 1e-06)
        out = jnp.einsum('blhd,bhde,blh->blhe', q_phi, kv, z)
        out = out.reshape(Bq, Lq, D_MODEL) @ Wo + bo
        x = _layernorm(x + out, ln1_g, ln1_b)
        ff = jax.nn.relu(x @ W1 + b1) @ W2 + b2
        x = _layernorm(x + ff, ln2_g, ln2_b)
        return x

    def _L1_ffn_ref(x, Wr, W1s, b1s, W2s, b2s, W1p, b1p, W2p, b2p):
        import jax, jax.numpy as jnp
        import numpy as np
        B, S, D, F, E, K = (8, 128, 256, 1024, 8, 2)
        gelu = lambda t: jax.nn.gelu(t, approximate=False)
        shared = gelu(x @ W1s + b1s) @ W2s + b2s
        rw = jax.nn.softmax(x @ Wr, axis=-1)
        topw, topi = jax.lax.top_k(rw, K)
        topw = topw / jnp.sum(topw, axis=-1, keepdims=True)
        mask = jnp.sum(jax.nn.one_hot(topi, E, dtype=topw.dtype) * topw[..., None], axis=-2)
        h = gelu(jnp.einsum('bsd,edf->bsef', x, W1p) + b1p)
        priv = jnp.einsum('bsef,efd->bsed', h, W2p) + b2p
        routed = jnp.einsum('bsed,bse->bsd', priv, mask)
        return shared + routed
    edge_index = jnp.stack([src, dst])
    xn = _layernorm(x, axis=-1)
    x = x + _L0_gnn_ref(xn, edge_index, L0_gnn_weight, L0_gnn_attn_l, L0_gnn_attn_r) + _L0_mix_ref(xn[None], L0_mix_w_qkv, L0_mix_bn_gamma, L0_mix_bn_beta, L0_mix_w_dw, L0_mix_w_pw, L0_mix_w_res, L0_mix_b_res)[0]
    x = x + _L0_ffn_ref(_layernorm(x, axis=-1)[None], L0_ffn_W_gat, L0_ffn_att_src, L0_ffn_att_dst, L0_ffn_b_gat, L0_ffn_ln_gamma, L0_ffn_ln_beta, L0_ffn_W1, L0_ffn_b1, L0_ffn_W2, L0_ffn_b2, L0_ffn_edge_index)[0]
    xn = _layernorm(x, axis=-1)
    x = x + _L1_gnn_ref(xn, edge_index, L1_gnn_W_w, L1_gnn_W_b, L1_gnn_a) + _L1_mix_ref(xn[None], L1_mix_Wq, L1_mix_bq, L1_mix_Wk, L1_mix_bk, L1_mix_Wv, L1_mix_bv, L1_mix_Wo, L1_mix_bo, L1_mix_W1, L1_mix_b1, L1_mix_W2, L1_mix_b2, L1_mix_ln1_g, L1_mix_ln1_b, L1_mix_ln2_g, L1_mix_ln2_b)[0]
    x = x + _L1_ffn_ref(_layernorm(x, axis=-1)[None], L1_ffn_Wr, L1_ffn_W1s, L1_ffn_b1s, L1_ffn_W2s, L1_ffn_b2s, L1_ffn_W1p, L1_ffn_b1p, L1_ffn_W2p, L1_ffn_b2p)[0]
    return x

_drawn_inputs = setup_inputs


def setup_inputs(seed=0):
    import zlib

    import numpy as np

    out = dict(_drawn_inputs(seed))
    spreads = {'L0_mix_bn_gamma': (1.0, 0.6),
     'L0_mix_bn_beta': (0.0, 0.293),
     'L0_mix_b_res': (0.0, 0.1),
     'L0_ffn_b_gat': (0.0, 0.1),
     'L0_ffn_ln_gamma': (1.0, 0.2),
     'L0_ffn_ln_beta': (0.0, 0.1),
     'L0_ffn_b1': (0.0, 0.1),
     'L0_ffn_b2': (0.0, 0.1),
     'L1_gnn_W_b': (0.0, 0.1),
     'L1_mix_bq': (0.0, 0.8),
     'L1_mix_bk': (0.0, 0.8),
     'L1_mix_bv': (0.0, 0.1),
     'L1_mix_bo': (0.0, 0.1),
     'L1_mix_b1': (0.0, 0.295),
     'L1_mix_b2': (0.0, 0.1),
     'L1_mix_ln1_g': (1.0, 0.2),
     'L1_mix_ln1_b': (0.0, 0.1),
     'L1_mix_ln2_g': (1.0, 0.2),
     'L1_mix_ln2_b': (0.0, 0.1),
     'L1_ffn_b1s': (0.0, 0.51),
     'L1_ffn_b2s': (0.0, 0.1),
     'L1_ffn_b1p': (0.0, 0.701),
     'L1_ffn_b2p': (0.0, 0.1)}
    factors = {'L0_mix_w_pw': 3.141, 'L1_mix_Wq': 8.0, 'L1_mix_Wk': 8.0}
    for name, (base, spread) in spreads.items():
        noise = np.random.default_rng([zlib.crc32(name.encode()), seed]).standard_normal(out[name].shape)
        drawn = base * np.exp(spread * noise) if base else spread * noise
        out[name] = jnp.asarray(drawn.astype(out[name].dtype))
    for name, factor in factors.items():
        out[name] = (out[name] * factor).astype(out[name].dtype)
    return out
```

```python
import math
import numpy as np
import concourse.bass as bass
from concourse import mybir
from contextlib import ExitStack

FP32 = mybir.dt.float32
FP16 = mybir.dt.float16
BF16 = mybir.dt.bfloat16
I32 = mybir.dt.int32
ALU = mybir.AluOpType
ACT = mybir.ActivationFunctionType
AX = mybir.AxisListType

N = 3125
P = 125
NT = N // P
D = 256
K2 = D // 128
CH = 4 * P
NCH = N // CH
BIG = 1e30
MIN_NORM = 1e-15
MAX_NORM = float(np.float32(1.0 - 1e-5))
MAX_ATANH = 0.5 * math.log((1 + MAX_NORM) / (1 - MAX_NORM))
KEYS = 4096
KB = 32
COLS0 = 512
COLS1 = 400
BC = 16


class Net:

    def __init__(self, nc, io):
        self.nc, self.io = nc, io
        self.keep = ExitStack()
        self.scope = self.keep
        self.sems = []

    def sem(self, name):
        self.sems.append(self.nc.alloc_semaphore(name))
        return self.sems[-1]

    def sb(self, name, shape, dt=FP32):
        return self.scope.enter_context(self.nc.sbuf_tensor(name, shape, dt))

    def dram(self, name, shape, dt=FP32):
        return self.nc.dram_tensor(name, shape, dt).ap()


class Stage:

    def __init__(self, m):
        self.m = m

    def __enter__(self):
        self.outer, self.m.scope = self.m.scope, ExitStack()
        self.sems, self.m.sems = self.m.sems, []
        return self

    def __exit__(self, *a):
        self.m.scope.close()
        self.m.scope = self.outer
        self.m.nc.clear_and_free_semaphores(self.m.sems)
        self.m.nc.all_engine_barrier()
        self.m.sems = self.sems


class Loads:

    def __init__(self, m, name):
        self.sem, self.all = m.sem(name), 0

    def __call__(self, eng, dst, src):
        self.all += 16
        eng.dma_start(dst, src).then_inc(self.sem, 16)


def tiles(eng, total, unroll, body):
    whole = total // unroll
    with eng.Fori(0, whole) as i:
        for j in range(unroll):
            body(i * unroll + j, j)
    for j in range(total - whole * unroll):
        body(whole * unroll + j, j)


def chunks(eng, body):
    with eng.Fori(0, NCH) as c:
        body(c, 4)
    body(NCH, 1)


def tiles_written_out(total, unroll, body):
    for t in range(total):
        body(t, t % unroll)


def chunks_written_out(body):
    for c in range(NCH):
        body(c, 4)
    body(NCH, 1)


def at(t, size):
    return bass.ds(t * size, size)


def constants(m):
    nc = m.nc
    m.X = m.sb("X", [P, NT * D])
    m.ident = m.sb("ident", [128, 128])
    m.ps = [m.keep.enter_context(nc.psum_tensor(f"bank{i}", [128, 512], FP32)) for i in range(8)]
    m.spare = m.sem("spare")
    loaded = m.sem("x_loaded")
    with nc.Block() as block:
        @block.sync
        def _(sp):
            sp.dma_start(m.X[:, :].rearrange("p (t d) -> p t d", d=D),
                         m.io["x"].rearrange("(t p) d -> p t d", p=P)).then_inc(loaded, 16)
            sp.wait_ge(loaded, 16)

        @block.gpsimd
        def _(pool):
            pool.memset(m.ident[:, :], 0.0)
            pool.drain()
            pool.affine_select(out=m.ident[:, :], in_=m.ident[:, :], compare_op=ALU.not_equal, fill=1.0,
                               base=0, pattern=[[-1, 128]], channel_multiplier=1)
            pool.drain()


def turn_tiles(m, block, tag, ready, first=None):
    turned, moved = m.sem(tag + "_turned"), m.sem(tag + "_moved")
    xt = m.XT[:, :].rearrange("p (k n) -> p k n", k=K2)

    @block.tensor
    def _(pe):
        def body(t, j):
            pe.wait_ge(ready, t + 1)
            pe.wait_ge(moved, t + 1)
            for k in range(K2):
                last = pe.transpose(m.ps[j][:, k * P:(k + 1) * P], m.XN[:, bass.ds(t * D + k * 128, 128)],
                                    m.ident[:P, :P])
            last.then_inc(turned, 1)
        tiles_written_out(NT, 4, body)

    @block.scalar
    def _(act):
        act.sem_inc(moved, 4)
        if first is not None:
            first(act)

        def body(t, j):
            act.wait_ge(turned, t + 1)
            act.copy(xt[:, :, at(t, P)],
                     m.ps[j][:, 0:K2 * P].rearrange("p (k n) -> p k n", k=K2)).then_inc(moved, 1)
        tiles(act, NT, 4, body)


def moments(dve, s3, mean, var, tmp, count):
    dve.tensor_tensor(mean, s3[:, :, 1], s3[:, :, 4], ALU.add)
    dve.tensor_tensor(tmp, s3[:, :, 1], s3[:, :, 4], ALU.subtract)
    dve.tensor_tensor(var, s3[:, :, 2], s3[:, :, 5], ALU.add)
    dve.drain()
    dve.tensor_scalar(mean, mean, 0.5, None, ALU.mult)
    dve.tensor_scalar(tmp, tmp, 0.5, None, ALU.mult)
    dve.tensor_scalar(var, var, 1.0 / count, 1e-5, ALU.mult, ALU.add)
    dve.drain()
    dve.tensor_tensor(tmp, tmp, tmp, ALU.mult)
    dve.drain()
    return dve.tensor_tensor(var, var, tmp, ALU.add)


def layer_norm(m, tag):
    nc = m.nc
    with Stage(m):
        st = m.sb(tag + "_stats", [P, NT * 6])
        mean, var, tmp, rstd = (m.sb(tag + x, [P, NT]) for x in ("_mean", "_var", "_tmp", "_rstd"))
        var_ready, std_ready, normed = m.sem(tag + "_var_ready"), m.sem(tag + "_std_ready"), m.sem(tag + "_normed")
        s3 = st[:, :].rearrange("p (t s) -> p t s", s=6)
        with nc.Block() as block:
            @block.vector
            def _(dve):
                tiles(dve, NT, 5, lambda t, j: dve.bn_stats(st[:, at(t, 6)], m.X[:, at(t, D)]))
                dve.drain()
                moments(dve, s3, mean[:, :], var[:, :], tmp[:, :], D).then_inc(var_ready, 1)
                dve.wait_ge(std_ready, 1)
                dve.reciprocal(rstd[:, :], var[:, :])
                dve.drain()
                tiles(dve, NT, 5, lambda t, j: dve.tensor_scalar(
                    m.XN[:, at(t, D)], m.X[:, at(t, D)], mean[:, at(t, 1)], rstd[:, at(t, 1)],
                    ALU.subtract, ALU.mult).then_inc(normed, 1))

            def root(act):
                act.wait_ge(var_ready, 1)
                act.sqrt(var[:, :], var[:, :]).then_inc(std_ready, 1)
            turn_tiles(m, block, tag, normed, root)


def gnn0_nodes(m):
    nc, io = m.nc, m.io
    H, C = 4, 64
    ROW = D + 2 * H
    m.xt_dram = m.dram("xt_dram", [N, D + H])
    m.al_dram = m.dram("al_dram", [N, H])
    with Stage(m):
        w = m.sb("g0_w", [128, K2, ROW])
        att = m.sb("g0_att", [128, 2, D])
        prod = m.sb("g0_prod", [128, 2, K2, D])
        table = m.sb("g0_table", [P, NT * ROW])
        loads, stored = Loads(m, "g0_loaded"), Loads(m, "g0_stored")
        w_ready, made, kept = m.sem("g0_w_ready"), m.sem("g0_made"), m.sem("g0_kept")
        with nc.Block() as block:
            @block.sync
            def _(sp):
                loads(sp, w[:, :, 0:D], io["L0_gnn_weight"].rearrange("(k p) d -> p k d", p=128))
                for i, name in enumerate(("L0_gnn_attn_r", "L0_gnn_attn_l")):
                    loads(sp, att[:, i, :], io[name].rearrange("h c -> (h c)").partition_broadcast(128))
                sp.wait_ge(kept, NT + 4)
                t3 = table[:, :].rearrange("p (t c) -> p t c", c=ROW)
                stored(sp, m.xt_dram.rearrange("(t p) c -> p t c", p=P), t3[:, :, 0:D + H])
                stored(sp, m.al_dram.rearrange("(t p) c -> p t c", p=P), t3[:, :, D + H:])
                sp.wait_ge(stored.sem, stored.all)

            @block.vector
            def _(dve):
                dve.wait_ge(loads.sem, 48)
                for i in range(2):
                    for k in range(K2):
                        dve.tensor_tensor(prod[:, i, k, :], w[:, k, 0:D], att[:, i, :], ALU.mult)
                dve.drain()
                for i in range(2):
                    for k in range(K2):
                        last = dve.tensor_reduce(w[:, k, D + H * i:D + H * (i + 1)],
                                                 prod[:, i, k, :].rearrange("p (h c) -> p h c", h=H), AX.X, ALU.add)
                last.then_inc(w_ready, 1)

            @block.tensor
            def _(pe):
                pe.wait_ge(w_ready, 1)

                def body(t, j):
                    pe.wait_ge(kept, t + 1)
                    for k in range(K2):
                        last = pe.matmul(m.ps[j][:P, 0:ROW], m.XT[:, bass.ds(t * P + k * N, P)], w[:, k, :],
                                         start=k == 0, stop=k == K2 - 1)
                    last.then_inc(made, 1)
                tiles_written_out(NT, 4, body)

            @block.scalar
            def _(act):
                act.sem_inc(kept, 4)

                def body(t, j):
                    act.wait_ge(made, t + 1)
                    act.copy(table[:, at(t, ROW)], m.ps[j][:P, 0:ROW]).then_inc(kept, 1)
                tiles(act, NT, 4, body)


def gnn0_edges(m):
    nc, io = m.nc, m.io
    H, C = 4, 64
    with Stage(m):
        idx = m.sb("g0_idx", [P, 2, NT], I32)
        near = m.sb("g0_near", [P, NT, D + H])
        al = m.sb("g0_al", [P, NT, H])
        e = m.sb("g0_e", [P, NT, H])
        tot = m.sb("g0_tot", [P, NT])
        mix = m.sb("g0_mix", [P, NT, C])
        loads, rows = Loads(m, "g0_idx_loaded"), Loads(m, "g0_rows")
        e_ready, e_exp = m.sem("g0_e_ready"), m.sem("g0_e_exp")
        with nc.Block() as block:
            @block.sync
            def _(sp):
                loads(sp, idx[:, 0, :], io["first_dst"])
                loads(sp, idx[:, 1, :], io["first_src"])

            @block.gpsimd
            def _(pool):
                pool.wait_ge(loads.sem, 32)
                for t in range(NT):
                    for dst, table, i in ((near, m.xt_dram, 0), (al, m.al_dram, 1)):
                        rows.all += 16
                        pool.indirect_dma_start(
                            out=dst[:, t, :], out_offset=None, in_=table,
                            in_offset=bass.IndirectOffsetOnAxis(ap=idx[:, i, t:t + 1], axis=0)).then_inc(rows.sem, 16)

            @block.vector
            def _(dve):
                dve.wait_ge(rows.sem, rows.all)
                dve.tensor_tensor(e[:, :, :], al[:, :, :], near[:, :, D:], ALU.add)
                dve.drain()
                dve.scalar_tensor_tensor(e[:, :, :], e[:, :, :], 0.01, e[:, :, :], ALU.mult, ALU.max)
                dve.drain()
                dve.tensor_reduce(tot[:, :], e[:, :, :], AX.X, ALU.max)
                dve.drain()
                wide = tot[:, :].unsqueeze(2).broadcast_to((P, NT, H))
                dve.tensor_tensor(e[:, :, :], e[:, :, :], wide, ALU.subtract).then_inc(e_ready, 1)
                dve.wait_ge(e_exp, 1)
                dve.tensor_reduce(tot[:, :], e[:, :, :], AX.X, ALU.add)
                dve.drain()
                dve.reciprocal(tot[:, :], tot[:, :])
                dve.drain()
                dve.tensor_tensor(e[:, :, :], e[:, :, :], wide, ALU.mult)
                dve.drain()
                heads = near[:, :, 0:D].rearrange("p t (h c) -> p t h c", h=H)
                for t in range(NT):
                    dve.tensor_tensor(heads[:, t], heads[:, t],
                                      e[:, t, :].unsqueeze(2).broadcast_to((P, H, C)), ALU.mult)
                dve.drain()
                dve.tensor_reduce(mix[:, :, :], near[:, :, 0:D].rearrange("p t (h c) -> p t c h", h=H), AX.X, ALU.add)
                dve.drain()
                x4 = m.X[:, :].rearrange("p (t h c) -> p t h c", t=NT, h=H)
                for h in range(H):
                    dve.tensor_tensor(x4[:, :, h, :], x4[:, :, h, :], mix[:, :, :], ALU.add)

            @block.scalar
            def _(act):
                act.wait_ge(e_ready, 1)
                act.activation(e[:, :, :], e[:, :, :], ACT.Exp).then_inc(e_exp, 1)


def mix0_log(m):
    nc = m.nc
    with Stage(m):
        junk = m.sb("lg_junk", [P, 5, D])
        ss, n, r, a, b, c = (m.sb("lg_" + x, [P, NT]) for x in ("ss", "n", "r", "a", "b", "c"))
        ss_ready, root, ratio, logged, scaled = (m.sem("lg_" + x) for x in ("ss_ready", "root", "ratio", "logged", "scaled"))
        with nc.Block() as block:
            @block.vector
            def _(dve):
                def squares(t, j):
                    if j == 0:
                        dve.drain()
                    dve.scalar_tensor_tensor(junk[:, j, :], m.XN[:, at(t, D)], 1.0, m.XN[:, at(t, D)],
                                             ALU.mult, ALU.mult, accum_out=ss[:, at(t, 1)])
                tiles(dve, NT, 5, squares)
                dve.drain().then_inc(ss_ready, 1)
                dve.wait_ge(root, 1)
                dve.tensor_scalar(n[:, :], n[:, :], MIN_NORM, None, ALU.max)
                dve.drain()
                dve.tensor_scalar(r[:, :], n[:, :], MAX_NORM, None, ALU.min)
                dve.drain()
                dve.tensor_scalar(a[:, :], r[:, :], -1.0, 1.0, ALU.mult, ALU.add)
                dve.tensor_scalar(b[:, :], r[:, :], 1.0, None, ALU.add)
                dve.drain()
                dve.reciprocal(a[:, :], a[:, :])
                dve.drain()
                dve.tensor_tensor(a[:, :], a[:, :], b[:, :], ALU.mult).then_inc(ratio, 1)
                dve.drain()
                dve.tensor_tensor(b[:, :], r[:, :], r[:, :], ALU.mult)
                dve.drain()
                dve.tensor_scalar(c[:, :], b[:, :], 1.0 / 7, 1.0 / 5, ALU.mult, ALU.add)
                for k in (1.0 / 3, 1.0):
                    dve.drain()
                    dve.tensor_tensor(c[:, :], c[:, :], b[:, :], ALU.mult)
                    dve.drain()
                    dve.tensor_scalar(c[:, :], c[:, :], k, None, ALU.add)
                dve.drain()
                dve.tensor_tensor(c[:, :], c[:, :], r[:, :], ALU.mult)
                dve.tensor_scalar(b[:, :], r[:, :], 0.1, None, ALU.is_lt)
                dve.wait_ge(logged, 1)
                dve.tensor_scalar(a[:, :], a[:, :], 0.5, None, ALU.mult)
                dve.drain()
                dve.tensor_tensor(c[:, :], c[:, :], a[:, :], ALU.subtract)
                dve.drain()
                dve.tensor_tensor(c[:, :], c[:, :], b[:, :], ALU.mult)
                dve.reciprocal(n[:, :], n[:, :])
                dve.drain()
                dve.tensor_tensor(a[:, :], a[:, :], c[:, :], ALU.add)
                dve.drain()
                dve.tensor_tensor(a[:, :], a[:, :], n[:, :], ALU.mult)
                dve.drain()
                tiles(dve, NT, 5, lambda t, j: dve.tensor_scalar(
                    m.XN[:, at(t, D)], m.XN[:, at(t, D)], a[:, at(t, 1)], None, ALU.mult).then_inc(scaled, 1))

            def first(act):
                act.wait_ge(ss_ready, 1)
                act.sqrt(n[:, :], ss[:, :]).then_inc(root, 1)
                act.wait_ge(ratio, 1)
                act.activation(a[:, :], a[:, :], ACT.Ln).then_inc(logged, 1)
            turn_tiles(m, block, "lg", scaled, first)


OC = 6


def mix0_qkv(m):
    nc, io = m.nc, m.io
    wq = m.sb("q0_w", [128, K2, OC * 128])
    gb = m.sb("q0_gb", [128, 2, OC])
    st = m.sb("q0_st", [128, OC, (NCH + 1) * 6])
    mv = m.sb("q0_mv", [128, OC, 2])
    sc = m.sb("q0_sc", [128, OC])
    sh = m.sb("q0_sh", [128, OC])
    loads = Loads(m, "q0_loaded")
    made, copied, var_ready, std_ready, affine = (
        m.sem("q0_" + x) for x in ("made", "copied", "var_ready", "std_ready", "affine"))
    with nc.Block() as block:
        @block.sync
        def _(sp):
            loads(sp, wq[:, :, :], io["w_qkv_t"].rearrange("(k p) o -> p k o", p=128))
            loads(sp, gb[:, 0, :], io["L0_mix_bn_gamma_cols"])
            loads(sp, gb[:, 1, :], io["L0_mix_bn_beta_cols"])

        @block.tensor
        def _(pe):
            pe.wait_ge(loads.sem, 48)

            def body(c, nt):
                for o in range(OC):
                    pe.wait_ge(copied, c * OC + o + 1)
                    for k in range(K2):
                        last = pe.matmul(m.ps[o][:, 0:nt * P], wq[:, k, o * 128:(o + 1) * 128],
                                         m.XT[:, bass.ds(c * CH + k * N, nt * P)], start=k == 0, stop=k == K2 - 1)
                    last.then_inc(made, 1)
            chunks(pe, body)

        @block.vector
        def _(dve):
            def body(c, nt):
                for o in range(OC):
                    dve.wait_ge(copied, c * OC + o + 1 + OC)
                    dve.bn_stats(st[:, o, at(c, 6)], m.QT[:, bass.ds(c * CH + o * N, nt * P)])
            chunks(dve, body)
            dve.drain()
            for o in range(OC):
                dve.bn_aggr(mv[:, o, :], st[:, o, :])
            dve.drain()
            dve.tensor_scalar(sc[:, :], mv[:, :, 1], 1e-5, None, ALU.add).then_inc(var_ready, 1)
            dve.wait_ge(std_ready, 1)
            dve.reciprocal(sc[:, :], sc[:, :])
            dve.wait_ge(loads.sem, 48)
            dve.drain()
            dve.tensor_tensor(sc[:, :], sc[:, :], gb[:, 0, :], ALU.mult)
            dve.drain()
            dve.tensor_tensor(sh[:, :], mv[:, :, 0], sc[:, :], ALU.mult)
            dve.drain()
            dve.tensor_tensor(sh[:, :], gb[:, 1, :], sh[:, :], ALU.subtract).then_inc(affine, 1)

        @block.scalar
        def _(act):
            act.sem_inc(copied, OC)

            def body(c, nt):
                for o in range(OC):
                    act.wait_ge(made, c * OC + o + 1)
                    act.copy(m.QT[:, bass.ds(c * CH + o * N, nt * P)], m.ps[o][:, 0:nt * P]).then_inc(copied, 1)
            chunks(act, body)
            act.wait_ge(var_ready, 1)
            act.sqrt(sc[:, :], sc[:, :]).then_inc(std_ready, 1)
            act.wait_ge(affine, 1)
            act.drain()
            for o in range(OC):
                act.activation(m.QT[:, o * N:(o + 1) * N], m.QT[:, o * N:(o + 1) * N], ACT.Relu,
                               bias=sh[:, o:o + 1], scale=sc[:, o:o + 1])


def log_exp_scale(dve, out, n, cap, tmp):
    dve.tensor_scalar(tmp, n, MIN_NORM, None, ALU.max)
    dve.tensor_scalar(out, n, cap, None, ALU.min)
    dve.drain()
    dve.reciprocal(tmp, tmp)
    dve.drain()
    dve.tensor_tensor(out, out, tmp, ALU.mult)
    dve.drain()


def mix0_attention(m):
    nc, io = m.nc, m.io
    G = 4
    U = OC * 128
    Z = 2 * U
    GR = Z // 96
    O = GR * 32
    z = m.XN[:, 0:G * Z].rearrange("p (g c) -> p g c", g=G)
    kr, vv, rec = (m.XT[:P, i * G * O:(i + 1) * G * O].rearrange("p (g c) -> p g c", g=G) for i in range(3))
    ks = m.sb("a0_ks", [P, G * GR])
    junk = m.sb("a0_junk", [P, U])
    pw = m.sb("a0_pw", [128, OC, 128])
    dw = m.sb("a0_dw", [128, OC])
    wres = m.sb("a0_wres", [128, 4, D])
    bres = m.sb("a0_bres", [128, D])
    ot = m.sb("a0_ot", [128, 2, 4 * P])
    ft = m.sb("a0_ft", [P, G, D])
    ss = m.sb("a0_ss", [P, 4, G])
    n = m.sb("a0_n", [P, 4, G])
    f = m.sb("a0_f", [P, 6, G])
    loads = Loads(m, "a0_loaded")
    (zeroed, w_ready, z_made, z_kept, uv_ss, uv_root, out_done, o_ss, o_root, o_turned, o_kept, res_made,
     ft_done, ft_ss, ft_root, ft_scaled) = (
        m.sem("a0_" + x) for x in (
            "zeroed", "w_ready", "z_made", "z_kept", "uv_ss", "uv_root", "out_done", "o_ss", "o_root",
            "o_turned", "o_kept", "res_made", "ft_done", "ft_ss", "ft_root", "ft_scaled"))
    zb = [m.ps[0], m.ps[1], m.ps[2]]
    with nc.Block() as block:
        @block.sync
        def _(sp):
            sp.wait_ge(zeroed, 1)
            for a in range(4):
                loads(sp, pw[32 * a:32 * a + 32, :, 32 * a:32 * a + 32],
                      io["w_pw_t"].rearrange("i (j a c) -> i j a c", a=4, c=32)[:, :, a, :])
            loads(sp, dw[:, :], io["w_dw_mid_cols"])
            loads(sp, wres[:, :, :], io["w_res_t"].rearrange("(k p) d -> p k d", p=128))
            loads(sp, bres[:, :], io["L0_mix_b_res"].partition_broadcast(128))

        n_loads = 16 * (4 + 3)

        @block.gpsimd
        def _(pool):
            pool.memset(pw[:, :, :], 0.0).then_inc(zeroed, 1)

        @block.tensor
        def _(pe):
            pe.wait_ge(w_ready, 1)

            def body(g, nt):
                for j in range(nt):
                    t = g * G + j
                    pe.wait_ge(z_kept, t + 1)
                    for o in range(OC):
                        pe.transpose(zb[o // 4][:P, (o % 4) * 128:(o % 4 + 1) * 128],
                                     m.QT[:, bass.ds(t * P + o * N, P)], m.ident[:, :])
                    for o in range(OC):
                        c = U + o * 128
                        last = pe.matmul(zb[c // 512][:P, c % 512:c % 512 + 128], m.QT[:, bass.ds(t * P + o * N, P)],
                                         pw[:, o, :], start=True, stop=True)
                    last.then_inc(z_made, 1)
                pe.wait_ge(out_done, g + 1)
                for j in range(nt):
                    t = g * G + j
                    for k in range(4):
                        last = pe.transpose(m.ps[4 + j % 2][:, k * P:(k + 1) * P], kr[:, j, k * 128:(k + 1) * 128],
                                            m.ident[:P, :P])
                    last.then_inc(o_turned, 1)
                    pe.wait_ge(o_kept, t + 1)
                    pe.wait_ge(ft_done, t + 1)
                    for k in range(4):
                        last = pe.matmul(m.ps[6][:P, 0:D], ot[:, j % 2, k * P:(k + 1) * P], wres[:, k, :],
                                         start=k == 0, stop=k == 3)
                    last.then_inc(res_made, 1)
            chunks_written_out(body)

        @block.scalar
        def _(act):
            act.sem_inc(z_kept, 1)

            def body(g, nt):
                act.wait_ge(ft_scaled, g + 1)
                for j in range(nt):
                    act.wait_ge(z_made, g * G + j + 1)
                    for i in range(2):
                        for lo in range(i * U, (i + 1) * U, 256):
                            act.copy(z[:, j, lo:lo + 256], zb[lo // 512][:P, lo % 512:lo % 512 + 256])
                    act.drain().then_inc(z_kept, 1)
                    for i in range(2):
                        act.activation(junk[:, :], z[:, j, i * U:(i + 1) * U], ACT.Square, accum_out=ss[:, i, j:j + 1])
                        act.drain()
                act.sem_inc(uv_ss, 1)
                act.wait_ge(uv_root, 2 * g + 1)
                act.sqrt(n[:, 0:2, 0:nt], ss[:, 0:2, 0:nt]).then_inc(uv_root, 1)
                act.wait_ge(out_done, g + 1)
                for j in range(nt):
                    act.activation(junk[:, 0:O], kr[:, j, :], ACT.Square, accum_out=ss[:, 2, j:j + 1])
                    act.drain()
                act.sqrt(n[:, 2, 0:nt], ss[:, 2, 0:nt]).then_inc(o_root, 1)
                for j in range(nt):
                    act.wait_ge(o_turned, g * G + j + 1)
                    act.copy(ot[:, j % 2, :], m.ps[4 + j % 2][:, 0:4 * P]).then_inc(o_kept, 1)
                act.wait_ge(ft_ss, g + 1)
                for j in range(nt):
                    act.activation(junk[:, 0:D], ft[:, j, :], ACT.Square, accum_out=ss[:, 3, j:j + 1])
                    act.drain()
                act.sqrt(n[:, 3, 0:nt], ss[:, 3, 0:nt])
                act.drain()
                act.activation(f[:, 5, 0:nt], n[:, 3, 0:nt], ACT.Tanh).then_inc(ft_root, 1)
            chunks(act, body)

        @block.vector
        def _(dve):
            dve.wait_ge(loads.sem, n_loads)
            for o in range(OC):
                last = dve.tensor_scalar(pw[:, o, :], pw[:, o, :], dw[:, o:o + 1], None, ALU.mult)
            last.then_inc(w_ready, 1)
            dve.sem_inc(ft_done, 1)
            dve.sem_inc(ft_scaled, 1)
            zg = z[:, :, :].rearrange("p g (r c) -> p (g r) c", c=96)
            flat = lambda x, nt: x[:, 0:nt, :].rearrange("p g (r c) -> p (g r) c", c=32)

            def body(g, nt):
                dve.wait_ge(uv_ss, g + 1)
                dve.tensor_tensor(ss[:, 1, 0:nt], ss[:, 0, 0:nt], ss[:, 1, 0:nt], ALU.add).then_inc(uv_root, 1)
                dve.tensor_scalar(flat(kr, nt), zg[:, 0:nt * GR, 32:64], 0.0, None, ALU.max)
                dve.drain()
                dve.tensor_reduce(ks[:, 0:nt * GR], flat(kr, nt), AX.X, ALU.add)
                dve.wait_ge(uv_root, 2 * g + 2)
                log_exp_scale(dve, f[:, 0, 0:nt], n[:, 0, 0:nt], MAX_ATANH, f[:, 1, 0:nt])
                dve.tensor_tensor(f[:, 2, 0:nt], n[:, 1, 0:nt], f[:, 0, 0:nt], ALU.mult)
                dve.drain()
                log_exp_scale(dve, f[:, 3, 0:nt], f[:, 2, 0:nt], MAX_ATANH, f[:, 1, 0:nt])
                dve.tensor_tensor(f[:, 0, 0:nt], f[:, 0, 0:nt], f[:, 3, 0:nt], ALU.mult)
                dve.drain()
                for j in range(nt):
                    dve.tensor_scalar(vv[:, j, :].rearrange("p (r c) -> p r c", c=32),
                                      zg[:, j * GR:(j + 1) * GR, 64:96], f[:, 0, j:j + 1], None, ALU.mult)
                dve.drain()
                dve.tensor_scalar(rec[:, 0:nt, :], vv[:, 0:nt, :], 1e-15, None, ALU.add)
                dve.drain()
                dve.reciprocal(rec[:, 0:nt, :], rec[:, 0:nt, :])
                dve.drain()
                dve.tensor_tensor(vv[:, 0:nt, :], vv[:, 0:nt, :], rec[:, 0:nt, :], ALU.mult)
                dve.drain()
                dve.scalar_tensor_tensor(flat(vv, nt), zg[:, 0:nt * GR, 0:32], 0.0, flat(vv, nt), ALU.max, ALU.mult)
                dve.drain()
                dve.tensor_tensor(flat(kr, nt), flat(vv, nt), ks[:, 0:nt * GR].unsqueeze(2).broadcast_to((P, nt * GR, 32)),
                                  ALU.mult).then_inc(out_done, 1)
                dve.tensor_tensor(f[:, 1, 0:nt], f[:, 0, 0:nt], f[:, 0, 0:nt], ALU.mult)
                dve.drain()
                dve.wait_ge(o_root, g + 1)
                dve.tensor_tensor(f[:, 2, 0:nt], f[:, 1, 0:nt], n[:, 2, 0:nt], ALU.mult)
                dve.drain()
                log_exp_scale(dve, f[:, 3, 0:nt], f[:, 2, 0:nt], MAX_ATANH, f[:, 4, 0:nt])
                dve.tensor_tensor(f[:, 4, 0:nt], f[:, 1, 0:nt], f[:, 3, 0:nt], ALU.mult)
                dve.drain()
                for j in range(nt):
                    dve.wait_ge(res_made, g * G + j + 1)
                    dve.scalar_tensor_tensor(ft[:, j, :], m.ps[6][:P, 0:D], f[:, 4, j:j + 1], bres[:P, :],
                                             ALU.mult, ALU.add).then_inc(ft_done, 1)
                dve.drain().then_inc(ft_ss, 1)
                dve.wait_ge(ft_root, g + 1)
                dve.tensor_scalar(f[:, 1, 0:nt], n[:, 3, 0:nt], MIN_NORM, None, ALU.max)
                dve.tensor_scalar(f[:, 0, 0:nt], f[:, 5, 0:nt], MAX_NORM, None, ALU.min)
                dve.drain()
                dve.reciprocal(f[:, 1, 0:nt], f[:, 1, 0:nt])
                dve.drain()
                dve.tensor_tensor(f[:, 0, 0:nt], f[:, 0, 0:nt], f[:, 1, 0:nt], ALU.mult)
                dve.drain()
                for j in range(nt):
                    x = m.X[:, bass.ds(g * (G * D) + j * D, D)]
                    dve.scalar_tensor_tensor(x, ft[:, j, :], f[:, 0, j:j + 1], x, ALU.mult, ALU.add)
                dve.drain().then_inc(ft_scaled, 1)
            chunks(dve, body)


class Edges:

    def __init__(self, m, tag, cols):
        self.tag, self.cols = tag, cols
        self.key = m.sb(tag + "_key", [128, cols])
        self.other = m.sb(tag + "_other", [128, cols], I32)
        self.start = m.dram(tag + "_start", [KEYS + 1], I32)


def floor_div(dve, q, r, pos, cols):
    magic = 12582912.0
    dve.tensor_scalar(q, pos, 0.5, 1.0 / cols, ALU.add, ALU.mult)
    dve.drain()
    dve.tensor_scalar(q, q, -0.5, magic, ALU.add, ALU.add)
    dve.drain()
    dve.tensor_scalar(q, q, -magic, None, ALU.add)
    dve.drain()
    last = dve.scalar_tensor_tensor(r, q, -float(cols), pos, ALU.mult, ALU.add)
    dve.drain()
    return last


def sort_constants(m):
    m.row16 = m.sb("row16", [128, 512], FP16)
    m.low16 = m.sb("low16", [128, 128], FP16)
    m.low = m.sb("low", [128, 128])
    m.high = m.sb("high", [128, 128])
    m.ones = m.sb("ones", [128, 512])
    m.zero16 = m.sb("zero16", [128, 512], FP16)
    m.ident16 = m.sb("ident16", [128, 128], FP16)
    with m.nc.Block() as block:
        @block.gpsimd
        def _(pool):
            pool.iota(m.row16[:, :], [[1, 512]], base=0, channel_multiplier=0,
                      allow_small_or_imprecise_dtypes=True)
            pool.memset(m.low[:, :], 1.0)
            pool.memset(m.high[:, :], 1.0)
            pool.memset(m.ones[:, :], 1.0)
            pool.memset(m.zero16[:, :], 0.0)
            pool.drain()
            pool.affine_select(out=m.low[:, :], in_=m.low[:, :], compare_op=ALU.is_gt, fill=0.0,
                               base=0, pattern=[[1, 128]], channel_multiplier=-1)
            pool.affine_select(out=m.high[:, :], in_=m.high[:, :], compare_op=ALU.is_gt, fill=0.0,
                               base=0, pattern=[[-1, 128]], channel_multiplier=1)
            pool.drain()
            pool.tensor_copy(m.low16[:, :], m.low[:, :])
            pool.tensor_copy(m.ident16[:, :], m.ident[:, :])
            pool.drain()


def sort_edges(m, ed, key_in, other_in, beside=lambda block, stage: None):
    nc, cols, tag = m.nc, ed.cols, ed.tag
    nb = cols // BC
    MID = 1562.0
    with Stage(m):
        ki = m.sb(tag + "_ki", [128, cols], I32)
        a = m.sb(tag + "_a", [128, cols])
        b = m.sb(tag + "_b", [128, cols])
        val = m.sb(tag + "_val", [128, cols])
        pos = m.sb(tag + "_pos", [128, cols])
        H = m.sb(tag + "_H", [128, (cols + 1) * KB])
        H3 = H[:, :].rearrange("p (t b) -> p t b", b=KB)
        half = lambda i, n=BC * 64: m.scratch[:, i * n:(i + 1) * n].bitcast(FP16).rearrange("p (c e) -> p c e", c=BC)
        oa, oat16, em = [half(0), half(1)], half(2), half(3)
        oat32 = m.scratch[:, 4 * BC * 64:6 * BC * 64].rearrange("p (c e) -> p c e", c=BC)
        ob = [m.sb(f"{tag}_ob{i}", [128, BC, KB], FP16) for i in range(3)]
        tot = m.sb(tag + "_tot", [128, KB])
        start = m.sb(tag + "_start_sb", [128, KB])
        start_i = m.sb(tag + "_start_i", [128, KB], I32)
        rsum = m.sb(tag + "_rsum", [128, 1])
        row128 = m.row16[:, 0:128]

        def one_hots(dve, t, j, i):
            for c in range(BC):
                dve.tensor_scalar(oa[j][:, c, :], row128, a[:, bass.ds(t * BC + c, 1)], None, ALU.is_equal)
            return dve.tensor_tensor(ob[i][:, :, :], b[:, at(t, BC)].unsqueeze(2).broadcast_to((128, BC, KB)),
                                     m.row16[:, 0:KB].unsqueeze(1).broadcast_to((128, BC, KB)), ALU.is_equal)

        loads = Loads(m, tag + "_in")
        hot, used, kept, tot_done, fin = (m.sem(f"{tag}_{x}") for x in ("hot", "used", "kept", "tot_done", "fin"))
        with nc.Block() as block:
            beside(block, 1)

            @block.sync
            def _(sp):
                loads(sp, ki[:, :], key_in)
                loads(sp, ed.other[:, :], other_in)

            @block.vector
            def _(dve):
                dve.wait_ge(loads.sem, loads.all)
                dve.tensor_scalar(ed.key[:, :].bitcast(I32), ki[:, :], 5, None, ALU.arith_shift_right)
                dve.tensor_scalar(val[:, :], ed.other[:, :], float(N - 1), -MID, ALU.min, ALU.add)
                dve.drain()
                dve.tensor_copy(a[:, :], ed.key[:, :].bitcast(I32))
                dve.drain()
                dve.tensor_scalar(ki[:, :], ki[:, :], 31, None, ALU.bitwise_and)
                dve.drain()
                dve.tensor_copy(b[:, :], ki[:, :])
                dve.drain()
                dve.sem_inc(used, 2)

                def body(t, j):
                    dve.wait_ge(used, t + 1)
                    one_hots(dve, t, j, j)
                    dve.drain().then_inc(hot, 1)
                tiles(dve, nb, 2, body)

            @block.tensor
            def _(pe):
                total = m.ps[7][:, 0:KB]
                pe.matmul(total, m.zero16[:, 0:128], m.zero16[:, 0:KB], start=True, stop=False)

                def body(t, j):
                    pe.wait_ge(hot, t + 1)
                    pe.wait_ge(kept, t + 1)
                    for c in range(BC):
                        pe.matmul(m.ps[j][:, c * KB:(c + 1) * KB], oa[j][:, c, :], ob[j][:, c, :], start=True, stop=True)
                        last = pe.matmul(total, oa[j][:, c, :], ob[j][:, c, :], start=False, stop=False)
                    last.then_inc(used, 1)
                tiles(pe, nb, 2, body)
                pe.matmul(total, m.zero16[:, 0:128], m.zero16[:, 0:KB], start=False, stop=True).then_inc(tot_done, 1)

            @block.scalar
            def _(act):
                act.sem_inc(kept, 2)

                def body(t, j):
                    act.wait_ge(used, t + 3)
                    act.copy(H[:, bass.ds(t * (BC * KB) + KB, BC * KB)], m.ps[j][:, :]).then_inc(kept, 1)
                tiles(act, nb, 2, body)
                act.wait_ge(tot_done, 1)
                act.copy(tot[:, :], m.ps[7][:, 0:KB])

        row_ready, row_sum, start_ready, stored = (m.sem(f"{tag}_{x}") for x in ("row_ready", "row_sum", "start_ready", "stored"))
        with nc.Block() as block:
            @block.vector
            def _(dve):
                dve.tensor_tensor_scan(start[:, :], m.ones[:, 0:KB], tot[:, :], 0.0, ALU.mult, ALU.add)
                dve.drain()
                dve.tensor_copy(rsum[:, :], start[:, KB - 1:KB]).then_inc(row_ready, 1)
                dve.drain()
                dve.tensor_tensor(start[:, :], start[:, :], tot[:, :], ALU.subtract)
                dve.drain()
                dve.wait_ge(row_sum, 1)
                dve.tensor_scalar(start[:, :], start[:, :], m.ps[0][:, 0:1], None, ALU.add)
                dve.drain()
                dve.tensor_copy(start_i[:, :], start[:, :]).then_inc(start_ready, 1)
                dve.tensor_copy(H3[:, 0, :], start[:, :])
                for i in range(KB):
                    dve.tensor_tensor_scan(H3[:, 1:, i], m.ones[:, 0:cols], H3[:, 1:, i], start[:, i:i + 1],
                                           ALU.mult, ALU.add)

            @block.tensor
            def _(pe):
                pe.wait_ge(row_ready, 1)
                pe.matmul(m.ps[0][:, 0:1], m.low[:, :], rsum[:, :], start=True, stop=True).then_inc(row_sum, 1)

            @block.sync
            def _(sp):
                sp.wait_ge(start_ready, 1)
                sp.dma_start(ed.start[0:KEYS].rearrange("(a b) -> a b", b=KB), start_i[:, :]).then_inc(stored, 16)
                sp.wait_ge(stored, 16)

        pick = m.sb(tag + "_pick", [128, BC, KB])
        hot2, turned, moved16, moved32, same, masked, ranked, picked = (
            m.sem(f"{tag}_{x}") for x in ("hot2", "turned", "moved16", "moved32", "same", "masked", "ranked", "picked"))
        with nc.Block() as block:
            beside(block, 3)

            @block.vector
            def _(dve):
                def hots(t, j):
                    one_hots(dve, t, j % 2, j % 3)
                    dve.drain().then_inc(hot2, 1)

                def mask(t, j):
                    for q in range(4):
                        dve.wait_ge(same, 4 * t + q + 1)
                        dve.tensor_tensor(em[:, 4 * q:4 * q + 4, :], m.ps[2 + q][:, :].rearrange("p (c e) -> p c e", c=4),
                                          m.low16[:, :].unsqueeze(1).broadcast_to((128, 4, 128)), ALU.mult).then_inc(masked, 1)

                def choose(t, j):
                    dve.wait_ge(ranked, t + 1)
                    dve.tensor_tensor(pick[:, :, :], m.ps[6][:, :].rearrange("p (c b) -> p c b", b=KB),
                                      ob[j % 3][:, :, :], ALU.mult)
                    dve.drain().then_inc(picked, 1)
                    dve.tensor_reduce(pos[:, at(t, BC)], pick[:, :, :], AX.X, ALU.add)
                    dve.drain()
                dve.sem_inc(picked, 1)
                hots(0, 0)
                hots(1, 1)
                mask(0, 0)

                def body(t, j):
                    hots(t + 2, j + 2)
                    choose(t, j)
                    mask(t + 1, j + 1)
                tiles(dve, nb - 2, 6, body)
                choose(nb - 2, nb - 2)
                mask(nb - 1, nb - 1)
                choose(nb - 1, nb - 1)

            @block.tensor
            def _(pe):
                def turn(t, j):
                    pe.wait_ge(hot2, t + 1)
                    pe.wait_ge(moved32, t + 1)
                    for c in range(BC):
                        bank = m.ps[c // 8][:, :].bitcast(FP16)
                        last = pe.transpose(bank[:, (c % 8) * 128:(c % 8 + 1) * 128], oa[j % 2][:, c, :], m.ident16[:, :])
                    last.then_inc(turned, 1)

                def compare(t, j):
                    pe.wait_ge(moved16, t + 1)
                    pe.wait_ge(masked, 4 * t)
                    for c in range(BC):
                        last = pe.matmul(m.ps[2 + c // 4][:, (c % 4) * 128:(c % 4 + 1) * 128], oat16[:, c, :],
                                         oat16[:, c, :], start=True, stop=True)
                        if c % 4 == 3:
                            last.then_inc(same, 1)

                def rank(t, j):
                    pe.wait_ge(moved32, t + 2)
                    pe.wait_ge(picked, t + 1)
                    pe.wait_ge(masked, 4 * t + 4)
                    for c in range(BC):
                        out = m.ps[6][:, c * KB:(c + 1) * KB]
                        pe.matmul(out, oat32[:, c, :], H[:, bass.ds(t * (BC * KB) + c * KB, KB)], start=True, stop=False)
                        last = pe.matmul(out, em[:, c, :], ob[j % 3][:, c, :], start=False, stop=True)
                    last.then_inc(ranked, 1)
                turn(0, 0)

                def body(t, j):
                    compare(t, j)
                    turn(t + 1, j + 1)
                    rank(t, j)
                tiles(pe, nb - 1, 6, body)
                compare(nb - 1, nb - 1)
                rank(nb - 1, nb - 1)

            @block.scalar
            def _(act):
                act.sem_inc(moved32, 1)

                def body(t, j):
                    act.wait_ge(turned, t + 1)
                    for dst, done in ((oat16, moved16), (oat32, moved32)):
                        if dst is oat32:
                            act.wait_ge(ranked, t)
                        for h in range(2):
                            last = act.copy(dst[:, 8 * h:8 * h + 8, :].rearrange("p c e -> p (c e)"),
                                            m.ps[h][:, :].bitcast(FP16))
                        last.then_inc(done, 1)
                tiles(act, nb, 2, body)

        q, r = a, b
        sq = m.sb(tag + "_sq", [128, KB])
        sr = m.sb(tag + "_sr", [128, KB])
        rv = [m.sb(f"{tag}_rv{i}", [128, 4, cols], FP16) for i in range(2)]
        hot3, used3, row3, pre3 = (m.sem(f"{tag}_{x}") for x in ("hot3", "used3", "row3", "pre3"))
        nq = cols // 4
        with nc.Block() as block:
            beside(block, 4)

            @block.vector
            def _(dve):
                floor_div(dve, q[:, :], r[:, :], pos[:, :], cols)
                floor_div(dve, sq[:, :], sr[:, :], start[:, :], cols)
                dve.sem_inc(used3, 2)

                def body(t, j):
                    dve.wait_ge(used3, t + 1)
                    for c in range(4):
                        e = bass.ds(t * 4 + c, 1)
                        dve.tensor_scalar(oa[j][:, c, :], row128, q[:, e], None, ALU.is_equal)
                        dve.tensor_scalar(rv[j][:, c, :], m.row16[:, 0:cols], r[:, e], val[:, e], ALU.is_equal, ALU.mult)
                    dve.drain().then_inc(hot3, 1)
                tiles(dve, nq, 2, body)

                def starts(t, j):
                    dve.wait_ge(used3, nq + t + 1)
                    for c in range(4):
                        e = bass.ds(t * 4 + c, 1)
                        dve.tensor_scalar(oa[j][:, c, :], row128, sq[:, e], None, ALU.is_equal)
                        dve.tensor_scalar(rv[j][:, c, :], m.row16[:, 0:cols], sr[:, e], None, ALU.is_equal)
                    dve.drain().then_inc(hot3, 1)
                tiles(dve, KB // 4, 2, starts)
                dve.wait_ge(used3, nq + KB // 4 + 3)
                dve.tensor_scalar(ed.other[:, :], m.ps[0][:, 0:cols], MID, None, ALU.add)
                dve.tensor_tensor_scan(ed.key[:, :], m.ones[:, 0:cols], m.ps[1][:, 0:cols], 0.0, ALU.mult, ALU.add)
                dve.drain()
                dve.tensor_copy(rsum[:, :], ed.key[:, cols - 1:cols]).then_inc(row3, 1)
                dve.wait_ge(pre3, 1)
                dve.tensor_scalar(ed.key[:, :], ed.key[:, :], m.ps[2][:, 0:1], -1.0, ALU.add, ALU.add)

            @block.tensor
            def _(pe):
                for half, count, first in ((0, nq, 0), (1, KB // 4, nq)):
                    out = m.ps[half][:, 0:cols]
                    pe.matmul(out, m.zero16[:, 0:128], m.zero16[:, 0:cols], start=True, stop=False)

                    def body(t, j):
                        pe.wait_ge(hot3, t + first + 1)
                        for c in range(4):
                            last = pe.matmul(out, oa[(j + first) % 2][:, c, :], rv[(j + first) % 2][:, c, :],
                                             start=False, stop=False)
                        last.then_inc(used3, 1)
                    assert nq % 2 == 0
                    tiles(pe, count, 2, body)
                    last = pe.matmul(out, m.zero16[:, 0:128], m.zero16[:, 0:cols], start=False, stop=True)
                last.then_inc(used3, 1)
                pe.wait_ge(row3, 1)
                pe.matmul(m.ps[2][:, 0:1], m.low[:, :], rsum[:, :], start=True, stop=True).then_inc(pre3, 1)


def nodes_of(table, lo=0):
    return table[lo:lo + N].rearrange("(t p) -> p t", p=P)


class Spread:

    def __init__(self, m, tag, ed, H):
        self.H = H
        self.ke = m.sb(tag + "_ke", [128, ed.cols, H])
        self.cont = m.sb(tag + "_cont", [128, ed.cols])
        self.pen = m.sb(tag + "_pen", [128, ed.cols])
        self.lo = m.sb(tag + "_lo", [P, NT])
        self.hi = m.sb(tag + "_hi", [P, NT])
        self.has = m.sb(tag + "_has", [P, NT])


def spread_logits(m, tag, ed, sp_, table, logits):
    nc, H, cols = m.nc, sp_.H, ed.cols
    E = 128 * cols
    placed = m.dram(tag + "_placed", [E, H])
    with Stage(m):
        zero = m.sb(tag + "_zero", [128, cols * H])
        lo_i, hi_i, dst_i = (m.sb(tag + x, [P, NT], I32) for x in ("_lo_i", "_hi_i", "_dst_i"))
        dst = m.sb(tag + "_dst", [P, NT])
        first_i = m.sb(tag + "_first_i", [128, 1], I32)
        first = m.sb(tag + "_first", [128, 1])
        own = m.sb(tag + "_own", [128, H])
        raw = m.sb(tag + "_raw", [128, cols, H])
        loads, rows, back = Loads(m, tag + "_bounds_loaded"), Loads(m, tag + "_rows_placed"), Loads(m, tag + "_raw_loaded")
        zeroed, cleared, idx_ready, own_sem = (m.sem(tag + x) for x in ("_zeroed", "_cleared", "_idx_ready", "_own"))
        with nc.Block() as block:
            @block.sync
            def _(sp):
                with nc.allow_non_contiguous_dma(reason="one word per node"):
                    loads(sp, lo_i[:, :], nodes_of(ed.start))
                    loads(sp, hi_i[:, :], nodes_of(ed.start, 1))
                sp.wait_ge(zeroed, 1)
                sp.dma_start(placed.rearrange("(p t) h -> p (t h)", p=128), zero[:, :]).then_inc(cleared, 16)
                sp.wait_ge(rows.sem, 16 * NT)
                back(sp, raw[:, :, :], placed.rearrange("(p t) h -> p t h", p=128))

            @block.gpsimd
            def _(pool):
                pool.memset(zero[:, :], 0.0).then_inc(zeroed, 1)
                pool.wait_ge(idx_ready, 1)
                pool.indirect_dma_start(out=own[:, :], out_offset=None, in_=table,
                                        in_offset=bass.IndirectOffsetOnAxis(ap=first_i[:, :], axis=0)).then_inc(own_sem, 16)
                pool.wait_ge(cleared, 16)
                for t in range(NT):
                    pool.indirect_dma_start(out=placed, out_offset=bass.IndirectOffsetOnAxis(ap=dst_i[:, t:t + 1], axis=0),
                                            in_=logits[:, t, :], in_offset=None,
                                            bounds_check=E - 1, oob_is_err=False).then_inc(rows.sem, 16)

            @block.vector
            def _(dve):
                dve.wait_ge(loads.sem, 32)
                dve.tensor_copy(sp_.lo[:, :], lo_i[:, :])
                dve.tensor_copy(sp_.hi[:, :], hi_i[:, :])
                dve.tensor_scalar(first[:, :], ed.key[:, 0:1], float(N - 1), None, ALU.min)
                dve.drain()
                dve.tensor_copy(first_i[:, :], first[:, :])
                dve.tensor_tensor(sp_.has[:, :], sp_.hi[:, :], sp_.lo[:, :], ALU.is_gt)
                dve.drain()
                dve.tensor_scalar(dst[:, :], sp_.has[:, :], -float(4 * E), float(4 * E), ALU.mult, ALU.add)
                dve.drain()
                dve.tensor_tensor(dst[:, :], dst[:, :], sp_.lo[:, :], ALU.add)
                dve.drain()
                dve.tensor_copy(dst_i[:, :], dst[:, :])
                dve.drain().then_inc(idx_ready, 1)
                dve.memset(sp_.cont[:, 0:1], 0.0)
                dve.tensor_tensor(sp_.cont[:, 1:], ed.key[:, 1:], ed.key[:, 0:cols - 1], ALU.is_equal)
                dve.drain()
                dve.tensor_scalar(sp_.pen[:, :], sp_.cont[:, :], -1.0, BIG, ALU.add, ALU.mult)
                dve.wait_ge(back.sem, 16)
                dve.wait_ge(own_sem, 16)
                dve.tensor_copy(raw[:, 0, :], own[:, :])
                dve.drain()
                for h in range(H):
                    dve.tensor_tensor_scan(sp_.ke[:, :, h], sp_.cont[:, :], raw[:, :, h], 0.0, ALU.mult, ALU.add)


def carry_rows(m, tag, ed, H, F, last, table):
    nc, cols = m.nc, ed.cols
    W = H * F + 2 * H
    with Stage(m):
        dg = m.sb(tag + "_dg", [128, H + 1, 128])
        mask = m.sb(tag + "_mask", [128, 128])
        neg = m.sb(tag + "_neg", [128, 128])
        a = m.sb(tag + "_a", [128, H, 128])
        wt = m.sb(tag + "_wt", [128, H, 128])
        wtt = m.sb(tag + "_wtt", [128, H, 128])
        cm = m.sb(tag + "_cm", [128, H])
        ncm = m.sb(tag + "_ncm", [128, H])
        row = m.sb(tag + "_row", [128, W + 1])
        dg_ready, wide, a_ready, expd, wt_ready, turned, back, summed, row_ready, stored = (
            m.sem(tag + x) for x in ("_dg_ready", "_wide", "_a_ready", "_expd", "_wt_ready", "_turned",
                                     "_back", "_summed", "_row_ready", "_stored"))
        with nc.Block() as block:
            @block.vector
            def _(dve):
                dve.tensor_scalar(dg[:, H, :], m.ident[:, :], ed.key[:, cols - 1:cols], None, ALU.mult)
                for h in range(H):
                    dve.tensor_scalar(dg[:, h, :], m.ident[:, :], last[:, H * F + H + h:H * F + H + h + 1], None, ALU.mult)
                dve.drain().then_inc(dg_ready, 1)
                dve.wait_ge(wide, 1)
                dve.scalar_tensor_tensor(mask[:, :], m.ps[H][:, 0:128], ed.key[:, 0:1], m.high[:, :], ALU.is_equal, ALU.mult)
                dve.drain()
                dve.tensor_scalar(neg[:, :], mask[:, :], -1.0, BIG, ALU.add, ALU.mult)
                for h in range(H):
                    dve.tensor_tensor(a[:, h, :], m.ps[h][:, 0:128], mask[:, :], ALU.mult)
                dve.drain()
                for h in range(H):
                    dve.tensor_tensor(a[:, h, :], a[:, h, :], neg[:, :], ALU.add)
                dve.drain()
                dve.tensor_reduce(cm[:, :], a[:, :, :], AX.X, ALU.max)
                dve.drain()
                for h in range(H):
                    dve.tensor_scalar(a[:, h, :], a[:, h, :], cm[:, h:h + 1], None, ALU.subtract)
                dve.drain().then_inc(a_ready, 1)
                dve.wait_ge(expd, 1)
                for h in range(H):
                    dve.tensor_tensor(wt[:, h, :], wt[:, h, :], mask[:, :], ALU.mult)
                dve.drain().then_inc(wt_ready, 1)
                dve.wait_ge(turned, 1)
                for h in range(H):
                    dve.tensor_copy(wtt[:, h, :], m.ps[h][:, 0:128])
                dve.drain().then_inc(back, 1)
                dve.wait_ge(summed, 1)
                for h in range(H):
                    dve.tensor_copy(row[:, h * F:(h + 1) * F], m.ps[4 + h][:, 0:F])
                    dve.tensor_copy(row[:, H * F + h:H * F + h + 1], m.ps[4 + h][:, F:F + 1])
                dve.tensor_copy(row[:, H * F + H:W], cm[:, :])
                dve.tensor_copy(row[:, W:W + 1], ed.key[:, 0:1])
                dve.drain().then_inc(row_ready, 1)

            @block.scalar
            def _(act):
                act.wait_ge(a_ready, 1)
                act.activation(wt[:, :, :], a[:, :, :], ACT.Exp).then_inc(expd, 1)

            @block.tensor
            def _(pe):
                pe.wait_ge(dg_ready, 1)
                for h in range(H + 1):
                    x = pe.matmul(m.ps[h][:, 0:128], m.ones[:, 0:128], dg[:, h, :], start=True, stop=True)
                x.then_inc(wide, 1)
                pe.wait_ge(wt_ready, 1)
                for h in range(H):
                    x = pe.transpose(m.ps[h][:, 0:128], wt[:, h, :], m.ident[:, :])
                x.then_inc(turned, 1)
                pe.wait_ge(back, 1)
                for h in range(H):
                    pe.matmul(m.ps[4 + h][:, 0:F], wtt[:, h, :], last[:, h * F:(h + 1) * F], start=True, stop=True)
                    x = pe.matmul(m.ps[4 + h][:, F:F + 1], wtt[:, h, :], last[:, H * F + h:H * F + h + 1],
                                  start=True, stop=True)
                x.then_inc(summed, 1)

            @block.sync
            def _(sp):
                sp.wait_ge(row_ready, 1)
                sp.dma_start(table, row[:, :]).then_inc(stored, 16)
                sp.wait_ge(stored, 16)


def merge_nodes(m, tag, ed, sp_, H, F, result, carry, agg, den, own_e=None, own_f=None):
    nc, cols = m.nc, ed.cols
    HF = H * F
    W = HF + 2 * H
    GT = 5
    with Stage(m):
        end = m.sb(tag + "_end", [P, NT])
        part = m.sb(tag + "_part", [P, NT])
        rest = m.sb(tag + "_rest", [P, NT])
        end_i = m.sb(tag + "_end_i", [P, NT], I32)
        part_i = m.sb(tag + "_part_i", [P, NT], I32)
        node = m.sb(tag + "_node", [P, NT])
        re = m.sb(tag + "_re", [P, GT, W])
        rc = m.sb(tag + "_rc", [P, GT, W + 1])
        use = m.sb(tag + "_use", [P, GT])
        me, mc, mx, we, wc, ws = (m.sb(tag + x, [P, GT, H]) for x in ("_me", "_mc", "_mx", "_we", "_wc", "_ws"))
        idx_ready, rows, exps, expd, free = (m.sem(tag + x) for x in ("_idx_ready", "_rows", "_exps", "_expd", "_free"))
        node_sem = m.sem(tag + "_node_sem")
        with nc.Block() as block:
            @block.gpsimd
            def _(pool):
                pool.iota(node[:, :], [[P, NT]], base=0, channel_multiplier=1,
                          allow_small_or_imprecise_dtypes=True).then_inc(node_sem, 1)
                pool.wait_ge(idx_ready, 1)
                for t in range(NT):
                    if t % GT == 0 and t:
                        pool.wait_ge(free, t // GT)
                    for dst, table, idx in ((re, result, end_i), (rc, carry, part_i)):
                        pool.indirect_dma_start(out=dst[:, t % GT, :], out_offset=None, in_=table,
                                                in_offset=bass.IndirectOffsetOnAxis(ap=idx[:, t:t + 1], axis=0)
                                                ).then_inc(rows, 16)

            @block.vector
            def _(dve):
                dve.tensor_scalar(end[:, :], sp_.hi[:, :], -1.0, 0.0, ALU.add, ALU.max)
                dve.drain()
                floor_div(dve, part[:, :], rest[:, :], end[:, :], cols)
                dve.tensor_copy(end_i[:, :], end[:, :])
                dve.tensor_copy(part_i[:, :], part[:, :])
                dve.drain().then_inc(idx_ready, 1)
                dve.wait_ge(node_sem, 1)
                for g in range(NT // GT):
                    ts = slice(g * GT, (g + 1) * GT)
                    has = sp_.has[:, ts]
                    wide = lambda x: x.unsqueeze(2).broadcast_to((P, GT, H))
                    dve.wait_ge(rows, 32 * GT * (g + 1))
                    dve.tensor_tensor(use[:, :], rc[:, :, W], node[:, ts], ALU.is_equal)
                    dve.tensor_tensor(me[:, :, :], re[:, :, HF + H:W], wide(has), ALU.mult)
                    dve.tensor_scalar(we[:, :, :], wide(has), -1.0, BIG, ALU.add, ALU.mult)
                    dve.drain()
                    dve.tensor_tensor(me[:, :, :], me[:, :, :], we[:, :, :], ALU.add)
                    dve.tensor_tensor(mc[:, :, :], rc[:, :, HF + H:W], wide(use[:, :]), ALU.mult)
                    dve.tensor_scalar(wc[:, :, :], wide(use[:, :]), -1.0, BIG, ALU.add, ALU.mult)
                    dve.drain()
                    dve.tensor_tensor(mc[:, :, :], mc[:, :, :], wc[:, :, :], ALU.add)
                    dve.drain()
                    dve.tensor_tensor(mx[:, :, :], me[:, :, :], mc[:, :, :], ALU.max)
                    dve.drain()
                    if own_e is not None:
                        dve.tensor_tensor(mx[:, :, :], mx[:, :, :], own_e[:, ts, :], ALU.max)
                        dve.drain()
                        dve.tensor_tensor(ws[:, :, :], own_e[:, ts, :], mx[:, :, :], ALU.subtract)
                    dve.tensor_tensor(we[:, :, :], me[:, :, :], mx[:, :, :], ALU.subtract)
                    dve.tensor_tensor(wc[:, :, :], mc[:, :, :], mx[:, :, :], ALU.subtract)
                    dve.drain().then_inc(exps, 1)
                    dve.wait_ge(expd, g + 1)
                    dve.tensor_tensor(we[:, :, :], we[:, :, :], wide(has), ALU.mult)
                    dve.tensor_tensor(wc[:, :, :], wc[:, :, :], wide(use[:, :]), ALU.mult)
                    dve.drain()
                    for j in range(GT):
                        for h in range(H):
                            f, d = slice(h * F, (h + 1) * F), slice(HF + h, HF + h + 1)
                            t = g * GT + j
                            dve.tensor_scalar(agg[:, t, f], re[:, j, f], we[:, j, h:h + 1], None, ALU.mult)
                            dve.tensor_scalar(den[:, t, h:h + 1], re[:, j, d], we[:, j, h:h + 1], None, ALU.mult)
                    dve.drain()
                    for j in range(GT):
                        for h in range(H):
                            f, d = slice(h * F, (h + 1) * F), slice(HF + h, HF + h + 1)
                            t = g * GT + j
                            dve.scalar_tensor_tensor(agg[:, t, f], rc[:, j, f], wc[:, j, h:h + 1], agg[:, t, f],
                                                     ALU.mult, ALU.add)
                            dve.scalar_tensor_tensor(den[:, t, h:h + 1], rc[:, j, d], wc[:, j, h:h + 1],
                                                     den[:, t, h:h + 1], ALU.mult, ALU.add)
                    if own_e is not None:
                        dve.drain()
                        for j in range(GT):
                            for h in range(H):
                                f, t = slice(h * F, (h + 1) * F), g * GT + j
                                dve.scalar_tensor_tensor(agg[:, t, f], own_f[:, t, f], ws[:, j, h:h + 1], agg[:, t, f],
                                                         ALU.mult, ALU.add)
                        dve.tensor_tensor(den[:, ts, :], den[:, ts, :], ws[:, :, :], ALU.add)
                    dve.drain().then_inc(free, 1)

            @block.scalar
            def _(act):
                for g in range(NT // GT):
                    act.wait_ge(exps, g + 1)
                    for x in (we, wc) + ((ws,) if own_e is not None else ()):
                        last = act.activation(x[:, :, :], x[:, :, :], ACT.Exp)
                    act.drain().then_inc(expd, 1)


def gat_nodes(m):
    nc, io = m.nc, m.io
    H, F = 4, 4
    ROW = H * F + 2 * H
    m.gat_src = m.dram("gat_src", [N, H * F + H])
    m.gat_dst = m.dram("gat_dst", [N, H])
    m.hg = m.sb("hg", [P, NT, ROW])
    with Stage(m):
        w = m.sb("gn_w", [128, K2, ROW])
        att = m.sb("gn_att", [128, 2, H * F])
        prod = m.sb("gn_prod", [128, 2, K2, H * F])
        loads, stored = Loads(m, "gn_loaded"), Loads(m, "gn_stored")
        w_ready, made, kept = m.sem("gn_w_ready"), m.sem("gn_made"), m.sem("gn_kept")
        with nc.Block() as block:
            @block.sync
            def _(sp):
                loads(sp, w[:, :, 0:H * F], io["L0_ffn_W_gat"].rearrange("(k p) d -> p k d", p=128))
                for i, name in enumerate(("L0_ffn_att_src", "L0_ffn_att_dst")):
                    loads(sp, att[:, i, :], io[name].rearrange("h c -> (h c)").partition_broadcast(128))
                sp.wait_ge(kept, NT + 4)
                stored(sp, m.gat_src.rearrange("(t p) c -> p t c", p=P), m.hg[:, :, 0:20])
                stored(sp, m.gat_dst.rearrange("(t p) c -> p t c", p=P), m.hg[:, :, 20:24])
                sp.wait_ge(stored.sem, stored.all)

            @block.vector
            def _(dve):
                dve.wait_ge(loads.sem, 48)
                for i in range(2):
                    for k in range(K2):
                        dve.tensor_tensor(prod[:, i, k, :], w[:, k, 0:16], att[:, i, :], ALU.mult)
                dve.drain()
                for i in range(2):
                    for k in range(K2):
                        dve.tensor_reduce(w[:, k, 16 + H * i:16 + H * (i + 1)],
                                          prod[:, i, k, :].rearrange("p (h c) -> p h c", h=H), AX.X, ALU.add)
                dve.drain().then_inc(w_ready, 1)

            @block.tensor
            def _(pe):
                pe.wait_ge(w_ready, 1)

                def body(t, j):
                    pe.wait_ge(kept, t + 1)
                    for k in range(K2):
                        last = pe.matmul(m.ps[j][:P, 0:ROW], m.XT[:, bass.ds(t * P + k * N, P)], w[:, k, :],
                                         start=k == 0, stop=k == K2 - 1)
                    last.then_inc(made, 1)
                tiles_written_out(NT, 4, body)

            @block.scalar
            def _(act):
                act.sem_inc(kept, 4)

                def body(t, j):
                    act.wait_ge(made, t + 1)
                    act.copy(m.hg[:, t, :], m.ps[j][:P, 0:ROW]).then_inc(kept, 1)
                tiles_written_out(NT, 4, body)


def gat_edges(m, ed, next_edges, next_lists):
    nc, io = m.nc, m.io
    H, F, cols = 4, 4, ed.cols
    HF, W = H * F, H * F + 2 * H
    nb = cols // BC
    m.agg0 = m.sb("agg0", [P, NT, HF])
    with Stage(m):
        last = m.sb("ge_last", [128, W])
        G = m.sb("ge_G", [128, cols, HF + H])
        idx = [m.sb(f"ge_idx{i}", [128, BC], I32) for i in range(2)]
        buf = [m.sb(f"ge_buf{i}", [128, BC, HF + H]) for i in range(2)]
        rows = [m.sem(f"ge_rows{i}") for i in range(2)]

        def gather_blocks(pool, lo, hi):
            assert lo % 2 == 0 and hi % 2 == 0

            def issue(t, j):
                pool.tensor_copy(idx[j][:, :], ed.other[:, at(t, BC)])
                pool.drain()
                for c in range(BC):
                    pool.indirect_dma_start(out=buf[j][:, c, :], out_offset=None, in_=m.gat_src,
                                            in_offset=bass.IndirectOffsetOnAxis(ap=idx[j][:, c:c + 1], axis=0)
                                            ).then_inc(rows[j], 16)

            def keep(t, j):
                pool.wait_ge(rows[j], (t - j) * (8 * BC) + 16 * BC)
                pool.tensor_copy(G[:, at(t, BC), :], buf[j][:, :, :])
                pool.drain()
            issue(lo, 0)
            with pool.Fori(0, (hi - lo) // 2 - 1) as i:
                issue(i * 2 + (lo + 1), 1)
                keep(i * 2 + lo, 0)
                issue(i * 2 + (lo + 2), 0)
                keep(i * 2 + (lo + 1), 1)
            issue(hi - 1, 1)
            keep(hi - 2, 0)
            keep(hi - 1, 1)

        share = {1: (0, 6), 3: (6, 20), 4: (20, cols // BC)}

        def beside(block, stage):
            @block.gpsimd
            def _(pool):
                gather_blocks(pool, *share[stage])
        sort_edges(m, next_edges, *next_lists, beside)
        spread = Spread(m, "ge", ed, H)
        own_e = m.sb("ge_own_e", [P, NT, H])
        den = m.sb("ge_den", [P, NT, H])
        dst_logits = m.sb("ge_dst_logits", [P, NT, H])
        result = m.dram("ge_result", [128 * cols, W])
        carry = m.dram("ge_carry", [128, W + 1])
        with nc.Block() as block:
            @block.vector
            def _(dve):
                dve.tensor_copy(dst_logits[:, :, :], m.hg[:, :, 20:24])
                dve.tensor_tensor(own_e[:, :, :], m.hg[:, :, 16:20], m.hg[:, :, 20:24], ALU.add)
                dve.drain()
                dve.scalar_tensor_tensor(own_e[:, :, :], own_e[:, :, :], 0.2, own_e[:, :, :], ALU.mult, ALU.max)
        spread_logits(m, "gs", ed, spread, m.gat_dst, dst_logits)
        with Stage(m):
            R = m.sb("ge_R", [128, cols, W])
            dec = m.sb("ge_dec", [128, cols, H])
            e_ready, e_exp, stored = m.sem("ge_e_ready"), m.sem("ge_e_exp"), m.sem("ge_stored")
            with nc.Block() as block:
                @block.vector
                def _(dve):
                    e = spread.ke
                    dve.tensor_tensor(e[:, :, :], G[:, :, HF:], e[:, :, :], ALU.add)
                    dve.drain()
                    dve.scalar_tensor_tensor(e[:, :, :], e[:, :, :], 0.2, e[:, :, :], ALU.mult, ALU.max)
                    dve.drain()
                    mx = R[:, :, HF + H:]
                    for h in range(H):
                        dve.tensor_tensor_scan(mx[:, :, h], spread.pen[:, :], e[:, :, h], -BIG, ALU.add, ALU.max)
                    dve.drain()
                    wide = spread.cont[:, :].unsqueeze(2).broadcast_to((128, cols, H))
                    dve.memset(dec[:, 0, :], 0.0)
                    dve.tensor_tensor(dec[:, 1:, :], mx[:, 0:cols - 1, :], mx[:, 1:, :], ALU.subtract)
                    dve.tensor_tensor(e[:, :, :], e[:, :, :], mx, ALU.subtract)
                    dve.drain()
                    dve.tensor_tensor(dec[:, :, :], dec[:, :, :], wide, ALU.mult)
                    dve.drain().then_inc(e_ready, 1)
                    dve.wait_ge(e_exp, 1)
                    dve.tensor_tensor(dec[:, :, :], dec[:, :, :], wide, ALU.mult)
                    for h in range(H):
                        f = G[:, :, h * F:(h + 1) * F]
                        dve.tensor_tensor(f, f, e[:, :, h].unsqueeze(2).broadcast_to((128, cols, F)), ALU.mult)
                    dve.drain()
                    for h in range(H):
                        for f in range(h * F, (h + 1) * F):
                            dve.tensor_tensor_scan(R[:, :, f], dec[:, :, h], G[:, :, f], 0.0, ALU.mult, ALU.add)
                        dve.tensor_tensor_scan(R[:, :, HF + h], dec[:, :, h], e[:, :, h], 0.0, ALU.mult, ALU.add)
                    dve.drain()
                    dve.tensor_copy(last[:, :], R[:, cols - 1, :])
                    dve.sem_inc(e_ready, 1)

                @block.scalar
                def _(act):
                    act.wait_ge(e_ready, 1)
                    act.activation(spread.ke[:, :, :], spread.ke[:, :, :], ACT.Exp)
                    act.activation(dec[:, :, :], dec[:, :, :], ACT.Exp)
                    act.drain().then_inc(e_exp, 1)

                @block.sync
                def _(sp):
                    sp.wait_ge(e_ready, 2)
                    sp.dma_start(result.rearrange("(p t) w -> p t w", p=128), R[:, :, :]).then_inc(stored, 16)
                    sp.wait_ge(stored, 16)
        carry_rows(m, "gc", ed, H, F, last, carry)
        merge_nodes(m, "gm", ed, spread, H, F, result, carry, m.agg0, den, own_e, m.hg)
        with nc.Block() as block:
            @block.vector
            def _(dve):
                dve.tensor_scalar(den[:, :, :], den[:, :, :], 1e-16, None, ALU.add)
                dve.drain()
                dve.reciprocal(den[:, :, :], den[:, :, :])
                dve.drain()
                for h in range(H):
                    f = m.agg0[:, :, h * F:(h + 1) * F]
                    dve.tensor_tensor(f, f, den[:, :, h].unsqueeze(2).broadcast_to((P, NT, F)), ALU.mult)


def top_two(dve, s, E, gt, eq, low, sel):
    def by_rank(op, out):
        for t in range(NT):
            dve.tensor_tensor(out[:, t], s[:, t, :].unsqueeze(1).broadcast_to((P, E, E)),
                              s[:, t, :].unsqueeze(2).broadcast_to((P, E, E)), op)
    by_rank(ALU.is_gt, gt)
    by_rank(ALU.is_equal, eq)
    dve.drain()
    for t in range(NT):
        dve.tensor_tensor(eq[:, t], eq[:, t], low, ALU.mult)
    dve.drain()
    dve.tensor_tensor(gt, gt, eq, ALU.add)
    dve.drain()
    dve.tensor_reduce(sel, gt, AX.X, ALU.add)
    dve.drain()
    dve.tensor_scalar(sel, sel, 1.5, None, ALU.is_lt)
    dve.drain()


def gates0(m):
    nc, io = m.nc, m.io
    H, E, C = 4, 4, 16
    m.gate0 = m.sb("gate0", [P, NT, E])
    with Stage(m):
        par = m.sb("gt_par", [P, 3, C])
        st = m.sb("gt_st", [P, NT, 6])
        mean, var, tmp = (m.sb("gt_" + x, [P, NT]) for x in ("mean", "var", "tmp"))
        s = m.sb("gt_s", [P, NT, E])
        gt = m.sb("gt_gt", [P, NT, E, E])
        eq = m.sb("gt_eq", [P, NT, E, E])
        low = m.sb("gt_low", [P, E, E])
        sel = m.sb("gt_sel", [P, NT, E])
        loads, low_ready, var_ready, std_ready, s_ready, s_exp = (
            Loads(m, "gt_loaded"), *(m.sem("gt_" + x) for x in ("low_ready", "var_ready", "std_ready", "s_ready", "s_exp")))
        with nc.Block() as block:
            @block.sync
            def _(sp):
                for i, name in enumerate(("L0_ffn_b_gat", "L0_ffn_ln_gamma", "L0_ffn_ln_beta")):
                    loads(sp, par[:, i, :], io[name].partition_broadcast(P))

            @block.gpsimd
            def _(pool):
                pool.memset(low[:, :, :], 1.0)
                pool.drain()
                pool.affine_select(out=low[:, :, :], in_=low[:, :, :], compare_op=ALU.is_gt, fill=0.0,
                                   base=0, pattern=[[1, E], [-1, E]], channel_multiplier=0)
                pool.drain().then_inc(low_ready, 1)

            @block.vector
            def _(dve):
                a = m.agg0
                all_nodes = lambda x: x.unsqueeze(1).broadcast_to((P, NT, C))
                by_node = lambda x: x.unsqueeze(2).broadcast_to((P, NT, C))
                dve.wait_ge(loads.sem, 48)
                dve.tensor_tensor(a[:, :, :], a[:, :, :], all_nodes(par[:, 0, :]), ALU.add)
                dve.drain()
                for t in range(NT):
                    dve.bn_stats(st[:, t, :], a[:, t, :])
                dve.drain()
                moments(dve, st, mean[:, :], var[:, :], tmp[:, :], C).then_inc(var_ready, 1)
                dve.wait_ge(std_ready, 1)
                dve.reciprocal(tmp[:, :], var[:, :])
                dve.tensor_tensor(a[:, :, :], a[:, :, :], by_node(mean[:, :]), ALU.subtract)
                dve.drain()
                dve.tensor_tensor(a[:, :, :], a[:, :, :], by_node(tmp[:, :]), ALU.mult)
                dve.drain()
                dve.tensor_tensor(a[:, :, :], a[:, :, :], all_nodes(par[:, 1, :]), ALU.mult)
                dve.drain()
                dve.tensor_tensor(a[:, :, :], a[:, :, :], all_nodes(par[:, 2, :]), ALU.add)
                dve.drain()
                dve.tensor_reduce(s[:, :, :], a[:, :, :].rearrange("p t (h e) -> p t e h", h=H), AX.X, ALU.add)
                dve.drain()
                dve.tensor_scalar(s[:, :, :], s[:, :, :], 1.0 / H, None, ALU.mult)
                dve.drain()
                dve.wait_ge(low_ready, 1)
                top_two(dve, s, E, gt[:, :, :, :], eq[:, :, :, :], low[:, :, :], sel[:, :, :])
                dve.tensor_reduce(tmp[:, :], s[:, :, :], AX.X, ALU.max)
                dve.drain()
                wide = tmp[:, :].unsqueeze(2).broadcast_to((P, NT, E))
                dve.tensor_tensor(s[:, :, :], s[:, :, :], wide, ALU.subtract).then_inc(s_ready, 1)
                dve.wait_ge(s_exp, 1)
                dve.tensor_tensor(s[:, :, :], s[:, :, :], sel[:, :, :], ALU.mult)
                dve.drain()
                dve.tensor_reduce(tmp[:, :], s[:, :, :], AX.X, ALU.add)
                dve.drain()
                dve.reciprocal(tmp[:, :], tmp[:, :])
                dve.drain()
                dve.tensor_tensor(m.gate0[:, :, :], s[:, :, :], wide, ALU.mult)

            @block.scalar
            def _(act):
                act.wait_ge(var_ready, 1)
                act.sqrt(var[:, :], var[:, :]).then_inc(std_ready, 1)
                act.wait_ge(s_ready, 1)
                act.activation(s[:, :, :], s[:, :, :], ACT.Exp).then_inc(s_exp, 1)


def experts(m, tag, parts, F, beside=None):
    nc = m.nc
    FC = F // 128
    with Stage(m):
        w1 = [m.sb(f"{tag}_w1_{i}", [128, K2, F]) for i in range(2)]
        w2 = [m.sb(f"{tag}_w2_{i}", [128, FC, D]) for i in range(2)]
        b1 = [m.sb(f"{tag}_b1_{i}", [128, FC]) for i in range(2)]
        b2 = [m.sb(f"{tag}_b2_{i}", [P, D]) for i in range(2)]
        hT = m.sb(tag + "_hT", [128, FC, CH])
        y = [m.sb(f"{tag}_y{i}", [P, D]) for i in range(2)]
        arrived = [m.sem(f"{tag}_arrived{i}") for i in range(2)]
        up, acted, down, added, read = (m.sem(f"{tag}_{x}") for x in ("up", "acted", "down", "added", "read"))
        with nc.Block() as block:
            if beside is not None:
                @block.gpsimd
                def _(pool):
                    beside(pool)

            @block.sync
            def _(sp):
                for e, (a, ab, b, bb, gate) in enumerate(parts):
                    i = e % 2
                    if e >= 2:
                        sp.wait_ge(added, (e - 1) * NT + 2)
                    sp.dma_start(w1[i][:, :, :], a.rearrange("(k p) f -> p k f", p=128)).then_inc(arrived[i], 16)
                    sp.dma_start(b1[i][:, :], ab).then_inc(arrived[i], 16)
                    sp.dma_start(w2[i][:, :, :], b.rearrange("(k p) d -> p k d", p=128)).then_inc(arrived[i], 16)
                    sp.dma_start(b2[i][:, :], bb.partition_broadcast(P)).then_inc(arrived[i], 16)

            @block.tensor
            def _(pe):
                for e in range(len(parts)):
                    i = e % 2
                    pe.wait_ge(arrived[i], 64 * (e // 2 + 1))

                    def body(c, nt):
                        for f in range(FC):
                            pe.wait_ge(acted, (e * (NCH + 1) + c) * FC + f + 1)
                            for k in range(K2):
                                last = pe.matmul(m.ps[f % 4][:, 0:nt * P], w1[i][:, k, f * 128:(f + 1) * 128],
                                                 m.XT[:, bass.ds(c * CH + k * N, nt * P)], start=k == 0, stop=k == K2 - 1)
                            last.then_inc(up, 1)
                        pe.wait_ge(acted, (e * (NCH + 1) + c) * FC + FC + 4)
                        for j in range(nt):
                            t = e * NT + c * 4 + j
                            pe.wait_ge(added, t + (2 if j == 0 else 1))
                            for f in range(FC):
                                last = pe.matmul(m.ps[4 + j % 2][:P, 0:D], hT[:, f, j * P:(j + 1) * P], w2[i][:, f, :],
                                                 start=f == 0, stop=f == FC - 1)
                            last.then_inc(down, 1)
                    chunks(pe, body)

            @block.scalar
            def _(act):
                act.sem_inc(acted, 4)
                for e in range(len(parts)):
                    i = e % 2

                    def body(c, nt):
                        act.wait_ge(read, e * NT + c * 4 + 1)
                        for f in range(FC):
                            act.wait_ge(up, (e * (NCH + 1) + c) * FC + f + 1)
                            act.activation(hT[:, f, 0:nt * P], m.ps[f % 4][:, 0:nt * P], ACT.Gelu,
                                           bias=b1[i][:, f:f + 1]).then_inc(acted, 1)
                    chunks(act, body)

            @block.vector
            def _(dve):
                dve.sem_inc(added, 2)
                dve.sem_inc(read, 1)
                for e, (a, ab, b, bb, gate) in enumerate(parts):
                    i = e % 2

                    def body(c, nt):
                        dve.drain()
                        for j in range(nt):
                            t = c * 4 + j
                            x = m.X[:, at(t, D)]
                            dve.wait_ge(down, e * NT + t + 1)
                            dve.tensor_tensor(y[j % 2][:, :], m.ps[4 + j % 2][:P, 0:D], b2[i][:, :], ALU.add
                                              ).then_inc(read, 1)
                            dve.drain()
                            if gate is None:
                                dve.tensor_tensor(x, y[j % 2][:, :], x, ALU.add).then_inc(added, 1)
                            else:
                                dve.scalar_tensor_tensor(x, y[j % 2][:, :], gate(t), x, ALU.mult, ALU.add).then_inc(added, 1)
                    chunks(dve, body)


TS = 256


class Routes:

    def __init__(self, m, tag, E):
        self.tag, self.E = tag, E
        self.tiles = (2 * N + E * (TS - 1)) // TS
        self.slot = m.sb(tag + "_slot", [P, 2, NT], I32)
        self.gate = m.sb(tag + "_gate", [P, 2, NT])
        self.rows = m.sb(tag + "_rows", [128, self.tiles], I32)
        self.x = m.dram(tag + "_x", [self.tiles * TS, D])
        self.y = m.dram(tag + "_y", [self.tiles * TS, D])


def find_routes(m, r, sel, gate):
    nc, E, tag, TL = m.nc, r.E, r.tag, r.tiles
    TOP = float(1 << 15)
    with Stage(m):
        zero = m.sb(tag + "_zero", [128, 16 * D])
        count, before, pos, pick = (m.sb(tag + x, [128, NT, E]) for x in ("_count", "_before", "_pos", "_pick"))
        need, num, rest, end = (m.sb(tag + x, [128, E]) for x in ("_need", "_num", "_rest", "_end"))
        slot = m.sb(tag + "_slot_f", [P, 2, NT])
        line = m.sb(tag + "_line", [128, 1])
        row = m.sb(tag + "_row", [128, TL])
        zeroed, counted, lined, cleared = (m.sem(tag + x) for x in ("_zeroed", "_counted", "_lined", "_cleared"))
        with nc.Block() as block:
            @block.gpsimd
            def _(pool):
                pool.memset(zero[:, :], 0.0).then_inc(zeroed, 1)
                pool.iota(line[:, :], [[1, 1]], base=0, channel_multiplier=1,
                          allow_small_or_imprecise_dtypes=True).then_inc(lined, 1)

            @block.sync
            def _(sp):
                sp.wait_ge(zeroed, 1)
                x = r.x.rearrange("(p s) d -> p (s d)", p=128)
                wide, count = TL * TS // 128 * D, 0
                for lo in range(0, wide, 16 * D):
                    size = min(16 * D, wide - lo)
                    sp.dma_start(x[:, lo:lo + size], zero[:, 0:size]).then_inc(cleared, 16)
                    count += 16
                sp.wait_ge(cleared, count)

            @block.tensor
            def _(pe):
                s = sel.rearrange("p t e -> p (t e)")
                pe.matmul(m.ps[0][:, 0:NT * E], m.low[:P, :], s, start=True, stop=True)
                pe.matmul(m.ps[1][:, 0:NT * E], m.ones[:P, 0:128], s, start=True, stop=True).then_inc(counted, 1)

            @block.vector
            def _(dve):
                dve.wait_ge(counted, 1)
                dve.tensor_copy(count[:, :, :], m.ps[1][:, 0:NT * E].rearrange("p (t e) -> p t e", e=E))
                dve.drain()
                for e in range(E):
                    dve.tensor_tensor_scan(before[:, :, e], m.ones[:, 0:NT], count[:, :, e], 0.0, ALU.mult, ALU.add)
                dve.drain()
                dve.tensor_scalar(need[:, :], before[:, NT - 1, :], float(TS - 1), None, ALU.add)
                dve.drain()
                dve.tensor_tensor(before[:, :, :], before[:, :, :], count[:, :, :], ALU.subtract)
                dve.drain()
                floor_div(dve, num[:, :], rest[:, :], need[:, :], TS)
                dve.tensor_tensor_scan(end[:, :], m.ones[:, 0:E], num[:, :], 0.0, ALU.mult, ALU.add)
                dve.drain()
                dve.tensor_tensor(rest[:, :], end[:, :], num[:, :], ALU.subtract)
                dve.tensor_tensor(pos[:, :, :], before[:, :, :],
                                  m.ps[0][:, 0:NT * E].rearrange("p (t e) -> p t e", e=E), ALU.add)
                dve.drain()
                dve.tensor_scalar(rest[:, :], rest[:, :], float(TS), None, ALU.mult)
                dve.drain()
                dve.tensor_tensor(pos[:, :, :], pos[:, :, :], rest[:, :].unsqueeze(1).broadcast_to((128, NT, E)), ALU.add)
                dve.drain()
                p = pos[:P, :, :]
                dve.tensor_tensor(pick[:P, :, :], p, sel, ALU.mult)
                dve.tensor_scalar(before[:P, :, :], p, -1.0, TOP, ALU.mult, ALU.add)
                dve.drain()
                dve.tensor_tensor(before[:P, :, :], before[:P, :, :], sel, ALU.mult)
                dve.tensor_reduce(slot[:, 1, :], pick[:P, :, :], AX.X, ALU.max)
                dve.drain()
                dve.tensor_reduce(slot[:, 0, :], before[:P, :, :], AX.X, ALU.max)
                dve.drain()
                dve.tensor_scalar(slot[:, 0, :], slot[:, 0, :], -1.0, TOP, ALU.mult, ALU.add)
                dve.drain()
                dve.tensor_copy(r.slot[:, :, :], slot[:, :, :])
                for i in range(2):
                    dve.tensor_tensor(pick[:P, :, :], p, slot[:, i, :].unsqueeze(2).broadcast_to((P, NT, E)), ALU.is_equal)
                    dve.drain()
                    dve.tensor_tensor(pick[:P, :, :], pick[:P, :, :], gate, ALU.mult)
                    dve.drain()
                    dve.tensor_reduce(r.gate[:, i, :], pick[:P, :, :], AX.X, ALU.add)
                    dve.drain()
                dve.tensor_scalar(row[:, :], m.row16[:, 0:TL], end[:, 0:1], None, ALU.is_ge)
                dve.drain()
                for e in range(1, E - 1):
                    dve.scalar_tensor_tensor(row[:, :], m.row16[:, 0:TL], end[:, e:e + 1], row[:, :], ALU.is_ge, ALU.add)
                    dve.drain()
                dve.wait_ge(lined, 1)
                dve.tensor_scalar(row[:, :], row[:, :], 128.0, line[:, 0:1], ALU.mult, ALU.add)
                dve.drain()
                dve.tensor_copy(r.rows[:, :], row[:, :])


def scatter_nodes(m, r, pool, placed):
    for t in range(NT):
        for i in range(2):
            pool.indirect_dma_start(out=r.x, out_offset=bass.IndirectOffsetOnAxis(ap=r.slot[:, i, t:t + 1], axis=0),
                                    in_=m.XN[:, t * D:(t + 1) * D], in_offset=None,
                                    bounds_check=r.tiles * TS - 1, oob_is_err=False).then_inc(placed, 16)


def routed_experts(m, r, packed, F):
    nc, tag, TL = m.nc, r.tag, r.tiles
    FC, S = F // 128, TS // 128
    O2, OB1, OB2 = K2 * F, K2 * F + FC * D, K2 * F + FC * D + FC
    assert TL % 2 == 0
    with Stage(m):
        w = [m.sb(f"{tag}_w{i}", [128, OB2 + D]) for i in range(2)]
        w1 = [x[:, 0:O2].rearrange("p (k f) -> p k f", k=K2) for x in w]
        w2 = [x[:, O2:OB1].rearrange("p (f d) -> p f d", d=D) for x in w]
        xs = [m.sb(f"{tag}_xs{i}", [128, S, D]) for i in range(2)]
        xT = [m.sb(f"{tag}_xT{i}", [128, K2, TS]) for i in range(2)]
        hT = [m.sb(f"{tag}_hT{i}", [128, FC, TS]) for i in range(2)]
        y = [m.sb(f"{tag}_ys{i}", [128, S, D]) for i in range(2)]
        w_loaded, x_loaded, y_stored = ([m.sem(f"{tag}_{x}{i}") for i in range(2)]
                                        for x in ("w_loaded", "x_loaded", "y_stored"))
        turned, x_ready, up, acted, down, y_read, y_made = (
            m.sem(f"{tag}_{x}") for x in ("turned", "x_ready", "up", "acted", "down", "y_read", "y_made"))

        def all_tiles(eng, body):
            with eng.Fori(0, TL // 2 - 1) as i:
                for j in range(2):
                    body(i * 2 + j, j, True, True)
            body(TL - 2, 0, True, False)
            body(TL - 1, 1, False, False)

        with nc.Block() as block:
            @block.gpsimd
            def _(pool):
                for i in range(TL):
                    if i >= 2:
                        pool.wait_ge(y_made, i - 1)
                    pool.indirect_dma_start(out=w[i % 2][:, :], out_offset=None, in_=packed,
                                            in_offset=bass.IndirectOffsetOnAxis(ap=r.rows[:, i:i + 1], axis=0)
                                            ).then_inc(w_loaded[i % 2], 16)

            @block.sync
            def _(sp):
                slots = lambda table, i: table[at(i, TS), :].rearrange("(s p) d -> p s d", p=128)
                load = lambda i, j: sp.dma_start(xs[j][:, :, :], slots(r.x, i)).then_inc(x_loaded[j], 16)
                load(0, 0)
                load(1, 1)

                def body(i, j, follows, follow2):
                    if follow2:
                        sp.wait_ge(turned, i + 1)
                        load(i + 2, j)
                    sp.wait_ge(y_made, i + 1)
                    sp.dma_start(slots(r.y, i), y[j][:, :, :]).then_inc(y_stored[j], 16)
                all_tiles(sp, body)
                for j in range(2):
                    sp.wait_ge(y_stored[j], 16 + 8 * TL)

            @block.tensor
            def _(pe):
                def turn(i, j):
                    pe.wait_ge(x_loaded[j], (i - j) * 8 + 16)
                    for k in range(K2):
                        for s in range(S):
                            c = (k * S + s) * 128
                            last = pe.transpose(m.ps[6][:, c:c + 128], xs[j][:, s, k * 128:(k + 1) * 128], m.ident[:, :])
                    last.then_inc(turned, 1)
                turn(0, 0)

                def body(i, j, follows, follow2):
                    pe.wait_ge(w_loaded[j], (i - j) * 8 + 16)
                    pe.wait_ge(x_ready, i + 1)
                    for f in range(FC):
                        pe.wait_ge(acted, i * FC + f + 1)
                        for k in range(K2):
                            last = pe.matmul(m.ps[f % 4][:, 0:TS], w1[j][:, k, f * 128:(f + 1) * 128], xT[j][:, k, :],
                                             start=k == 0, stop=k == K2 - 1)
                        last.then_inc(up, 1)
                    if follows:
                        turn(i + 1, 1 - j)
                    pe.wait_ge(acted, i * FC + FC + 4)
                    for s in range(S):
                        pe.wait_ge(y_read, i * S + s + 1)
                        for f in range(FC):
                            last = pe.matmul(m.ps[4 + s][:, 0:D], hT[j][:, f, s * 128:(s + 1) * 128], w2[j][:, f, :],
                                             start=f == 0, stop=f == FC - 1)
                        last.then_inc(down, 1)
                all_tiles(pe, body)

            @block.scalar
            def _(act):
                act.sem_inc(acted, 4)

                def body(i, j, follows, follow2):
                    act.wait_ge(y_read, i * S + 1)
                    for f in range(FC):
                        act.wait_ge(up, i * FC + f + 1)
                        act.activation(hT[j][:, f, :], m.ps[f % 4][:, 0:TS], ACT.Gelu,
                                       bias=w[j][:, OB1 + f:OB1 + f + 1]).then_inc(acted, 1)
                all_tiles(act, body)

            @block.vector
            def _(dve):
                dve.sem_inc(y_read, S)
                for j in range(2):
                    dve.sem_inc(y_stored[j], 16)

                def take(i, j):
                    dve.wait_ge(turned, i + 1)
                    dve.tensor_copy(xT[j][:, :, :], m.ps[6][:, :].rearrange("p (k c) -> p k c", k=K2)).then_inc(x_ready, 1)
                take(0, 0)

                def body(i, j, follows, follow2):
                    if follows:
                        take(i + 1, 1 - j)
                    dve.wait_ge(y_stored[j], (i - j) * 8 + 16)
                    for s in range(S):
                        dve.wait_ge(down, i * S + s + 1)
                        last = dve.tensor_tensor(y[j][:, s, :], m.ps[4 + s][:, 0:D], w[j][:, OB2:OB2 + D], ALU.add)
                        last.then_inc(y_read, 1)
                    dve.drain().then_inc(y_made, 1)
                all_tiles(dve, body)

    with Stage(m):
        R = 5
        near = [m.sb(f"{tag}_near{j}", [P, 2, D]) for j in range(R)]
        rows = [m.sem(f"{tag}_rows{j}") for j in range(R)]
        free = m.sem(tag + "_free")
        with nc.Block() as block:
            @block.gpsimd
            def _(pool):
                for t in range(NT):
                    if t >= R:
                        pool.wait_ge(free, t - R + 1)
                    for i in range(2):
                        pool.indirect_dma_start(out=near[t % R][:, i, :], out_offset=None, in_=r.y,
                                                in_offset=bass.IndirectOffsetOnAxis(ap=r.slot[:, i, t:t + 1], axis=0)
                                                ).then_inc(rows[t % R], 16)

            @block.vector
            def _(dve):
                with dve.Fori(0, NT // R) as g:
                    for j in range(R):
                        x = m.X[:, bass.ds(g * (R * D) + j * D, D)]
                        dve.wait_ge(rows[j], g * 32 + 32)
                        for i in range(2):
                            last = dve.scalar_tensor_tensor(x, near[j][:, i, :],
                                                            r.gate[:, i, :][:, bass.ds(g * R + j, 1)], x, ALU.mult, ALU.add)
                            if i == 0:
                                dve.drain()
                        last.then_inc(free, 1)


def gnn1_nodes(m):
    nc, io = m.nc, m.io
    H, F = 2, 128
    ROW = D + 2 * H
    m.wh_dram = m.dram("wh_dram", [N, D + H])
    m.s_dram = m.dram("s_dram", [N, H])
    m.s_logits = m.sb("s_logits", [P, NT, H])
    with Stage(m):
        w = m.sb("h1_w", [128, K2, ROW])
        bias = m.sb("h1_bias", [128, ROW])
        att = m.sb("h1_att", [128, 2, D])
        prod = m.sb("h1_prod", [128, 2, K2 + 1, D])
        row = [m.sb(f"h1_row{i}", [P, ROW]) for i in range(4)]
        loads, stored = Loads(m, "h1_loaded"), [m.sem(f"h1_stored{i}") for i in range(4)]
        w_ready, made, kept = m.sem("h1_w_ready"), m.sem("h1_made"), m.sem("h1_kept")
        s_stored = m.sem("h1_s_stored")
        with nc.Block() as block:
            @block.sync
            def _(sp):
                loads(sp, w[:, :, 0:D], io["L1_gnn_W_w"].rearrange("(k p) d -> p k d", p=128))
                loads(sp, bias[:, 0:D], io["L1_gnn_W_b"].partition_broadcast(128))
                for i in range(2):
                    half = io["L1_gnn_a"][(1 - i) * F:(2 - i) * F].partition_broadcast(128)
                    for h in range(H):
                        loads(sp, att[:, i, h * F:(h + 1) * F], half)

                def body(t, j):
                    sp.wait_ge(kept, t + 5)
                    sp.dma_start(m.wh_dram[t * P:(t + 1) * P, :], row[j][:, 0:D + H]).then_inc(stored[j], 16)
                tiles_written_out(NT, 4, body)
                sp.dma_start(m.s_dram.rearrange("(t p) h -> p t h", p=P), m.s_logits[:, :, :]).then_inc(s_stored, 16)
                sp.wait_ge(s_stored, 16)
                for i in range(4):
                    sp.wait_ge(stored[i], 16 * len(range(i, NT, 4)))

            @block.vector
            def _(dve):
                dve.wait_ge(loads.sem, 96)
                for i in range(2):
                    for k in range(K2):
                        dve.tensor_tensor(prod[:, i, k, :], w[:, k, 0:D], att[:, i, :], ALU.mult)
                    dve.tensor_tensor(prod[:, i, K2, :], bias[:, 0:D], att[:, i, :], ALU.mult)
                dve.drain()
                for i in range(2):
                    lo = D + H * i
                    for k in range(K2):
                        dve.tensor_reduce(w[:, k, lo:lo + H], prod[:, i, k, :].rearrange("p (h c) -> p h c", h=H),
                                          AX.X, ALU.add)
                    dve.tensor_reduce(bias[:, lo:lo + H], prod[:, i, K2, :].rearrange("p (h c) -> p h c", h=H),
                                      AX.X, ALU.add)
                dve.drain().then_inc(w_ready, 1)
                dve.sem_inc(kept, 4)

                def body(t, j):
                    dve.wait_ge(made, t + 1)
                    if t >= 4:
                        dve.wait_ge(stored[j], 16 * (t // 4))
                    dve.tensor_tensor(row[j][:, :], m.ps[j][:P, 0:ROW], bias[:P, :], ALU.add)
                    dve.drain()
                    dve.tensor_copy(m.s_logits[:, t, :], row[j][:, D + H:])
                    dve.drain().then_inc(kept, 1)
                tiles_written_out(NT, 4, body)

            @block.tensor
            def _(pe):
                pe.wait_ge(w_ready, 1)

                def body(t, j):
                    pe.wait_ge(kept, t + 1)
                    for k in range(K2):
                        last = pe.matmul(m.ps[j][:P, 0:ROW], m.XT[:, bass.ds(t * P + k * N, P)], w[:, k, :],
                                         start=k == 0, stop=k == K2 - 1)
                    last.then_inc(made, 1)
                tiles_written_out(NT, 4, body)


def gnn1_edges(m, ed):
    nc, io = m.nc, m.io
    H, F, cols = 2, 128, ed.cols
    HF, W = D, D + 2 * H
    nb = cols // BC
    with Stage(m):
        spread = Spread(m, "he", ed, H)
        spread_logits(m, "hs", ed, spread, m.s_dram, m.s_logits)
        result = m.dram("he_result", [128 * cols, W])
        carry = m.dram("he_carry", [128, W + 1])
        last = m.sb("he_last", [128, W])
        with Stage(m):
            idx = [m.sb(f"he_idx{i}", [128, BC], I32) for i in range(2)]
            buf = [m.sb(f"he_buf{i}", [128, BC, W]) for i in range(2)]
            e = [m.sb(f"he_e{i}", [128, BC, H]) for i in range(2)]
            dec = [m.sb(f"he_dec{i}", [128, BC, H]) for i in range(2)]
            pen_b = m.sb("he_pen_b", [128, BC])
            con_b = m.sb("he_con_b", [128, BC])
            rows, stored = ([m.sem(f"he_{x}{i}") for i in range(2)] for x in ("rows", "stored"))
            idx_ready, free, e_ready, e_exp, weighted, summed = (
                m.sem("he_" + x) for x in ("idx_ready", "free", "e_ready", "e_exp", "weighted", "summed"))
            with nc.Block() as block:
                @block.gpsimd
                def _(pool):
                    def body(t, j):
                        pool.wait_ge(idx_ready, t + 1)
                        pool.sem_inc(m.spare, 1)
                        for c in range(BC):
                            pool.indirect_dma_start(out=buf[j][:, c, 0:HF + H], out_offset=None, in_=m.wh_dram,
                                                    in_offset=bass.IndirectOffsetOnAxis(ap=idx[j][:, c:c + 1], axis=0)
                                                    ).then_inc(rows[j], 16)
                    tiles(pool, nb, 2, body)

                @block.vector
                def _(dve):
                    def fetch(t, j):
                        dve.tensor_scalar(idx[j][:, :], ed.other[:, at(t, BC)], 0.0, None, ALU.add)
                        dve.drain().then_inc(idx_ready, 1)
                    dve.memset(last[:, 0:HF + H], 0.0)
                    dve.memset(last[:, HF + H:], -BIG)
                    fetch(0, 0)
                    fetch(1, 1)

                    def body(t, j, more=True):
                        v = buf[j]
                        k = (t - j) * 8 * BC + 16 * BC
                        dve.wait_ge(rows[j], k)
                        dve.tensor_tensor(e[j][:, :, :], v[:, :, HF:HF + H], spread.ke[:, at(t, BC), :], ALU.add)
                        dve.tensor_scalar(pen_b[:, :], spread.pen[:, at(t, BC)], 0.0, None, ALU.add)
                        dve.tensor_scalar(con_b[:, :], spread.cont[:, at(t, BC)], 0.0, None, ALU.add)
                        dve.drain()
                        dve.scalar_tensor_tensor(e[j][:, :, :], e[j][:, :, :], 0.2, e[j][:, :, :], ALU.mult, ALU.max)
                        dve.drain()
                        mx = v[:, :, HF + H:]
                        for h in range(H):
                            dve.tensor_tensor_scan(mx[:, :, h], pen_b[:, :], e[j][:, :, h],
                                                   last[:, HF + H + h:HF + H + h + 1], ALU.add, ALU.max)
                        dve.drain()
                        wide = con_b[:, :].unsqueeze(2).broadcast_to((128, BC, H))
                        dve.tensor_tensor(dec[j][:, 0, :], last[:, HF + H:], mx[:, 0, :], ALU.subtract)
                        dve.tensor_tensor(dec[j][:, 1:, :], mx[:, 0:BC - 1, :], mx[:, 1:, :], ALU.subtract)
                        dve.tensor_tensor(e[j][:, :, :], e[j][:, :, :], mx, ALU.subtract)
                        dve.drain()
                        dve.tensor_tensor(dec[j][:, :, :], dec[j][:, :, :], wide, ALU.mult)
                        dve.drain().then_inc(e_ready, 1)
                        dve.wait_ge(e_exp, t + 1)
                        dve.tensor_tensor(dec[j][:, :, :], dec[j][:, :, :], wide, ALU.mult)
                        dve.drain()
                        for h in range(H):
                            dve.tensor_tensor_scan(v[:, :, HF + h], dec[j][:, :, h], e[j][:, :, h],
                                                   last[:, HF + h:HF + h + 1], ALU.mult, ALU.add)
                        for c in range(BC):
                            dve.wait_ge(weighted, t * BC + c + 1)
                            prev = last if c == 0 else v[:, c - 1, :]
                            for h in range(H):
                                f = slice(h * F, (h + 1) * F)
                                dve.scalar_tensor_tensor(v[:, c, f], prev[:, f], dec[j][:, c, h:h + 1], v[:, c, f],
                                                         ALU.mult, ALU.add)
                            dve.drain()
                        dve.tensor_scalar(last[:, :], v[:, BC - 1, :], 0.0, None, ALU.add)
                        dve.drain().then_inc(summed, 1)
                        if more:
                            dve.wait_ge(stored[j], (t - j) * 8 + 16)
                            fetch(t + 2, j)
                    half = (nb - 2) // 2
                    with dve.Fori(0, half) as i:
                        for j in range(2):
                            body(i * 2 + j, j)
                    for t in range(half * 2, nb):
                        body(t, t % 2, t + 2 < nb)

                @block.scalar
                def _(act):
                    def body(t, j):
                        act.wait_ge(e_ready, t + 1)
                        act.activation(e[j][:, :, :], e[j][:, :, :], ACT.Exp)
                        act.activation(dec[j][:, :, :], dec[j][:, :, :], ACT.Exp)
                        act.drain().then_inc(e_exp, 1)
                        for c in range(BC):
                            for h in range(H):
                                f = buf[j][:, c, h * F:(h + 1) * F]
                                x = act.activation(f, f, ACT.Copy, scale=e[j][:, c, h:h + 1])
                            x.then_inc(weighted, 1)
                    tiles(act, nb, 2, body)

                @block.sync
                def _(sp):
                    def body(t, j):
                        sp.wait_ge(summed, t + 1)
                        sp.sem_inc(m.spare, 1)
                        sp.dma_start(result.rearrange("(p t) w -> p t w", p=128)[:, at(t, BC), :], buf[j][:, :, :]
                                     ).then_inc(stored[j], 16)
                    tiles(sp, nb, 2, body)
                    for i in range(2):
                        sp.wait_ge(stored[i], 16 * len(range(i, nb, 2)))
        carry_rows(m, "hc", ed, H, F, last, carry)
        agg = m.sb("he_agg", [P, NT, HF])
        den = m.sb("he_den", [P, NT, H])
        merge_nodes(m, "hm", ed, spread, H, F, result, carry, agg, den)
        own = m.sb("he_own", [P, NT, HF])
        none = m.sb("he_none", [P, NT])
        own_loaded = m.sem("he_own_loaded")
        with nc.Block() as block:
            @block.sync
            def _(sp):
                sp.dma_start(own[:, :, :], m.wh_dram.rearrange("(t p) c -> p t c", p=P)[:, :, 0:HF]).then_inc(own_loaded, 16)

            @block.vector
            def _(dve):
                has = spread.has
                dve.tensor_scalar(none[:, :], has[:, :], -1.0, 1.0, ALU.mult, ALU.add)
                dve.drain()
                dve.tensor_tensor(den[:, :, :], den[:, :, :], none[:, :].unsqueeze(2).broadcast_to((P, NT, H)), ALU.add)
                dve.drain()
                dve.reciprocal(den[:, :, :], den[:, :, :])
                dve.drain()
                for t in range(NT):
                    for h in range(H):
                        lo = t * D + h * F
                        x = m.X[:, lo:lo + F]
                        dve.scalar_tensor_tensor(x, agg[:, t, h * F:(h + 1) * F], den[:, t, h:h + 1], x, ALU.mult, ALU.add)
                dve.wait_ge(own_loaded, 16)
                dve.drain()
                for t in range(NT):
                    x = m.X[:, t * D:(t + 1) * D]
                    dve.scalar_tensor_tensor(x, own[:, t, :], none[:, t:t + 1], x, ALU.mult, ALU.add)


def mix1(m):
    nc, io = m.nc, m.io
    HD = 32
    FF = 1024
    FC = FF // 128
    with Stage(m):
        wq, wk, wv, wo = (m.sb("m1_w" + x, [128, K2, D]) for x in "qkvo")
        bq = m.sb("m1_bq", [128, K2])
        rowb = m.sb("m1_rows", [P, 8, D])
        w1 = m.sb("m1_w1", [128, K2, FF])
        b1 = m.sb("m1_b1", [128, FC])
        w2 = m.sb("m1_w2", [128, FC, D])
        k_raw = [m.sb(f"m1_kraw{i}", [P, D]) for i in range(2)]
        k_low = [m.sb(f"m1_klow{i}", [P, D]) for i in range(2)]
        kp = [m.sb(f"m1_kp{i}", [P, D]) for i in range(2)]
        v1 = [m.sb(f"m1_v1{i}", [P, K2, 129]) for i in range(2)]
        bmask = m.sb("m1_bmask", [128, 128])
        kv = m.sb("m1_kv", [128, K2, 128])
        ks = m.sb("m1_ks", [128, K2, 128])
        loads = Loads(m, "m1_loaded")
        made, kv_in, kv_used, kv_done, kx, kexp, mask_ready = (
            m.sem("m1_" + x) for x in ("made", "kv_in", "kv_used", "kv_done", "kx", "kexp", "mask_ready"))
        with nc.Block() as block:
            @block.sync
            def _(sp):
                for t, name in ((wk, "Wk"), (wv, "Wv")):
                    loads(sp, t[:, :, :], io["L1_mix_" + name].rearrange("(k p) d -> p k d", p=128))
                for i, name in enumerate(("bk", "bv", "bo", "b2", "ln1_g", "ln1_b", "ln2_g", "ln2_b")):
                    loads(sp, rowb[:, i, :], io["L1_mix_" + name].partition_broadcast(P))
                for t, name in ((wq, "Wq"), (wo, "Wo"), (w1, "W1"), (w2, "W2")):
                    loads(sp, t[:, :, :], io["L1_mix_" + name].rearrange("(k p) d -> p k d", p=128))
                loads(sp, bq[:, :], io["L1_mix_bq_cols"])
                loads(sp, b1[:, :], io["L1_mix_b1_cols"])

            @block.gpsimd
            def _(pool):
                pool.memset(bmask[:, :], 1.0)
                pool.drain()
                blocks = bmask[:, :].rearrange("p (h c) -> p h c", c=HD)
                pool.affine_select(out=blocks, in_=blocks, compare_op=ALU.is_ge, fill=0.0, base=0,
                                   pattern=[[-HD, 4], [0, HD]], channel_multiplier=1)
                pool.drain()
                pool.affine_select(out=blocks, in_=blocks, compare_op=ALU.is_ge, fill=0.0, base=HD - 1,
                                   pattern=[[HD, 4], [0, HD]], channel_multiplier=-1)
                pool.drain().then_inc(mask_ready, 1)

            @block.tensor
            def _(pe):
                pe.wait_ge(loads.sem, 16 * 16)
                for k in range(K2):
                    pe.matmul(m.ps[4 + k][:, 0:129], m.zero16[:, 0:128], m.zero16[:, 0:129], start=True, stop=False)

                def keys(t):
                    pe.wait_ge(kx, t + 1)
                    for half, w in ((0, wk), (1, wv)):
                        for k in range(K2):
                            x = pe.matmul(m.ps[t % 2][:P, half * D:(half + 1) * D], m.XT[:, bass.ds(t * P + k * N, P)],
                                          w[:, k, :], start=k == 0, stop=k == K2 - 1)
                    x.then_inc(made, 1)

                def outer(t):
                    j = t % 2
                    pe.wait_ge(kv_in, t + 1)
                    for k in range(K2):
                        x = pe.matmul(m.ps[4 + k][:, 0:129], kp[j][:, k * 128:(k + 1) * 128], v1[j][:, k, :],
                                      start=False, stop=t == NT - 1)
                    x.then_inc(kv_used, 1)
                keys(0)
                for t in range(NT):
                    if t + 1 < NT:
                        keys(t + 1)
                    outer(t)

            @block.vector
            def _(dve):
                dve.wait_ge(loads.sem, 16 * 16)
                for j in range(2):
                    dve.memset(v1[j][:, :, 128:129], 1.0)
                dve.sem_inc(kv_used, 2)
                dve.sem_inc(kx, 2)

                def body(t, j):
                    dve.wait_ge(made, t + 1)
                    dve.wait_ge(kv_used, t + 1)
                    dve.tensor_tensor(k_raw[j][:, :], m.ps[j][:P, 0:D], rowb[:, 0, :], ALU.add)
                    dve.tensor_tensor(v1[j][:, :, 0:128], m.ps[j][:P, D:2 * D].rearrange("p (k c) -> p k c", k=K2),
                                      rowb[:, 1, :].rearrange("p (k c) -> p k c", k=K2), ALU.add)
                    dve.drain().then_inc(kx, 1)
                    dve.tensor_scalar(k_low[j][:, :], k_raw[j][:, :], 0.0, None, ALU.min)
                    dve.drain().then_inc(kexp, 1)
                    dve.wait_ge(kexp, 2 * t + 2)
                    dve.scalar_tensor_tensor(kp[j][:, :], k_raw[j][:, :], 0.0, k_low[j][:, :], ALU.max, ALU.add)
                    dve.drain().then_inc(kv_in, 1)
                tiles(dve, NT, 2, body)
                dve.wait_ge(kv_used, NT + 2)
                dve.wait_ge(mask_ready, 1)
                for k in range(K2):
                    dve.tensor_tensor(kv[:, k, :], m.ps[4 + k][:, 0:128], bmask[:, :], ALU.mult)
                    dve.tensor_scalar(ks[:, k, :], bmask[:, :], m.ps[4 + k][:, 128:129], None, ALU.mult)

            @block.scalar
            def _(act):
                def body(t, j):
                    act.wait_ge(kexp, 2 * t + 1)
                    act.activation(k_low[j][:, :], k_low[j][:, :], ACT.Exp).then_inc(kexp, 1)
                tiles(act, NT, 2, body)

        qr = m.sb("m1_qr", [128, K2, CH])
        ql = m.sb("m1_ql", [128, K2, CH])
        oT = m.sb("m1_oT", [128, K2, CH])
        y = m.sb("m1_y", [P, 4, D])
        yT = m.sb("m1_yT", [128, K2, CH])
        hT = m.sb("m1_hT", [128, FC, CH])
        st = m.sb("m1_st", [P, 2, 4, 6])
        mv = m.sb("m1_mv", [P, 2, 4, 2])
        rs = m.sb("m1_rs", [P, 2, 4])
        names = ("q_made", "q_low", "q_exp", "q_phi", "o_made", "o_ready", "o_made2", "y_free", "var1", "std1",
                 "y_ready", "y_turned", "y_moved", "up", "acted", "f_made", "f_read", "var2", "std2", "done")
        S = {x: m.sem("m2_" + x) for x in names}
        with nc.Block() as block:
            @block.tensor
            def _(pe):
                def body(c, nt):
                    w = nt * P
                    pe.wait_ge(S["done"], c + 1)
                    for o in range(K2):
                        for k in range(K2):
                            x = pe.matmul(m.ps[o][:, 0:w], wq[:, k, o * 128:(o + 1) * 128],
                                          m.XT[:, bass.ds(c * CH + k * N, w)], start=k == 0, stop=k == K2 - 1)
                    x.then_inc(S["q_made"], 1)
                    pe.wait_ge(S["q_phi"], c + 1)
                    for o in range(K2):
                        pe.matmul(m.ps[2 + o][:, 0:w], kv[:, o, :], qr[:, o, 0:w], start=True, stop=True)
                        x = pe.matmul(m.ps[o][:, 0:w], ks[:, o, :], qr[:, o, 0:w], start=True, stop=True)
                    x.then_inc(S["o_made"], 1)
                    pe.wait_ge(S["o_ready"], c + 1)
                    for j in range(nt):
                        for k in range(K2):
                            x = pe.matmul(m.ps[4 + j][:P, 0:D], oT[:, k, j * P:(j + 1) * P], wo[:, k, :],
                                          start=k == 0, stop=k == K2 - 1)
                    x.then_inc(S["o_made2"], 1)
                    pe.wait_ge(S["y_ready"], c + 1)
                    for k in range(K2):
                        for j in range(nt):
                            x = pe.transpose(m.ps[k][:, j * P:(j + 1) * P], y[:, j, k * 128:(k + 1) * 128], m.ident[:P, :P])
                    x.then_inc(S["y_turned"], 1)
                    pe.wait_ge(S["y_moved"], c + 1)
                    for f in range(FC):
                        pe.wait_ge(S["acted"], c * FC + f + 1)
                        for k in range(K2):
                            x = pe.matmul(m.ps[f % 4][:, 0:w], w1[:, k, f * 128:(f + 1) * 128], yT[:, k, 0:w],
                                          start=k == 0, stop=k == K2 - 1)
                        x.then_inc(S["up"], 1)
                    pe.wait_ge(S["acted"], c * FC + FC + 4)
                    for j in range(nt):
                        for f in range(FC):
                            x = pe.matmul(m.ps[4 + j][:P, 0:D], hT[:, f, j * P:(j + 1) * P], w2[:, f, :],
                                          start=f == 0, stop=f == FC - 1)
                        x.then_inc(S["f_made"], 1)
                chunks(pe, body)

            @block.scalar
            def _(act):
                act.sem_inc(S["acted"], 4)

                def body(c, nt):
                    w = nt * P
                    act.wait_ge(S["q_low"], c + 1)
                    act.activation(ql[:, :, 0:w], ql[:, :, 0:w], ACT.Exp).then_inc(S["q_exp"], 1)
                    act.wait_ge(S["var1"], c + 1)
                    act.sqrt(rs[:, 0, 0:nt], rs[:, 0, 0:nt]).then_inc(S["std1"], 1)
                    act.wait_ge(S["y_turned"], c + 1)
                    for k in range(K2):
                        x = act.copy(yT[:, k, 0:w], m.ps[k][:, 0:w])
                    act.drain().then_inc(S["y_moved"], 1)
                    for f in range(FC):
                        act.wait_ge(S["up"], c * FC + f + 1)
                        act.activation(hT[:, f, 0:w], m.ps[f % 4][:, 0:w], ACT.Relu, bias=b1[:, f:f + 1]
                                       ).then_inc(S["acted"], 1)
                    act.wait_ge(S["var2"], c + 1)
                    act.sqrt(rs[:, 1, 0:nt], rs[:, 1, 0:nt]).then_inc(S["std2"], 1)
                chunks(act, body)

            @block.vector
            def _(dve):
                dve.sem_inc(S["done"], 1)

                def normalize(c, nt, i):
                    dve.drain()
                    for j in range(nt):
                        dve.bn_stats(st[:, i, j, :], y[:, j, :])
                    dve.drain()
                    for j in range(nt):
                        dve.bn_aggr(mv[:, i, j, :], st[:, i, j, :])
                    dve.drain()
                    dve.tensor_scalar(rs[:, i, 0:nt], mv[:, i, 0:nt, 1], 1e-5, None, ALU.add)
                    dve.drain().then_inc(S[f"var{i + 1}"], 1)
                    dve.wait_ge(S[f"std{i + 1}"], c + 1)
                    dve.reciprocal(rs[:, i, 0:nt], rs[:, i, 0:nt])
                    dve.drain()
                    for j in range(nt):
                        dve.tensor_scalar(y[:, j, :], y[:, j, :], mv[:, i, j, 0:1], rs[:, i, j:j + 1],
                                          ALU.subtract, ALU.mult)
                    for b, op in ((4 + 2 * i, ALU.mult), (5 + 2 * i, ALU.add)):
                        dve.drain()
                        dve.tensor_tensor(y[:, 0:nt, :], y[:, 0:nt, :],
                                          rowb[:, b, :].unsqueeze(1).broadcast_to((P, nt, D)), op)
                    dve.drain()

                def body(c, nt):
                    w = nt * P
                    dve.wait_ge(S["q_made"], c + 1)
                    for o in range(K2):
                        dve.tensor_scalar(ql[:, o, 0:w], m.ps[o][:, 0:w], bq[:, o:o + 1], 0.0, ALU.add, ALU.min)
                        dve.tensor_scalar(qr[:, o, 0:w], m.ps[o][:, 0:w], bq[:, o:o + 1], 0.0, ALU.add, ALU.max)
                    dve.drain().then_inc(S["q_low"], 1)
                    dve.wait_ge(S["q_exp"], c + 1)
                    dve.tensor_tensor(qr[:, :, 0:w], qr[:, :, 0:w], ql[:, :, 0:w], ALU.add)
                    dve.drain().then_inc(S["q_phi"], 1)
                    dve.wait_ge(S["o_made"], c + 1)
                    for o in range(K2):
                        dve.tensor_scalar(ql[:, o, 0:w], m.ps[o][:, 0:w], 1e-6, None, ALU.add)
                    dve.drain()
                    dve.reciprocal(ql[:, :, 0:w], ql[:, :, 0:w])
                    dve.drain()
                    for o in range(K2):
                        dve.tensor_tensor(oT[:, o, 0:w], m.ps[2 + o][:, 0:w], ql[:, o, 0:w], ALU.mult)
                    dve.drain().then_inc(S["o_ready"], 1)
                    dve.wait_ge(S["o_made2"], c + 1)
                    for j in range(nt):
                        dve.tensor_tensor(y[:, j, :], m.ps[4 + j][:P, 0:D], rowb[:, 2, :], ALU.add)
                    dve.drain()
                    for j in range(nt):
                        dve.tensor_tensor(y[:, j, :], y[:, j, :], m.XN[:, bass.ds(c * (4 * D) + j * D, D)], ALU.add)
                    normalize(c, nt, 0)
                    dve.sem_inc(S["y_ready"], 1)
                    for j in range(nt):
                        dve.wait_ge(S["f_made"], c * 4 + j + 1)
                        if j == 0:
                            dve.wait_ge(S["y_moved"], c + 1)
                        dve.tensor_tensor(y[:, j, :], y[:, j, :], m.ps[4 + j][:P, 0:D], ALU.add)
                    dve.drain()
                    dve.tensor_tensor(y[:, 0:nt, :], y[:, 0:nt, :],
                                      rowb[:, 3, :].unsqueeze(1).broadcast_to((P, nt, D)), ALU.add)
                    normalize(c, nt, 1)
                    for j in range(nt):
                        x = m.X[:, bass.ds(c * (4 * D) + j * D, D)]
                        dve.tensor_tensor(x, y[:, j, :], x, ALU.add)
                    dve.drain().then_inc(S["done"], 1)
                chunks(dve, body)


def gates1(m):
    nc, io = m.nc, m.io
    E = 8
    with Stage(m):
        wr = m.sb("r1_wr", [128, K2, E])
        s = m.sb("r1_s", [P, NT, E])
        tmp = m.sb("r1_tmp", [P, NT])
        gt = m.sb("r1_gt", [P, NT, E, E])
        eq = m.sb("r1_eq", [P, NT, E, E])
        low = m.sb("r1_low", [P, E, E])
        sel = m.sel1
        loads = Loads(m, "r1_loaded")
        low_ready, made, s_ready, s_exp = (m.sem("r1_" + x) for x in ("low_ready", "made", "s_ready", "s_exp"))
        with nc.Block() as block:
            @block.sync
            def _(sp):
                loads(sp, wr[:, :, :], io["L1_ffn_Wr"].rearrange("(k p) e -> p k e", p=128))

            @block.gpsimd
            def _(pool):
                pool.memset(low[:, :, :], 1.0)
                pool.drain()
                pool.affine_select(out=low[:, :, :], in_=low[:, :, :], compare_op=ALU.is_gt, fill=0.0,
                                   base=0, pattern=[[1, E], [-1, E]], channel_multiplier=0)
                pool.drain().then_inc(low_ready, 1)

            @block.tensor
            def _(pe):
                pe.wait_ge(loads.sem, 16)

                def body(t, j):
                    for k in range(K2):
                        x = pe.matmul(m.ps[0][:P, t * E:(t + 1) * E], m.XT[:, bass.ds(t * P + k * N, P)], wr[:, k, :],
                                      start=k == 0, stop=k == K2 - 1)
                    x.then_inc(made, 1)
                tiles_written_out(NT, 1, body)

            @block.vector
            def _(dve):
                wide = tmp[:, :].unsqueeze(2).broadcast_to((P, NT, E))
                dve.wait_ge(made, NT)
                dve.tensor_copy(s[:, :, :], m.ps[0][:P, 0:NT * E].rearrange("p (t e) -> p t e", e=E))
                dve.drain()
                dve.tensor_reduce(tmp[:, :], s[:, :, :], AX.X, ALU.max)
                dve.drain()
                dve.tensor_tensor(s[:, :, :], s[:, :, :], wide, ALU.subtract)
                dve.drain().then_inc(s_ready, 1)
                dve.wait_ge(s_exp, 1)
                dve.tensor_reduce(tmp[:, :], s[:, :, :], AX.X, ALU.add)
                dve.drain()
                dve.reciprocal(tmp[:, :], tmp[:, :])
                dve.drain()
                dve.tensor_tensor(s[:, :, :], s[:, :, :], wide, ALU.mult)
                dve.drain()
                dve.wait_ge(low_ready, 1)
                top_two(dve, s, E, gt[:, :, :, :], eq[:, :, :, :], low[:, :, :], sel[:, :, :])
                dve.tensor_tensor(s[:, :, :], s[:, :, :], sel[:, :, :], ALU.mult)
                dve.drain()
                dve.tensor_reduce(tmp[:, :], s[:, :, :], AX.X, ALU.add)
                dve.drain()
                dve.reciprocal(tmp[:, :], tmp[:, :])
                dve.drain()
                dve.tensor_tensor(m.gate1[:, :, :], s[:, :, :], wide, ALU.mult)

            @block.scalar
            def _(act):
                act.wait_ge(s_ready, 1)
                act.activation(s[:, :, :], s[:, :, :], ACT.Exp).then_inc(s_exp, 1)


def store(m):
    out_stored = m.sem("out_stored")
    with m.nc.Block() as block:
        @block.sync
        def _(sp):
            sp.dma_start(m.io["out"].rearrange("(t p) d -> p t d", p=P),
                         m.X[:, :].rearrange("p (t d) -> p t d", d=D)).then_inc(out_stored, 16)
            sp.wait_ge(out_stored, 16)


def program(nc, io, stop=99):
    m = Net(nc, io)
    with m.keep:
        constants(m)
        sort_constants(m)
        m.scratch = m.sb("XN", [128, NT * D])
        m.XN = m.scratch[:P, :]
        ed1 = Edges(m, "s1", COLS1)
        if stop >= 3:
            ed0 = Edges(m, "s0", COLS0)
            sort_edges(m, ed0, io["key0"], io["other0"])
        m.XT = m.sb("XT", [128, K2 * N])
        layer_norm(m, "ln0")
        if stop >= 1:
            gnn0_nodes(m)
            gnn0_edges(m)
        if stop >= 2:
            mix0_log(m)
            with Stage(m):
                m.QT = m.sb("QT", [128, OC * N])
                mix0_qkv(m)
                mix0_attention(m)
        if stop >= 3:
            layer_norm(m, "ln1")
            with Stage(m):
                gat_nodes(m)
                gat_edges(m, ed0, ed1, (io["key1"], io["other1"]))
                gates0(m)
                experts(m, "x0", [(io["L0_ffn_W1"][e], io["L0_ffn_b1_cols"][e], io["L0_ffn_W2"][e], io["L0_ffn_b2"][e],
                                   lambda t, e=e: m.gate0[:, :, e][:, at(t, 1)]) for e in range(4)], 512)
        if stop >= 4:
            layer_norm(m, "ln2")
            with Stage(m):
                gnn1_nodes(m)
                gnn1_edges(m, ed1)
            mix1(m)
        if stop >= 5:
            layer_norm(m, "ln3")
            with Stage(m):
                m.gate1 = m.sb("gate1", [P, NT, 8])
                m.sel1 = m.sb("sel1", [P, NT, 8])
                routes = Routes(m, "x1", 8)
                gates1(m)
                find_routes(m, routes, m.sel1[:, :, :], m.gate1[:, :, :])
                placed = Loads(m, "x1_placed")
                placed.all = 16 * 2 * NT

                def beside(pool):
                    scatter_nodes(m, routes, pool, placed.sem)
                    pool.wait_ge(placed.sem, placed.all)
                experts(m, "xs", [(io["L1_ffn_W1s"], io["L1_ffn_b1s_cols"], io["L1_ffn_W2s"], io["L1_ffn_b2s"], None)],
                        1024, beside)
                routed_experts(m, routes, io["L1_ffn_packed"], 1024)
        store(m)


def columns(v, cols, pad):
    out = np.full(cols * 128, pad, v.dtype)
    out[:v.size] = v
    return np.ascontiguousarray(out.reshape(cols, 128).T)


def pack_experts(W1, b1, W2, b2):
    E, _, F = W1.shape
    by_line = lambda w: w.reshape(E, -1, 128, w.shape[-1]).transpose(0, 2, 1, 3).reshape(E, 128, -1)
    parts = [by_line(W1), by_line(W2), by_line(b1[:, :, None]), np.repeat(b2[:, None, :], 128, axis=1)]
    return np.ascontiguousarray(np.concatenate(parts, axis=2).reshape(E * 128, -1))


def layouts(inputs):
    f = {k: np.ascontiguousarray(v) for k, v in inputs.items()}
    skip = ("src", "dst", "L0_mix_w_qkv", "L0_mix_w_dw", "L0_mix_w_pw", "L0_mix_w_res", "L0_ffn_edge_index")
    out = {k: v for k, v in f.items() if k not in skip}
    src, dst = f["src"], f["dst"]
    out["first_dst"] = np.ascontiguousarray(dst[:N].reshape(NT, P).T)
    out["first_src"] = np.ascontiguousarray(src[:N].reshape(NT, P).T)
    ei = f["L0_ffn_edge_index"]
    out["key0"], out["other0"] = columns(ei[1], COLS0, 0), columns(ei[0], COLS0, 0)
    out["key1"], out["other1"] = columns(src, COLS1, KEYS - 1), columns(dst, COLS1, 0)
    out["w_qkv_t"] = np.ascontiguousarray(f["L0_mix_w_qkv"][:, :, 2].T)
    cols = lambda v: np.ascontiguousarray(v.reshape(-1, 128).T)
    out["w_dw_mid_cols"] = cols(f["L0_mix_w_dw"][:, 0, 2])
    for name in ("L0_mix_bn_gamma", "L0_mix_bn_beta", "L1_mix_bq", "L1_mix_b1", "L1_ffn_b1s"):
        out[name + "_cols"] = cols(out.pop(name))
    out["L0_ffn_b1_cols"] = np.ascontiguousarray(np.stack([cols(v) for v in out.pop("L0_ffn_b1")]))
    out["L1_ffn_packed"] = pack_experts(*(out.pop("L1_ffn_" + x) for x in ("W1p", "b1p", "W2p", "b2p")))
    out["w_pw_t"] = np.ascontiguousarray(f["L0_mix_w_pw"][:, :, 0].T)
    out["w_res_t"] = np.ascontiguousarray(f["L0_mix_w_res"][:, :, 0].T)
    return out


def kernel(**inputs):
    import concourse.bacc as bacc
    from concourse.bass_utils import run_bass_kernel_spmd as run

    arrays = layouts({k: np.asarray(v) for k, v in inputs.items()})
    nc = bacc.Bacc("TRN2", target_bir_lowering=False, num_devices=1)
    io = {k: nc.dram_tensor("in_" + k, a.shape, mybir.dt.from_np(a.dtype), kind="ExternalInput").ap()
          for k, a in arrays.items()}
    io["out"] = nc.dram_tensor("out", (N, D), FP32, kind="ExternalOutput").ap()
    program(nc, io)
    r = run(nc, [{"in_" + k: a for k, a in arrays.items()}], core_ids=[0])
    return r.results[0]["out"]
```

```python
import math
import numpy as np
import concourse.bass as bass
from concourse import mybir
from contextlib import ExitStack

FP32 = mybir.dt.float32
FP16 = mybir.dt.float16
BF16 = mybir.dt.bfloat16
I32 = mybir.dt.int32
ALU = mybir.AluOpType
ACT = mybir.ActivationFunctionType
AX = mybir.AxisListType

N = 3125
P = 125
NT = N // P
D = 256
K2 = D // 128
CH = 4 * P
NCH = N // CH
BIG = 1e30
MIN_NORM = 1e-15
MAX_NORM = float(np.float32(1.0 - 1e-5))
MAX_ATANH = 0.5 * math.log((1 + MAX_NORM) / (1 - MAX_NORM))
KEYS = 4096
KB = 32
COLS0 = 512
COLS1 = 400
BC = 16


class Net:

    def __init__(self, nc, io):
        self.nc, self.io = nc, io
        self.keep = ExitStack()
        self.scope = self.keep
        self.sems = []

    def sem(self, name):
        self.sems.append(self.nc.alloc_semaphore(name))
        return self.sems[-1]

    def sb(self, name, shape, dt=FP32):
        return self.scope.enter_context(self.nc.sbuf_tensor(name, shape, dt))

    def dram(self, name, shape, dt=FP32):
        return self.nc.dram_tensor(name, shape, dt).ap()


class Stage:

    def __init__(self, m):
        self.m = m

    def __enter__(self):
        self.outer, self.m.scope = self.m.scope, ExitStack()
        self.sems, self.m.sems = self.m.sems, []
        return self

    def __exit__(self, *a):
        self.m.scope.close()
        self.m.scope = self.outer
        self.m.nc.clear_and_free_semaphores(self.m.sems)
        self.m.nc.all_engine_barrier()
        self.m.sems = self.sems


class Loads:

    def __init__(self, m, name):
        self.sem, self.all = m.sem(name), 0

    def __call__(self, eng, dst, src):
        self.all += 16
        eng.dma_start(dst, src).then_inc(self.sem, 16)


def tiles(eng, total, unroll, body):
    whole = total // unroll
    with eng.Fori(0, whole) as i:
        for j in range(unroll):
            body(i * unroll + j, j)
    for j in range(total - whole * unroll):
        body(whole * unroll + j, j)


def chunks(eng, body):
    with eng.Fori(0, NCH) as c:
        body(c, 4)
    body(NCH, 1)


def tiles_written_out(total, unroll, body):
    for t in range(total):
        body(t, t % unroll)


def chunks_written_out(body):
    for c in range(NCH):
        body(c, 4)
    body(NCH, 1)


def at(t, size):
    return bass.ds(t * size, size)


def constants(m):
    nc = m.nc
    m.X = m.sb("X", [P, NT * D])
    m.ident = m.sb("ident", [128, 128])
    m.ps = [m.keep.enter_context(nc.psum_tensor(f"bank{i}", [128, 512], FP32)) for i in range(8)]
    m.spare = m.sem("spare")
    loaded = m.sem("x_loaded")
    with nc.Block() as block:
        @block.sync
        def _(sp):
            sp.dma_start(m.X[:, :].rearrange("p (t d) -> p t d", d=D),
                         m.io["x"].rearrange("(t p) d -> p t d", p=P)).then_inc(loaded, 16)
            sp.wait_ge(loaded, 16)

        @block.gpsimd
        def _(pool):
            pool.memset(m.ident[:, :], 0.0)
            pool.drain()
            pool.affine_select(out=m.ident[:, :], in_=m.ident[:, :], compare_op=ALU.not_equal, fill=1.0,
                               base=0, pattern=[[-1, 128]], channel_multiplier=1)
            pool.drain()


def turn_tiles(m, block, tag, ready, first=None):
    turned, moved = m.sem(tag + "_turned"), m.sem(tag + "_moved")
    xt = m.XT[:, :].rearrange("p (k n) -> p k n", k=K2)

    @block.tensor
    def _(pe):
        def body(t, j):
            pe.wait_ge(ready, t + 1)
            pe.wait_ge(moved, t + 1)
            for k in range(K2):
                last = pe.transpose(m.ps[j][:, k * P:(k + 1) * P], m.XN[:, bass.ds(t * D + k * 128, 128)],
                                    m.ident[:P, :P])
            last.then_inc(turned, 1)
        tiles_written_out(NT, 4, body)

    @block.scalar
    def _(act):
        act.sem_inc(moved, 4)
        if first is not None:
            first(act)

        def body(t, j):
            act.wait_ge(turned, t + 1)
            act.copy(xt[:, :, at(t, P)],
                     m.ps[j][:, 0:K2 * P].rearrange("p (k n) -> p k n", k=K2)).then_inc(moved, 1)
        tiles(act, NT, 4, body)


def moments(dve, s3, mean, var, tmp, count):
    dve.tensor_tensor(mean, s3[:, :, 1], s3[:, :, 4], ALU.add)
    dve.tensor_tensor(tmp, s3[:, :, 1], s3[:, :, 4], ALU.subtract)
    dve.tensor_tensor(var, s3[:, :, 2], s3[:, :, 5], ALU.add)
    dve.drain()
    dve.tensor_scalar(mean, mean, 0.5, None, ALU.mult)
    dve.tensor_scalar(tmp, tmp, 0.5, None, ALU.mult)
    dve.tensor_scalar(var, var, 1.0 / count, 1e-5, ALU.mult, ALU.add)
    dve.drain()
    dve.tensor_tensor(tmp, tmp, tmp, ALU.mult)
    dve.drain()
    return dve.tensor_tensor(var, var, tmp, ALU.add)


def layer_norm(m, tag):
    nc = m.nc
    with Stage(m):
        st = m.sb(tag + "_stats", [P, NT * 6])
        mean, var, tmp, rstd = (m.sb(tag + x, [P, NT]) for x in ("_mean", "_var", "_tmp", "_rstd"))
        var_ready, std_ready, normed = m.sem(tag + "_var_ready"), m.sem(tag + "_std_ready"), m.sem(tag + "_normed")
        s3 = st[:, :].rearrange("p (t s) -> p t s", s=6)
        with nc.Block() as block:
            @block.vector
            def _(dve):
                tiles(dve, NT, 5, lambda t, j: dve.bn_stats(st[:, at(t, 6)], m.X[:, at(t, D)]))
                dve.drain()
                moments(dve, s3, mean[:, :], var[:, :], tmp[:, :], D).then_inc(var_ready, 1)
                dve.wait_ge(std_ready, 1)
                dve.reciprocal(rstd[:, :], var[:, :])
                dve.drain()
                tiles(dve, NT, 5, lambda t, j: dve.tensor_scalar(
                    m.XN[:, at(t, D)], m.X[:, at(t, D)], mean[:, at(t, 1)], rstd[:, at(t, 1)],
                    ALU.subtract, ALU.mult).then_inc(normed, 1))

            def root(act):
                act.wait_ge(var_ready, 1)
                act.sqrt(var[:, :], var[:, :]).then_inc(std_ready, 1)
            turn_tiles(m, block, tag, normed, root)


def gnn0_nodes(m):
    nc, io = m.nc, m.io
    H, C = 4, 64
    ROW = D + 2 * H
    m.xt_dram = m.dram("xt_dram", [N, D + H])
    m.al_dram = m.dram("al_dram", [N, H])
    with Stage(m):
        w = m.sb("g0_w", [128, K2, ROW])
        att = m.sb("g0_att", [128, 2, D])
        prod = m.sb("g0_prod", [128, 2, K2, D])
        table = m.sb("g0_table", [P, NT * ROW])
        loads, stored = Loads(m, "g0_loaded"), Loads(m, "g0_stored")
        w_ready, made, kept = m.sem("g0_w_ready"), m.sem("g0_made"), m.sem("g0_kept")
        with nc.Block() as block:
            @block.sync
            def _(sp):
                loads(sp, w[:, :, 0:D], io["L0_gnn_weight"].rearrange("(k p) d -> p k d", p=128))
                for i, name in enumerate(("L0_gnn_attn_r", "L0_gnn_attn_l")):
                    loads(sp, att[:, i, :], io[name].rearrange("h c -> (h c)").partition_broadcast(128))
                sp.wait_ge(kept, NT + 4)
                t3 = table[:, :].rearrange("p (t c) -> p t c", c=ROW)
                stored(sp, m.xt_dram.rearrange("(t p) c -> p t c", p=P), t3[:, :, 0:D + H])
                stored(sp, m.al_dram.rearrange("(t p) c -> p t c", p=P), t3[:, :, D + H:])
                sp.wait_ge(stored.sem, stored.all)

            @block.vector
            def _(dve):
                dve.wait_ge(loads.sem, 48)
                for i in range(2):
                    for k in range(K2):
                        dve.tensor_tensor(prod[:, i, k, :], w[:, k, 0:D], att[:, i, :], ALU.mult)
                dve.drain()
                for i in range(2):
                    for k in range(K2):
                        last = dve.tensor_reduce(w[:, k, D + H * i:D + H * (i + 1)],
                                                 prod[:, i, k, :].rearrange("p (h c) -> p h c", h=H), AX.X, ALU.add)
                last.then_inc(w_ready, 1)

            @block.tensor
            def _(pe):
                pe.wait_ge(w_ready, 1)

                def body(t, j):
                    pe.wait_ge(kept, t + 1)
                    for k in range(K2):
                        last = pe.matmul(m.ps[j][:P, 0:ROW], m.XT[:, bass.ds(t * P + k * N, P)], w[:, k, :],
                                         start=k == 0, stop=k == K2 - 1)
                    last.then_inc(made, 1)
                tiles_written_out(NT, 4, body)

            @block.scalar
            def _(act):
                act.sem_inc(kept, 4)

                def body(t, j):
                    act.wait_ge(made, t + 1)
                    act.copy(table[:, at(t, ROW)], m.ps[j][:P, 0:ROW]).then_inc(kept, 1)
                tiles(act, NT, 4, body)


class Gnn0Edges:

    H, C = 4, 64

    def __init__(self, m):
        H, C = self.H, self.C
        self.m = m
        self.idx = m.sb("g0_idx", [P, 2, NT], I32)
        self.near = m.sb("g0_near", [P, NT, D + H])
        self.al = m.sb("g0_al", [P, NT, H])
        self.e = m.sb("g0_e", [P, NT, H])
        self.tot = m.sb("g0_tot", [P, NT])
        self.mix = m.sb("g0_mix", [P, NT, C])
        self.loads, self.rows = Loads(m, "g0_idx_loaded"), Loads(m, "g0_rows")
        self.e_ready, self.e_exp = m.sem("g0_e_ready"), m.sem("g0_e_exp")

    def load(self, sp):
        self.loads(sp, self.idx[:, 0, :], self.m.io["first_dst"])
        self.loads(sp, self.idx[:, 1, :], self.m.io["first_src"])

    def gather(self, pool):
        pool.wait_ge(self.loads.sem, 32)
        for t in range(NT):
            for dst, table, i in ((self.near, self.m.xt_dram, 0), (self.al, self.m.al_dram, 1)):
                self.rows.all += 16
                pool.indirect_dma_start(
                    out=dst[:, t, :], out_offset=None, in_=table,
                    in_offset=bass.IndirectOffsetOnAxis(ap=self.idx[:, i, t:t + 1], axis=0)).then_inc(self.rows.sem, 16)

    def logits(self, dve):
        e, tot = self.e, self.tot
        dve.wait_ge(self.rows.sem, 16 * 2 * NT)
        dve.tensor_tensor(e[:, :, :], self.al[:, :, :], self.near[:, :, D:], ALU.add)
        dve.drain()
        dve.scalar_tensor_tensor(e[:, :, :], e[:, :, :], 0.01, e[:, :, :], ALU.mult, ALU.max)
        dve.drain()
        dve.tensor_reduce(tot[:, :], e[:, :, :], AX.X, ALU.max)
        dve.drain()
        wide = tot[:, :].unsqueeze(2).broadcast_to((P, NT, self.H))
        dve.tensor_tensor(e[:, :, :], e[:, :, :], wide, ALU.subtract).then_inc(self.e_ready, 1)

    def exponentials(self, act):
        act.wait_ge(self.e_ready, 1)
        act.activation(self.e[:, :, :], self.e[:, :, :], ACT.Exp).then_inc(self.e_exp, 1)

    def sums(self, dve):
        m, H, C, e, tot, near, mix = self.m, self.H, self.C, self.e, self.tot, self.near, self.mix
        wide = tot[:, :].unsqueeze(2).broadcast_to((P, NT, H))
        dve.wait_ge(self.e_exp, 1)
        dve.tensor_reduce(tot[:, :], e[:, :, :], AX.X, ALU.add)
        dve.drain()
        dve.reciprocal(tot[:, :], tot[:, :])
        dve.drain()
        dve.tensor_tensor(e[:, :, :], e[:, :, :], wide, ALU.mult)
        dve.drain()
        heads = near[:, :, 0:D].rearrange("p t (h c) -> p t h c", h=H)
        for t in range(NT):
            dve.tensor_tensor(heads[:, t], heads[:, t],
                              e[:, t, :].unsqueeze(2).broadcast_to((P, H, C)), ALU.mult)
        dve.drain()
        dve.tensor_reduce(mix[:, :, :], near[:, :, 0:D].rearrange("p t (h c) -> p t c h", h=H), AX.X, ALU.add)
        dve.drain()
        x4 = m.X[:, :].rearrange("p (t h c) -> p t h c", t=NT, h=H)
        for h in range(H):
            dve.tensor_tensor(x4[:, :, h, :], x4[:, :, h, :], mix[:, :, :], ALU.add)


def mix0_log(m):
    nc = m.nc
    with Stage(m):
        junk = m.sb("lg_junk", [P, 5, D])
        ss, n, r, a, b, c = (m.sb("lg_" + x, [P, NT]) for x in ("ss", "n", "r", "a", "b", "c"))
        ss_ready, root, ratio, logged, scaled = (m.sem("lg_" + x) for x in ("ss_ready", "root", "ratio", "logged", "scaled"))
        with nc.Block() as block:
            @block.vector
            def _(dve):
                def squares(t, j):
                    if j == 0:
                        dve.drain()
                    dve.scalar_tensor_tensor(junk[:, j, :], m.XN[:, at(t, D)], 1.0, m.XN[:, at(t, D)],
                                             ALU.mult, ALU.mult, accum_out=ss[:, at(t, 1)])
                tiles(dve, NT, 5, squares)
                dve.drain().then_inc(ss_ready, 1)
                dve.wait_ge(root, 1)
                dve.tensor_scalar(n[:, :], n[:, :], MIN_NORM, None, ALU.max)
                dve.drain()
                dve.tensor_scalar(r[:, :], n[:, :], MAX_NORM, None, ALU.min)
                dve.drain()
                dve.tensor_scalar(a[:, :], r[:, :], -1.0, 1.0, ALU.mult, ALU.add)
                dve.tensor_scalar(b[:, :], r[:, :], 1.0, None, ALU.add)
                dve.drain()
                dve.reciprocal(a[:, :], a[:, :])
                dve.drain()
                dve.tensor_tensor(a[:, :], a[:, :], b[:, :], ALU.mult).then_inc(ratio, 1)
                dve.drain()
                dve.tensor_tensor(b[:, :], r[:, :], r[:, :], ALU.mult)
                dve.drain()
                dve.tensor_scalar(c[:, :], b[:, :], 1.0 / 7, 1.0 / 5, ALU.mult, ALU.add)
                for k in (1.0 / 3, 1.0):
                    dve.drain()
                    dve.tensor_tensor(c[:, :], c[:, :], b[:, :], ALU.mult)
                    dve.drain()
                    dve.tensor_scalar(c[:, :], c[:, :], k, None, ALU.add)
                dve.drain()
                dve.tensor_tensor(c[:, :], c[:, :], r[:, :], ALU.mult)
                dve.tensor_scalar(b[:, :], r[:, :], 0.1, None, ALU.is_lt)
                dve.wait_ge(logged, 1)
                dve.tensor_scalar(a[:, :], a[:, :], 0.5, None, ALU.mult)
                dve.drain()
                dve.tensor_tensor(c[:, :], c[:, :], a[:, :], ALU.subtract)
                dve.drain()
                dve.tensor_tensor(c[:, :], c[:, :], b[:, :], ALU.mult)
                dve.reciprocal(n[:, :], n[:, :])
                dve.drain()
                dve.tensor_tensor(a[:, :], a[:, :], c[:, :], ALU.add)
                dve.drain()
                dve.tensor_tensor(a[:, :], a[:, :], n[:, :], ALU.mult)
                dve.drain()
                tiles(dve, NT, 5, lambda t, j: dve.tensor_scalar(
                    m.XN[:, at(t, D)], m.XN[:, at(t, D)], a[:, at(t, 1)], None, ALU.mult).then_inc(scaled, 1))

            def first(act):
                act.wait_ge(ss_ready, 1)
                act.sqrt(n[:, :], ss[:, :]).then_inc(root, 1)
                act.wait_ge(ratio, 1)
                act.activation(a[:, :], a[:, :], ACT.Ln).then_inc(logged, 1)
            turn_tiles(m, block, "lg", scaled, first)


OC = 6


def mix0_qkv(m, edges):
    nc, io = m.nc, m.io
    wq = m.sb("q0_w", [128, K2, OC * 128])
    gb = m.sb("q0_gb", [128, 2, OC])
    st = m.sb("q0_st", [128, OC, (NCH + 1) * 6])
    mv = m.sb("q0_mv", [128, OC, 2])
    sc = m.sb("q0_sc", [128, OC])
    sh = m.sb("q0_sh", [128, OC])
    loads = Loads(m, "q0_loaded")
    made, copied, var_ready, std_ready, affine = (
        m.sem("q0_" + x) for x in ("made", "copied", "var_ready", "std_ready", "affine"))
    with nc.Block() as block:
        @block.sync
        def _(sp):
            edges.load(sp)
            loads(sp, wq[:, :, :], io["w_qkv_t"].rearrange("(k p) o -> p k o", p=128))
            loads(sp, gb[:, 0, :], io["L0_mix_bn_gamma_cols"])
            loads(sp, gb[:, 1, :], io["L0_mix_bn_beta_cols"])

        @block.gpsimd
        def _(pool):
            edges.gather(pool)

        @block.tensor
        def _(pe):
            pe.wait_ge(loads.sem, 48)

            def body(c, nt):
                for o in range(OC):
                    pe.wait_ge(copied, c * OC + o + 1)
                    for k in range(K2):
                        last = pe.matmul(m.ps[o][:, 0:nt * P], wq[:, k, o * 128:(o + 1) * 128],
                                         m.XT[:, bass.ds(c * CH + k * N, nt * P)], start=k == 0, stop=k == K2 - 1)
                    last.then_inc(made, 1)
            chunks(pe, body)

        @block.vector
        def _(dve):
            def body(c, nt):
                for o in range(OC):
                    dve.wait_ge(copied, c * OC + o + 1 + OC)
                    dve.bn_stats(st[:, o, at(c, 6)], m.QT[:, bass.ds(c * CH + o * N, nt * P)])
            chunks(dve, body)
            dve.drain()
            for o in range(OC):
                dve.bn_aggr(mv[:, o, :], st[:, o, :])
            dve.drain()
            dve.tensor_scalar(sc[:, :], mv[:, :, 1], 1e-5, None, ALU.add).then_inc(var_ready, 1)
            edges.logits(dve)
            dve.wait_ge(std_ready, 1)
            dve.reciprocal(sc[:, :], sc[:, :])
            dve.wait_ge(loads.sem, 48)
            dve.drain()
            dve.tensor_tensor(sc[:, :], sc[:, :], gb[:, 0, :], ALU.mult)
            dve.drain()
            dve.tensor_tensor(sh[:, :], mv[:, :, 0], sc[:, :], ALU.mult)
            dve.drain()
            dve.tensor_tensor(sh[:, :], gb[:, 1, :], sh[:, :], ALU.subtract).then_inc(affine, 1)
            edges.sums(dve)

        @block.scalar
        def _(act):
            act.sem_inc(copied, OC)

            def body(c, nt):
                for o in range(OC):
                    act.wait_ge(made, c * OC + o + 1)
                    act.copy(m.QT[:, bass.ds(c * CH + o * N, nt * P)], m.ps[o][:, 0:nt * P]).then_inc(copied, 1)
            chunks(act, body)
            act.wait_ge(var_ready, 1)
            act.sqrt(sc[:, :], sc[:, :]).then_inc(std_ready, 1)
            edges.exponentials(act)
            act.wait_ge(affine, 1)
            act.drain()
            for o in range(OC):
                act.activation(m.QT[:, o * N:(o + 1) * N], m.QT[:, o * N:(o + 1) * N], ACT.Relu,
                               bias=sh[:, o:o + 1], scale=sc[:, o:o + 1])


def log_exp_scale(dve, out, n, cap, tmp):
    dve.tensor_scalar(tmp, n, MIN_NORM, None, ALU.max)
    dve.tensor_scalar(out, n, cap, None, ALU.min)
    dve.drain()
    dve.reciprocal(tmp, tmp)
    dve.drain()
    dve.tensor_tensor(out, out, tmp, ALU.mult)
    dve.drain()


def mix0_attention(m):
    nc, io = m.nc, m.io
    G = 4
    U = OC * 128
    Z = 2 * U
    GR = Z // 96
    O = GR * 32
    z = [v.rearrange("p (g c) -> p g c", g=G) for v in (m.XN[:, 0:G * Z], m.sb("a0_z1", [P, G * Z])[:, :])]
    kr, vv, rec = (m.XT[:P, i * G * O:(i + 1) * G * O].rearrange("p (g c) -> p g c", g=G) for i in range(3))
    ks = m.sb("a0_ks", [P, G * GR])
    junk = m.sb("a0_junk", [P, U])
    pw = m.sb("a0_pw", [128, OC, 128])
    dw = m.sb("a0_dw", [128, OC])
    wres = m.sb("a0_wres", [128, 4, D])
    bres = m.XN[:, G * Z:G * Z + D]
    ot = m.sb("a0_ot", [128, 2, 4 * P])
    ft = [m.sb(f"a0_ft{i}", [P, G, D]) for i in range(2)]
    ss = m.sb("a0_ss", [P, 4, G])
    n = [m.sb(f"a0_n{i}", [P, 4, G]) for i in range(2)]
    f = [m.sb(f"a0_f{i}", [P, G]) for i in range(2)]
    th = [m.sb(f"a0_th{i}", [P, G]) for i in range(2)]
    s1, s2, s3, s4, s5, s6 = (m.sb(f"a0_s{i}", [P, G]) for i in range(6))
    loads = Loads(m, "a0_loaded")
    (zeroed, w_ready, z_made, z_kept, uv_root, out_done, o_root, o_turned, o_kept, res_made, ft_ss, ft_root) = (
        m.sem("a0_" + x) for x in (
            "zeroed", "w_ready", "z_made", "z_kept", "uv_root", "out_done", "o_root",
            "o_turned", "o_kept", "res_made", "ft_ss", "ft_root"))
    zb = [m.ps[0], m.ps[1], m.ps[2]]
    with nc.Block() as block:
        @block.sync
        def _(sp):
            sp.wait_ge(zeroed, 1)
            for a in range(4):
                loads(sp, pw[32 * a:32 * a + 32, :, 32 * a:32 * a + 32],
                      io["w_pw_t"].rearrange("i (j a c) -> i j a c", a=4, c=32)[:, :, a, :])
            loads(sp, dw[:, :], io["w_dw_mid_cols"])
            loads(sp, wres[:, :, :], io["w_res_t"].rearrange("(k p) d -> p k d", p=128))
            loads(sp, bres[:, :], io["L0_mix_b_res"].partition_broadcast(P))

        n_loads = 16 * (4 + 3)

        @block.gpsimd
        def _(pool):
            pool.memset(pw[:, :, :], 0.0).then_inc(zeroed, 1)

        @block.tensor
        def _(pe):
            pe.wait_ge(w_ready, 1)

            def project(g, nt):
                for j in range(nt):
                    t = g * G + j
                    pe.wait_ge(z_kept, t + 1)
                    for o in range(OC):
                        pe.transpose(zb[o // 4][:P, (o % 4) * 128:(o % 4 + 1) * 128],
                                     m.QT[:, bass.ds(t * P + o * N, P)], m.ident[:, :])
                    for o in range(OC):
                        c = U + o * 128
                        last = pe.matmul(zb[c // 512][:P, c % 512:c % 512 + 128], m.QT[:, bass.ds(t * P + o * N, P)],
                                         pw[:, o, :], start=True, stop=True)
                    last.then_inc(z_made, 1)

            def resolve(g, nt):
                pe.wait_ge(out_done, g + 1)
                pe.wait_ge(ft_ss, g + 1)
                for j in range(nt):
                    t = g * G + j
                    for k in range(4):
                        last = pe.transpose(m.ps[4 + j % 2][:, k * P:(k + 1) * P], kr[:, j, k * 128:(k + 1) * 128],
                                            m.ident[:P, :P])
                    last.then_inc(o_turned, 1)
                    pe.wait_ge(o_kept, t + 1)
                    for k in range(4):
                        last = pe.matmul(m.ps[6 + j // 2][:P, j % 2 * D:(j % 2 + 1) * D], ot[:, j % 2, k * P:(k + 1) * P],
                                         wres[:, k, :], start=k == 0, stop=k == 3)
                last.then_inc(res_made, 1)
            project(0, G)
            for g in range(NCH):
                project(g + 1, G if g + 1 < NCH else 1)
                resolve(g, G)
            resolve(NCH, 1)

        @block.scalar
        def _(act):
            act.sem_inc(z_kept, 1)

            def keep_z(g, i, nt):
                for j in range(nt):
                    act.wait_ge(z_made, g * G + j + 1)
                    for lo in range(0, 2 * U, 256):
                        act.copy(z[i][:, j, lo:lo + 256], zb[lo // 512][:P, lo % 512:lo % 512 + 256])
                    act.drain().then_inc(z_kept, 1)
                    for h in range(2):
                        act.activation(junk[:, :], z[i][:, j, h * U:(h + 1) * U], ACT.Square,
                                       accum_out=ss[:, h, j:j + 1])
                        act.drain()
                act.sqrt(n[i][:, 0, 0:nt], ss[:, 0, 0:nt])
                for j in range(nt):
                    act.activation(n[i][:, 1, j:j + 1], ss[:, 1, j:j + 1], ACT.Sqrt, bias=ss[:, 0, j:j + 1])
                act.drain().then_inc(uv_root, 1)

            def turn_out(g, i, nt):
                act.wait_ge(out_done, g + 1)
                for j in range(nt):
                    act.activation(junk[:, 0:O], kr[:, j, :], ACT.Square, accum_out=ss[:, 2, j:j + 1])
                    act.drain()
                act.sqrt(n[i][:, 2, 0:nt], ss[:, 2, 0:nt]).then_inc(o_root, 1)
                for j in range(nt):
                    act.wait_ge(o_turned, g * G + j + 1)
                    act.copy(ot[:, j % 2, :], m.ps[4 + j % 2][:, 0:4 * P]).then_inc(o_kept, 1)

            def result_norm(g, i, nt):
                act.wait_ge(ft_ss, g + 2)
                for j in range(nt):
                    act.activation(junk[:, 0:D], ft[i][:, j, :], ACT.Square, accum_out=ss[:, 3, j:j + 1])
                    act.drain()
                act.sqrt(n[i][:, 3, 0:nt], ss[:, 3, 0:nt])
                act.drain()
                act.activation(th[i][:, 0:nt], n[i][:, 3, 0:nt], ACT.Tanh).then_inc(ft_root, 1)
            keep_z(0, 0, G)
            keep_z(1, 1, G)
            turn_out(0, 0, G)
            assert NCH == 6
            with act.Fori(0, 2) as r:
                for j in range(2):
                    keep_z(r * 2 + (j + 2), j, G)
                    turn_out(r * 2 + (j + 1), 1 - j, G)
                    result_norm(r * 2 + j, j, G)
            keep_z(6, 0, 1)
            turn_out(5, 1, G)
            result_norm(4, 0, G)
            turn_out(6, 0, 1)
            result_norm(5, 1, G)
            result_norm(6, 0, 1)

        @block.vector
        def _(dve):
            dve.wait_ge(loads.sem, n_loads)
            for o in range(OC):
                last = dve.tensor_scalar(pw[:, o, :], pw[:, o, :], dw[:, o:o + 1], None, ALU.mult)
            last.then_inc(w_ready, 1)
            dve.sem_inc(ft_ss, 1)
            flat = lambda x, nt: x[:, 0:nt, :].rearrange("p g (r c) -> p (g r) c", c=32)

            def attend(g, i, nt):
                zg = z[i].rearrange("p g (r c) -> p (g r) c", c=96)
                dve.wait_ge(uv_root, g + 1)
                log_exp_scale(dve, f[i][:, 0:nt], n[i][:, 0, 0:nt], MAX_ATANH, s1[:, 0:nt])
                dve.tensor_tensor(s2[:, 0:nt], n[i][:, 1, 0:nt], f[i][:, 0:nt], ALU.mult)
                dve.drain()
                log_exp_scale(dve, s3[:, 0:nt], s2[:, 0:nt], MAX_ATANH, s1[:, 0:nt])
                dve.tensor_tensor(f[i][:, 0:nt], f[i][:, 0:nt], s3[:, 0:nt], ALU.mult)
                dve.drain()
                for j in range(nt):
                    dve.tensor_scalar(vv[:, j, :].rearrange("p (r c) -> p r c", c=32),
                                      zg[:, j * GR:(j + 1) * GR, 64:96], f[i][:, j:j + 1], None, ALU.mult)
                dve.wait_ge(o_kept, g * G)
                dve.wait_ge(o_root, g)
                dve.tensor_scalar(flat(kr, nt), zg[:, 0:nt * GR, 32:64], 0.0, None, ALU.max)
                dve.drain()
                dve.tensor_reduce(ks[:, 0:nt * GR], flat(kr, nt), AX.X, ALU.add)
                dve.tensor_scalar(rec[:, 0:nt, :], vv[:, 0:nt, :], 1e-15, None, ALU.add)
                dve.drain()
                dve.reciprocal(rec[:, 0:nt, :], rec[:, 0:nt, :])
                dve.drain()
                dve.tensor_tensor(vv[:, 0:nt, :], vv[:, 0:nt, :], rec[:, 0:nt, :], ALU.mult)
                dve.drain()
                dve.scalar_tensor_tensor(flat(vv, nt), zg[:, 0:nt * GR, 0:32], 0.0, flat(vv, nt), ALU.max, ALU.mult)
                dve.drain()
                dve.tensor_tensor(flat(kr, nt), flat(vv, nt), ks[:, 0:nt * GR].unsqueeze(2).broadcast_to((P, nt * GR, 32)),
                                  ALU.mult).then_inc(out_done, 1)

            def scale_result(g, i, nt):
                dve.tensor_tensor(s4[:, 0:nt], f[i][:, 0:nt], f[i][:, 0:nt], ALU.mult)
                dve.drain()
                dve.wait_ge(o_root, g + 1)
                dve.tensor_tensor(s2[:, 0:nt], s4[:, 0:nt], n[i][:, 2, 0:nt], ALU.mult)
                dve.drain()
                log_exp_scale(dve, s3[:, 0:nt], s2[:, 0:nt], MAX_ATANH, s1[:, 0:nt])
                dve.tensor_tensor(s4[:, 0:nt], s4[:, 0:nt], s3[:, 0:nt], ALU.mult)
                dve.drain()
                dve.wait_ge(res_made, g + 1)
                for j in range(nt):
                    dve.scalar_tensor_tensor(ft[i][:, j, :], m.ps[6 + j // 2][:P, j % 2 * D:(j % 2 + 1) * D],
                                             s4[:, j:j + 1], bres[:P, :], ALU.mult, ALU.add)
                dve.drain().then_inc(ft_ss, 1)

            def add_result(g, i, nt):
                dve.wait_ge(ft_root, g + 1)
                dve.tensor_scalar(s5[:, 0:nt], n[i][:, 3, 0:nt], MIN_NORM, None, ALU.max)
                dve.tensor_scalar(s6[:, 0:nt], th[i][:, 0:nt], MAX_NORM, None, ALU.min)
                dve.drain()
                dve.reciprocal(s5[:, 0:nt], s5[:, 0:nt])
                dve.drain()
                dve.tensor_tensor(s6[:, 0:nt], s6[:, 0:nt], s5[:, 0:nt], ALU.mult)
                dve.drain()
                for j in range(nt):
                    x = m.X[:, bass.ds(g * (G * D) + j * D, D)]
                    dve.scalar_tensor_tensor(x, ft[i][:, j, :], s6[:, j:j + 1], x, ALU.mult, ALU.add)
                dve.drain()
            attend(0, 0, G)
            attend(1, 1, G)
            scale_result(0, 0, G)
            with dve.Fori(0, 2) as r:
                for j in range(2):
                    attend(r * 2 + (j + 2), j, G)
                    scale_result(r * 2 + (j + 1), 1 - j, G)
                    add_result(r * 2 + j, j, G)
            attend(6, 0, 1)
            scale_result(5, 1, G)
            add_result(4, 0, G)
            scale_result(6, 0, 1)
            add_result(5, 1, G)
            add_result(6, 0, 1)


class Edges:

    def __init__(self, m, tag, cols):
        self.tag, self.cols = tag, cols
        self.key = m.sb(tag + "_key", [128, cols])
        self.other = m.sb(tag + "_other", [128, cols], I32)
        self.start = m.dram(tag + "_start", [KEYS + 1], I32)


def floor_div(dve, q, r, pos, cols):
    magic = 12582912.0
    dve.tensor_scalar(q, pos, 0.5, 1.0 / cols, ALU.add, ALU.mult)
    dve.drain()
    dve.tensor_scalar(q, q, -0.5, magic, ALU.add, ALU.add)
    dve.drain()
    dve.tensor_scalar(q, q, -magic, None, ALU.add)
    dve.drain()
    last = dve.scalar_tensor_tensor(r, q, -float(cols), pos, ALU.mult, ALU.add)
    dve.drain()
    return last


def sort_constants(m):
    m.row16 = m.sb("row16", [128, 512], FP16)
    m.low16 = m.sb("low16", [128, 128], FP16)
    m.low = m.sb("low", [128, 128])
    m.high = m.sb("high", [128, 128])
    m.ones = m.sb("ones", [128, 512])
    m.zero16 = m.sb("zero16", [128, 512], FP16)
    m.ident16 = m.sb("ident16", [128, 128], FP16)
    with m.nc.Block() as block:
        @block.gpsimd
        def _(pool):
            pool.iota(m.row16[:, :], [[1, 512]], base=0, channel_multiplier=0,
                      allow_small_or_imprecise_dtypes=True)
            pool.memset(m.low[:, :], 1.0)
            pool.memset(m.high[:, :], 1.0)
            pool.memset(m.ones[:, :], 1.0)
            pool.memset(m.zero16[:, :], 0.0)
            pool.drain()
            pool.affine_select(out=m.low[:, :], in_=m.low[:, :], compare_op=ALU.is_gt, fill=0.0,
                               base=0, pattern=[[1, 128]], channel_multiplier=-1)
            pool.affine_select(out=m.high[:, :], in_=m.high[:, :], compare_op=ALU.is_gt, fill=0.0,
                               base=0, pattern=[[-1, 128]], channel_multiplier=1)
            pool.drain()
            pool.tensor_copy(m.low16[:, :], m.low[:, :])
            pool.tensor_copy(m.ident16[:, :], m.ident[:, :])
            pool.drain()


def sort_edges(m, ed, key_in, other_in, beside=lambda block, stage: None):
    nc, cols, tag = m.nc, ed.cols, ed.tag
    nb = cols // BC
    MID = 1562.0
    with Stage(m):
        ki = m.sb(tag + "_ki", [128, cols], I32)
        a = m.sb(tag + "_a", [128, cols])
        b = m.sb(tag + "_b", [128, cols])
        val = m.sb(tag + "_val", [128, cols])
        pos = m.sb(tag + "_pos", [128, cols])
        H = m.sb(tag + "_H", [128, (cols + 1) * KB])
        H3 = H[:, :].rearrange("p (t b) -> p t b", b=KB)
        half = lambda i, n=BC * 64: m.scratch[:, i * n:(i + 1) * n].bitcast(FP16).rearrange("p (c e) -> p c e", c=BC)
        oa, oat16, em = [half(0), half(1)], half(2), half(3)
        oat32 = m.scratch[:, 4 * BC * 64:6 * BC * 64].rearrange("p (c e) -> p c e", c=BC)
        ob = [m.sb(f"{tag}_ob{i}", [128, BC, KB], FP16) for i in range(3)]
        tot = m.sb(tag + "_tot", [128, KB])
        start = m.sb(tag + "_start_sb", [128, KB])
        start_i = m.sb(tag + "_start_i", [128, KB], I32)
        rsum = m.sb(tag + "_rsum", [128, 1])
        row128 = m.row16[:, 0:128]

        def one_hots(dve, t, j, i):
            for c in range(BC):
                dve.tensor_scalar(oa[j][:, c, :], row128, a[:, bass.ds(t * BC + c, 1)], None, ALU.is_equal)
            return dve.tensor_tensor(ob[i][:, :, :], b[:, at(t, BC)].unsqueeze(2).broadcast_to((128, BC, KB)),
                                     m.row16[:, 0:KB].unsqueeze(1).broadcast_to((128, BC, KB)), ALU.is_equal)

        loads = Loads(m, tag + "_in")
        hot, used, kept, tot_done, fin = (m.sem(f"{tag}_{x}") for x in ("hot", "used", "kept", "tot_done", "fin"))
        with nc.Block() as block:
            beside(block, 1)

            @block.sync
            def _(sp):
                loads(sp, ki[:, :], key_in)
                loads(sp, ed.other[:, :], other_in)

            @block.vector
            def _(dve):
                dve.wait_ge(loads.sem, loads.all)
                dve.tensor_scalar(ed.key[:, :].bitcast(I32), ki[:, :], 5, None, ALU.arith_shift_right)
                dve.tensor_scalar(val[:, :], ed.other[:, :], float(N - 1), -MID, ALU.min, ALU.add)
                dve.drain()
                dve.tensor_copy(a[:, :], ed.key[:, :].bitcast(I32))
                dve.drain()
                dve.tensor_scalar(ki[:, :], ki[:, :], 31, None, ALU.bitwise_and)
                dve.drain()
                dve.tensor_copy(b[:, :], ki[:, :])
                dve.drain()
                dve.sem_inc(used, 2)

                def body(t, j):
                    dve.wait_ge(used, t + 1)
                    one_hots(dve, t, j, j)
                    dve.drain().then_inc(hot, 1)
                tiles(dve, nb, 2, body)

            @block.tensor
            def _(pe):
                total = m.ps[7][:, 0:KB]
                pe.matmul(total, m.zero16[:, 0:128], m.zero16[:, 0:KB], start=True, stop=False)

                def body(t, j):
                    pe.wait_ge(hot, t + 1)
                    pe.wait_ge(kept, t + 1)
                    for c in range(BC):
                        pe.matmul(m.ps[j][:, c * KB:(c + 1) * KB], oa[j][:, c, :], ob[j][:, c, :], start=True, stop=True)
                        last = pe.matmul(total, oa[j][:, c, :], ob[j][:, c, :], start=False, stop=False)
                    last.then_inc(used, 1)
                tiles(pe, nb, 2, body)
                pe.matmul(total, m.zero16[:, 0:128], m.zero16[:, 0:KB], start=False, stop=True).then_inc(tot_done, 1)

            @block.scalar
            def _(act):
                act.sem_inc(kept, 2)

                def body(t, j):
                    act.wait_ge(used, t + 3)
                    act.copy(H[:, bass.ds(t * (BC * KB) + KB, BC * KB)], m.ps[j][:, :]).then_inc(kept, 1)
                tiles(act, nb, 2, body)
                act.wait_ge(tot_done, 1)
                act.copy(tot[:, :], m.ps[7][:, 0:KB])

        row_ready, row_sum, start_ready, stored = (m.sem(f"{tag}_{x}") for x in ("row_ready", "row_sum", "start_ready", "stored"))
        with nc.Block() as block:
            @block.vector
            def _(dve):
                dve.tensor_tensor_scan(start[:, :], m.ones[:, 0:KB], tot[:, :], 0.0, ALU.mult, ALU.add)
                dve.drain()
                dve.tensor_copy(rsum[:, :], start[:, KB - 1:KB]).then_inc(row_ready, 1)
                dve.drain()
                dve.tensor_tensor(start[:, :], start[:, :], tot[:, :], ALU.subtract)
                dve.drain()
                dve.wait_ge(row_sum, 1)
                dve.tensor_scalar(start[:, :], start[:, :], m.ps[0][:, 0:1], None, ALU.add)
                dve.drain()
                dve.tensor_copy(start_i[:, :], start[:, :]).then_inc(start_ready, 1)
                dve.tensor_copy(H3[:, 0, :], start[:, :])
                for i in range(KB):
                    dve.tensor_tensor_scan(H3[:, 1:, i], m.ones[:, 0:cols], H3[:, 1:, i], start[:, i:i + 1],
                                           ALU.mult, ALU.add)

            @block.tensor
            def _(pe):
                pe.wait_ge(row_ready, 1)
                pe.matmul(m.ps[0][:, 0:1], m.low[:, :], rsum[:, :], start=True, stop=True).then_inc(row_sum, 1)

            @block.sync
            def _(sp):
                sp.wait_ge(start_ready, 1)
                sp.dma_start(ed.start[0:KEYS].rearrange("(a b) -> a b", b=KB), start_i[:, :]).then_inc(stored, 16)
                sp.wait_ge(stored, 16)

        pick = m.sb(tag + "_pick", [128, BC, KB])
        hot2, turned, moved16, moved32, same, masked, ranked, picked = (
            m.sem(f"{tag}_{x}") for x in ("hot2", "turned", "moved16", "moved32", "same", "masked", "ranked", "picked"))
        with nc.Block() as block:
            beside(block, 3)

            @block.vector
            def _(dve):
                def hots(t, j):
                    one_hots(dve, t, j % 2, j % 3)
                    dve.drain().then_inc(hot2, 1)

                def mask(t, j):
                    for q in range(4):
                        dve.wait_ge(same, 4 * t + q + 1)
                        dve.tensor_tensor(em[:, 4 * q:4 * q + 4, :], m.ps[2 + q][:, :].rearrange("p (c e) -> p c e", c=4),
                                          m.low16[:, :].unsqueeze(1).broadcast_to((128, 4, 128)), ALU.mult).then_inc(masked, 1)

                def choose(t, j):
                    dve.wait_ge(ranked, t + 1)
                    dve.tensor_tensor(pick[:, :, :], m.ps[6][:, :].rearrange("p (c b) -> p c b", b=KB),
                                      ob[j % 3][:, :, :], ALU.mult)
                    dve.drain().then_inc(picked, 1)
                    dve.tensor_reduce(pos[:, at(t, BC)], pick[:, :, :], AX.X, ALU.add)
                    dve.drain()
                dve.sem_inc(picked, 1)
                hots(0, 0)
                hots(1, 1)
                mask(0, 0)

                def body(t, j):
                    hots(t + 2, j + 2)
                    choose(t, j)
                    mask(t + 1, j + 1)
                tiles(dve, nb - 2, 6, body)
                choose(nb - 2, nb - 2)
                mask(nb - 1, nb - 1)
                choose(nb - 1, nb - 1)

            @block.tensor
            def _(pe):
                def turn(t, j):
                    pe.wait_ge(hot2, t + 1)
                    pe.wait_ge(moved32, t + 1)
                    for c in range(BC):
                        bank = m.ps[c // 8][:, :].bitcast(FP16)
                        last = pe.transpose(bank[:, (c % 8) * 128:(c % 8 + 1) * 128], oa[j % 2][:, c, :], m.ident16[:, :])
                    last.then_inc(turned, 1)

                def compare(t, j):
                    pe.wait_ge(moved16, t + 1)
                    pe.wait_ge(masked, 4 * t)
                    for c in range(BC):
                        last = pe.matmul(m.ps[2 + c // 4][:, (c % 4) * 128:(c % 4 + 1) * 128], oat16[:, c, :],
                                         oat16[:, c, :], start=True, stop=True)
                        if c % 4 == 3:
                            last.then_inc(same, 1)

                def rank(t, j):
                    pe.wait_ge(moved32, t + 2)
                    pe.wait_ge(picked, t + 1)
                    pe.wait_ge(masked, 4 * t + 4)
                    for c in range(BC):
                        out = m.ps[6][:, c * KB:(c + 1) * KB]
                        pe.matmul(out, oat32[:, c, :], H[:, bass.ds(t * (BC * KB) + c * KB, KB)], start=True, stop=False)
                        last = pe.matmul(out, em[:, c, :], ob[j % 3][:, c, :], start=False, stop=True)
                    last.then_inc(ranked, 1)
                turn(0, 0)

                def body(t, j):
                    compare(t, j)
                    turn(t + 1, j + 1)
                    rank(t, j)
                tiles(pe, nb - 1, 6, body)
                compare(nb - 1, nb - 1)
                rank(nb - 1, nb - 1)

            @block.scalar
            def _(act):
                act.sem_inc(moved32, 1)

                def body(t, j):
                    act.wait_ge(turned, t + 1)
                    for dst, done in ((oat16, moved16), (oat32, moved32)):
                        if dst is oat32:
                            act.wait_ge(ranked, t)
                        for h in range(2):
                            last = act.copy(dst[:, 8 * h:8 * h + 8, :].rearrange("p c e -> p (c e)"),
                                            m.ps[h][:, :].bitcast(FP16))
                        last.then_inc(done, 1)
                tiles(act, nb, 2, body)

        q, r = a, b
        sq = m.sb(tag + "_sq", [128, KB])
        sr = m.sb(tag + "_sr", [128, KB])
        rv = [m.sb(f"{tag}_rv{i}", [128, 4, cols], FP16) for i in range(2)]
        neg = m.sb(tag + "_neg_q", [128, cols + KB])
        far = [m.sb(f"{tag}_far{i}", [128, 3, 128], FP16) for i in range(2)]
        negated, line_hot, hot3, used3, row3, pre3 = (
            m.sem(f"{tag}_{x}") for x in ("negated", "line_hot", "hot3", "used3", "row3", "pre3"))
        nq = cols // 4
        with nc.Block() as block:
            beside(block, 4)

            @block.vector
            def _(dve):
                floor_div(dve, q[:, :], r[:, :], pos[:, :], cols)
                floor_div(dve, sq[:, :], sr[:, :], start[:, :], cols)
                dve.tensor_scalar(neg[:, 0:cols], q[:, :], -1.0, None, ALU.mult)
                dve.tensor_scalar(neg[:, cols:], sq[:, :], -1.0, None, ALU.mult)
                dve.drain().then_inc(negated, 1)
                dve.sem_inc(used3, 2)

                def body(t, j):
                    dve.wait_ge(used3, t + 1)
                    for c in range(4):
                        e = bass.ds(t * 4 + c, 1)
                        dve.tensor_scalar(rv[j % 2][:, c, :], m.row16[:, 0:cols], r[:, e], val[:, e], ALU.is_equal, ALU.mult)
                    dve.tensor_scalar(oa[j % 2][:, 3, :], row128, q[:, e], None, ALU.is_equal)
                    dve.drain().then_inc(hot3, 1)
                tiles(dve, nq, 8, body)

                def starts(t, j):
                    dve.wait_ge(used3, nq + t + 1)
                    for c in range(4):
                        e = bass.ds(t * 4 + c, 1)
                        dve.tensor_scalar(rv[j % 2][:, c, :], m.row16[:, 0:cols], sr[:, e], None, ALU.is_equal)
                    dve.tensor_scalar(oa[j % 2][:, 3, :], row128, sq[:, e], None, ALU.is_equal)
                    dve.drain().then_inc(hot3, 1)
                tiles(dve, KB // 4, 8, starts)
                dve.wait_ge(used3, nq + KB // 4 + 3)
                dve.tensor_scalar(ed.other[:, :], m.ps[0][:, 0:cols], MID, None, ALU.add)
                dve.tensor_tensor_scan(ed.key[:, :], m.ones[:, 0:cols], m.ps[1][:, 0:cols], 0.0, ALU.mult, ALU.add)
                dve.drain()
                dve.tensor_copy(rsum[:, :], ed.key[:, cols - 1:cols]).then_inc(row3, 1)
                dve.wait_ge(pre3, 1)
                dve.tensor_scalar(ed.key[:, :], ed.key[:, :], m.ps[2][:, 0:1], -1.0, ALU.add, ALU.add)

            @block.scalar
            def _(act):
                act.wait_ge(negated, 1)

                def body(t, j):
                    act.wait_ge(used3, t + 1)
                    for c in range(3):
                        act.activation(far[j % 2][:, c, :], row128, ACT.Square, bias=neg[:, bass.ds(t * 4 + c, 1)])
                    act.drain()
                    act.activation(oa[j % 2][:, 0:3, :], far[j % 2][:, :, :], ACT.Relu, bias=m.ones[:, 0:1],
                                   scale=-1.0).then_inc(line_hot, 1)
                tiles(act, nq + KB // 4, 8, body)

            @block.tensor
            def _(pe):
                for half, count, first in ((0, nq, 0), (1, KB // 4, nq)):
                    out = m.ps[half][:, 0:cols]
                    pe.matmul(out, m.zero16[:, 0:128], m.zero16[:, 0:cols], start=True, stop=False)

                    def body(t, j):
                        pe.wait_ge(hot3, t + first + 1)
                        pe.wait_ge(line_hot, t + first + 1)
                        for c in range(4):
                            last = pe.matmul(out, oa[(j + first) % 2][:, c, :], rv[(j + first) % 2][:, c, :],
                                             start=False, stop=False)
                        last.then_inc(used3, 1)
                    assert nq % 2 == 0
                    tiles(pe, count, 2, body)
                    last = pe.matmul(out, m.zero16[:, 0:128], m.zero16[:, 0:cols], start=False, stop=True)
                last.then_inc(used3, 1)
                pe.wait_ge(row3, 1)
                pe.matmul(m.ps[2][:, 0:1], m.low[:, :], rsum[:, :], start=True, stop=True).then_inc(pre3, 1)


def nodes_of(table, lo=0):
    return table[lo:lo + N].rearrange("(t p) -> p t", p=P)


class Spread:

    def __init__(self, m, tag, ed, H):
        self.H = H
        self.ke = m.sb(tag + "_ke", [128, ed.cols, H])
        self.cont = m.sb(tag + "_cont", [128, ed.cols])
        self.pen = m.sb(tag + "_pen", [128, ed.cols])
        self.lo = m.sb(tag + "_lo", [P, NT])
        self.hi = m.sb(tag + "_hi", [P, NT])
        self.has = m.sb(tag + "_has", [P, NT])


def spread_logits(m, tag, ed, sp_, table, logits):
    nc, H, cols = m.nc, sp_.H, ed.cols
    E = 128 * cols
    placed = m.dram(tag + "_placed", [E, H])
    with Stage(m):
        zero = m.sb(tag + "_zero", [128, cols * H])
        lo_i, hi_i, dst_i = (m.sb(tag + x, [P, NT], I32) for x in ("_lo_i", "_hi_i", "_dst_i"))
        dst = m.sb(tag + "_dst", [P, NT])
        first_i = m.sb(tag + "_first_i", [128, 1], I32)
        first = m.sb(tag + "_first", [128, 1])
        own = m.sb(tag + "_own", [128, H])
        raw = m.sb(tag + "_raw", [128, cols, H])
        loads, rows, back = Loads(m, tag + "_bounds_loaded"), Loads(m, tag + "_rows_placed"), Loads(m, tag + "_raw_loaded")
        zeroed, cleared, idx_ready, own_sem = (m.sem(tag + x) for x in ("_zeroed", "_cleared", "_idx_ready", "_own"))
        with nc.Block() as block:
            @block.sync
            def _(sp):
                with nc.allow_non_contiguous_dma(reason="one word per node"):
                    loads(sp, lo_i[:, :], nodes_of(ed.start))
                    loads(sp, hi_i[:, :], nodes_of(ed.start, 1))
                sp.wait_ge(zeroed, 1)
                sp.dma_start(placed.rearrange("(p t) h -> p (t h)", p=128), zero[:, :]).then_inc(cleared, 16)
                sp.wait_ge(rows.sem, 16 * NT)
                back(sp, raw[:, :, :], placed.rearrange("(p t) h -> p t h", p=128))

            @block.gpsimd
            def _(pool):
                pool.memset(zero[:, :], 0.0).then_inc(zeroed, 1)
                pool.wait_ge(idx_ready, 1)
                pool.indirect_dma_start(out=own[:, :], out_offset=None, in_=table,
                                        in_offset=bass.IndirectOffsetOnAxis(ap=first_i[:, :], axis=0)).then_inc(own_sem, 16)
                pool.wait_ge(cleared, 16)
                for t in range(NT):
                    pool.indirect_dma_start(out=placed, out_offset=bass.IndirectOffsetOnAxis(ap=dst_i[:, t:t + 1], axis=0),
                                            in_=logits[:, t, :], in_offset=None,
                                            bounds_check=E - 1, oob_is_err=False).then_inc(rows.sem, 16)

            @block.vector
            def _(dve):
                dve.wait_ge(loads.sem, 32)
                dve.tensor_copy(sp_.lo[:, :], lo_i[:, :])
                dve.tensor_copy(sp_.hi[:, :], hi_i[:, :])
                dve.tensor_scalar(first[:, :], ed.key[:, 0:1], float(N - 1), None, ALU.min)
                dve.drain()
                dve.tensor_copy(first_i[:, :], first[:, :])
                dve.tensor_tensor(sp_.has[:, :], sp_.hi[:, :], sp_.lo[:, :], ALU.is_gt)
                dve.drain()
                dve.tensor_scalar(dst[:, :], sp_.has[:, :], -float(4 * E), float(4 * E), ALU.mult, ALU.add)
                dve.drain()
                dve.tensor_tensor(dst[:, :], dst[:, :], sp_.lo[:, :], ALU.add)
                dve.drain()
                dve.tensor_copy(dst_i[:, :], dst[:, :])
                dve.drain().then_inc(idx_ready, 1)
                dve.memset(sp_.cont[:, 0:1], 0.0)
                dve.tensor_tensor(sp_.cont[:, 1:], ed.key[:, 1:], ed.key[:, 0:cols - 1], ALU.is_equal)
                dve.drain()
                dve.tensor_scalar(sp_.pen[:, :], sp_.cont[:, :], -1.0, BIG, ALU.add, ALU.mult)
                dve.wait_ge(back.sem, 16)
                dve.wait_ge(own_sem, 16)
                dve.tensor_copy(raw[:, 0, :], own[:, :])
                dve.drain()
                for h in range(H):
                    dve.tensor_tensor_scan(sp_.ke[:, :, h], sp_.cont[:, :], raw[:, :, h], 0.0, ALU.mult, ALU.add)


def carry_rows(m, tag, ed, H, F, last, table):
    nc, cols = m.nc, ed.cols
    W = H * F + 2 * H
    with Stage(m):
        dg = m.sb(tag + "_dg", [128, H + 1, 128])
        mask = m.sb(tag + "_mask", [128, 128])
        neg = m.sb(tag + "_neg", [128, 128])
        a = m.sb(tag + "_a", [128, H, 128])
        wt = m.sb(tag + "_wt", [128, H, 128])
        wtt = m.sb(tag + "_wtt", [128, H, 128])
        cm = m.sb(tag + "_cm", [128, H])
        ncm = m.sb(tag + "_ncm", [128, H])
        row = m.sb(tag + "_row", [128, W + 1])
        dg_ready, wide, a_ready, expd, wt_ready, turned, back, summed, row_ready, stored = (
            m.sem(tag + x) for x in ("_dg_ready", "_wide", "_a_ready", "_expd", "_wt_ready", "_turned",
                                     "_back", "_summed", "_row_ready", "_stored"))
        with nc.Block() as block:
            @block.vector
            def _(dve):
                dve.tensor_scalar(dg[:, H, :], m.ident[:, :], ed.key[:, cols - 1:cols], None, ALU.mult)
                for h in range(H):
                    dve.tensor_scalar(dg[:, h, :], m.ident[:, :], last[:, H * F + H + h:H * F + H + h + 1], None, ALU.mult)
                dve.drain().then_inc(dg_ready, 1)
                dve.wait_ge(wide, 1)
                dve.scalar_tensor_tensor(mask[:, :], m.ps[H][:, 0:128], ed.key[:, 0:1], m.high[:, :], ALU.is_equal, ALU.mult)
                dve.drain()
                dve.tensor_scalar(neg[:, :], mask[:, :], -1.0, BIG, ALU.add, ALU.mult)
                for h in range(H):
                    dve.tensor_tensor(a[:, h, :], m.ps[h][:, 0:128], mask[:, :], ALU.mult)
                dve.drain()
                for h in range(H):
                    dve.tensor_tensor(a[:, h, :], a[:, h, :], neg[:, :], ALU.add)
                dve.drain()
                dve.tensor_reduce(cm[:, :], a[:, :, :], AX.X, ALU.max)
                dve.drain()
                for h in range(H):
                    dve.tensor_scalar(a[:, h, :], a[:, h, :], cm[:, h:h + 1], None, ALU.subtract)
                dve.drain().then_inc(a_ready, 1)
                dve.wait_ge(expd, 1)
                for h in range(H):
                    dve.tensor_tensor(wt[:, h, :], wt[:, h, :], mask[:, :], ALU.mult)
                dve.drain().then_inc(wt_ready, 1)
                dve.wait_ge(turned, 1)
                for h in range(H):
                    dve.tensor_copy(wtt[:, h, :], m.ps[h][:, 0:128])
                dve.drain().then_inc(back, 1)
                dve.wait_ge(summed, 1)
                for h in range(H):
                    dve.tensor_copy(row[:, h * F:(h + 1) * F], m.ps[4 + h][:, 0:F])
                    dve.tensor_copy(row[:, H * F + h:H * F + h + 1], m.ps[4 + h][:, F:F + 1])
                dve.tensor_copy(row[:, H * F + H:W], cm[:, :])
                dve.tensor_copy(row[:, W:W + 1], ed.key[:, 0:1])
                dve.drain().then_inc(row_ready, 1)

            @block.scalar
            def _(act):
                act.wait_ge(a_ready, 1)
                act.activation(wt[:, :, :], a[:, :, :], ACT.Exp).then_inc(expd, 1)

            @block.tensor
            def _(pe):
                pe.wait_ge(dg_ready, 1)
                for h in range(H + 1):
                    x = pe.matmul(m.ps[h][:, 0:128], m.ones[:, 0:128], dg[:, h, :], start=True, stop=True)
                x.then_inc(wide, 1)
                pe.wait_ge(wt_ready, 1)
                for h in range(H):
                    x = pe.transpose(m.ps[h][:, 0:128], wt[:, h, :], m.ident[:, :])
                x.then_inc(turned, 1)
                pe.wait_ge(back, 1)
                for h in range(H):
                    pe.matmul(m.ps[4 + h][:, 0:F], wtt[:, h, :], last[:, h * F:(h + 1) * F], start=True, stop=True)
                    x = pe.matmul(m.ps[4 + h][:, F:F + 1], wtt[:, h, :], last[:, H * F + h:H * F + h + 1],
                                  start=True, stop=True)
                x.then_inc(summed, 1)

            @block.sync
            def _(sp):
                sp.wait_ge(row_ready, 1)
                sp.dma_start(table, row[:, :]).then_inc(stored, 16)
                sp.wait_ge(stored, 16)


def merge_nodes(m, tag, ed, sp_, H, F, result, carry, agg, den, own_e=None, own_f=None):
    nc, cols = m.nc, ed.cols
    HF = H * F
    W = HF + 2 * H
    GT = 5
    with Stage(m):
        end = m.sb(tag + "_end", [P, NT])
        part = m.sb(tag + "_part", [P, NT])
        rest = m.sb(tag + "_rest", [P, NT])
        end_i = m.sb(tag + "_end_i", [P, NT], I32)
        part_i = m.sb(tag + "_part_i", [P, NT], I32)
        node = m.sb(tag + "_node", [P, NT])
        re = m.sb(tag + "_re", [P, GT, W])
        rc = m.sb(tag + "_rc", [P, GT, W + 1])
        use = m.sb(tag + "_use", [P, GT])
        me, mc, mx, we, wc, ws = (m.sb(tag + x, [P, GT, H]) for x in ("_me", "_mc", "_mx", "_we", "_wc", "_ws"))
        idx_ready, rows, exps, expd, free = (m.sem(tag + x) for x in ("_idx_ready", "_rows", "_exps", "_expd", "_free"))
        node_sem = m.sem(tag + "_node_sem")
        with nc.Block() as block:
            @block.gpsimd
            def _(pool):
                pool.iota(node[:, :], [[P, NT]], base=0, channel_multiplier=1,
                          allow_small_or_imprecise_dtypes=True).then_inc(node_sem, 1)
                pool.wait_ge(idx_ready, 1)
                for t in range(NT):
                    if t % GT == 0 and t:
                        pool.wait_ge(free, t // GT)
                    for dst, table, idx in ((re, result, end_i), (rc, carry, part_i)):
                        pool.indirect_dma_start(out=dst[:, t % GT, :], out_offset=None, in_=table,
                                                in_offset=bass.IndirectOffsetOnAxis(ap=idx[:, t:t + 1], axis=0)
                                                ).then_inc(rows, 16)

            @block.vector
            def _(dve):
                dve.tensor_scalar(end[:, :], sp_.hi[:, :], -1.0, 0.0, ALU.add, ALU.max)
                dve.drain()
                floor_div(dve, part[:, :], rest[:, :], end[:, :], cols)
                dve.tensor_copy(end_i[:, :], end[:, :])
                dve.tensor_copy(part_i[:, :], part[:, :])
                dve.drain().then_inc(idx_ready, 1)
                dve.wait_ge(node_sem, 1)
                for g in range(NT // GT):
                    ts = slice(g * GT, (g + 1) * GT)
                    has = sp_.has[:, ts]
                    wide = lambda x: x.unsqueeze(2).broadcast_to((P, GT, H))
                    dve.wait_ge(rows, 32 * GT * (g + 1))
                    dve.tensor_tensor(use[:, :], rc[:, :, W], node[:, ts], ALU.is_equal)
                    dve.tensor_tensor(me[:, :, :], re[:, :, HF + H:W], wide(has), ALU.mult)
                    dve.tensor_scalar(we[:, :, :], wide(has), -1.0, BIG, ALU.add, ALU.mult)
                    dve.drain()
                    dve.tensor_tensor(me[:, :, :], me[:, :, :], we[:, :, :], ALU.add)
                    dve.tensor_tensor(mc[:, :, :], rc[:, :, HF + H:W], wide(use[:, :]), ALU.mult)
                    dve.tensor_scalar(wc[:, :, :], wide(use[:, :]), -1.0, BIG, ALU.add, ALU.mult)
                    dve.drain()
                    dve.tensor_tensor(mc[:, :, :], mc[:, :, :], wc[:, :, :], ALU.add)
                    dve.drain()
                    dve.tensor_tensor(mx[:, :, :], me[:, :, :], mc[:, :, :], ALU.max)
                    dve.drain()
                    if own_e is not None:
                        dve.tensor_tensor(mx[:, :, :], mx[:, :, :], own_e[:, ts, :], ALU.max)
                        dve.drain()
                        dve.tensor_tensor(ws[:, :, :], own_e[:, ts, :], mx[:, :, :], ALU.subtract)
                    dve.tensor_tensor(we[:, :, :], me[:, :, :], mx[:, :, :], ALU.subtract)
                    dve.tensor_tensor(wc[:, :, :], mc[:, :, :], mx[:, :, :], ALU.subtract)
                    dve.drain().then_inc(exps, 1)
                    dve.wait_ge(expd, g + 1)
                    dve.tensor_tensor(we[:, :, :], we[:, :, :], wide(has), ALU.mult)
                    dve.tensor_tensor(wc[:, :, :], wc[:, :, :], wide(use[:, :]), ALU.mult)
                    dve.drain()
                    for j in range(GT):
                        for h in range(H):
                            f, d = slice(h * F, (h + 1) * F), slice(HF + h, HF + h + 1)
                            t = g * GT + j
                            dve.tensor_scalar(agg[:, t, f], re[:, j, f], we[:, j, h:h + 1], None, ALU.mult)
                            dve.tensor_scalar(den[:, t, h:h + 1], re[:, j, d], we[:, j, h:h + 1], None, ALU.mult)
                    dve.drain()
                    for j in range(GT):
                        for h in range(H):
                            f, d = slice(h * F, (h + 1) * F), slice(HF + h, HF + h + 1)
                            t = g * GT + j
                            dve.scalar_tensor_tensor(agg[:, t, f], rc[:, j, f], wc[:, j, h:h + 1], agg[:, t, f],
                                                     ALU.mult, ALU.add)
                            dve.scalar_tensor_tensor(den[:, t, h:h + 1], rc[:, j, d], wc[:, j, h:h + 1],
                                                     den[:, t, h:h + 1], ALU.mult, ALU.add)
                    if own_e is not None:
                        dve.drain()
                        for j in range(GT):
                            for h in range(H):
                                f, t = slice(h * F, (h + 1) * F), g * GT + j
                                dve.scalar_tensor_tensor(agg[:, t, f], own_f[:, t, f], ws[:, j, h:h + 1], agg[:, t, f],
                                                         ALU.mult, ALU.add)
                        dve.tensor_tensor(den[:, ts, :], den[:, ts, :], ws[:, :, :], ALU.add)
                    dve.drain().then_inc(free, 1)

            @block.scalar
            def _(act):
                for g in range(NT // GT):
                    act.wait_ge(exps, g + 1)
                    for x in (we, wc) + ((ws,) if own_e is not None else ()):
                        last = act.activation(x[:, :, :], x[:, :, :], ACT.Exp)
                    act.drain().then_inc(expd, 1)


def gat_nodes(m):
    nc, io = m.nc, m.io
    H, F = 4, 4
    ROW = H * F + 2 * H
    m.gat_src = m.dram("gat_src", [N, H * F + H])
    m.gat_dst = m.dram("gat_dst", [N, H])
    m.hg = m.sb("hg", [P, NT, ROW])
    with Stage(m):
        w = m.sb("gn_w", [128, K2, ROW])
        att = m.sb("gn_att", [128, 2, H * F])
        prod = m.sb("gn_prod", [128, 2, K2, H * F])
        loads, stored = Loads(m, "gn_loaded"), Loads(m, "gn_stored")
        w_ready, made, kept = m.sem("gn_w_ready"), m.sem("gn_made"), m.sem("gn_kept")
        with nc.Block() as block:
            @block.sync
            def _(sp):
                loads(sp, w[:, :, 0:H * F], io["L0_ffn_W_gat"].rearrange("(k p) d -> p k d", p=128))
                for i, name in enumerate(("L0_ffn_att_src", "L0_ffn_att_dst")):
                    loads(sp, att[:, i, :], io[name].rearrange("h c -> (h c)").partition_broadcast(128))
                sp.wait_ge(kept, NT + 4)
                stored(sp, m.gat_src.rearrange("(t p) c -> p t c", p=P), m.hg[:, :, 0:20])
                stored(sp, m.gat_dst.rearrange("(t p) c -> p t c", p=P), m.hg[:, :, 20:24])
                sp.wait_ge(stored.sem, stored.all)

            @block.vector
            def _(dve):
                dve.wait_ge(loads.sem, 48)
                for i in range(2):
                    for k in range(K2):
                        dve.tensor_tensor(prod[:, i, k, :], w[:, k, 0:16], att[:, i, :], ALU.mult)
                dve.drain()
                for i in range(2):
                    for k in range(K2):
                        dve.tensor_reduce(w[:, k, 16 + H * i:16 + H * (i + 1)],
                                          prod[:, i, k, :].rearrange("p (h c) -> p h c", h=H), AX.X, ALU.add)
                dve.drain().then_inc(w_ready, 1)

            @block.tensor
            def _(pe):
                pe.wait_ge(w_ready, 1)

                def body(t, j):
                    pe.wait_ge(kept, t + 1)
                    for k in range(K2):
                        last = pe.matmul(m.ps[j][:P, 0:ROW], m.XT[:, bass.ds(t * P + k * N, P)], w[:, k, :],
                                         start=k == 0, stop=k == K2 - 1)
                    last.then_inc(made, 1)
                tiles_written_out(NT, 4, body)

            @block.scalar
            def _(act):
                act.sem_inc(kept, 4)

                def body(t, j):
                    act.wait_ge(made, t + 1)
                    act.copy(m.hg[:, t, :], m.ps[j][:P, 0:ROW]).then_inc(kept, 1)
                tiles_written_out(NT, 4, body)


def gat_edges(m, ed, next_edges, next_lists):
    nc, io = m.nc, m.io
    H, F, cols = 4, 4, ed.cols
    HF, W = H * F, H * F + 2 * H
    nb = cols // BC
    m.agg0 = m.sb("agg0", [P, NT, HF])
    with Stage(m):
        last = m.sb("ge_last", [128, W])
        G = m.sb("ge_G", [128, cols, HF + H])
        idx = [m.sb(f"ge_idx{i}", [128, BC], I32) for i in range(2)]
        buf = [m.sb(f"ge_buf{i}", [128, BC, HF + H]) for i in range(2)]
        rows = [m.sem(f"ge_rows{i}") for i in range(2)]

        def gather_blocks(pool, lo, hi):
            assert lo % 2 == 0 and hi % 2 == 0

            def issue(t, j):
                pool.tensor_copy(idx[j][:, :], ed.other[:, at(t, BC)])
                pool.drain()
                for c in range(BC):
                    pool.indirect_dma_start(out=buf[j][:, c, :], out_offset=None, in_=m.gat_src,
                                            in_offset=bass.IndirectOffsetOnAxis(ap=idx[j][:, c:c + 1], axis=0)
                                            ).then_inc(rows[j], 16)

            def keep(t, j):
                pool.wait_ge(rows[j], (t - j) * (8 * BC) + 16 * BC)
                pool.tensor_copy(G[:, at(t, BC), :], buf[j][:, :, :])
                pool.drain()
            issue(lo, 0)
            with pool.Fori(0, (hi - lo) // 2 - 1) as i:
                issue(i * 2 + (lo + 1), 1)
                keep(i * 2 + lo, 0)
                issue(i * 2 + (lo + 2), 0)
                keep(i * 2 + (lo + 1), 1)
            issue(hi - 1, 1)
            keep(hi - 2, 0)
            keep(hi - 1, 1)

        share = {1: (0, 6), 3: (6, 20), 4: (20, cols // BC)}

        def beside(block, stage):
            @block.gpsimd
            def _(pool):
                gather_blocks(pool, *share[stage])
        sort_edges(m, next_edges, *next_lists, beside)
        spread = Spread(m, "ge", ed, H)
        own_e = m.sb("ge_own_e", [P, NT, H])
        den = m.sb("ge_den", [P, NT, H])
        dst_logits = m.sb("ge_dst_logits", [P, NT, H])
        result = m.dram("ge_result", [128 * cols, W])
        carry = m.dram("ge_carry", [128, W + 1])
        with nc.Block() as block:
            @block.vector
            def _(dve):
                dve.tensor_copy(dst_logits[:, :, :], m.hg[:, :, 20:24])
                dve.tensor_tensor(own_e[:, :, :], m.hg[:, :, 16:20], m.hg[:, :, 20:24], ALU.add)
                dve.drain()
                dve.scalar_tensor_tensor(own_e[:, :, :], own_e[:, :, :], 0.2, own_e[:, :, :], ALU.mult, ALU.max)
        spread_logits(m, "gs", ed, spread, m.gat_dst, dst_logits)
        with Stage(m):
            R = m.sb("ge_R", [128, cols, W])
            dec = m.sb("ge_dec", [128, cols, H])
            e_ready, e_exp, stored = m.sem("ge_e_ready"), m.sem("ge_e_exp"), m.sem("ge_stored")
            with nc.Block() as block:
                @block.vector
                def _(dve):
                    e = spread.ke
                    dve.tensor_tensor(e[:, :, :], G[:, :, HF:], e[:, :, :], ALU.add)
                    dve.drain()
                    dve.scalar_tensor_tensor(e[:, :, :], e[:, :, :], 0.2, e[:, :, :], ALU.mult, ALU.max)
                    dve.drain()
                    mx = R[:, :, HF + H:]
                    for h in range(H):
                        dve.tensor_tensor_scan(mx[:, :, h], spread.pen[:, :], e[:, :, h], -BIG, ALU.add, ALU.max)
                    dve.drain()
                    wide = spread.cont[:, :].unsqueeze(2).broadcast_to((128, cols, H))
                    dve.memset(dec[:, 0, :], 0.0)
                    dve.tensor_tensor(dec[:, 1:, :], mx[:, 0:cols - 1, :], mx[:, 1:, :], ALU.subtract)
                    dve.tensor_tensor(e[:, :, :], e[:, :, :], mx, ALU.subtract)
                    dve.drain()
                    dve.tensor_tensor(dec[:, :, :], dec[:, :, :], wide, ALU.mult)
                    dve.drain().then_inc(e_ready, 1)
                    dve.wait_ge(e_exp, 1)
                    dve.tensor_tensor(dec[:, :, :], dec[:, :, :], wide, ALU.mult)
                    for h in range(H):
                        f = G[:, :, h * F:(h + 1) * F]
                        dve.tensor_tensor(f, f, e[:, :, h].unsqueeze(2).broadcast_to((128, cols, F)), ALU.mult)
                    dve.drain()
                    for h in range(H):
                        for f in range(h * F, (h + 1) * F):
                            dve.tensor_tensor_scan(R[:, :, f], dec[:, :, h], G[:, :, f], 0.0, ALU.mult, ALU.add)
                        dve.tensor_tensor_scan(R[:, :, HF + h], dec[:, :, h], e[:, :, h], 0.0, ALU.mult, ALU.add)
                    dve.drain()
                    dve.tensor_copy(last[:, :], R[:, cols - 1, :])
                    dve.sem_inc(e_ready, 1)

                @block.scalar
                def _(act):
                    act.wait_ge(e_ready, 1)
                    act.activation(spread.ke[:, :, :], spread.ke[:, :, :], ACT.Exp)
                    act.activation(dec[:, :, :], dec[:, :, :], ACT.Exp)
                    act.drain().then_inc(e_exp, 1)

                @block.sync
                def _(sp):
                    sp.wait_ge(e_ready, 2)
                    sp.dma_start(result.rearrange("(p t) w -> p t w", p=128), R[:, :, :]).then_inc(stored, 16)
                    sp.wait_ge(stored, 16)
        carry_rows(m, "gc", ed, H, F, last, carry)
        merge_nodes(m, "gm", ed, spread, H, F, result, carry, m.agg0, den, own_e, m.hg)
        with nc.Block() as block:
            @block.vector
            def _(dve):
                dve.tensor_scalar(den[:, :, :], den[:, :, :], 1e-16, None, ALU.add)
                dve.drain()
                dve.reciprocal(den[:, :, :], den[:, :, :])
                dve.drain()
                for h in range(H):
                    f = m.agg0[:, :, h * F:(h + 1) * F]
                    dve.tensor_tensor(f, f, den[:, :, h].unsqueeze(2).broadcast_to((P, NT, F)), ALU.mult)


def top_two(dve, s, E, gt, eq, low, sel):
    def by_rank(op, out):
        for t in range(NT):
            dve.tensor_tensor(out[:, t], s[:, t, :].unsqueeze(1).broadcast_to((P, E, E)),
                              s[:, t, :].unsqueeze(2).broadcast_to((P, E, E)), op)
    by_rank(ALU.is_gt, gt)
    by_rank(ALU.is_equal, eq)
    dve.drain()
    for t in range(NT):
        dve.tensor_tensor(eq[:, t], eq[:, t], low, ALU.mult)
    dve.drain()
    dve.tensor_tensor(gt, gt, eq, ALU.add)
    dve.drain()
    dve.tensor_reduce(sel, gt, AX.X, ALU.add)
    dve.drain()
    dve.tensor_scalar(sel, sel, 1.5, None, ALU.is_lt)
    dve.drain()


def gates0(m):
    nc, io = m.nc, m.io
    H, E, C = 4, 4, 16
    m.gate0 = m.sb("gate0", [P, NT, E])
    with Stage(m):
        par = m.sb("gt_par", [P, 3, C])
        st = m.sb("gt_st", [P, NT, 6])
        mean, var, tmp = (m.sb("gt_" + x, [P, NT]) for x in ("mean", "var", "tmp"))
        s = m.sb("gt_s", [P, NT, E])
        gt = m.sb("gt_gt", [P, NT, E, E])
        eq = m.sb("gt_eq", [P, NT, E, E])
        low = m.sb("gt_low", [P, E, E])
        sel = m.sb("gt_sel", [P, NT, E])
        loads, low_ready, var_ready, std_ready, s_ready, s_exp = (
            Loads(m, "gt_loaded"), *(m.sem("gt_" + x) for x in ("low_ready", "var_ready", "std_ready", "s_ready", "s_exp")))
        with nc.Block() as block:
            @block.sync
            def _(sp):
                for i, name in enumerate(("L0_ffn_b_gat", "L0_ffn_ln_gamma", "L0_ffn_ln_beta")):
                    loads(sp, par[:, i, :], io[name].partition_broadcast(P))

            @block.gpsimd
            def _(pool):
                pool.memset(low[:, :, :], 1.0)
                pool.drain()
                pool.affine_select(out=low[:, :, :], in_=low[:, :, :], compare_op=ALU.is_gt, fill=0.0,
                                   base=0, pattern=[[1, E], [-1, E]], channel_multiplier=0)
                pool.drain().then_inc(low_ready, 1)

            @block.vector
            def _(dve):
                a = m.agg0
                all_nodes = lambda x: x.unsqueeze(1).broadcast_to((P, NT, C))
                by_node = lambda x: x.unsqueeze(2).broadcast_to((P, NT, C))
                dve.wait_ge(loads.sem, 48)
                dve.tensor_tensor(a[:, :, :], a[:, :, :], all_nodes(par[:, 0, :]), ALU.add)
                dve.drain()
                for t in range(NT):
                    dve.bn_stats(st[:, t, :], a[:, t, :])
                dve.drain()
                moments(dve, st, mean[:, :], var[:, :], tmp[:, :], C).then_inc(var_ready, 1)
                dve.wait_ge(std_ready, 1)
                dve.reciprocal(tmp[:, :], var[:, :])
                dve.tensor_tensor(a[:, :, :], a[:, :, :], by_node(mean[:, :]), ALU.subtract)
                dve.drain()
                dve.tensor_tensor(a[:, :, :], a[:, :, :], by_node(tmp[:, :]), ALU.mult)
                dve.drain()
                dve.tensor_tensor(a[:, :, :], a[:, :, :], all_nodes(par[:, 1, :]), ALU.mult)
                dve.drain()
                dve.tensor_tensor(a[:, :, :], a[:, :, :], all_nodes(par[:, 2, :]), ALU.add)
                dve.drain()
                dve.tensor_reduce(s[:, :, :], a[:, :, :].rearrange("p t (h e) -> p t e h", h=H), AX.X, ALU.add)
                dve.drain()
                dve.tensor_scalar(s[:, :, :], s[:, :, :], 1.0 / H, None, ALU.mult)
                dve.drain()
                dve.wait_ge(low_ready, 1)
                top_two(dve, s, E, gt[:, :, :, :], eq[:, :, :, :], low[:, :, :], sel[:, :, :])
                dve.tensor_reduce(tmp[:, :], s[:, :, :], AX.X, ALU.max)
                dve.drain()
                wide = tmp[:, :].unsqueeze(2).broadcast_to((P, NT, E))
                dve.tensor_tensor(s[:, :, :], s[:, :, :], wide, ALU.subtract).then_inc(s_ready, 1)
                dve.wait_ge(s_exp, 1)
                dve.tensor_tensor(s[:, :, :], s[:, :, :], sel[:, :, :], ALU.mult)
                dve.drain()
                dve.tensor_reduce(tmp[:, :], s[:, :, :], AX.X, ALU.add)
                dve.drain()
                dve.reciprocal(tmp[:, :], tmp[:, :])
                dve.drain()
                dve.tensor_tensor(m.gate0[:, :, :], s[:, :, :], wide, ALU.mult)

            @block.scalar
            def _(act):
                act.wait_ge(var_ready, 1)
                act.sqrt(var[:, :], var[:, :]).then_inc(std_ready, 1)
                act.wait_ge(s_ready, 1)
                act.activation(s[:, :, :], s[:, :, :], ACT.Exp).then_inc(s_exp, 1)


def experts(m, tag, parts, F, beside=None):
    nc = m.nc
    FC = F // 128
    with Stage(m):
        w1 = [m.sb(f"{tag}_w1_{i}", [128, K2, F]) for i in range(2)]
        w2 = [m.sb(f"{tag}_w2_{i}", [128, FC, D]) for i in range(2)]
        b1 = [m.sb(f"{tag}_b1_{i}", [128, FC]) for i in range(2)]
        b2 = [m.sb(f"{tag}_b2_{i}", [P, D]) for i in range(2)]
        hT = m.sb(tag + "_hT", [128, FC, CH])
        y = [m.sb(f"{tag}_y{i}", [P, D]) for i in range(2)]
        arrived = [m.sem(f"{tag}_arrived{i}") for i in range(2)]
        up, acted, down, added, read = (m.sem(f"{tag}_{x}") for x in ("up", "acted", "down", "added", "read"))
        with nc.Block() as block:
            if beside is not None:
                @block.gpsimd
                def _(pool):
                    beside(pool)

            @block.sync
            def _(sp):
                for e, (a, ab, b, bb, gate) in enumerate(parts):
                    i = e % 2
                    if e >= 2:
                        sp.wait_ge(added, (e - 1) * NT + 2)
                    sp.dma_start(w1[i][:, :, :], a.rearrange("(k p) f -> p k f", p=128)).then_inc(arrived[i], 16)
                    sp.dma_start(b1[i][:, :], ab).then_inc(arrived[i], 16)
                    sp.dma_start(w2[i][:, :, :], b.rearrange("(k p) d -> p k d", p=128)).then_inc(arrived[i], 16)
                    sp.dma_start(b2[i][:, :], bb.partition_broadcast(P)).then_inc(arrived[i], 16)

            @block.tensor
            def _(pe):
                for e in range(len(parts)):
                    i = e % 2
                    pe.wait_ge(arrived[i], 64 * (e // 2 + 1))

                    def body(c, nt):
                        for f in range(FC):
                            pe.wait_ge(acted, (e * (NCH + 1) + c) * FC + f + 1)
                            for k in range(K2):
                                last = pe.matmul(m.ps[f % 4][:, 0:nt * P], w1[i][:, k, f * 128:(f + 1) * 128],
                                                 m.XT[:, bass.ds(c * CH + k * N, nt * P)], start=k == 0, stop=k == K2 - 1)
                            last.then_inc(up, 1)
                        pe.wait_ge(acted, (e * (NCH + 1) + c) * FC + FC + 4)
                        for j in range(nt):
                            t = e * NT + c * 4 + j
                            pe.wait_ge(added, t + (2 if j == 0 else 1))
                            for f in range(FC):
                                last = pe.matmul(m.ps[4 + j % 2][:P, 0:D], hT[:, f, j * P:(j + 1) * P], w2[i][:, f, :],
                                                 start=f == 0, stop=f == FC - 1)
                            last.then_inc(down, 1)
                    chunks(pe, body)

            @block.scalar
            def _(act):
                act.sem_inc(acted, 4)
                for e in range(len(parts)):
                    i = e % 2

                    def body(c, nt):
                        act.wait_ge(read, e * NT + c * 4 + 1)
                        for f in range(FC):
                            act.wait_ge(up, (e * (NCH + 1) + c) * FC + f + 1)
                            act.activation(hT[:, f, 0:nt * P], m.ps[f % 4][:, 0:nt * P], ACT.Gelu,
                                           bias=b1[i][:, f:f + 1]).then_inc(acted, 1)
                    chunks(act, body)

            @block.vector
            def _(dve):
                dve.sem_inc(added, 2)
                dve.sem_inc(read, 1)
                for e, (a, ab, b, bb, gate) in enumerate(parts):
                    i = e % 2

                    def body(c, nt):
                        dve.drain()
                        for j in range(nt):
                            t = c * 4 + j
                            x = m.X[:, at(t, D)]
                            dve.wait_ge(down, e * NT + t + 1)
                            dve.tensor_tensor(y[j % 2][:, :], m.ps[4 + j % 2][:P, 0:D], b2[i][:, :], ALU.add
                                              ).then_inc(read, 1)
                            dve.drain()
                            if gate is None:
                                dve.tensor_tensor(x, y[j % 2][:, :], x, ALU.add).then_inc(added, 1)
                            else:
                                dve.scalar_tensor_tensor(x, y[j % 2][:, :], gate(t), x, ALU.mult, ALU.add).then_inc(added, 1)
                    chunks(dve, body)


FF = 1024
TS = 256


class Routes:

    def __init__(self, m, tag, E):
        self.tag, self.E = tag, E
        self.tiles = (2 * N + E * (TS - 1)) // TS
        self.slot = m.sb(tag + "_slot", [P, 2, NT], I32)
        self.gate = m.sb(tag + "_gate", [P, 2, NT])
        self.rows = m.sb(tag + "_rows", [128, self.tiles], I32)
        self.x = m.dram(tag + "_x", [self.tiles * TS, D])
        self.y = m.dram(tag + "_y", [self.tiles * TS, D])


def find_routes(m, r, sel, gate):
    nc, E, tag, TL = m.nc, r.E, r.tag, r.tiles
    TOP = float(1 << 15)
    with Stage(m):
        zero = m.sb(tag + "_zero", [128, 16 * D])
        count, before, pos, pick = (m.sb(tag + x, [128, NT, E]) for x in ("_count", "_before", "_pos", "_pick"))
        need, num, rest, end = (m.sb(tag + x, [128, E]) for x in ("_need", "_num", "_rest", "_end"))
        slot = m.sb(tag + "_slot_f", [P, 2, NT])
        line = m.sb(tag + "_line", [128, 1])
        row = m.sb(tag + "_row", [128, TL])
        zeroed, counted, lined, cleared = (m.sem(tag + x) for x in ("_zeroed", "_counted", "_lined", "_cleared"))
        with nc.Block() as block:
            @block.gpsimd
            def _(pool):
                pool.memset(zero[:, :], 0.0).then_inc(zeroed, 1)
                pool.iota(line[:, :], [[1, 1]], base=0, channel_multiplier=1,
                          allow_small_or_imprecise_dtypes=True).then_inc(lined, 1)

            @block.sync
            def _(sp):
                sp.wait_ge(zeroed, 1)
                x = r.x.rearrange("(p s) d -> p (s d)", p=128)
                wide, count = TL * TS // 128 * D, 0
                for lo in range(0, wide, 16 * D):
                    size = min(16 * D, wide - lo)
                    sp.dma_start(x[:, lo:lo + size], zero[:, 0:size]).then_inc(cleared, 16)
                    count += 16
                sp.wait_ge(cleared, count)

            @block.tensor
            def _(pe):
                s = sel.rearrange("p t e -> p (t e)")
                pe.matmul(m.ps[0][:, 0:NT * E], m.low[:P, :], s, start=True, stop=True)
                pe.matmul(m.ps[1][:, 0:NT * E], m.ones[:P, 0:128], s, start=True, stop=True).then_inc(counted, 1)

            @block.vector
            def _(dve):
                dve.wait_ge(counted, 1)
                dve.tensor_copy(count[:, :, :], m.ps[1][:, 0:NT * E].rearrange("p (t e) -> p t e", e=E))
                dve.drain()
                for e in range(E):
                    dve.tensor_tensor_scan(before[:, :, e], m.ones[:, 0:NT], count[:, :, e], 0.0, ALU.mult, ALU.add)
                dve.drain()
                dve.tensor_scalar(need[:, :], before[:, NT - 1, :], float(TS - 1), None, ALU.add)
                dve.drain()
                dve.tensor_tensor(before[:, :, :], before[:, :, :], count[:, :, :], ALU.subtract)
                dve.drain()
                floor_div(dve, num[:, :], rest[:, :], need[:, :], TS)
                dve.tensor_tensor_scan(end[:, :], m.ones[:, 0:E], num[:, :], 0.0, ALU.mult, ALU.add)
                dve.drain()
                dve.tensor_tensor(rest[:, :], end[:, :], num[:, :], ALU.subtract)
                dve.tensor_tensor(pos[:, :, :], before[:, :, :],
                                  m.ps[0][:, 0:NT * E].rearrange("p (t e) -> p t e", e=E), ALU.add)
                dve.drain()
                dve.tensor_scalar(rest[:, :], rest[:, :], float(TS), None, ALU.mult)
                dve.drain()
                dve.tensor_tensor(pos[:, :, :], pos[:, :, :], rest[:, :].unsqueeze(1).broadcast_to((128, NT, E)), ALU.add)
                dve.drain()
                p = pos[:P, :, :]
                dve.tensor_tensor(pick[:P, :, :], p, sel, ALU.mult)
                dve.tensor_scalar(before[:P, :, :], p, -1.0, TOP, ALU.mult, ALU.add)
                dve.drain()
                dve.tensor_tensor(before[:P, :, :], before[:P, :, :], sel, ALU.mult)
                dve.tensor_reduce(slot[:, 1, :], pick[:P, :, :], AX.X, ALU.max)
                dve.drain()
                dve.tensor_reduce(slot[:, 0, :], before[:P, :, :], AX.X, ALU.max)
                dve.drain()
                dve.tensor_scalar(slot[:, 0, :], slot[:, 0, :], -1.0, TOP, ALU.mult, ALU.add)
                dve.drain()
                dve.tensor_copy(r.slot[:, :, :], slot[:, :, :])
                for i in range(2):
                    dve.tensor_tensor(pick[:P, :, :], p, slot[:, i, :].unsqueeze(2).broadcast_to((P, NT, E)), ALU.is_equal)
                    dve.drain()
                    dve.tensor_tensor(pick[:P, :, :], pick[:P, :, :], gate, ALU.mult)
                    dve.drain()
                    dve.tensor_reduce(r.gate[:, i, :], pick[:P, :, :], AX.X, ALU.add)
                    dve.drain()
                dve.tensor_scalar(row[:, :], m.row16[:, 0:TL], end[:, 0:1], None, ALU.is_ge)
                dve.drain()
                for e in range(1, E - 1):
                    dve.scalar_tensor_tensor(row[:, :], m.row16[:, 0:TL], end[:, e:e + 1], row[:, :], ALU.is_ge, ALU.add)
                    dve.drain()
                dve.wait_ge(lined, 1)
                dve.tensor_scalar(row[:, :], row[:, :], 128.0, line[:, 0:1], ALU.mult, ALU.add)
                dve.drain()
                dve.tensor_copy(r.rows[:, :], row[:, :])


def scatter_nodes(m, r, pool, placed):
    for t in range(NT):
        for i in range(2):
            pool.indirect_dma_start(out=r.x, out_offset=bass.IndirectOffsetOnAxis(ap=r.slot[:, i, t:t + 1], axis=0),
                                    in_=m.XN[:, t * D:(t + 1) * D], in_offset=None,
                                    bounds_check=r.tiles * TS - 1, oob_is_err=False).then_inc(placed, 16)


def routed_experts(m, r, packed, F):
    nc, tag, TL = m.nc, r.tag, r.tiles
    FC, S = F // 128, TS // 128
    O2, OB1, OB2 = K2 * F, K2 * F + FC * D, K2 * F + FC * D + FC
    assert TL % 2 == 0
    with Stage(m):
        w = [m.sb(f"{tag}_w{i}", [128, OB2 + D]) for i in range(2)]
        w1 = [x[:, 0:O2].rearrange("p (k f) -> p k f", k=K2) for x in w]
        w2 = [x[:, O2:OB1].rearrange("p (f d) -> p f d", d=D) for x in w]
        xs = [m.sb(f"{tag}_xs{i}", [128, S, D]) for i in range(2)]
        xT = [m.sb(f"{tag}_xT{i}", [128, K2, TS]) for i in range(2)]
        hT = [m.sb(f"{tag}_hT{i}", [128, FC, TS]) for i in range(2)]
        y = [m.sb(f"{tag}_ys{i}", [128, S, D]) for i in range(2)]
        w_loaded, x_loaded, y_stored = ([m.sem(f"{tag}_{x}{i}") for i in range(2)]
                                        for x in ("w_loaded", "x_loaded", "y_stored"))
        turned, x_ready, up, acted, down, y_read, y_made = (
            m.sem(f"{tag}_{x}") for x in ("turned", "x_ready", "up", "acted", "down", "y_read", "y_made"))

        def all_tiles(eng, body):
            with eng.Fori(0, TL // 2 - 1) as i:
                for j in range(2):
                    body(i * 2 + j, j, True, True)
            body(TL - 2, 0, True, False)
            body(TL - 1, 1, False, False)

        with nc.Block() as block:
            @block.gpsimd
            def _(pool):
                for i in range(TL):
                    if i >= 2:
                        pool.wait_ge(y_made, i - 1)
                    pool.indirect_dma_start(out=w[i % 2][:, :], out_offset=None, in_=packed,
                                            in_offset=bass.IndirectOffsetOnAxis(ap=r.rows[:, i:i + 1], axis=0)
                                            ).then_inc(w_loaded[i % 2], 16)

            @block.sync
            def _(sp):
                slots = lambda table, i: table[at(i, TS), :].rearrange("(s p) d -> p s d", p=128)
                load = lambda i, j: sp.dma_start(xs[j][:, :, :], slots(r.x, i)).then_inc(x_loaded[j], 16)
                load(0, 0)
                load(1, 1)

                def body(i, j, follows, follow2):
                    if follow2:
                        sp.wait_ge(turned, i + 1)
                        load(i + 2, j)
                    sp.wait_ge(y_made, i + 1)
                    sp.dma_start(slots(r.y, i), y[j][:, :, :]).then_inc(y_stored[j], 16)
                all_tiles(sp, body)
                for j in range(2):
                    sp.wait_ge(y_stored[j], 16 + 8 * TL)

            @block.tensor
            def _(pe):
                def turn(i, j):
                    pe.wait_ge(x_loaded[j], (i - j) * 8 + 16)
                    for k in range(K2):
                        for s in range(S):
                            c = (k * S + s) * 128
                            last = pe.transpose(m.ps[6][:, c:c + 128], xs[j][:, s, k * 128:(k + 1) * 128], m.ident[:, :])
                    last.then_inc(turned, 1)
                turn(0, 0)

                def body(i, j, follows, follow2):
                    pe.wait_ge(w_loaded[j], (i - j) * 8 + 16)
                    pe.wait_ge(x_ready, i + 1)
                    for f in range(FC):
                        pe.wait_ge(acted, i * FC + f + 1)
                        for k in range(K2):
                            last = pe.matmul(m.ps[f % 4][:, 0:TS], w1[j][:, k, f * 128:(f + 1) * 128], xT[j][:, k, :],
                                             start=k == 0, stop=k == K2 - 1)
                        last.then_inc(up, 1)
                    if follows:
                        turn(i + 1, 1 - j)
                    pe.wait_ge(acted, i * FC + FC + 4)
                    for s in range(S):
                        pe.wait_ge(y_read, i * S + s + 1)
                        for f in range(FC):
                            last = pe.matmul(m.ps[4 + s][:, 0:D], hT[j][:, f, s * 128:(s + 1) * 128], w2[j][:, f, :],
                                             start=f == 0, stop=f == FC - 1)
                        last.then_inc(down, 1)
                all_tiles(pe, body)

            @block.scalar
            def _(act):
                act.sem_inc(acted, 4)

                def body(i, j, follows, follow2):
                    act.wait_ge(y_read, i * S + 1)
                    for f in range(FC):
                        act.wait_ge(up, i * FC + f + 1)
                        act.activation(hT[j][:, f, :], m.ps[f % 4][:, 0:TS], ACT.Gelu,
                                       bias=w[j][:, OB1 + f:OB1 + f + 1]).then_inc(acted, 1)
                all_tiles(act, body)

            @block.vector
            def _(dve):
                dve.sem_inc(y_read, S)
                for j in range(2):
                    dve.sem_inc(y_stored[j], 16)

                def take(i, j):
                    dve.wait_ge(turned, i + 1)
                    dve.tensor_copy(xT[j][:, :, :], m.ps[6][:, :].rearrange("p (k c) -> p k c", k=K2)).then_inc(x_ready, 1)
                take(0, 0)

                def body(i, j, follows, follow2):
                    if follows:
                        take(i + 1, 1 - j)
                    dve.wait_ge(y_stored[j], (i - j) * 8 + 16)
                    for s in range(S):
                        dve.wait_ge(down, i * S + s + 1)
                        last = dve.tensor_tensor(y[j][:, s, :], m.ps[4 + s][:, 0:D], w[j][:, OB2:OB2 + D], ALU.add)
                        last.then_inc(y_read, 1)
                    dve.drain().then_inc(y_made, 1)
                all_tiles(dve, body)

    with Stage(m):
        R = 5
        near = [m.sb(f"{tag}_near{j}", [P, 2, D]) for j in range(R)]
        rows = [m.sem(f"{tag}_rows{j}") for j in range(R)]
        free = m.sem(tag + "_free")
        with nc.Block() as block:
            @block.gpsimd
            def _(pool):
                for t in range(NT):
                    if t >= R:
                        pool.wait_ge(free, t - R + 1)
                    for i in range(2):
                        pool.indirect_dma_start(out=near[t % R][:, i, :], out_offset=None, in_=r.y,
                                                in_offset=bass.IndirectOffsetOnAxis(ap=r.slot[:, i, t:t + 1], axis=0)
                                                ).then_inc(rows[t % R], 16)

            @block.vector
            def _(dve):
                with dve.Fori(0, NT // R) as g:
                    for j in range(R):
                        x = m.X[:, bass.ds(g * (R * D) + j * D, D)]
                        dve.wait_ge(rows[j], g * 32 + 32)
                        for i in range(2):
                            last = dve.scalar_tensor_tensor(x, near[j][:, i, :],
                                                            r.gate[:, i, :][:, bass.ds(g * R + j, 1)], x, ALU.mult, ALU.add)
                            if i == 0:
                                dve.drain()
                        last.then_inc(free, 1)


def gnn1_nodes(m):
    nc, io = m.nc, m.io
    H, F = 2, 128
    ROW = D + 2 * H
    m.wh_dram = m.dram("wh_dram", [N, D + H])
    m.s_dram = m.dram("s_dram", [N, H])
    m.s_logits = m.sb("s_logits", [P, NT, H])
    with Stage(m):
        w = m.sb("h1_w", [128, K2, ROW])
        bias = m.sb("h1_bias", [128, ROW])
        att = m.sb("h1_att", [128, 2, D])
        prod = m.sb("h1_prod", [128, 2, K2 + 1, D])
        row = [m.sb(f"h1_row{i}", [P, ROW]) for i in range(4)]
        loads, stored = Loads(m, "h1_loaded"), [m.sem(f"h1_stored{i}") for i in range(4)]
        w_ready, made, kept = m.sem("h1_w_ready"), m.sem("h1_made"), m.sem("h1_kept")
        s_stored = m.sem("h1_s_stored")
        with nc.Block() as block:
            @block.sync
            def _(sp):
                loads(sp, w[:, :, 0:D], io["L1_gnn_W_w"].rearrange("(k p) d -> p k d", p=128))
                loads(sp, bias[:, 0:D], io["L1_gnn_W_b"].partition_broadcast(128))
                for i in range(2):
                    half = io["L1_gnn_a"][(1 - i) * F:(2 - i) * F].partition_broadcast(128)
                    for h in range(H):
                        loads(sp, att[:, i, h * F:(h + 1) * F], half)

                def body(t, j):
                    sp.wait_ge(kept, t + 5)
                    sp.dma_start(m.wh_dram[t * P:(t + 1) * P, :], row[j][:, 0:D + H]).then_inc(stored[j], 16)
                tiles_written_out(NT, 4, body)
                sp.dma_start(m.s_dram.rearrange("(t p) h -> p t h", p=P), m.s_logits[:, :, :]).then_inc(s_stored, 16)
                sp.wait_ge(s_stored, 16)
                for i in range(4):
                    sp.wait_ge(stored[i], 16 * len(range(i, NT, 4)))

            @block.vector
            def _(dve):
                dve.wait_ge(loads.sem, 96)
                for i in range(2):
                    for k in range(K2):
                        dve.tensor_tensor(prod[:, i, k, :], w[:, k, 0:D], att[:, i, :], ALU.mult)
                    dve.tensor_tensor(prod[:, i, K2, :], bias[:, 0:D], att[:, i, :], ALU.mult)
                dve.drain()
                for i in range(2):
                    lo = D + H * i
                    for k in range(K2):
                        dve.tensor_reduce(w[:, k, lo:lo + H], prod[:, i, k, :].rearrange("p (h c) -> p h c", h=H),
                                          AX.X, ALU.add)
                    dve.tensor_reduce(bias[:, lo:lo + H], prod[:, i, K2, :].rearrange("p (h c) -> p h c", h=H),
                                      AX.X, ALU.add)
                dve.drain().then_inc(w_ready, 1)
                dve.sem_inc(kept, 4)

                def body(t, j):
                    dve.wait_ge(made, t + 1)
                    if t >= 4:
                        dve.wait_ge(stored[j], 16 * (t // 4))
                    dve.tensor_tensor(row[j][:, :], m.ps[j][:P, 0:ROW], bias[:P, :], ALU.add)
                    dve.drain()
                    dve.tensor_copy(m.s_logits[:, t, :], row[j][:, D + H:])
                    dve.drain().then_inc(kept, 1)
                tiles_written_out(NT, 4, body)

            @block.tensor
            def _(pe):
                pe.wait_ge(w_ready, 1)

                def body(t, j):
                    pe.wait_ge(kept, t + 1)
                    for k in range(K2):
                        last = pe.matmul(m.ps[j][:P, 0:ROW], m.XT[:, bass.ds(t * P + k * N, P)], w[:, k, :],
                                         start=k == 0, stop=k == K2 - 1)
                    last.then_inc(made, 1)
                tiles_written_out(NT, 4, body)


def gnn1_edges_mix1(m, ed):
    nc, io = m.nc, m.io
    H, F, cols = 2, 128, ed.cols
    HF, W = D, D + 2 * H
    with Stage(m):
        spread = Spread(m, "he", ed, H)
        spread_logits(m, "hs", ed, spread, m.s_dram, m.s_logits)
        result = m.dram("he_result", [128 * cols, W])
        carry = m.dram("he_carry", [128, W + 1])
        last = m.sb("he_last", [128, W])
        with Stage(m):
            mix = Mix1(m)
            mix1_keys(m, mix)
            sums_and_mix1(m, mix, ed, spread, result, last)
        carry_rows(m, "hc", ed, H, F, last, carry)
        agg = m.sb("he_agg", [P, NT, HF])
        den = m.sb("he_den", [P, NT, H])
        merge_nodes(m, "hm", ed, spread, H, F, result, carry, agg, den)
        own = m.sb("he_own", [P, NT, HF])
        none = m.sb("he_none", [P, NT])
        own_loaded = m.sem("he_own_loaded")
        with nc.Block() as block:
            @block.sync
            def _(sp):
                sp.dma_start(own[:, :, :], m.wh_dram.rearrange("(t p) c -> p t c", p=P)[:, :, 0:HF]).then_inc(own_loaded, 16)

            @block.vector
            def _(dve):
                has = spread.has
                dve.tensor_scalar(none[:, :], has[:, :], -1.0, 1.0, ALU.mult, ALU.add)
                dve.drain()
                dve.tensor_tensor(den[:, :, :], den[:, :, :], none[:, :].unsqueeze(2).broadcast_to((P, NT, H)), ALU.add)
                dve.drain()
                dve.reciprocal(den[:, :, :], den[:, :, :])
                dve.drain()
                for t in range(NT):
                    for h in range(H):
                        lo = t * D + h * F
                        x = m.X[:, lo:lo + F]
                        dve.scalar_tensor_tensor(x, agg[:, t, h * F:(h + 1) * F], den[:, t, h:h + 1], x, ALU.mult, ALU.add)
                dve.wait_ge(own_loaded, 16)
                dve.drain()
                for t in range(NT):
                    x = m.X[:, t * D:(t + 1) * D]
                    dve.scalar_tensor_tensor(x, own[:, t, :], none[:, t:t + 1], x, ALU.mult, ALU.add)


class Mix1:

    def __init__(self, m):
        self.wq, self.wo = (m.sb("m1_w" + x, [128, K2, D]) for x in "qo")
        self.w1 = m.sb("m1_w1", [128, K2, FF])
        self.w2 = m.sb("m1_w2", [128, FF // 128, D])
        self.bq = m.sb("m1_bq", [128, K2])
        self.b1 = m.sb("m1_b1", [128, FF // 128])
        self.rowb = m.sb("m1_rows", [P, 6, D])
        self.kv = m.sb("m1_kv", [128, K2, 128])
        self.ks = m.sb("m1_ks", [128, K2, 128])


def mix1_keys(m, x):
    nc, io = m.nc, m.io
    HD = 32
    with Stage(m):
        wk, wv = (m.sb("m1_w" + x, [128, K2, D]) for x in "kv")
        bkv = m.sb("m1_bkv", [P, 2, D])
        k_raw = [m.sb(f"m1_kraw{i}", [P, D]) for i in range(2)]
        k_low = [m.sb(f"m1_klow{i}", [P, D]) for i in range(2)]
        kp = [m.sb(f"m1_kp{i}", [P, D]) for i in range(2)]
        v1 = [m.sb(f"m1_v1{i}", [P, K2, 129]) for i in range(2)]
        bmask = m.sb("m1_bmask", [128, 128])
        loads = Loads(m, "m1_loaded")
        made, kv_in, kv_used, kv_done, kx, kexp, mask_ready = (
            m.sem("m1_" + x) for x in ("made", "kv_in", "kv_used", "kv_done", "kx", "kexp", "mask_ready"))
        with nc.Block() as block:
            @block.sync
            def _(sp):
                for t, name in ((wk, "Wk"), (wv, "Wv")):
                    loads(sp, t[:, :, :], io["L1_mix_" + name].rearrange("(k p) d -> p k d", p=128))
                for i, name in enumerate(("bk", "bv")):
                    loads(sp, bkv[:, i, :], io["L1_mix_" + name].partition_broadcast(P))
                for i, name in enumerate(("bo", "b2", "ln1_g", "ln1_b", "ln2_g", "ln2_b")):
                    loads(sp, x.rowb[:, i, :], io["L1_mix_" + name].partition_broadcast(P))
                for t, name in ((x.wq, "Wq"), (x.wo, "Wo"), (x.w1, "W1"), (x.w2, "W2")):
                    loads(sp, t[:, :, :], io["L1_mix_" + name].rearrange("(k p) d -> p k d", p=128))
                loads(sp, x.bq[:, :], io["L1_mix_bq_cols"])
                loads(sp, x.b1[:, :], io["L1_mix_b1_cols"])

            @block.gpsimd
            def _(pool):
                pool.memset(bmask[:, :], 1.0)
                pool.drain()
                blocks = bmask[:, :].rearrange("p (h c) -> p h c", c=HD)
                pool.affine_select(out=blocks, in_=blocks, compare_op=ALU.is_ge, fill=0.0, base=0,
                                   pattern=[[-HD, 4], [0, HD]], channel_multiplier=1)
                pool.drain()
                pool.affine_select(out=blocks, in_=blocks, compare_op=ALU.is_ge, fill=0.0, base=HD - 1,
                                   pattern=[[HD, 4], [0, HD]], channel_multiplier=-1)
                pool.drain().then_inc(mask_ready, 1)

            @block.tensor
            def _(pe):
                pe.wait_ge(loads.sem, 16 * 16)
                for k in range(K2):
                    pe.matmul(m.ps[4 + k][:, 0:129], m.zero16[:, 0:128], m.zero16[:, 0:129], start=True, stop=False)

                def keys(t):
                    pe.wait_ge(kx, t + 1)
                    for half, w in ((0, wk), (1, wv)):
                        for k in range(K2):
                            last = pe.matmul(m.ps[t % 2][:P, half * D:(half + 1) * D], m.XT[:, bass.ds(t * P + k * N, P)],
                                          w[:, k, :], start=k == 0, stop=k == K2 - 1)
                    last.then_inc(made, 1)

                def outer(t):
                    j = t % 2
                    pe.wait_ge(kv_in, t + 1)
                    for k in range(K2):
                        last = pe.matmul(m.ps[4 + k][:, 0:129], kp[j][:, k * 128:(k + 1) * 128], v1[j][:, k, :],
                                      start=False, stop=t == NT - 1)
                    last.then_inc(kv_used, 1)
                keys(0)
                for t in range(NT):
                    if t + 1 < NT:
                        keys(t + 1)
                    outer(t)

            @block.vector
            def _(dve):
                dve.wait_ge(loads.sem, 16 * 16)
                for j in range(2):
                    dve.memset(v1[j][:, :, 128:129], 1.0)
                dve.sem_inc(kv_used, 2)
                dve.sem_inc(kx, 2)

                def body(t, j):
                    dve.wait_ge(made, t + 1)
                    dve.wait_ge(kv_used, t + 1)
                    dve.tensor_tensor(k_raw[j][:, :], m.ps[j][:P, 0:D], bkv[:, 0, :], ALU.add)
                    dve.tensor_tensor(v1[j][:, :, 0:128], m.ps[j][:P, D:2 * D].rearrange("p (k c) -> p k c", k=K2),
                                      bkv[:, 1, :].rearrange("p (k c) -> p k c", k=K2), ALU.add)
                    dve.drain().then_inc(kx, 1)
                    dve.tensor_scalar(k_low[j][:, :], k_raw[j][:, :], 0.0, None, ALU.min)
                    dve.drain().then_inc(kexp, 1)
                    dve.wait_ge(kexp, 2 * t + 2)
                    dve.scalar_tensor_tensor(kp[j][:, :], k_raw[j][:, :], 0.0, k_low[j][:, :], ALU.max, ALU.add)
                    dve.drain().then_inc(kv_in, 1)
                tiles(dve, NT, 2, body)
                dve.wait_ge(kv_used, NT + 2)
                dve.wait_ge(mask_ready, 1)
                for k in range(K2):
                    dve.tensor_tensor(x.kv[:, k, :], m.ps[4 + k][:, 0:128], bmask[:, :], ALU.mult)
                    dve.tensor_scalar(x.ks[:, k, :], bmask[:, :], m.ps[4 + k][:, 128:129], None, ALU.mult)

            @block.scalar
            def _(act):
                def body(t, j):
                    act.wait_ge(kexp, 2 * t + 1)
                    act.activation(k_low[j][:, :], k_low[j][:, :], ACT.Exp).then_inc(kexp, 1)
                tiles(act, NT, 2, body)


def sums_and_mix1(m, x, ed, spread, result, last):
    nc = m.nc
    H, F, cols = 2, 128, ed.cols
    HF, W = D, D + 2 * H
    FC = FF // 128
    nb = cols // BC
    R = 4
    assert nb == NCH * R + 1
    with Stage(m):
        idx = [m.sb(f"he_idx{i}", [128, BC], I32) for i in range(R)]
        buf = [m.sb(f"he_buf{i}", [128, BC, W]) for i in range(R)]
        e = [m.sb(f"he_e{i}", [128, BC, H]) for i in range(R)]
        dec = [m.sb(f"he_dec{i}", [128, BC, H]) for i in range(R)]
        con_b = [m.sb(f"he_con_b{i}", [128, BC]) for i in range(R)]
        pen_b = m.sb("he_pen_b", [128, BC])
        top = m.sb("he_top", [128, H])
        hT = m.sb("m1_hT", [128, FC, CH])
        qr, ql = hT[:, 0:K2, :], hT[:, K2:2 * K2, :]
        oT = hT[:, 2 * K2:3 * K2, :]
        xt = m.XT[:, :].rearrange("p (k n) -> p k n", k=K2)
        yT = lambda c, w: xt[:, :, bass.ds(c * CH, w)]
        y = m.sb("m1_y", [P, 4, D])
        st = m.sb("m1_st", [P, 2, 4, 6])
        mv = m.sb("m1_mv", [P, 2, 4, 2])
        rs = m.sb("m1_rs", [P, 2, 4])
        rows, stored = ([m.sem(f"he_{k}{i}") for i in range(R)] for k in ("rows", "stored"))
        e_ready, e_exp, weighted, summed = (m.sem("he_" + k) for k in ("e_ready", "e_exp", "weighted", "summed"))
        names = ("q_made", "q_low", "q_exp", "q_phi", "o_made", "o_ready", "o_made2", "var1", "std1",
                 "y_ready", "y_turned", "y_moved", "up", "acted", "f_made", "var2", "std2")
        S = {k: m.sem("m2_" + k) for k in names}
        with nc.Block() as block:
            @block.gpsimd
            def _(pool):
                for j in range(R):
                    pool.sem_inc(stored[j], 16)

                def body(t, j):
                    pool.wait_ge(stored[j], (t - j) * (16 // R) + 16)
                    pool.tensor_copy(idx[j][:, :], ed.other[:, at(t, BC)])
                    pool.drain()
                    for c in range(BC):
                        pool.indirect_dma_start(out=buf[j][:, c, 0:HF + H], out_offset=None, in_=m.wh_dram,
                                                in_offset=bass.IndirectOffsetOnAxis(ap=idx[j][:, c:c + 1], axis=0)
                                                ).then_inc(rows[j], 16)
                tiles(pool, nb, R, body)

            @block.sync
            def _(sp):
                def body(t, j):
                    sp.wait_ge(summed, t + 1)
                    sp.sem_inc(m.spare, 1)
                    sp.dma_start(result.rearrange("(p t) w -> p t w", p=128)[:, at(t, BC), :], buf[j][:, :, :]
                                 ).then_inc(stored[j], 16)
                tiles(sp, nb, R, body)
                for j in range(R):
                    sp.wait_ge(stored[j], 16 + 16 * len(range(j, nb, R)))

            @block.tensor
            def _(pe):
                def body(c, nt):
                    w = nt * P
                    for o in range(K2):
                        for k in range(K2):
                            last = pe.matmul(m.ps[o][:, 0:w], x.wq[:, k, o * 128:(o + 1) * 128],
                                          m.XT[:, bass.ds(c * CH + k * N, w)], start=k == 0, stop=k == K2 - 1)
                    last.then_inc(S["q_made"], 1)
                    pe.wait_ge(S["q_phi"], c + 1)
                    for o in range(K2):
                        pe.matmul(m.ps[2 + o][:, 0:w], x.kv[:, o, :], qr[:, o, 0:w], start=True, stop=True)
                        last = pe.matmul(m.ps[o][:, 0:w], x.ks[:, o, :], qr[:, o, 0:w], start=True, stop=True)
                    last.then_inc(S["o_made"], 1)
                    pe.wait_ge(S["o_ready"], c + 1)
                    for j in range(nt):
                        for k in range(K2):
                            last = pe.matmul(m.ps[4 + j][:P, 0:D], oT[:, k, j * P:(j + 1) * P], x.wo[:, k, :],
                                          start=k == 0, stop=k == K2 - 1)
                    last.then_inc(S["o_made2"], 1)
                    pe.wait_ge(S["y_ready"], c + 1)
                    for k in range(K2):
                        for j in range(nt):
                            last = pe.transpose(m.ps[k][:, j * P:(j + 1) * P], y[:, j, k * 128:(k + 1) * 128], m.ident[:P, :P])
                    last.then_inc(S["y_turned"], 1)
                    pe.wait_ge(S["y_moved"], c + 1)
                    for f in range(FC):
                        pe.wait_ge(S["acted"], c * FC + f + 1)
                        for k in range(K2):
                            last = pe.matmul(m.ps[f % 4][:, 0:w], x.w1[:, k, f * 128:(f + 1) * 128], yT(c, w)[:, k, :],
                                          start=k == 0, stop=k == K2 - 1)
                        last.then_inc(S["up"], 1)
                    pe.wait_ge(S["acted"], c * FC + FC + 4)
                    for j in range(nt):
                        for f in range(FC):
                            last = pe.matmul(m.ps[4 + j][:P, 0:D], hT[:, f, j * P:(j + 1) * P], x.w2[:, f, :],
                                          start=f == 0, stop=f == FC - 1)
                        last.then_inc(S["f_made"], 1)
                chunks(pe, body)

            @block.scalar
            def _(act):
                act.sem_inc(S["acted"], 4)

                def weights(t, j):
                    act.wait_ge(e_ready, t + 1)
                    act.activation(e[j][:, :, :], e[j][:, :, :], ACT.Exp)
                    act.activation(dec[j][:, :, :], dec[j][:, :, :], ACT.Exp)
                    act.drain().then_inc(e_exp, 1)

                def weigh(j, columns):
                    for c in columns:
                        for h in range(H):
                            f = buf[j][:, c, h * F:(h + 1) * F]
                            done = act.activation(f, f, ACT.Copy, scale=e[j][:, c, h:h + 1])
                        done.then_inc(weighted, 1)

                def hidden(c, w, fs):
                    for f in fs:
                        act.wait_ge(S["up"], c * FC + f + 1)
                        act.activation(hT[:, f, 0:w], m.ps[f % 4][:, 0:w], ACT.Relu, bias=x.b1[:, f:f + 1]
                                       ).then_inc(S["acted"], 1)

                def body(c, nt):
                    w, more = nt * P, nt == 4
                    act.wait_ge(S["q_low"], c + 1)
                    act.activation(ql[:, :, 0:w], ql[:, :, 0:w], ACT.Exp).then_inc(S["q_exp"], 1)
                    if more:
                        weights(c * R + 1, 1)
                        weigh(1, range(BC))
                    act.wait_ge(S["var1"], c + 1)
                    act.sqrt(rs[:, 0, 0:nt], rs[:, 0, 0:nt]).then_inc(S["std1"], 1)
                    if more:
                        weights(c * R + 2, 2)
                        weigh(2, range(BC))
                    act.wait_ge(S["y_turned"], c + 1)
                    for k in range(K2):
                        act.copy(yT(c, w)[:, k, :], m.ps[k][:, 0:w])
                    act.drain().then_inc(S["y_moved"], 1)
                    if more:
                        hidden(c, w, range(0, 2))
                        weights(c * R + 3, 3)
                        for i in range(4):
                            weigh(3, range(4 * i, 4 * i + 4))
                            if i < 3:
                                hidden(c, w, range(2 * i + 2, 2 * i + 4))
                        weights(c * R + R, 0)
                        weigh(0, range(BC))
                    else:
                        hidden(c, w, range(FC))
                    act.wait_ge(S["var2"], c + 1)
                    act.sqrt(rs[:, 1, 0:nt], rs[:, 1, 0:nt]).then_inc(S["std2"], 1)
                weights(0, 0)
                weigh(0, range(BC))
                chunks(act, body)

            @block.vector
            def _(dve):
                dve.memset(last[:, 0:HF + H], 0.0)
                dve.memset(top[:, :], -BIG)
                dve.drain()

                def logits(t, j):
                    v = buf[j]
                    dve.wait_ge(rows[j], (t - j) * (16 * BC // R) + 16 * BC)
                    dve.tensor_tensor(e[j][:, :, :], v[:, :, HF:HF + H], spread.ke[:, at(t, BC), :], ALU.add)
                    dve.tensor_scalar(pen_b[:, :], spread.pen[:, at(t, BC)], 0.0, None, ALU.add)
                    dve.tensor_scalar(con_b[j][:, :], spread.cont[:, at(t, BC)], 0.0, None, ALU.add)
                    dve.drain()
                    dve.scalar_tensor_tensor(e[j][:, :, :], e[j][:, :, :], 0.2, e[j][:, :, :], ALU.mult, ALU.max)
                    dve.drain()
                    mx = v[:, :, HF + H:]
                    for h in range(H):
                        dve.tensor_tensor_scan(mx[:, :, h], pen_b[:, :], e[j][:, :, h], top[:, h:h + 1], ALU.add, ALU.max)
                    dve.drain()
                    wide = con_b[j][:, :].unsqueeze(2).broadcast_to((128, BC, H))
                    dve.tensor_tensor(dec[j][:, 0, :], top[:, :], mx[:, 0, :], ALU.subtract)
                    dve.tensor_tensor(dec[j][:, 1:, :], mx[:, 0:BC - 1, :], mx[:, 1:, :], ALU.subtract)
                    dve.tensor_tensor(e[j][:, :, :], e[j][:, :, :], mx, ALU.subtract)
                    dve.drain()
                    dve.tensor_copy(top[:, :], mx[:, BC - 1, :])
                    dve.tensor_tensor(dec[j][:, :, :], dec[j][:, :, :], wide, ALU.mult)
                    dve.drain().then_inc(e_ready, 1)

                def sums(t, j):
                    v = buf[j]
                    wide = con_b[j][:, :].unsqueeze(2).broadcast_to((128, BC, H))
                    dve.wait_ge(e_exp, t + 1)
                    dve.tensor_tensor(dec[j][:, :, :], dec[j][:, :, :], wide, ALU.mult)
                    dve.drain()
                    for h in range(H):
                        dve.tensor_tensor_scan(v[:, :, HF + h], dec[j][:, :, h], e[j][:, :, h],
                                               last[:, HF + h:HF + h + 1], ALU.mult, ALU.add)
                    for c in range(BC):
                        dve.wait_ge(weighted, t * BC + c + 1)
                        prev = last if c == 0 else v[:, c - 1, :]
                        for h in range(H):
                            f = slice(h * F, (h + 1) * F)
                            dve.scalar_tensor_tensor(v[:, c, f], prev[:, f], dec[j][:, c, h:h + 1], v[:, c, f],
                                                     ALU.mult, ALU.add)
                        dve.drain()
                    dve.tensor_copy(last[:, 0:HF + H], v[:, BC - 1, 0:HF + H])
                    dve.drain().then_inc(summed, 1)

                def normal_sums(nt, i):
                    dve.drain()
                    for j in range(nt):
                        dve.bn_stats(st[:, i, j, :], y[:, j, :])
                    dve.drain()
                    for j in range(nt):
                        dve.bn_aggr(mv[:, i, j, :], st[:, i, j, :])
                    dve.drain()
                    dve.tensor_scalar(rs[:, i, 0:nt], mv[:, i, 0:nt, 1], 1e-5, None, ALU.add)
                    dve.drain().then_inc(S[f"var{i + 1}"], 1)

                def normalize(c, nt, i):
                    dve.wait_ge(S[f"std{i + 1}"], c + 1)
                    dve.reciprocal(rs[:, i, 0:nt], rs[:, i, 0:nt])
                    dve.drain()
                    for j in range(nt):
                        dve.tensor_scalar(y[:, j, :], y[:, j, :], mv[:, i, j, 0:1], rs[:, i, j:j + 1],
                                          ALU.subtract, ALU.mult)
                    for b, op in ((2 + 2 * i, ALU.mult), (3 + 2 * i, ALU.add)):
                        dve.drain()
                        dve.tensor_tensor(y[:, 0:nt, :], y[:, 0:nt, :],
                                          x.rowb[:, b, :].unsqueeze(1).broadcast_to((P, nt, D)), op)
                    dve.drain()

                def queries(c, w):
                    dve.wait_ge(S["q_made"], c + 1)
                    for o in range(K2):
                        dve.tensor_scalar(ql[:, o, 0:w], m.ps[o][:, 0:w], x.bq[:, o:o + 1], 0.0, ALU.add, ALU.min)
                        dve.tensor_scalar(qr[:, o, 0:w], m.ps[o][:, 0:w], x.bq[:, o:o + 1], 0.0, ALU.add, ALU.max)
                    dve.drain().then_inc(S["q_low"], 1)
                    dve.wait_ge(S["q_exp"], c + 1)
                    dve.tensor_tensor(qr[:, :, 0:w], qr[:, :, 0:w], ql[:, :, 0:w], ALU.add)
                    dve.drain().then_inc(S["q_phi"], 1)

                def attention(c, w):
                    dve.wait_ge(S["o_made"], c + 1)
                    for o in range(K2):
                        dve.tensor_scalar(ql[:, o, 0:w], m.ps[o][:, 0:w], 1e-6, None, ALU.add)
                    dve.drain()
                    dve.reciprocal(ql[:, :, 0:w], ql[:, :, 0:w])
                    dve.drain()
                    for o in range(K2):
                        dve.tensor_tensor(oT[:, o, 0:w], m.ps[2 + o][:, 0:w], ql[:, o, 0:w], ALU.mult)
                    dve.drain().then_inc(S["o_ready"], 1)

                def after_attention(c, nt):
                    dve.wait_ge(S["o_made2"], c + 1)
                    for j in range(nt):
                        dve.tensor_tensor(y[:, j, :], m.ps[4 + j][:P, 0:D], x.rowb[:, 0, :], ALU.add)
                    dve.drain()
                    for j in range(nt):
                        dve.tensor_tensor(y[:, j, :], y[:, j, :], m.XN[:, bass.ds(c * (4 * D) + j * D, D)], ALU.add)
                    normal_sums(nt, 0)
                    normalize(c, nt, 0)
                    dve.sem_inc(S["y_ready"], 1)

                def after_feed_forward(c, nt):
                    for j in range(nt):
                        dve.wait_ge(S["f_made"], c * 4 + j + 1)
                        if j == 0:
                            dve.wait_ge(S["y_moved"], c + 1)
                        dve.tensor_tensor(y[:, j, :], y[:, j, :], m.ps[4 + j][:P, 0:D], ALU.add)
                    dve.drain()
                    dve.tensor_tensor(y[:, 0:nt, :], y[:, 0:nt, :],
                                      x.rowb[:, 1, :].unsqueeze(1).broadcast_to((P, nt, D)), ALU.add)
                    normal_sums(nt, 1)
                    normalize(c, nt, 1)
                    for j in range(nt):
                        xx = m.X[:, bass.ds(c * (4 * D) + j * D, D)]
                        dve.tensor_tensor(xx, y[:, j, :], xx, ALU.add)
                    dve.drain()

                def body(c, nt):
                    w, more = nt * P, nt == 4
                    queries(c, w)
                    if more:
                        logits(c * R + 1, 1)
                    sums(c * R, 0)
                    attention(c, w)
                    if more:
                        logits(c * R + 2, 2)
                    after_attention(c, nt)
                    if more:
                        sums(c * R + 1, 1)
                        logits(c * R + 3, 3)
                        sums(c * R + 2, 2)
                        logits(c * R + R, 0)
                        sums(c * R + 3, 3)
                    after_feed_forward(c, nt)
                logits(0, 0)
                chunks(dve, body)
                dve.tensor_copy(last[:, HF + H:], top[:, :])


def gates1(m):
    nc, io = m.nc, m.io
    E = 8
    with Stage(m):
        wr = m.sb("r1_wr", [128, K2, E])
        s = m.sb("r1_s", [P, NT, E])
        tmp = m.sb("r1_tmp", [P, NT])
        gt = m.sb("r1_gt", [P, NT, E, E])
        eq = m.sb("r1_eq", [P, NT, E, E])
        low = m.sb("r1_low", [P, E, E])
        sel = m.sel1
        loads = Loads(m, "r1_loaded")
        low_ready, made, s_ready, s_exp = (m.sem("r1_" + x) for x in ("low_ready", "made", "s_ready", "s_exp"))
        with nc.Block() as block:
            @block.sync
            def _(sp):
                loads(sp, wr[:, :, :], io["L1_ffn_Wr"].rearrange("(k p) e -> p k e", p=128))

            @block.gpsimd
            def _(pool):
                pool.memset(low[:, :, :], 1.0)
                pool.drain()
                pool.affine_select(out=low[:, :, :], in_=low[:, :, :], compare_op=ALU.is_gt, fill=0.0,
                                   base=0, pattern=[[1, E], [-1, E]], channel_multiplier=0)
                pool.drain().then_inc(low_ready, 1)

            @block.tensor
            def _(pe):
                pe.wait_ge(loads.sem, 16)

                def body(t, j):
                    for k in range(K2):
                        x = pe.matmul(m.ps[0][:P, t * E:(t + 1) * E], m.XT[:, bass.ds(t * P + k * N, P)], wr[:, k, :],
                                      start=k == 0, stop=k == K2 - 1)
                    x.then_inc(made, 1)
                tiles_written_out(NT, 1, body)

            @block.vector
            def _(dve):
                wide = tmp[:, :].unsqueeze(2).broadcast_to((P, NT, E))
                dve.wait_ge(made, NT)
                dve.tensor_copy(s[:, :, :], m.ps[0][:P, 0:NT * E].rearrange("p (t e) -> p t e", e=E))
                dve.drain()
                dve.tensor_reduce(tmp[:, :], s[:, :, :], AX.X, ALU.max)
                dve.drain()
                dve.tensor_tensor(s[:, :, :], s[:, :, :], wide, ALU.subtract)
                dve.drain().then_inc(s_ready, 1)
                dve.wait_ge(s_exp, 1)
                dve.tensor_reduce(tmp[:, :], s[:, :, :], AX.X, ALU.add)
                dve.drain()
                dve.reciprocal(tmp[:, :], tmp[:, :])
                dve.drain()
                dve.tensor_tensor(s[:, :, :], s[:, :, :], wide, ALU.mult)
                dve.drain()
                dve.wait_ge(low_ready, 1)
                top_two(dve, s, E, gt[:, :, :, :], eq[:, :, :, :], low[:, :, :], sel[:, :, :])
                dve.tensor_tensor(s[:, :, :], s[:, :, :], sel[:, :, :], ALU.mult)
                dve.drain()
                dve.tensor_reduce(tmp[:, :], s[:, :, :], AX.X, ALU.add)
                dve.drain()
                dve.reciprocal(tmp[:, :], tmp[:, :])
                dve.drain()
                dve.tensor_tensor(m.gate1[:, :, :], s[:, :, :], wide, ALU.mult)

            @block.scalar
            def _(act):
                act.wait_ge(s_ready, 1)
                act.activation(s[:, :, :], s[:, :, :], ACT.Exp).then_inc(s_exp, 1)


def store(m):
    out_stored = m.sem("out_stored")
    with m.nc.Block() as block:
        @block.sync
        def _(sp):
            sp.dma_start(m.io["out"].rearrange("(t p) d -> p t d", p=P),
                         m.X[:, :].rearrange("p (t d) -> p t d", d=D)).then_inc(out_stored, 16)
            sp.wait_ge(out_stored, 16)


def program(nc, io, stop=99):
    m = Net(nc, io)
    with m.keep:
        constants(m)
        sort_constants(m)
        m.scratch = m.sb("XN", [128, NT * D])
        m.XN = m.scratch[:P, :]
        ed1 = Edges(m, "s1", COLS1)
        m.XT = m.sb("XT", [128, K2 * N])
        with Stage(m):
            if stop >= 3:
                ed0 = Edges(m, "s0", COLS0)
                sort_edges(m, ed0, io["key0"], io["other0"])
            layer_norm(m, "ln0")
            if stop >= 1:
                gnn0_nodes(m)
            if stop >= 2:
                mix0_log(m)
                with Stage(m):
                    m.QT = m.sb("QT", [128, OC * N])
                    with Stage(m):
                        mix0_qkv(m, Gnn0Edges(m))
                    mix0_attention(m)
            if stop >= 3:
                layer_norm(m, "ln1")
                gat_nodes(m)
                gat_edges(m, ed0, ed1, (io["key1"], io["other1"]))
                gates0(m)
                experts(m, "x0", [(io["L0_ffn_W1"][e], io["L0_ffn_b1_cols"][e], io["L0_ffn_W2"][e], io["L0_ffn_b2"][e],
                                   lambda t, e=e: m.gate0[:, :, e][:, at(t, 1)]) for e in range(4)], 512)
        if stop >= 4:
            layer_norm(m, "ln2")
            with Stage(m):
                gnn1_nodes(m)
                gnn1_edges_mix1(m, ed1)
        if stop >= 5:
            layer_norm(m, "ln3")
            with Stage(m):
                m.gate1 = m.sb("gate1", [P, NT, 8])
                m.sel1 = m.sb("sel1", [P, NT, 8])
                routes = Routes(m, "x1", 8)
                gates1(m)
                find_routes(m, routes, m.sel1[:, :, :], m.gate1[:, :, :])
                placed = Loads(m, "x1_placed")
                placed.all = 16 * 2 * NT

                def beside(pool):
                    scatter_nodes(m, routes, pool, placed.sem)
                    pool.wait_ge(placed.sem, placed.all)
                experts(m, "xs", [(io["L1_ffn_W1s"], io["L1_ffn_b1s_cols"], io["L1_ffn_W2s"], io["L1_ffn_b2s"], None)],
                        1024, beside)
                routed_experts(m, routes, io["L1_ffn_packed"], 1024)
        store(m)


def columns(v, cols, pad):
    out = np.full(cols * 128, pad, v.dtype)
    out[:v.size] = v
    return np.ascontiguousarray(out.reshape(cols, 128).T)


def pack_experts(W1, b1, W2, b2):
    E, _, F = W1.shape
    by_line = lambda w: w.reshape(E, -1, 128, w.shape[-1]).transpose(0, 2, 1, 3).reshape(E, 128, -1)
    parts = [by_line(W1), by_line(W2), by_line(b1[:, :, None]), np.repeat(b2[:, None, :], 128, axis=1)]
    return np.ascontiguousarray(np.concatenate(parts, axis=2).reshape(E * 128, -1))


def layouts(inputs):
    f = {k: np.ascontiguousarray(v) for k, v in inputs.items()}
    skip = ("src", "dst", "L0_mix_w_qkv", "L0_mix_w_dw", "L0_mix_w_pw", "L0_mix_w_res", "L0_ffn_edge_index")
    out = {k: v for k, v in f.items() if k not in skip}
    src, dst = f["src"], f["dst"]
    out["first_dst"] = np.ascontiguousarray(dst[:N].reshape(NT, P).T)
    out["first_src"] = np.ascontiguousarray(src[:N].reshape(NT, P).T)
    ei = f["L0_ffn_edge_index"]
    out["key0"], out["other0"] = columns(ei[1], COLS0, 0), columns(ei[0], COLS0, 0)
    out["key1"], out["other1"] = columns(src, COLS1, KEYS - 1), columns(dst, COLS1, 0)
    out["w_qkv_t"] = np.ascontiguousarray(f["L0_mix_w_qkv"][:, :, 2].T)
    cols = lambda v: np.ascontiguousarray(v.reshape(-1, 128).T)
    out["w_dw_mid_cols"] = cols(f["L0_mix_w_dw"][:, 0, 2])
    for name in ("L0_mix_bn_gamma", "L0_mix_bn_beta", "L1_mix_bq", "L1_mix_b1", "L1_ffn_b1s"):
        out[name + "_cols"] = cols(out.pop(name))
    out["L0_ffn_b1_cols"] = np.ascontiguousarray(np.stack([cols(v) for v in out.pop("L0_ffn_b1")]))
    out["L1_ffn_packed"] = pack_experts(*(out.pop("L1_ffn_" + x) for x in ("W1p", "b1p", "W2p", "b2p")))
    out["w_pw_t"] = np.ascontiguousarray(f["L0_mix_w_pw"][:, :, 0].T)
    out["w_res_t"] = np.ascontiguousarray(f["L0_mix_w_res"][:, :, 0].T)
    return out


def kernel(**inputs):
    import concourse.bacc as bacc
    from concourse.bass_utils import run_bass_kernel_spmd as run

    arrays = layouts({k: np.asarray(v) for k, v in inputs.items()})
    nc = bacc.Bacc("TRN2", target_bir_lowering=False, num_devices=1)
    io = {k: nc.dram_tensor("in_" + k, a.shape, mybir.dt.from_np(a.dtype), kind="ExternalInput").ap()
          for k, a in arrays.items()}
    io["out"] = nc.dram_tensor("out", (N, D), FP32, kind="ExternalOutput").ap()
    program(nc, io)
    r = run(nc, [{"in_" + k: a for k, a in arrays.items()}], core_ids=[0])
    return r.results[0]["out"]
```

```python
import math
import numpy as np
import concourse.bass as bass
from concourse import mybir
from contextlib import ExitStack

FP32 = mybir.dt.float32
FP16 = mybir.dt.float16
BF16 = mybir.dt.bfloat16
I32 = mybir.dt.int32
ALU = mybir.AluOpType
ACT = mybir.ActivationFunctionType
AX = mybir.AxisListType

N = 3125
P = 125
NT = N // P
D = 256
K2 = D // 128
CH = 4 * P
NCH = N // CH
BIG = 1e30
MIN_NORM = 1e-15
MAX_NORM = float(np.float32(1.0 - 1e-5))
MAX_ATANH = 0.5 * math.log((1 + MAX_NORM) / (1 - MAX_NORM))
KEYS = 4096
KB = 32
COLS0 = 512
COLS1 = 400
BC = 16


class Net:

    def __init__(self, nc, io):
        self.nc, self.io = nc, io
        self.keep = ExitStack()
        self.scope = self.keep
        self.sems = []

    def sem(self, name):
        self.sems.append(self.nc.alloc_semaphore(name))
        return self.sems[-1]

    def sb(self, name, shape, dt=FP32):
        return self.scope.enter_context(self.nc.sbuf_tensor(name, shape, dt))

    def dram(self, name, shape, dt=FP32):
        return self.nc.dram_tensor(name, shape, dt).ap()


class Stage:

    def __init__(self, m):
        self.m = m

    def __enter__(self):
        self.outer, self.m.scope = self.m.scope, ExitStack()
        self.sems, self.m.sems = self.m.sems, []
        return self

    def __exit__(self, *a):
        self.m.scope.close()
        self.m.scope = self.outer
        self.m.nc.clear_and_free_semaphores(self.m.sems)
        self.m.nc.all_engine_barrier()
        self.m.sems = self.sems


class Arena:

    def __init__(self, m, name, size):
        self.all = m.sb(name, [128, size])
        self.used = 0

    def take(self, name, shape):
        lo, size = self.used, math.prod(shape[1:])
        self.used += size
        piece = self.all[:shape[0], lo:lo + size]
        return piece if len(shape) == 2 else piece.rearrange("p (a b) -> p a b", a=shape[1])


class Loads:

    def __init__(self, m, name):
        self.sem, self.all = m.sem(name), 0

    def __call__(self, eng, dst, src):
        self.all += 16
        eng.dma_start(dst, src).then_inc(self.sem, 16)


def tiles(eng, total, unroll, body):
    whole = total // unroll
    with eng.Fori(0, whole) as i:
        for j in range(unroll):
            body(i * unroll + j, j)
    for j in range(total - whole * unroll):
        body(whole * unroll + j, j)


def chunks(eng, body):
    with eng.Fori(0, NCH) as c:
        body(c, 4)
    body(NCH, 1)


def tiles_written_out(total, unroll, body):
    for t in range(total):
        body(t, t % unroll)


def chunks_written_out(body):
    for c in range(NCH):
        body(c, 4)
    body(NCH, 1)


def at(t, size):
    return bass.ds(t * size, size)


def constants(m):
    nc = m.nc
    m.X = m.sb("X", [P, NT * D])
    m.ident = m.sb("ident", [128, 128])
    m.ps = [m.keep.enter_context(nc.psum_tensor(f"bank{i}", [128, 512], FP32)) for i in range(8)]
    m.spare = m.sem("spare")
    loaded = m.sem("x_loaded")
    with nc.Block() as block:
        @block.sync
        def _(sp):
            sp.dma_start(m.X[:, :].rearrange("p (t d) -> p t d", d=D),
                         m.io["x"].rearrange("(t p) d -> p t d", p=P)).then_inc(loaded, 16)
            sp.wait_ge(loaded, 16)

        @block.gpsimd
        def _(pool):
            pool.memset(m.ident[:, :], 0.0)
            pool.drain()
            pool.affine_select(out=m.ident[:, :], in_=m.ident[:, :], compare_op=ALU.not_equal, fill=1.0,
                               base=0, pattern=[[-1, 128]], channel_multiplier=1)
            pool.drain()


LAG = 3


def turn_tiles(m, block, tag, ready, first=None, product=None):
    turned, moved = m.sem(tag + "_turned"), m.sem(tag + "_moved")
    xt = m.XT[:, :].rearrange("p (k n) -> p k n", k=K2)

    @block.tensor
    def _(pe):
        def body(t, j):
            pe.wait_ge(ready, t + 1)
            pe.wait_ge(moved, t + 1)
            for k in range(K2):
                last = pe.transpose(m.ps[j][:, k * P:(k + 1) * P], m.XN[:, bass.ds(t * D + k * 128, 128)],
                                    m.ident[:P, :P])
            last.then_inc(turned, 1)
            if product is not None and t >= LAG:
                multiply(t - LAG)

        def multiply(t):
            pe.wait_ge(moved, t + 5)
            product.multiply(pe, t)
        tiles_written_out(NT, 4, body)
        if product is not None:
            for t in range(NT - LAG, NT):
                multiply(t)

    @block.scalar
    def _(act):
        act.sem_inc(moved, 4)
        if first is not None:
            first(act)

        def body(t, j):
            act.wait_ge(turned, t + 1)
            act.copy(xt[:, :, at(t, P)],
                     m.ps[j][:, 0:K2 * P].rearrange("p (k n) -> p k n", k=K2)).then_inc(moved, 1)
        if product is None:
            tiles(act, NT, 4, body)
        else:
            product.start(act)
            for t in range(NT + LAG + 1):
                if t < NT:
                    body(t, t % 4)
                if t > LAG:
                    product.keep(act, t - LAG - 1)


def moments(dve, s3, mean, var, tmp, count):
    dve.tensor_tensor(mean, s3[:, :, 1], s3[:, :, 4], ALU.add)
    dve.tensor_tensor(tmp, s3[:, :, 1], s3[:, :, 4], ALU.subtract)
    dve.tensor_tensor(var, s3[:, :, 2], s3[:, :, 5], ALU.add)
    dve.drain()
    dve.tensor_scalar(mean, mean, 0.5, None, ALU.mult)
    dve.tensor_scalar(tmp, tmp, 0.5, None, ALU.mult)
    dve.tensor_scalar(var, var, 1.0 / count, 1e-5, ALU.mult, ALU.add)
    dve.drain()
    dve.tensor_tensor(tmp, tmp, tmp, ALU.mult)
    dve.drain()
    return dve.tensor_tensor(var, var, tmp, ALU.add)


class NodeProduct:

    def __init__(self, m, tag, ROW):
        self.m, self.ROW = m, ROW
        self.w = m.sb(tag + "_w", [128, K2, ROW])
        self.loads, self.stored = Loads(m, tag + "_loaded"), Loads(m, tag + "_stored")
        self.w_ready, self.made, self.kept = m.sem(tag + "_w_ready"), m.sem(tag + "_made"), m.sem(tag + "_kept")

    def multiply(self, pe, t):
        m, ROW = self.m, self.ROW
        if t == 0:
            pe.wait_ge(self.w_ready, 1)
        pe.wait_ge(self.kept, t + 1)
        for k in range(K2):
            last = pe.matmul(m.ps[4 + t % 4][:P, 0:ROW], m.XT[:, bass.ds(t * P + k * N, P)], self.w[:, k, :],
                             start=k == 0, stop=k == K2 - 1)
        last.then_inc(self.made, 1)

    def start(self, act):
        act.sem_inc(self.kept, 4)

    def keep(self, act, t):
        act.wait_ge(self.made, t + 1)
        act.copy(self.rows(t), self.m.ps[4 + t % 4][:P, 0:self.ROW]).then_inc(self.kept, 1)

    def after(self, dve):
        pass


def layer_norm(m, tag, product=None):
    nc = m.nc
    with Stage(m):
        st = m.sb(tag + "_stats", [P, NT * 6])
        mean, var, tmp, rstd = (m.sb(tag + x, [P, NT]) for x in ("_mean", "_var", "_tmp", "_rstd"))
        var_ready, std_ready, normed = m.sem(tag + "_var_ready"), m.sem(tag + "_std_ready"), m.sem(tag + "_normed")
        s3 = st[:, :].rearrange("p (t s) -> p t s", s=6)
        with nc.Block() as block:
            @block.vector
            def _(dve):
                tiles(dve, NT, 5, lambda t, j: dve.bn_stats(st[:, at(t, 6)], m.X[:, at(t, D)]))
                dve.drain()
                moments(dve, s3, mean[:, :], var[:, :], tmp[:, :], D).then_inc(var_ready, 1)
                if product is not None:
                    product.prepare(dve)
                dve.wait_ge(std_ready, 1)
                dve.reciprocal(rstd[:, :], var[:, :])
                dve.drain()
                tiles(dve, NT, 5, lambda t, j: dve.tensor_scalar(
                    m.XN[:, at(t, D)], m.X[:, at(t, D)], mean[:, at(t, 1)], rstd[:, at(t, 1)],
                    ALU.subtract, ALU.mult).then_inc(normed, 1))
                if product is not None:
                    product.after(dve)

            if product is not None:
                @block.sync
                def _(sp):
                    product.load(sp)
                    product.store(sp)

            def root(act):
                act.wait_ge(var_ready, 1)
                act.sqrt(var[:, :], var[:, :]).then_inc(std_ready, 1)
            turn_tiles(m, block, tag, normed, root, product)


class Gnn0Nodes(NodeProduct):

    H, C = 4, 64

    def __init__(self, m):
        super().__init__(m, "g0", D + 2 * self.H)
        m.xt_dram = m.dram("xt_dram", [N, D + self.H])
        m.al_dram = m.dram("al_dram", [N, self.H])
        self.att = m.sb("g0_att", [128, 2, D])
        self.prod = m.sb("g0_prod", [128, 2, K2, D])
        self.table = m.sb("g0_table", [P, NT * self.ROW])

    def load(self, sp):
        io = self.m.io
        self.loads(sp, self.w[:, :, 0:D], io["L0_gnn_weight"].rearrange("(k p) d -> p k d", p=128))
        for i, name in enumerate(("L0_gnn_attn_r", "L0_gnn_attn_l")):
            self.loads(sp, self.att[:, i, :], io[name].rearrange("h c -> (h c)").partition_broadcast(128))

    def store(self, sp):
        m, H = self.m, self.H
        t3 = self.table[:, :].rearrange("p (t c) -> p t c", c=self.ROW)
        for t in range(0, NT, 5):
            ts = slice(t, t + 5)
            sp.wait_ge(self.kept, t + 5 + 4)
            self.stored(sp, m.xt_dram.rearrange("(t p) c -> p t c", p=P)[:, ts, :], t3[:, ts, 0:D + H])
            self.stored(sp, m.al_dram.rearrange("(t p) c -> p t c", p=P)[:, ts, :], t3[:, ts, D + H:])
        sp.wait_ge(self.stored.sem, self.stored.all)

    def prepare(self, dve):
        w, att, prod, H = self.w, self.att, self.prod, self.H
        dve.wait_ge(self.loads.sem, 48)
        for i in range(2):
            for k in range(K2):
                dve.tensor_tensor(prod[:, i, k, :], w[:, k, 0:D], att[:, i, :], ALU.mult)
        dve.drain()
        for i in range(2):
            for k in range(K2):
                last = dve.tensor_reduce(w[:, k, D + H * i:D + H * (i + 1)],
                                         prod[:, i, k, :].rearrange("p (h c) -> p h c", h=H), AX.X, ALU.add)
        last.then_inc(self.w_ready, 1)

    def rows(self, t):
        return self.table[:, t * self.ROW:(t + 1) * self.ROW]


class Gnn0Edges:

    H, C = 4, 64

    def __init__(self, m):
        H, C = self.H, self.C
        self.m = m
        self.idx = m.sb("g0_idx", [P, 2, NT], I32)
        self.near = m.sb("g0_near", [P, NT, D + H])
        self.al = m.sb("g0_al", [P, NT, H])
        self.e = m.sb("g0_e", [P, NT, H])
        self.tot = m.sb("g0_tot", [P, NT])
        self.mix = m.sb("g0_mix", [P, NT, C])
        self.loads, self.rows = Loads(m, "g0_idx_loaded"), Loads(m, "g0_rows")
        self.e_ready, self.e_exp = m.sem("g0_e_ready"), m.sem("g0_e_exp")

    def load(self, sp):
        self.loads(sp, self.idx[:, 0, :], self.m.io["first_dst"])
        self.loads(sp, self.idx[:, 1, :], self.m.io["first_src"])

    def gather(self, pool):
        pool.wait_ge(self.loads.sem, 32)
        for t in range(NT):
            for dst, table, i in ((self.near, self.m.xt_dram, 0), (self.al, self.m.al_dram, 1)):
                self.rows.all += 16
                pool.indirect_dma_start(
                    out=dst[:, t, :], out_offset=None, in_=table,
                    in_offset=bass.IndirectOffsetOnAxis(ap=self.idx[:, i, t:t + 1], axis=0)).then_inc(self.rows.sem, 16)

    def logits(self, dve):
        e, tot = self.e, self.tot
        dve.wait_ge(self.rows.sem, 16 * 2 * NT)
        dve.tensor_tensor(e[:, :, :], self.al[:, :, :], self.near[:, :, D:], ALU.add)
        dve.drain()
        dve.scalar_tensor_tensor(e[:, :, :], e[:, :, :], 0.01, e[:, :, :], ALU.mult, ALU.max)
        dve.drain()
        dve.tensor_reduce(tot[:, :], e[:, :, :], AX.X, ALU.max)
        dve.drain()
        wide = tot[:, :].unsqueeze(2).broadcast_to((P, NT, self.H))
        dve.tensor_tensor(e[:, :, :], e[:, :, :], wide, ALU.subtract).then_inc(self.e_ready, 1)

    def exponentials(self, act):
        act.wait_ge(self.e_ready, 1)
        act.activation(self.e[:, :, :], self.e[:, :, :], ACT.Exp).then_inc(self.e_exp, 1)

    def sums(self, dve):
        m, H, C, e, tot, near, mix = self.m, self.H, self.C, self.e, self.tot, self.near, self.mix
        wide = tot[:, :].unsqueeze(2).broadcast_to((P, NT, H))
        dve.wait_ge(self.e_exp, 1)
        dve.tensor_reduce(tot[:, :], e[:, :, :], AX.X, ALU.add)
        dve.drain()
        dve.reciprocal(tot[:, :], tot[:, :])
        dve.drain()
        dve.tensor_tensor(e[:, :, :], e[:, :, :], wide, ALU.mult)
        dve.drain()
        heads = near[:, :, 0:D].rearrange("p t (h c) -> p t h c", h=H)
        for t in range(NT):
            dve.tensor_tensor(heads[:, t], heads[:, t],
                              e[:, t, :].unsqueeze(2).broadcast_to((P, H, C)), ALU.mult)
        dve.drain()
        dve.tensor_reduce(mix[:, :, :], near[:, :, 0:D].rearrange("p t (h c) -> p t c h", h=H), AX.X, ALU.add)
        dve.drain()
        x4 = m.X[:, :].rearrange("p (t h c) -> p t h c", t=NT, h=H)
        for h in range(H):
            dve.tensor_tensor(x4[:, :, h, :], x4[:, :, h, :], mix[:, :, :], ALU.add)


def mix0_log(m):
    nc = m.nc
    with Stage(m):
        junk = m.sb("lg_junk", [P, 5, D])
        ss, n, r, a, b, c = (m.sb("lg_" + x, [P, NT]) for x in ("ss", "n", "r", "a", "b", "c"))
        ss_ready, root, ratio, logged, scaled = (m.sem("lg_" + x) for x in ("ss_ready", "root", "ratio", "logged", "scaled"))
        with nc.Block() as block:
            @block.vector
            def _(dve):
                def squares(t, j):
                    if j == 0:
                        dve.drain()
                    dve.scalar_tensor_tensor(junk[:, j, :], m.XN[:, at(t, D)], 1.0, m.XN[:, at(t, D)],
                                             ALU.mult, ALU.mult, accum_out=ss[:, at(t, 1)])
                tiles(dve, NT, 5, squares)
                dve.drain().then_inc(ss_ready, 1)
                dve.wait_ge(root, 1)
                dve.tensor_scalar(n[:, :], n[:, :], MIN_NORM, None, ALU.max)
                dve.drain()
                dve.tensor_scalar(r[:, :], n[:, :], MAX_NORM, None, ALU.min)
                dve.drain()
                dve.tensor_scalar(a[:, :], r[:, :], -1.0, 1.0, ALU.mult, ALU.add)
                dve.tensor_scalar(b[:, :], r[:, :], 1.0, None, ALU.add)
                dve.drain()
                dve.reciprocal(a[:, :], a[:, :])
                dve.drain()
                dve.tensor_tensor(a[:, :], a[:, :], b[:, :], ALU.mult).then_inc(ratio, 1)
                dve.drain()
                dve.tensor_tensor(b[:, :], r[:, :], r[:, :], ALU.mult)
                dve.drain()
                dve.tensor_scalar(c[:, :], b[:, :], 1.0 / 7, 1.0 / 5, ALU.mult, ALU.add)
                for k in (1.0 / 3, 1.0):
                    dve.drain()
                    dve.tensor_tensor(c[:, :], c[:, :], b[:, :], ALU.mult)
                    dve.drain()
                    dve.tensor_scalar(c[:, :], c[:, :], k, None, ALU.add)
                dve.drain()
                dve.tensor_tensor(c[:, :], c[:, :], r[:, :], ALU.mult)
                dve.tensor_scalar(b[:, :], r[:, :], 0.1, None, ALU.is_lt)
                dve.wait_ge(logged, 1)
                dve.tensor_scalar(a[:, :], a[:, :], 0.5, None, ALU.mult)
                dve.drain()
                dve.tensor_tensor(c[:, :], c[:, :], a[:, :], ALU.subtract)
                dve.drain()
                dve.tensor_tensor(c[:, :], c[:, :], b[:, :], ALU.mult)
                dve.reciprocal(n[:, :], n[:, :])
                dve.drain()
                dve.tensor_tensor(a[:, :], a[:, :], c[:, :], ALU.add)
                dve.drain()
                dve.tensor_tensor(a[:, :], a[:, :], n[:, :], ALU.mult)
                dve.drain()
                tiles(dve, NT, 5, lambda t, j: dve.tensor_scalar(
                    m.XN[:, at(t, D)], m.XN[:, at(t, D)], a[:, at(t, 1)], None, ALU.mult).then_inc(scaled, 1))

            def first(act):
                act.wait_ge(ss_ready, 1)
                act.sqrt(n[:, :], ss[:, :]).then_inc(root, 1)
                act.wait_ge(ratio, 1)
                act.activation(a[:, :], a[:, :], ACT.Ln).then_inc(logged, 1)
            turn_tiles(m, block, "lg", scaled, first)


OC = 6


def mix0_qkv(m, edges):
    nc, io = m.nc, m.io
    wq = m.sb("q0_w", [128, K2, OC * 128])
    gb = m.sb("q0_gb", [128, 2, OC])
    st = m.sb("q0_st", [128, OC, (NCH + 1) * 6])
    mv = m.sb("q0_mv", [128, OC, 2])
    sc = m.sb("q0_sc", [128, OC])
    sh = m.sb("q0_sh", [128, OC])
    loads = Loads(m, "q0_loaded")
    made, copied, var_ready, std_ready, affine = (
        m.sem("q0_" + x) for x in ("made", "copied", "var_ready", "std_ready", "affine"))
    with nc.Block() as block:
        @block.sync
        def _(sp):
            edges.load(sp)
            loads(sp, wq[:, :, :], io["w_qkv_t"].rearrange("(k p) o -> p k o", p=128))
            loads(sp, gb[:, 0, :], io["L0_mix_bn_gamma_cols"])
            loads(sp, gb[:, 1, :], io["L0_mix_bn_beta_cols"])

        @block.gpsimd
        def _(pool):
            edges.gather(pool)

        @block.tensor
        def _(pe):
            pe.wait_ge(loads.sem, 48)

            def body(c, nt):
                for o in range(OC):
                    pe.wait_ge(copied, c * OC + o + 1)
                    for k in range(K2):
                        last = pe.matmul(m.ps[o][:, 0:nt * P], wq[:, k, o * 128:(o + 1) * 128],
                                         m.XT[:, bass.ds(c * CH + k * N, nt * P)], start=k == 0, stop=k == K2 - 1)
                    last.then_inc(made, 1)
            chunks(pe, body)

        @block.vector
        def _(dve):
            def body(c, nt):
                for o in range(OC):
                    dve.wait_ge(copied, c * OC + o + 1 + OC)
                    dve.bn_stats(st[:, o, at(c, 6)], m.QT[:, bass.ds(c * CH + o * N, nt * P)])
            chunks(dve, body)
            dve.drain()
            for o in range(OC):
                dve.bn_aggr(mv[:, o, :], st[:, o, :])
            dve.drain()
            dve.tensor_scalar(sc[:, :], mv[:, :, 1], 1e-5, None, ALU.add).then_inc(var_ready, 1)
            edges.logits(dve)
            dve.wait_ge(std_ready, 1)
            dve.reciprocal(sc[:, :], sc[:, :])
            dve.wait_ge(loads.sem, 48)
            dve.drain()
            dve.tensor_tensor(sc[:, :], sc[:, :], gb[:, 0, :], ALU.mult)
            dve.drain()
            dve.tensor_tensor(sh[:, :], mv[:, :, 0], sc[:, :], ALU.mult)
            dve.drain()
            dve.tensor_tensor(sh[:, :], gb[:, 1, :], sh[:, :], ALU.subtract).then_inc(affine, 1)
            edges.sums(dve)

        @block.scalar
        def _(act):
            act.sem_inc(copied, OC)

            def body(c, nt):
                for o in range(OC):
                    act.wait_ge(made, c * OC + o + 1)
                    act.copy(m.QT[:, bass.ds(c * CH + o * N, nt * P)], m.ps[o][:, 0:nt * P]).then_inc(copied, 1)
            chunks(act, body)
            act.wait_ge(var_ready, 1)
            act.sqrt(sc[:, :], sc[:, :]).then_inc(std_ready, 1)
            edges.exponentials(act)
            act.wait_ge(affine, 1)
            act.drain()
            for o in range(OC):
                act.activation(m.QT[:, o * N:(o + 1) * N], m.QT[:, o * N:(o + 1) * N], ACT.Relu,
                               bias=sh[:, o:o + 1], scale=sc[:, o:o + 1])


def log_exp_scale(dve, out, n, cap, tmp):
    dve.tensor_scalar(tmp, n, MIN_NORM, None, ALU.max)
    dve.tensor_scalar(out, n, cap, None, ALU.min)
    dve.drain()
    dve.reciprocal(tmp, tmp)
    dve.drain()
    dve.tensor_tensor(out, out, tmp, ALU.mult)
    dve.drain()


def mix0_attention(m, routes):
    nc, io = m.nc, m.io
    G = 4
    U = OC * 128
    Z = 2 * U
    GR = Z // 96
    O = GR * 32
    z = [v.rearrange("p (g c) -> p g c", g=G) for v in (m.XN[:, 0:G * Z], m.sb("a0_z1", [P, G * Z])[:, :])]
    kr, vv, rec = (m.XT[:P, i * G * O:(i + 1) * G * O].rearrange("p (g c) -> p g c", g=G) for i in range(3))
    ks = m.sb("a0_ks", [P, G * GR])
    junk = m.sb("a0_junk", [P, U])
    pw = m.sb("a0_pw", [128, OC, 128])
    dw = m.sb("a0_dw", [128, OC])
    wres = m.sb("a0_wres", [128, 4, D])
    bres = m.XN[:, G * Z:G * Z + D]
    ot = m.sb("a0_ot", [128, 2, 4 * P])
    ft = [m.sb(f"a0_ft{i}", [P, G, D]) for i in range(2)]
    ss = m.sb("a0_ss", [P, 4, G])
    n = [m.sb(f"a0_n{i}", [P, 4, G]) for i in range(2)]
    f = [m.sb(f"a0_f{i}", [P, G]) for i in range(2)]
    th = [m.sb(f"a0_th{i}", [P, G]) for i in range(2)]
    s1, s2, s3, s4, s5, s6 = (m.sb(f"a0_s{i}", [P, G]) for i in range(6))
    loads = Loads(m, "a0_loaded")
    (zeroed, w_ready, z_made, z_kept, uv_root, out_done, o_root, o_turned, o_kept, res_made, ft_ss, ft_root) = (
        m.sem("a0_" + x) for x in (
            "zeroed", "w_ready", "z_made", "z_kept", "uv_root", "out_done", "o_root",
            "o_turned", "o_kept", "res_made", "ft_ss", "ft_root"))
    zb = [m.ps[0], m.ps[1], m.ps[2]]
    with nc.Block() as block:
        @block.sync
        def _(sp):
            sp.wait_ge(zeroed, 1)
            for a in range(4):
                loads(sp, pw[32 * a:32 * a + 32, :, 32 * a:32 * a + 32],
                      io["w_pw_t"].rearrange("i (j a c) -> i j a c", a=4, c=32)[:, :, a, :])
            loads(sp, dw[:, :], io["w_dw_mid_cols"])
            loads(sp, wres[:, :, :], io["w_res_t"].rearrange("(k p) d -> p k d", p=128))
            loads(sp, bres[:, :], io["L0_mix_b_res"].partition_broadcast(P))
            routes.clear(sp)

        n_loads = 16 * (4 + 3)

        @block.gpsimd
        def _(pool):
            pool.memset(pw[:, :, :], 0.0).then_inc(zeroed, 1)

        @block.tensor
        def _(pe):
            pe.wait_ge(w_ready, 1)

            def project(g, nt):
                for j in range(nt):
                    t = g * G + j
                    pe.wait_ge(z_kept, t + 1)
                    for o in range(OC):
                        pe.transpose(zb[o // 4][:P, (o % 4) * 128:(o % 4 + 1) * 128],
                                     m.QT[:, bass.ds(t * P + o * N, P)], m.ident[:, :])
                    for o in range(OC):
                        c = U + o * 128
                        last = pe.matmul(zb[c // 512][:P, c % 512:c % 512 + 128], m.QT[:, bass.ds(t * P + o * N, P)],
                                         pw[:, o, :], start=True, stop=True)
                    last.then_inc(z_made, 1)

            def resolve(g, nt):
                pe.wait_ge(out_done, g + 1)
                pe.wait_ge(ft_ss, g + 1)
                for j in range(nt):
                    t = g * G + j
                    for k in range(4):
                        last = pe.transpose(m.ps[4 + j % 2][:, k * P:(k + 1) * P], kr[:, j, k * 128:(k + 1) * 128],
                                            m.ident[:P, :P])
                    last.then_inc(o_turned, 1)
                    pe.wait_ge(o_kept, t + 1)
                    for k in range(4):
                        last = pe.matmul(m.ps[6 + j // 2][:P, j % 2 * D:(j % 2 + 1) * D], ot[:, j % 2, k * P:(k + 1) * P],
                                         wres[:, k, :], start=k == 0, stop=k == 3)
                last.then_inc(res_made, 1)
            project(0, G)
            for g in range(NCH):
                project(g + 1, G if g + 1 < NCH else 1)
                resolve(g, G)
            resolve(NCH, 1)

        @block.scalar
        def _(act):
            act.sem_inc(z_kept, 1)

            def keep_z(g, i, nt):
                for j in range(nt):
                    act.wait_ge(z_made, g * G + j + 1)
                    for lo in range(0, 2 * U, 256):
                        act.copy(z[i][:, j, lo:lo + 256], zb[lo // 512][:P, lo % 512:lo % 512 + 256])
                    act.drain().then_inc(z_kept, 1)
                    for h in range(2):
                        act.activation(junk[:, :], z[i][:, j, h * U:(h + 1) * U], ACT.Square,
                                       accum_out=ss[:, h, j:j + 1])
                        act.drain()
                act.sqrt(n[i][:, 0, 0:nt], ss[:, 0, 0:nt])
                for j in range(nt):
                    act.activation(n[i][:, 1, j:j + 1], ss[:, 1, j:j + 1], ACT.Sqrt, bias=ss[:, 0, j:j + 1])
                act.drain().then_inc(uv_root, 1)

            def turn_out(g, i, nt):
                act.wait_ge(out_done, g + 1)
                for j in range(nt):
                    act.activation(junk[:, 0:O], kr[:, j, :], ACT.Square, accum_out=ss[:, 2, j:j + 1])
                    act.drain()
                act.sqrt(n[i][:, 2, 0:nt], ss[:, 2, 0:nt]).then_inc(o_root, 1)
                for j in range(nt):
                    act.wait_ge(o_turned, g * G + j + 1)
                    act.copy(ot[:, j % 2, :], m.ps[4 + j % 2][:, 0:4 * P]).then_inc(o_kept, 1)

            def result_norm(g, i, nt):
                act.wait_ge(ft_ss, g + 2)
                for j in range(nt):
                    act.activation(junk[:, 0:D], ft[i][:, j, :], ACT.Square, accum_out=ss[:, 3, j:j + 1])
                    act.drain()
                act.sqrt(n[i][:, 3, 0:nt], ss[:, 3, 0:nt])
                act.drain()
                act.activation(th[i][:, 0:nt], n[i][:, 3, 0:nt], ACT.Tanh).then_inc(ft_root, 1)
            keep_z(0, 0, G)
            keep_z(1, 1, G)
            turn_out(0, 0, G)
            assert NCH == 6
            with act.Fori(0, 2) as r:
                for j in range(2):
                    keep_z(r * 2 + (j + 2), j, G)
                    turn_out(r * 2 + (j + 1), 1 - j, G)
                    result_norm(r * 2 + j, j, G)
            keep_z(6, 0, 1)
            turn_out(5, 1, G)
            result_norm(4, 0, G)
            turn_out(6, 0, 1)
            result_norm(5, 1, G)
            result_norm(6, 0, 1)

        @block.vector
        def _(dve):
            dve.wait_ge(loads.sem, n_loads)
            for o in range(OC):
                last = dve.tensor_scalar(pw[:, o, :], pw[:, o, :], dw[:, o:o + 1], None, ALU.mult)
            last.then_inc(w_ready, 1)
            dve.sem_inc(ft_ss, 1)
            flat = lambda x, nt: x[:, 0:nt, :].rearrange("p g (r c) -> p (g r) c", c=32)

            def attend(g, i, nt):
                zg = z[i].rearrange("p g (r c) -> p (g r) c", c=96)
                dve.wait_ge(uv_root, g + 1)
                log_exp_scale(dve, f[i][:, 0:nt], n[i][:, 0, 0:nt], MAX_ATANH, s1[:, 0:nt])
                dve.tensor_tensor(s2[:, 0:nt], n[i][:, 1, 0:nt], f[i][:, 0:nt], ALU.mult)
                dve.drain()
                log_exp_scale(dve, s3[:, 0:nt], s2[:, 0:nt], MAX_ATANH, s1[:, 0:nt])
                dve.tensor_tensor(f[i][:, 0:nt], f[i][:, 0:nt], s3[:, 0:nt], ALU.mult)
                dve.drain()
                for j in range(nt):
                    dve.tensor_scalar(vv[:, j, :].rearrange("p (r c) -> p r c", c=32),
                                      zg[:, j * GR:(j + 1) * GR, 64:96], f[i][:, j:j + 1], None, ALU.mult)
                dve.wait_ge(o_kept, g * G)
                dve.wait_ge(o_root, g)
                dve.tensor_scalar(flat(kr, nt), zg[:, 0:nt * GR, 32:64], 0.0, None, ALU.max)
                dve.drain()
                dve.tensor_reduce(ks[:, 0:nt * GR], flat(kr, nt), AX.X, ALU.add)
                dve.tensor_scalar(rec[:, 0:nt, :], vv[:, 0:nt, :], 1e-15, None, ALU.add)
                dve.drain()
                dve.reciprocal(rec[:, 0:nt, :], rec[:, 0:nt, :])
                dve.drain()
                dve.tensor_tensor(vv[:, 0:nt, :], vv[:, 0:nt, :], rec[:, 0:nt, :], ALU.mult)
                dve.drain()
                dve.scalar_tensor_tensor(flat(vv, nt), zg[:, 0:nt * GR, 0:32], 0.0, flat(vv, nt), ALU.max, ALU.mult)
                dve.drain()
                dve.tensor_tensor(flat(kr, nt), flat(vv, nt), ks[:, 0:nt * GR].unsqueeze(2).broadcast_to((P, nt * GR, 32)),
                                  ALU.mult).then_inc(out_done, 1)

            def scale_result(g, i, nt):
                dve.tensor_tensor(s4[:, 0:nt], f[i][:, 0:nt], f[i][:, 0:nt], ALU.mult)
                dve.drain()
                dve.wait_ge(o_root, g + 1)
                dve.tensor_tensor(s2[:, 0:nt], s4[:, 0:nt], n[i][:, 2, 0:nt], ALU.mult)
                dve.drain()
                log_exp_scale(dve, s3[:, 0:nt], s2[:, 0:nt], MAX_ATANH, s1[:, 0:nt])
                dve.tensor_tensor(s4[:, 0:nt], s4[:, 0:nt], s3[:, 0:nt], ALU.mult)
                dve.drain()
                dve.wait_ge(res_made, g + 1)
                for j in range(nt):
                    dve.scalar_tensor_tensor(ft[i][:, j, :], m.ps[6 + j // 2][:P, j % 2 * D:(j % 2 + 1) * D],
                                             s4[:, j:j + 1], bres[:P, :], ALU.mult, ALU.add)
                dve.drain().then_inc(ft_ss, 1)

            def add_result(g, i, nt):
                dve.wait_ge(ft_root, g + 1)
                dve.tensor_scalar(s5[:, 0:nt], n[i][:, 3, 0:nt], MIN_NORM, None, ALU.max)
                dve.tensor_scalar(s6[:, 0:nt], th[i][:, 0:nt], MAX_NORM, None, ALU.min)
                dve.drain()
                dve.reciprocal(s5[:, 0:nt], s5[:, 0:nt])
                dve.drain()
                dve.tensor_tensor(s6[:, 0:nt], s6[:, 0:nt], s5[:, 0:nt], ALU.mult)
                dve.drain()
                for j in range(nt):
                    x = m.X[:, bass.ds(g * (G * D) + j * D, D)]
                    dve.scalar_tensor_tensor(x, ft[i][:, j, :], s6[:, j:j + 1], x, ALU.mult, ALU.add)
                dve.drain()
            attend(0, 0, G)
            attend(1, 1, G)
            scale_result(0, 0, G)
            with dve.Fori(0, 2) as r:
                for j in range(2):
                    attend(r * 2 + (j + 2), j, G)
                    scale_result(r * 2 + (j + 1), 1 - j, G)
                    add_result(r * 2 + j, j, G)
            attend(6, 0, 1)
            scale_result(5, 1, G)
            add_result(4, 0, G)
            scale_result(6, 0, 1)
            add_result(5, 1, G)
            add_result(6, 0, 1)


class Edges:

    def __init__(self, m, tag, cols):
        self.tag, self.cols = tag, cols
        self.key = m.sb(tag + "_key", [128, cols])
        self.other = m.sb(tag + "_other", [128, cols], I32)
        self.start = m.dram(tag + "_start", [KEYS + 1], I32)


def floor_div(dve, q, r, pos, cols):
    magic = 12582912.0
    dve.tensor_scalar(q, pos, 0.5, 1.0 / cols, ALU.add, ALU.mult)
    dve.drain()
    dve.tensor_scalar(q, q, -0.5, magic, ALU.add, ALU.add)
    dve.drain()
    dve.tensor_scalar(q, q, -magic, None, ALU.add)
    dve.drain()
    last = dve.scalar_tensor_tensor(r, q, -float(cols), pos, ALU.mult, ALU.add)
    dve.drain()
    return last


def sort_constants(m):
    m.row16 = m.sb("row16", [128, 512], FP16)
    m.low16 = m.sb("low16", [128, 128], FP16)
    m.low = m.sb("low", [128, 128])
    m.high = m.sb("high", [128, 128])
    m.ones = m.sb("ones", [128, 512])
    m.zero16 = m.sb("zero16", [128, 512], FP16)
    m.ident16 = m.sb("ident16", [128, 128], FP16)
    with m.nc.Block() as block:
        @block.gpsimd
        def _(pool):
            pool.iota(m.row16[:, :], [[1, 512]], base=0, channel_multiplier=0,
                      allow_small_or_imprecise_dtypes=True)
            pool.memset(m.low[:, :], 1.0)
            pool.memset(m.high[:, :], 1.0)
            pool.memset(m.ones[:, :], 1.0)
            pool.memset(m.zero16[:, :], 0.0)
            pool.drain()
            pool.affine_select(out=m.low[:, :], in_=m.low[:, :], compare_op=ALU.is_gt, fill=0.0,
                               base=0, pattern=[[1, 128]], channel_multiplier=-1)
            pool.affine_select(out=m.high[:, :], in_=m.high[:, :], compare_op=ALU.is_gt, fill=0.0,
                               base=0, pattern=[[-1, 128]], channel_multiplier=1)
            pool.drain()
            pool.tensor_copy(m.low16[:, :], m.low[:, :])
            pool.tensor_copy(m.ident16[:, :], m.ident[:, :])
            pool.drain()


def sort_edges(m, ed, key_in, other_in, beside=lambda block, stage: None, arena=None):
    nc, cols, tag = m.nc, ed.cols, ed.tag
    nb = cols // BC
    MID = 1562.0
    with Stage(m):
        ki = m.sb(tag + "_ki", [128, cols], I32)
        a = m.sb(tag + "_a", [128, cols])
        b = m.sb(tag + "_b", [128, cols])
        val = m.sb(tag + "_val", [128, cols])
        pos = m.sb(tag + "_pos", [128, cols])
        H = arena.all if arena is not None else m.sb(tag + "_H", [128, (cols + 1) * KB])
        H3 = H[:, :].rearrange("p (t b) -> p t b", b=KB)
        half = lambda i, n=BC * 64: m.scratch[:, i * n:(i + 1) * n].bitcast(FP16).rearrange("p (c e) -> p c e", c=BC)
        oa, oat16, em = [half(0), half(1)], half(2), half(3)
        oat32 = m.scratch[:, 4 * BC * 64:6 * BC * 64].rearrange("p (c e) -> p c e", c=BC)
        ob = [m.sb(f"{tag}_ob{i}", [128, BC, KB], FP16) for i in range(3)]
        tot = m.sb(tag + "_tot", [128, KB])
        start = m.sb(tag + "_start_sb", [128, KB])
        start_i = m.sb(tag + "_start_i", [128, KB], I32)
        rsum = m.sb(tag + "_rsum", [128, 1])
        row128 = m.row16[:, 0:128]

        def one_hots(dve, t, j, i, columns=BC):
            for c in range(columns):
                dve.tensor_scalar(oa[j][:, c, :], row128, a[:, bass.ds(t * BC + c, 1)], None, ALU.is_equal)
            return dve.tensor_tensor(ob[i][:, :, :], b[:, at(t, BC)].unsqueeze(2).broadcast_to((128, BC, KB)),
                                     m.row16[:, 0:KB].unsqueeze(1).broadcast_to((128, BC, KB)), ALU.is_equal)

        loads = Loads(m, tag + "_in")
        hot, line_hot1, negated1, used, kept, tot_done = (
            m.sem(f"{tag}_{x}") for x in ("hot", "line_hot1", "negated1", "used", "kept", "tot_done"))
        neg_a, far1 = pos, [oat16, em]
        MINE = 11
        with nc.Block() as block:
            beside(block, 1)

            @block.sync
            def _(sp):
                loads(sp, ki[:, :], key_in)
                loads(sp, ed.other[:, :], other_in)

            @block.vector
            def _(dve):
                dve.wait_ge(loads.sem, loads.all)
                dve.tensor_scalar(ed.key[:, :].bitcast(I32), ki[:, :], 5, None, ALU.arith_shift_right)
                dve.tensor_scalar(val[:, :], ed.other[:, :], float(N - 1), -MID, ALU.min, ALU.add)
                dve.drain()
                dve.tensor_copy(a[:, :], ed.key[:, :].bitcast(I32))
                dve.drain()
                dve.tensor_scalar(ki[:, :], ki[:, :], 31, None, ALU.bitwise_and)
                dve.drain()
                dve.tensor_copy(b[:, :], ki[:, :])
                dve.tensor_scalar(neg_a[:, :], a[:, :], -1.0, None, ALU.mult)
                dve.drain().then_inc(negated1, 1)
                dve.sem_inc(used, 2)

                def body(t, j):
                    dve.wait_ge(used, t + 1)
                    one_hots(dve, t, j % 2, j % 2, MINE)
                    dve.drain().then_inc(hot, 1)
                tiles(dve, nb, 6, body)

            @block.tensor
            def _(pe):
                total = m.ps[7][:, 0:KB]
                pe.matmul(total, m.zero16[:, 0:128], m.zero16[:, 0:KB], start=True, stop=False)

                def body(t, j):
                    pe.wait_ge(hot, t + 1)
                    pe.wait_ge(line_hot1, t + 1)
                    pe.wait_ge(kept, t + 1)
                    for c in range(BC):
                        pe.matmul(m.ps[j][:, c * KB:(c + 1) * KB], oa[j][:, c, :], ob[j][:, c, :], start=True, stop=True)
                        last = pe.matmul(total, oa[j][:, c, :], ob[j][:, c, :], start=False, stop=False)
                    last.then_inc(used, 1)
                tiles(pe, nb, 2, body)
                pe.matmul(total, m.zero16[:, 0:128], m.zero16[:, 0:KB], start=False, stop=True).then_inc(tot_done, 1)

            @block.scalar
            def _(act):
                act.sem_inc(kept, 2)
                act.wait_ge(negated1, 1)

                def line_hots(t, j):
                    act.wait_ge(used, t + 1)
                    for c in range(MINE, BC):
                        act.activation(far1[j][:, c, :], row128, ACT.Square, bias=neg_a[:, bass.ds(t * BC + c, 1)])
                    act.drain()
                    act.activation(oa[j][:, MINE:BC, :], far1[j][:, MINE:BC, :], ACT.Relu, bias=m.ones[:, 0:1],
                                   scale=-1.0).then_inc(line_hot1, 1)

                def keep(t, j):
                    act.wait_ge(used, t + 3)
                    act.copy(H[:, bass.ds(t * (BC * KB) + KB, BC * KB)], m.ps[j][:, :]).then_inc(kept, 1)

                def body(t, j):
                    line_hots(t + 1, (j + 1) % 2)
                    keep(t, j % 2)
                line_hots(0, 0)
                tiles(act, nb - 1, 6, body)
                keep(nb - 1, (nb - 1) % 2)
                act.wait_ge(tot_done, 1)
                act.copy(tot[:, :], m.ps[7][:, 0:KB])

        row_ready, row_sum, start_ready, stored = (m.sem(f"{tag}_{x}") for x in ("row_ready", "row_sum", "start_ready", "stored"))
        with nc.Block() as block:
            beside(block, 2)

            @block.vector
            def _(dve):
                dve.tensor_tensor_scan(start[:, :], m.ones[:, 0:KB], tot[:, :], 0.0, ALU.mult, ALU.add)
                dve.drain()
                dve.tensor_copy(rsum[:, :], start[:, KB - 1:KB]).then_inc(row_ready, 1)
                dve.drain()
                dve.tensor_tensor(start[:, :], start[:, :], tot[:, :], ALU.subtract)
                dve.drain()
                dve.wait_ge(row_sum, 1)
                dve.tensor_scalar(start[:, :], start[:, :], m.ps[0][:, 0:1], None, ALU.add)
                dve.drain()
                dve.tensor_copy(start_i[:, :], start[:, :]).then_inc(start_ready, 1)
                dve.tensor_copy(H3[:, 0, :], start[:, :])
                for i in range(KB):
                    dve.tensor_tensor_scan(H3[:, 1:, i], m.ones[:, 0:cols], H3[:, 1:, i], start[:, i:i + 1],
                                           ALU.mult, ALU.add)

            @block.tensor
            def _(pe):
                pe.wait_ge(row_ready, 1)
                pe.matmul(m.ps[0][:, 0:1], m.low[:, :], rsum[:, :], start=True, stop=True).then_inc(row_sum, 1)

            @block.sync
            def _(sp):
                sp.wait_ge(start_ready, 1)
                sp.dma_start(ed.start[0:KEYS].rearrange("(a b) -> a b", b=KB), start_i[:, :]).then_inc(stored, 16)
                sp.wait_ge(stored, 16)

        pick = m.sb(tag + "_pick", [128, BC, KB])
        hot2, turned, moved16, moved32, same, masked, ranked, picked = (
            m.sem(f"{tag}_{x}") for x in ("hot2", "turned", "moved16", "moved32", "same", "masked", "ranked", "picked"))
        with nc.Block() as block:
            beside(block, 3)

            @block.vector
            def _(dve):
                def hots(t, j):
                    one_hots(dve, t, j % 2, j % 3)
                    dve.drain().then_inc(hot2, 1)

                def mask(t, j):
                    for q in range(4):
                        dve.wait_ge(same, 4 * t + q + 1)
                        dve.tensor_tensor(em[:, 4 * q:4 * q + 4, :], m.ps[2 + q][:, :].rearrange("p (c e) -> p c e", c=4),
                                          m.low16[:, :].unsqueeze(1).broadcast_to((128, 4, 128)), ALU.mult).then_inc(masked, 1)

                def choose(t, j):
                    dve.wait_ge(ranked, t + 1)
                    dve.tensor_tensor(pick[:, :, :], m.ps[6][:, :].rearrange("p (c b) -> p c b", b=KB),
                                      ob[j % 3][:, :, :], ALU.mult)
                    dve.drain().then_inc(picked, 1)
                    dve.tensor_reduce(pos[:, at(t, BC)], pick[:, :, :], AX.X, ALU.add)
                    dve.drain()
                dve.sem_inc(picked, 1)
                hots(0, 0)
                hots(1, 1)
                mask(0, 0)

                def body(t, j):
                    hots(t + 2, j + 2)
                    choose(t, j)
                    mask(t + 1, j + 1)
                tiles(dve, nb - 2, 6, body)
                choose(nb - 2, nb - 2)
                mask(nb - 1, nb - 1)
                choose(nb - 1, nb - 1)

            @block.tensor
            def _(pe):
                def turn(t, j):
                    pe.wait_ge(hot2, t + 1)
                    pe.wait_ge(moved32, t + 1)
                    for c in range(BC):
                        bank = m.ps[c // 8][:, :].bitcast(FP16)
                        last = pe.transpose(bank[:, (c % 8) * 128:(c % 8 + 1) * 128], oa[j % 2][:, c, :], m.ident16[:, :])
                    last.then_inc(turned, 1)

                def compare(t, j):
                    pe.wait_ge(moved16, t + 1)
                    pe.wait_ge(masked, 4 * t)
                    for c in range(BC):
                        last = pe.matmul(m.ps[2 + c // 4][:, (c % 4) * 128:(c % 4 + 1) * 128], oat16[:, c, :],
                                         oat16[:, c, :], start=True, stop=True)
                        if c % 4 == 3:
                            last.then_inc(same, 1)

                def rank(t, j):
                    pe.wait_ge(moved32, t + 2)
                    pe.wait_ge(picked, t + 1)
                    pe.wait_ge(masked, 4 * t + 4)
                    for c in range(BC):
                        out = m.ps[6][:, c * KB:(c + 1) * KB]
                        pe.matmul(out, oat32[:, c, :], H[:, bass.ds(t * (BC * KB) + c * KB, KB)], start=True, stop=False)
                        last = pe.matmul(out, em[:, c, :], ob[j % 3][:, c, :], start=False, stop=True)
                    last.then_inc(ranked, 1)
                turn(0, 0)

                def body(t, j):
                    compare(t, j)
                    turn(t + 1, j + 1)
                    rank(t, j)
                tiles(pe, nb - 1, 6, body)
                compare(nb - 1, nb - 1)
                rank(nb - 1, nb - 1)

            @block.scalar
            def _(act):
                act.sem_inc(moved32, 1)

                def body(t, j):
                    act.wait_ge(turned, t + 1)
                    for dst, done in ((oat16, moved16), (oat32, moved32)):
                        if dst is oat32:
                            act.wait_ge(ranked, t)
                        for h in range(2):
                            last = act.copy(dst[:, 8 * h:8 * h + 8, :].rearrange("p c e -> p (c e)"),
                                            m.ps[h][:, :].bitcast(FP16))
                        last.then_inc(done, 1)
                tiles(act, nb, 2, body)

        q, r = a, b
        sq = m.sb(tag + "_sq", [128, KB])
        sr = m.sb(tag + "_sr", [128, KB])
        rv = [m.sb(f"{tag}_rv{i}", [128, 4, cols], FP16) for i in range(2)]
        neg = m.sb(tag + "_neg_q", [128, cols + KB])
        far = [m.sb(f"{tag}_far{i}", [128, 3, 128], FP16) for i in range(2)]
        negated, line_hot, hot3, used3, row3, pre3 = (
            m.sem(f"{tag}_{x}") for x in ("negated", "line_hot", "hot3", "used3", "row3", "pre3"))
        nq = cols // 4
        with nc.Block() as block:
            beside(block, 4)

            @block.vector
            def _(dve):
                floor_div(dve, q[:, :], r[:, :], pos[:, :], cols)
                floor_div(dve, sq[:, :], sr[:, :], start[:, :], cols)
                dve.tensor_scalar(neg[:, 0:cols], q[:, :], -1.0, None, ALU.mult)
                dve.tensor_scalar(neg[:, cols:], sq[:, :], -1.0, None, ALU.mult)
                dve.drain().then_inc(negated, 1)
                dve.sem_inc(used3, 2)

                def body(t, j):
                    dve.wait_ge(used3, t + 1)
                    for c in range(4):
                        e = bass.ds(t * 4 + c, 1)
                        dve.tensor_scalar(rv[j % 2][:, c, :], m.row16[:, 0:cols], r[:, e], val[:, e], ALU.is_equal, ALU.mult)
                    dve.tensor_scalar(oa[j % 2][:, 3, :], row128, q[:, e], None, ALU.is_equal)
                    dve.drain().then_inc(hot3, 1)
                tiles(dve, nq, 8, body)

                def starts(t, j):
                    dve.wait_ge(used3, nq + t + 1)
                    for c in range(4):
                        e = bass.ds(t * 4 + c, 1)
                        dve.tensor_scalar(rv[j % 2][:, c, :], m.row16[:, 0:cols], sr[:, e], None, ALU.is_equal)
                    dve.tensor_scalar(oa[j % 2][:, 3, :], row128, sq[:, e], None, ALU.is_equal)
                    dve.drain().then_inc(hot3, 1)
                tiles(dve, KB // 4, 8, starts)
                dve.wait_ge(used3, nq + KB // 4 + 3)
                dve.tensor_scalar(ed.other[:, :], m.ps[0][:, 0:cols], MID, None, ALU.add)
                dve.tensor_tensor_scan(ed.key[:, :], m.ones[:, 0:cols], m.ps[1][:, 0:cols], 0.0, ALU.mult, ALU.add)
                dve.drain()
                dve.tensor_copy(rsum[:, :], ed.key[:, cols - 1:cols]).then_inc(row3, 1)
                dve.wait_ge(pre3, 1)
                dve.tensor_scalar(ed.key[:, :], ed.key[:, :], m.ps[2][:, 0:1], -1.0, ALU.add, ALU.add)

            @block.scalar
            def _(act):
                act.wait_ge(negated, 1)

                def body(t, j):
                    act.wait_ge(used3, t + 1)
                    for c in range(3):
                        act.activation(far[j % 2][:, c, :], row128, ACT.Square, bias=neg[:, bass.ds(t * 4 + c, 1)])
                    act.drain()
                    act.activation(oa[j % 2][:, 0:3, :], far[j % 2][:, :, :], ACT.Relu, bias=m.ones[:, 0:1],
                                   scale=-1.0).then_inc(line_hot, 1)
                tiles(act, nq + KB // 4, 8, body)

            @block.tensor
            def _(pe):
                for half, count, first in ((0, nq, 0), (1, KB // 4, nq)):
                    out = m.ps[half][:, 0:cols]
                    pe.matmul(out, m.zero16[:, 0:128], m.zero16[:, 0:cols], start=True, stop=False)

                    def body(t, j):
                        pe.wait_ge(hot3, t + first + 1)
                        pe.wait_ge(line_hot, t + first + 1)
                        for c in range(4):
                            last = pe.matmul(out, oa[(j + first) % 2][:, c, :], rv[(j + first) % 2][:, c, :],
                                             start=False, stop=False)
                        last.then_inc(used3, 1)
                    assert nq % 2 == 0
                    tiles(pe, count, 2, body)
                    last = pe.matmul(out, m.zero16[:, 0:128], m.zero16[:, 0:cols], start=False, stop=True)
                last.then_inc(used3, 1)
                pe.wait_ge(row3, 1)
                pe.matmul(m.ps[2][:, 0:1], m.low[:, :], rsum[:, :], start=True, stop=True).then_inc(pre3, 1)


def nodes_of(table, lo=0):
    return table[lo:lo + N].rearrange("(t p) -> p t", p=P)


class Spread:

    def __init__(self, m, tag, ed, H):
        self.H = H
        self.ke = m.sb(tag + "_ke", [128, ed.cols, H])
        self.cont = m.sb(tag + "_cont", [128, ed.cols])
        self.pen = m.sb(tag + "_pen", [128, ed.cols])
        self.lo = m.sb(tag + "_lo", [P, NT])
        self.hi = m.sb(tag + "_hi", [P, NT])
        self.has = m.sb(tag + "_has", [P, NT])


class SpreadLogits:

    def __init__(self, m, tag, ed, sp_, table, logits):
        H, cols = sp_.H, ed.cols
        self.m, self.ed, self.sp_, self.table, self.logits = m, ed, sp_, table, logits
        self.placed = m.dram(tag + "_placed", [128 * cols, H])
        self.zero = m.sb(tag + "_zero", [128, cols * H])
        self.raw = self.zero[:, :].rearrange("p (t h) -> p t h", h=H)
        self.lo_i, self.hi_i, self.dst_i = (m.sb(tag + x, [P, NT], I32) for x in ("_lo_i", "_hi_i", "_dst_i"))
        self.dst = m.sb(tag + "_dst", [P, NT])
        self.first_i = m.sb(tag + "_first_i", [128, 1], I32)
        self.first = m.sb(tag + "_first", [128, 1])
        self.own = m.sb(tag + "_own", [128, H])
        self.loads, self.rows, self.back = (Loads(m, tag + x) for x in ("_bounds_loaded", "_rows_placed", "_raw_loaded"))
        self.zeroed, self.cleared, self.idx_ready, self.own_sem = (
            m.sem(tag + x) for x in ("_zeroed", "_cleared", "_idx_ready", "_own"))

    def bounds(self, sp):
        with self.m.nc.allow_non_contiguous_dma(reason="one word per node"):
            self.loads(sp, self.lo_i[:, :], nodes_of(self.ed.start))
            self.loads(sp, self.hi_i[:, :], nodes_of(self.ed.start, 1))

    def sync(self, sp):
        sp.wait_ge(self.zeroed, 1)
        sp.dma_start(self.placed.rearrange("(p t) h -> p (t h)", p=128), self.zero[:, :]).then_inc(self.cleared, 16)
        sp.wait_ge(self.rows.sem, 16 * NT)
        self.back(sp, self.raw, self.placed.rearrange("(p t) h -> p t h", p=128))

    def gpsimd(self, pool):
        pool.memset(self.zero[:, :], 0.0).then_inc(self.zeroed, 1)
        pool.wait_ge(self.idx_ready, 1)
        pool.indirect_dma_start(out=self.own[:, :], out_offset=None, in_=self.table,
                                in_offset=bass.IndirectOffsetOnAxis(ap=self.first_i[:, :], axis=0)
                                ).then_inc(self.own_sem, 16)
        pool.wait_ge(self.cleared, 16)
        for t in range(NT):
            pool.indirect_dma_start(out=self.placed,
                                    out_offset=bass.IndirectOffsetOnAxis(ap=self.dst_i[:, t:t + 1], axis=0),
                                    in_=self.logits[:, t, :], in_offset=None,
                                    bounds_check=128 * self.ed.cols - 1, oob_is_err=False).then_inc(self.rows.sem, 16)

    def positions(self, dve):
        sp_, ed, cols, first, dst = self.sp_, self.ed, self.ed.cols, self.first, self.dst
        E = 128 * cols
        dve.wait_ge(self.loads.sem, 32)
        dve.tensor_copy(sp_.lo[:, :], self.lo_i[:, :])
        dve.tensor_copy(sp_.hi[:, :], self.hi_i[:, :])
        dve.tensor_scalar(first[:, :], ed.key[:, 0:1], float(N - 1), None, ALU.min)
        dve.drain()
        dve.tensor_copy(self.first_i[:, :], first[:, :])
        dve.tensor_tensor(sp_.has[:, :], sp_.hi[:, :], sp_.lo[:, :], ALU.is_gt)
        dve.drain()
        dve.tensor_scalar(dst[:, :], sp_.has[:, :], -float(4 * E), float(4 * E), ALU.mult, ALU.add)
        dve.drain()
        dve.tensor_tensor(dst[:, :], dst[:, :], sp_.lo[:, :], ALU.add)
        dve.drain()
        dve.tensor_copy(self.dst_i[:, :], dst[:, :])
        dve.drain().then_inc(self.idx_ready, 1)
        dve.memset(sp_.cont[:, 0:1], 0.0)
        dve.tensor_tensor(sp_.cont[:, 1:], ed.key[:, 1:], ed.key[:, 0:cols - 1], ALU.is_equal)
        dve.drain()
        dve.tensor_scalar(sp_.pen[:, :], sp_.cont[:, :], -1.0, BIG, ALU.add, ALU.mult)

    def spread(self, dve):
        sp_ = self.sp_
        dve.wait_ge(self.back.sem, 16)
        dve.wait_ge(self.own_sem, 16)
        dve.tensor_copy(self.raw[:, 0, :], self.own[:, :])
        dve.drain()
        for h in range(sp_.H):
            dve.tensor_tensor_scan(sp_.ke[:, :, h], sp_.cont[:, :], self.raw[:, :, h], 0.0, ALU.mult, ALU.add)


def spread_logits(m, tag, ed, sp_, table, logits, beside=lambda block: None):
    with Stage(m):
        s = SpreadLogits(m, tag, ed, sp_, table, logits)
        with m.nc.Block() as block:
            beside(block)

            @block.sync
            def _(sp):
                s.bounds(sp)
                s.sync(sp)

            @block.gpsimd
            def _(pool):
                s.gpsimd(pool)

            @block.vector
            def _(dve):
                s.positions(dve)
                s.spread(dve)


def carry_rows(m, tag, ed, H, F, last, table, beside=None):
    nc, cols = m.nc, ed.cols
    W = H * F + 2 * H
    with Stage(m):
        dg = m.sb(tag + "_dg", [128, H + 1, 128])
        mask = m.sb(tag + "_mask", [128, 128])
        neg = m.sb(tag + "_neg", [128, 128])
        a = m.sb(tag + "_a", [128, H, 128])
        wt = m.sb(tag + "_wt", [128, H, 128])
        wtt = m.sb(tag + "_wtt", [128, H, 128])
        cm = m.sb(tag + "_cm", [128, H])
        ncm = m.sb(tag + "_ncm", [128, H])
        row = m.sb(tag + "_row", [128, W + 1])
        dg_ready, wide, a_ready, expd, wt_ready, turned, back, summed, row_ready, stored = (
            m.sem(tag + x) for x in ("_dg_ready", "_wide", "_a_ready", "_expd", "_wt_ready", "_turned",
                                     "_back", "_summed", "_row_ready", "_stored"))
        with nc.Block() as block:
            @block.vector
            def _(dve):
                dve.tensor_scalar(dg[:, H, :], m.ident[:, :], ed.key[:, cols - 1:cols], None, ALU.mult)
                for h in range(H):
                    dve.tensor_scalar(dg[:, h, :], m.ident[:, :], last[:, H * F + H + h:H * F + H + h + 1], None, ALU.mult)
                dve.drain().then_inc(dg_ready, 1)
                dve.wait_ge(wide, 1)
                dve.scalar_tensor_tensor(mask[:, :], m.ps[H][:, 0:128], ed.key[:, 0:1], m.high[:, :], ALU.is_equal, ALU.mult)
                dve.drain()
                dve.tensor_scalar(neg[:, :], mask[:, :], -1.0, BIG, ALU.add, ALU.mult)
                for h in range(H):
                    dve.tensor_tensor(a[:, h, :], m.ps[h][:, 0:128], mask[:, :], ALU.mult)
                dve.drain()
                for h in range(H):
                    dve.tensor_tensor(a[:, h, :], a[:, h, :], neg[:, :], ALU.add)
                dve.drain()
                dve.tensor_reduce(cm[:, :], a[:, :, :], AX.X, ALU.max)
                dve.drain()
                for h in range(H):
                    dve.tensor_scalar(a[:, h, :], a[:, h, :], cm[:, h:h + 1], None, ALU.subtract)
                dve.drain().then_inc(a_ready, 1)
                dve.wait_ge(expd, 1)
                for h in range(H):
                    dve.tensor_tensor(wt[:, h, :], wt[:, h, :], mask[:, :], ALU.mult)
                dve.drain().then_inc(wt_ready, 1)
                dve.wait_ge(turned, 1)
                for h in range(H):
                    dve.tensor_copy(wtt[:, h, :], m.ps[h][:, 0:128])
                dve.drain().then_inc(back, 1)
                dve.wait_ge(summed, 1)
                for h in range(H):
                    dve.tensor_copy(row[:, h * F:(h + 1) * F], m.ps[4 + h][:, 0:F])
                    dve.tensor_copy(row[:, H * F + h:H * F + h + 1], m.ps[4 + h][:, F:F + 1])
                dve.tensor_copy(row[:, H * F + H:W], cm[:, :])
                dve.tensor_copy(row[:, W:W + 1], ed.key[:, 0:1])
                dve.drain().then_inc(row_ready, 1)

            @block.scalar
            def _(act):
                act.wait_ge(a_ready, 1)
                act.activation(wt[:, :, :], a[:, :, :], ACT.Exp).then_inc(expd, 1)

            @block.tensor
            def _(pe):
                pe.wait_ge(dg_ready, 1)
                for h in range(H + 1):
                    x = pe.matmul(m.ps[h][:, 0:128], m.ones[:, 0:128], dg[:, h, :], start=True, stop=True)
                x.then_inc(wide, 1)
                pe.wait_ge(wt_ready, 1)
                for h in range(H):
                    x = pe.transpose(m.ps[h][:, 0:128], wt[:, h, :], m.ident[:, :])
                x.then_inc(turned, 1)
                pe.wait_ge(back, 1)
                for h in range(H):
                    pe.matmul(m.ps[4 + h][:, 0:F], wtt[:, h, :], last[:, h * F:(h + 1) * F], start=True, stop=True)
                    x = pe.matmul(m.ps[4 + h][:, F:F + 1], wtt[:, h, :], last[:, H * F + h:H * F + h + 1],
                                  start=True, stop=True)
                x.then_inc(summed, 1)

            @block.sync
            def _(sp):
                if beside is not None:
                    beside(sp)
                sp.wait_ge(row_ready, 1)
                sp.dma_start(table, row[:, :]).then_inc(stored, 16)
                sp.wait_ge(stored, 16)


def merge_nodes(m, tag, ed, sp_, H, F, result, carry, agg, den, own_e=None, own_f=None, early=None, first=0):
    nc, cols = m.nc, ed.cols
    HF = H * F
    W = HF + 2 * H
    GT = 5
    with Stage(m):
        end = m.sb(tag + "_end", [P, NT])
        part = m.sb(tag + "_part", [P, NT])
        rest = m.sb(tag + "_rest", [P, NT])
        end_i = m.sb(tag + "_end_i", [P, NT], I32)
        part_i = m.sb(tag + "_part_i", [P, NT], I32)
        node = m.sb(tag + "_node", [P, NT])
        ends = [m.sb(f"{tag}_re{i}", [P, GT, W]) for i in range(2)]
        carried = [m.sb(f"{tag}_rc{i}", [P, GT, W + 1]) for i in range(2)]
        use = m.sb(tag + "_use", [P, GT])
        me, mc, mx, we, wc, ws = (m.sb(tag + x, [P, GT, H]) for x in ("_me", "_mc", "_mx", "_we", "_wc", "_ws"))
        idx_ready, exps, expd, free = (m.sem(tag + x) for x in ("_idx_ready", "_exps", "_expd", "_free"))
        rows = [m.sem(f"{tag}_rows{i}") for i in range(2)]
        node_sem = m.sem(tag + "_node_sem")
        with nc.Block() as block:
            @block.gpsimd
            def _(pool):
                pool.iota(node[:, :], [[P, NT]], base=0, channel_multiplier=1,
                          allow_small_or_imprecise_dtypes=True).then_inc(node_sem, 1)
                pool.wait_ge(idx_ready, 1)
                for t in range(NT):
                    i = t // GT % 2
                    if t % GT == 0 and t >= 2 * GT:
                        pool.wait_ge(free, t // GT - 1)
                    for dst, table, idx in ((ends[i], result, end_i), (carried[i], carry, part_i)):
                        pool.indirect_dma_start(out=dst[:, t % GT, :], out_offset=None, in_=table,
                                                in_offset=bass.IndirectOffsetOnAxis(ap=idx[:, t:t + 1], axis=0)
                                                ).then_inc(rows[i], 16)

            @block.vector
            def _(dve):
                dve.tensor_scalar(end[:, :], sp_.hi[:, :], -1.0, 0.0, ALU.add, ALU.max)
                dve.drain()
                floor_div(dve, part[:, :], rest[:, :], end[:, :], cols)
                dve.tensor_copy(end_i[:, :], end[:, :])
                dve.tensor_copy(part_i[:, :], part[:, :])
                dve.drain().then_inc(idx_ready, 1)
                dve.wait_ge(node_sem, 1)
                for g in range(NT // GT):
                    ts = slice(g * GT, (g + 1) * GT)
                    has = sp_.has[:, ts]
                    wide = lambda x: x.unsqueeze(2).broadcast_to((P, GT, H))
                    re, rc = ends[g % 2], carried[g % 2]
                    dve.wait_ge(rows[g % 2], 32 * GT * (g // 2 + 1))
                    dve.tensor_tensor(use[:, :], rc[:, :, W], node[:, ts], ALU.is_equal)
                    dve.tensor_tensor(me[:, :, :], re[:, :, HF + H:W], wide(has), ALU.mult)
                    dve.tensor_scalar(we[:, :, :], wide(has), -1.0, BIG, ALU.add, ALU.mult)
                    dve.drain()
                    dve.tensor_tensor(me[:, :, :], me[:, :, :], we[:, :, :], ALU.add)
                    dve.tensor_tensor(mc[:, :, :], rc[:, :, HF + H:W], wide(use[:, :]), ALU.mult)
                    dve.tensor_scalar(wc[:, :, :], wide(use[:, :]), -1.0, BIG, ALU.add, ALU.mult)
                    dve.drain()
                    dve.tensor_tensor(mc[:, :, :], mc[:, :, :], wc[:, :, :], ALU.add)
                    dve.drain()
                    dve.tensor_tensor(mx[:, :, :], me[:, :, :], mc[:, :, :], ALU.max)
                    dve.drain()
                    if own_e is not None:
                        dve.tensor_tensor(mx[:, :, :], mx[:, :, :], own_e[:, ts, :], ALU.max)
                        dve.drain()
                        dve.tensor_tensor(ws[:, :, :], own_e[:, ts, :], mx[:, :, :], ALU.subtract)
                    dve.tensor_tensor(we[:, :, :], me[:, :, :], mx[:, :, :], ALU.subtract)
                    dve.tensor_tensor(wc[:, :, :], mc[:, :, :], mx[:, :, :], ALU.subtract)
                    dve.drain().then_inc(exps, 1)
                    dve.wait_ge(expd, g + 1)
                    dve.tensor_tensor(we[:, :, :], we[:, :, :], wide(has), ALU.mult)
                    dve.tensor_tensor(wc[:, :, :], wc[:, :, :], wide(use[:, :]), ALU.mult)
                    dve.drain()
                    for j in range(GT):
                        for h in range(H):
                            f, d = slice(h * F, (h + 1) * F), slice(HF + h, HF + h + 1)
                            t = g * GT + j
                            dve.tensor_scalar(agg[:, t, f], re[:, j, f], we[:, j, h:h + 1], None, ALU.mult)
                            dve.tensor_scalar(den[:, t, h:h + 1], re[:, j, d], we[:, j, h:h + 1], None, ALU.mult)
                    dve.drain()
                    for j in range(GT):
                        for h in range(H):
                            f, d = slice(h * F, (h + 1) * F), slice(HF + h, HF + h + 1)
                            t = g * GT + j
                            dve.scalar_tensor_tensor(agg[:, t, f], rc[:, j, f], wc[:, j, h:h + 1], agg[:, t, f],
                                                     ALU.mult, ALU.add)
                            dve.scalar_tensor_tensor(den[:, t, h:h + 1], rc[:, j, d], wc[:, j, h:h + 1],
                                                     den[:, t, h:h + 1], ALU.mult, ALU.add)
                    if own_e is not None:
                        dve.drain()
                        for j in range(GT):
                            for h in range(H):
                                f, t = slice(h * F, (h + 1) * F), g * GT + j
                                dve.scalar_tensor_tensor(agg[:, t, f], own_f[:, t, f], ws[:, j, h:h + 1], agg[:, t, f],
                                                         ALU.mult, ALU.add)
                        dve.tensor_tensor(den[:, ts, :], den[:, ts, :], ws[:, :, :], ALU.add)
                    dve.drain().then_inc(free, 1)

            if early is not None:
                @block.tensor
                def _(pe):
                    early.tensor(pe, 0, first, NCH + 1)
                    early.tensor(pe, 1, 0, NCH + 1)

            @block.scalar
            def _(act):
                parts = [(0, first, first + 1), (0, first + 1, first + 2), (0, first + 2, NCH + 1), (1, 0, 1), (1, 1, 2)]
                for g in range(NT // GT):
                    if early is not None:
                        early.scalar(act, *parts[g])
                    act.wait_ge(exps, g + 1)
                    for x in (we, wc) + ((ws,) if own_e is not None else ()):
                        last = act.activation(x[:, :, :], x[:, :, :], ACT.Exp)
                    act.drain().then_inc(expd, 1)
                if early is not None:
                    early.scalar(act, 1, 2, NCH + 1)


class GatNodes(NodeProduct):

    H, F = 4, 4

    def __init__(self, m, hg):
        super().__init__(m, "gn", self.H * self.F + 2 * self.H)
        HF, H = self.H * self.F, self.H
        m.gat_src = m.dram("gat_src", [N, HF + H])
        m.gat_dst = m.dram("gat_dst", [N, H])
        self.hg = hg
        self.att = m.sb("gn_att", [128, 2, HF])
        self.prod = m.sb("gn_prod", [128, 2, K2, HF])

    def load(self, sp):
        io, HF = self.m.io, self.H * self.F
        self.loads(sp, self.w[:, :, 0:HF], io["L0_ffn_W_gat"].rearrange("(k p) d -> p k d", p=128))
        for i, name in enumerate(("L0_ffn_att_src", "L0_ffn_att_dst")):
            self.loads(sp, self.att[:, i, :], io[name].rearrange("h c -> (h c)").partition_broadcast(128))

    def store(self, sp):
        m = self.m
        for t in range(0, NT, 5):
            ts = slice(t, t + 5)
            sp.wait_ge(self.kept, t + 5 + 4)
            self.stored(sp, m.gat_src.rearrange("(t p) c -> p t c", p=P)[:, ts, :], self.hg[:, ts, 0:20])
            self.stored(sp, m.gat_dst.rearrange("(t p) c -> p t c", p=P)[:, ts, :], self.hg[:, ts, 20:24])
        sp.wait_ge(self.stored.sem, self.stored.all)

    def prepare(self, dve):
        w, H, HF = self.w, self.H, self.H * self.F
        dve.wait_ge(self.loads.sem, 48)
        for i in range(2):
            for k in range(K2):
                dve.tensor_tensor(self.prod[:, i, k, :], w[:, k, 0:HF], self.att[:, i, :], ALU.mult)
        dve.drain()
        for i in range(2):
            for k in range(K2):
                dve.tensor_reduce(w[:, k, HF + H * i:HF + H * (i + 1)],
                                  self.prod[:, i, k, :].rearrange("p (h c) -> p h c", h=H), AX.X, ALU.add)
        dve.drain().then_inc(self.w_ready, 1)

    def rows(self, t):
        return self.hg[:, t, :]


def gat_edges(m, ed, next_edges, next_lists, w, near, early, load_early, arena):
    nc, io = m.nc, m.io
    H, F, cols = 4, 4, ed.cols
    HF, W = H * F, H * F + 2 * H
    nb = cols // BC
    m.agg0 = m.sb("agg0", [P, NT, HF])
    with Stage(m):
        last = m.sb("ge_last", [128, W])
        G = near[:, :].rearrange("p (t f) -> p t f", f=HF + H)
        idx = [m.sb(f"ge_idx{i}", [128, BC], I32) for i in range(2)]
        buf = [m.sb(f"ge_buf{i}", [128, BC, HF + H]) for i in range(2)]
        rows = [m.sem(f"ge_rows{i}") for i in range(2)]

        def gather_blocks(pool, lo, hi):
            assert lo % 2 == 0 and hi % 2 == 0

            def issue(t, j):
                pool.tensor_copy(idx[j][:, :], ed.other[:, at(t, BC)])
                pool.drain()
                for c in range(BC):
                    pool.indirect_dma_start(out=buf[j][:, c, :], out_offset=None, in_=m.gat_src,
                                            in_offset=bass.IndirectOffsetOnAxis(ap=idx[j][:, c:c + 1], axis=0)
                                            ).then_inc(rows[j], 16)

            def keep(t, j):
                pool.wait_ge(rows[j], (t - j) * (8 * BC) + 16 * BC)
                pool.tensor_copy(G[:, at(t, BC), :], buf[j][:, :, :])
                pool.drain()
            issue(lo, 0)
            if hi - lo > 2:
                with pool.Fori(0, (hi - lo) // 2 - 1) as i:
                    issue(i * 2 + (lo + 1), 1)
                    keep(i * 2 + lo, 0)
                    issue(i * 2 + (lo + 2), 0)
                    keep(i * 2 + (lo + 1), 1)
            issue(hi - 1, 1)
            keep(hi - 2, 0)
            keep(hi - 1, 1)

        share = {1: (0, 4), 2: (4, 6), 3: (6, 20), 4: (20, cols // BC)}

        def beside(block, stage):
            @block.gpsimd
            def _(pool):
                gather_blocks(pool, *share[stage])
        sort_edges(m, next_edges, *next_lists, beside, arena)
        with nc.Block() as block:
            @block.sync
            def _(sp):
                load_early(sp, 1)
        spread = Spread(m, "ge", ed, H)
        own_e = m.sb("ge_own_e", [P, NT, H])
        den = m.sb("ge_den", [P, NT, H])
        dst_logits = m.sb("ge_dst_logits", [P, NT, H])
        result = m.dram("ge_result", [128 * cols, W])
        carry = m.dram("ge_carry", [128, W + 1])
        with nc.Block() as block:
            @block.vector
            def _(dve):
                dve.tensor_copy(dst_logits[:, :, :], m.hg[:, :, 20:24])
                dve.tensor_tensor(own_e[:, :, :], m.hg[:, :, 16:20], m.hg[:, :, 20:24], ALU.add)
                dve.drain()
                dve.scalar_tensor_tensor(own_e[:, :, :], own_e[:, :, :], 0.2, own_e[:, :, :], ALU.mult, ALU.max)
        early = early()
        r_stored = m.sem("ge_r_stored")
        FIRST = 3

        def beside_spread(block):
            @block.tensor
            def _(pe):
                early.tensor(pe, 0, 0, FIRST)

            @block.scalar
            def _(act):
                early.scalar(act, 0, 0, FIRST)
        spread_logits(m, "gs", ed, spread, m.gat_dst, dst_logits, beside_spread)
        with Stage(m):
            R = arena.all[:, 0:cols * W].rearrange("p (t w) -> p t w", w=W)
            dec = m.sb("ge_dec", [128, cols, H])
            e_ready, e_exp = m.sem("ge_e_ready"), m.sem("ge_e_exp")
            with nc.Block() as block:
                @block.vector
                def _(dve):
                    e = spread.ke
                    dve.tensor_tensor(e[:, :, :], G[:, :, HF:], e[:, :, :], ALU.add)
                    dve.drain()
                    dve.scalar_tensor_tensor(e[:, :, :], e[:, :, :], 0.2, e[:, :, :], ALU.mult, ALU.max)
                    dve.drain()
                    mx = R[:, :, HF + H:]
                    for h in range(H):
                        dve.tensor_tensor_scan(mx[:, :, h], spread.pen[:, :], e[:, :, h], -BIG, ALU.add, ALU.max)
                    dve.drain()
                    wide = spread.cont[:, :].unsqueeze(2).broadcast_to((128, cols, H))
                    dve.memset(dec[:, 0, :], 0.0)
                    dve.tensor_tensor(dec[:, 1:, :], mx[:, 0:cols - 1, :], mx[:, 1:, :], ALU.subtract)
                    dve.tensor_tensor(e[:, :, :], e[:, :, :], mx, ALU.subtract)
                    dve.drain()
                    dve.tensor_tensor(dec[:, :, :], dec[:, :, :], wide, ALU.mult)
                    dve.drain().then_inc(e_ready, 1)
                    dve.wait_ge(e_exp, 1)
                    dve.tensor_tensor(dec[:, :, :], dec[:, :, :], wide, ALU.mult)
                    for h in range(H):
                        f = G[:, :, h * F:(h + 1) * F]
                        dve.tensor_tensor(f, f, e[:, :, h].unsqueeze(2).broadcast_to((128, cols, F)), ALU.mult)
                    dve.drain()
                    for h in range(H):
                        for f in range(h * F, (h + 1) * F):
                            dve.tensor_tensor_scan(R[:, :, f], dec[:, :, h], G[:, :, f], 0.0, ALU.mult, ALU.add)
                        dve.tensor_tensor_scan(R[:, :, HF + h], dec[:, :, h], e[:, :, h], 0.0, ALU.mult, ALU.add)
                    dve.drain()
                    dve.tensor_copy(last[:, :], R[:, cols - 1, :])
                    dve.sem_inc(e_ready, 1)

                @block.scalar
                def _(act):
                    act.wait_ge(e_ready, 1)
                    act.activation(spread.ke[:, :, :], spread.ke[:, :, :], ACT.Exp)
                    act.activation(dec[:, :, :], dec[:, :, :], ACT.Exp)
                    act.drain().then_inc(e_exp, 1)

                @block.sync
                def _(sp):
                    sp.wait_ge(e_ready, 2)
                    sp.dma_start(result.rearrange("(p t) w -> p t w", p=128), R[:, :, :]).then_inc(r_stored, 16)

        def reload(sp):
            sp.wait_ge(r_stored, 16)
            load_early(sp, 2)
        carry_rows(m, "gc", ed, H, F, last, carry, reload)
        merge_nodes(m, "gm", ed, spread, H, F, result, carry, m.agg0, den, own_e, m.hg, early, FIRST)
        with nc.Block() as block:
            @block.vector
            def _(dve):
                dve.tensor_scalar(den[:, :, :], den[:, :, :], 1e-16, None, ALU.add)
                dve.drain()
                dve.reciprocal(den[:, :, :], den[:, :, :])
                dve.drain()
                for h in range(H):
                    f = m.agg0[:, :, h * F:(h + 1) * F]
                    dve.tensor_tensor(f, f, den[:, :, h].unsqueeze(2).broadcast_to((P, NT, F)), ALU.mult)


def top_two(dve, s, E, gt, eq, low, sel):
    def by_rank(op, out):
        for t in range(NT):
            dve.tensor_tensor(out[:, t], s[:, t, :].unsqueeze(1).broadcast_to((P, E, E)),
                              s[:, t, :].unsqueeze(2).broadcast_to((P, E, E)), op)
    by_rank(ALU.is_gt, gt)
    by_rank(ALU.is_equal, eq)
    dve.drain()
    for t in range(NT):
        dve.tensor_tensor(eq[:, t], eq[:, t], low, ALU.mult)
    dve.drain()
    dve.tensor_tensor(gt, gt, eq, ALU.add)
    dve.drain()
    dve.tensor_reduce(sel, gt, AX.X, ALU.add)
    dve.drain()
    dve.tensor_scalar(sel, sel, 1.5, None, ALU.is_lt)
    dve.drain()


def gates0(m):
    nc, io = m.nc, m.io
    H, E, C = 4, 4, 16
    m.gate0 = m.sb("gate0", [P, NT, E])
    with Stage(m):
        par = m.sb("gt_par", [P, 3, C])
        st = m.sb("gt_st", [P, NT, 6])
        mean, var, tmp = (m.sb("gt_" + x, [P, NT]) for x in ("mean", "var", "tmp"))
        s = m.sb("gt_s", [P, NT, E])
        gt = m.sb("gt_gt", [P, NT, E, E])
        eq = m.sb("gt_eq", [P, NT, E, E])
        low = m.sb("gt_low", [P, E, E])
        sel = m.sb("gt_sel", [P, NT, E])
        loads, low_ready, var_ready, std_ready, s_ready, s_exp = (
            Loads(m, "gt_loaded"), *(m.sem("gt_" + x) for x in ("low_ready", "var_ready", "std_ready", "s_ready", "s_exp")))
        with nc.Block() as block:
            @block.sync
            def _(sp):
                for i, name in enumerate(("L0_ffn_b_gat", "L0_ffn_ln_gamma", "L0_ffn_ln_beta")):
                    loads(sp, par[:, i, :], io[name].partition_broadcast(P))

            @block.gpsimd
            def _(pool):
                pool.memset(low[:, :, :], 1.0)
                pool.drain()
                pool.affine_select(out=low[:, :, :], in_=low[:, :, :], compare_op=ALU.is_gt, fill=0.0,
                                   base=0, pattern=[[1, E], [-1, E]], channel_multiplier=0)
                pool.drain().then_inc(low_ready, 1)

            @block.vector
            def _(dve):
                a = m.agg0
                all_nodes = lambda x: x.unsqueeze(1).broadcast_to((P, NT, C))
                by_node = lambda x: x.unsqueeze(2).broadcast_to((P, NT, C))
                dve.wait_ge(loads.sem, 48)
                dve.tensor_tensor(a[:, :, :], a[:, :, :], all_nodes(par[:, 0, :]), ALU.add)
                dve.drain()
                for t in range(NT):
                    dve.bn_stats(st[:, t, :], a[:, t, :])
                dve.drain()
                moments(dve, st, mean[:, :], var[:, :], tmp[:, :], C).then_inc(var_ready, 1)
                dve.wait_ge(std_ready, 1)
                dve.reciprocal(tmp[:, :], var[:, :])
                dve.tensor_tensor(a[:, :, :], a[:, :, :], by_node(mean[:, :]), ALU.subtract)
                dve.drain()
                dve.tensor_tensor(a[:, :, :], a[:, :, :], by_node(tmp[:, :]), ALU.mult)
                dve.drain()
                dve.tensor_tensor(a[:, :, :], a[:, :, :], all_nodes(par[:, 1, :]), ALU.mult)
                dve.drain()
                dve.tensor_tensor(a[:, :, :], a[:, :, :], all_nodes(par[:, 2, :]), ALU.add)
                dve.drain()
                dve.tensor_reduce(s[:, :, :], a[:, :, :].rearrange("p t (h e) -> p t e h", h=H), AX.X, ALU.add)
                dve.drain()
                dve.tensor_scalar(s[:, :, :], s[:, :, :], 1.0 / H, None, ALU.mult)
                dve.drain()
                dve.wait_ge(low_ready, 1)
                top_two(dve, s, E, gt[:, :, :, :], eq[:, :, :, :], low[:, :, :], sel[:, :, :])
                dve.tensor_reduce(tmp[:, :], s[:, :, :], AX.X, ALU.max)
                dve.drain()
                wide = tmp[:, :].unsqueeze(2).broadcast_to((P, NT, E))
                dve.tensor_tensor(s[:, :, :], s[:, :, :], wide, ALU.subtract).then_inc(s_ready, 1)
                dve.wait_ge(s_exp, 1)
                dve.tensor_tensor(s[:, :, :], s[:, :, :], sel[:, :, :], ALU.mult)
                dve.drain()
                dve.tensor_reduce(tmp[:, :], s[:, :, :], AX.X, ALU.add)
                dve.drain()
                dve.reciprocal(tmp[:, :], tmp[:, :])
                dve.drain()
                dve.tensor_tensor(m.gate0[:, :, :], s[:, :, :], wide, ALU.mult)

            @block.scalar
            def _(act):
                act.wait_ge(var_ready, 1)
                act.sqrt(var[:, :], var[:, :]).then_inc(std_ready, 1)
                act.wait_ge(s_ready, 1)
                act.activation(s[:, :, :], s[:, :, :], ACT.Exp).then_inc(s_exp, 1)


class ExpertWeights:

    def __init__(self, m, tag, F, ring, place=None):
        FC, self.ring = F // 128, ring
        place = place or m.sb
        self.w1 = [place(f"{tag}_w1_{i}", [128, K2, F]) for i in range(ring)]
        self.w2 = [place(f"{tag}_w2_{i}", [128, FC, D]) for i in range(ring)]
        self.b1 = [place(f"{tag}_b1_{i}", [128, FC]) for i in range(ring)]
        self.b2 = [place(f"{tag}_b2_{i}", [P, D]) for i in range(ring)]
        self.arrived = [m.sem(f"{tag}_arrived{i}") for i in range(ring)]
        self.landed = [0] * ring

    def load(self, sp, e, w1, b1, w2, b2):
        i = e % self.ring
        self.landed[i] += 64
        sp.dma_start(self.w1[i][:, :, :], w1.rearrange("(k p) f -> p k f", p=128)).then_inc(self.arrived[i], 16)
        sp.dma_start(self.b1[i][:, :], b1).then_inc(self.arrived[i], 16)
        sp.dma_start(self.w2[i][:, :, :], w2.rearrange("(k p) d -> p k d", p=128)).then_inc(self.arrived[i], 16)
        sp.dma_start(self.b2[i][:, :], b2.partition_broadcast(P)).then_inc(self.arrived[i], 16)


class EarlyExperts:

    def __init__(self, m, tag, w, F, hT, out):
        self.m, self.w, self.FC, self.hT, self.out = m, w, F // 128, hT, out
        self.up, self.acted, self.down, self.moved = (m.sem(f"{tag}_{x}") for x in ("up", "acted", "down", "moved"))

    def some_chunks(self, eng, lo, hi, body):
        with eng.Fori(0, min(hi, NCH) - lo) as c:
            body(c + lo if lo else c, 4)
        if hi > NCH:
            body(NCH, 1)

    def tensor(self, pe, e, lo, hi):
        m, w, FC, i = self.m, self.w, self.FC, e % self.w.ring
        pe.wait_ge(w.arrived[i], w.landed[i])

        def body(c, nt):
            for f in range(FC):
                pe.wait_ge(self.acted, c * FC + (e * (NCH + 1) * FC + f + 1))
                for k in range(K2):
                    last = pe.matmul(m.ps[f % 4][:, 0:nt * P], w.w1[i][:, k, f * 128:(f + 1) * 128],
                                     m.XT[:, bass.ds(c * CH + k * N, nt * P)], start=k == 0, stop=k == K2 - 1)
                last.then_inc(self.up, 1)
            pe.wait_ge(self.acted, c * FC + (e * (NCH + 1) * FC + FC + 4))
            for j in range(nt):
                pe.wait_ge(self.moved, c * 4 + (e * NT + j + (2 if j == 0 else 1)))
                for f in range(FC):
                    last = pe.matmul(m.ps[4 + j % 2][:P, 0:D], self.hT[:, f, j * P:(j + 1) * P], w.w2[i][:, f, :],
                                     start=f == 0, stop=f == FC - 1)
                last.then_inc(self.down, 1)
        self.some_chunks(pe, lo, hi, body)

    def scalar(self, act, e, lo, hi):
        m, w, FC, i = self.m, self.w, self.FC, e % self.w.ring
        if e == 0 and lo == 0:
            act.sem_inc(self.acted, 4)
            act.sem_inc(self.moved, 2)

        def body(c, nt):
            for f in range(FC):
                act.wait_ge(self.up, c * FC + (e * (NCH + 1) * FC + f + 1))
                act.activation(self.hT[:, f, 0:nt * P], m.ps[f % 4][:, 0:nt * P], ACT.Gelu,
                               bias=w.b1[i][:, f:f + 1]).then_inc(self.acted, 1)
            for j in range(nt):
                act.wait_ge(self.down, c * 4 + (e * NT + j + 1))
                act.copy(self.out[e][:, bass.ds(c * (4 * D) + j * D, D)], m.ps[4 + j % 2][:P, 0:D]
                         ).then_inc(self.moved, 1)
        self.some_chunks(act, lo, hi, body)


def experts(m, tag, w, gates, F, load=None, first=0, lo=0, hi=NCH + 1, beside=None, after_tile=None):
    nc = m.nc
    FC = F // 128
    full = min(hi, NCH)
    per_expert = 4 * (full - lo) + (hi - full)
    with Stage(m):
        hT = m.sb(tag + "_hT", [128, FC, CH])
        y = [m.sb(f"{tag}_y{i}", [P, D]) for i in range(2)]
        landed = {}
        up, acted, down, added, read = (m.sem(f"{tag}_{x}") for x in ("up", "acted", "down", "added", "read"))

        def some_chunks(eng, body):
            with eng.Fori(0, full - lo) as c:
                body(c, 4)
            if hi > NCH:
                body(NCH - lo, 1)

        with nc.Block() as block:
            if beside is not None:
                @block.gpsimd
                def _(pool):
                    beside(pool)

            if load is not None:
                @block.sync
                def _(sp):
                    for e in range(len(gates)):
                        if e >= w.ring:
                            sp.wait_ge(added, (e - w.ring + 1) * per_expert + 2)
                        load(sp, first + e)
                        landed[e] = w.landed[(first + e) % w.ring]

            @block.tensor
            def _(pe):
                for e in range(len(gates)):
                    i = (first + e) % w.ring
                    pe.wait_ge(w.arrived[i], landed.get(e, w.landed[i]))

                    def body(c, nt):
                        for f in range(FC):
                            pe.wait_ge(acted, (e * (hi - lo) + c) * FC + f + 1)
                            for k in range(K2):
                                last = pe.matmul(m.ps[f % 4][:, 0:nt * P], w.w1[i][:, k, f * 128:(f + 1) * 128],
                                                 m.XT[:, bass.ds(c * CH + (k * N + lo * CH), nt * P)],
                                                 start=k == 0, stop=k == K2 - 1)
                            last.then_inc(up, 1)
                        pe.wait_ge(acted, (e * (hi - lo) + c) * FC + FC + 4)
                        for j in range(nt):
                            t = e * per_expert + c * 4 + j
                            pe.wait_ge(added, t + (2 if j == 0 else 1))
                            for f in range(FC):
                                last = pe.matmul(m.ps[4 + j % 2][:P, 0:D], hT[:, f, j * P:(j + 1) * P], w.w2[i][:, f, :],
                                                 start=f == 0, stop=f == FC - 1)
                            last.then_inc(down, 1)
                    some_chunks(pe, body)

            @block.scalar
            def _(act):
                act.sem_inc(acted, 4)
                for e in range(len(gates)):
                    i = (first + e) % w.ring

                    def body(c, nt):
                        act.wait_ge(read, e * per_expert + c * 4 + 1)
                        for f in range(FC):
                            act.wait_ge(up, (e * (hi - lo) + c) * FC + f + 1)
                            act.activation(hT[:, f, 0:nt * P], m.ps[f % 4][:, 0:nt * P], ACT.Gelu,
                                           bias=w.b1[i][:, f:f + 1]).then_inc(acted, 1)
                    some_chunks(act, body)

            @block.vector
            def _(dve):
                dve.sem_inc(added, 2)
                dve.sem_inc(read, 1)
                for e, gate in enumerate(gates):
                    i = (first + e) % w.ring

                    def body(c, nt):
                        dve.drain()
                        for j in range(nt):
                            x = m.X[:, bass.ds(c * (4 * D) + (lo * 4 + j) * D, D)]
                            dve.wait_ge(down, e * per_expert + c * 4 + j + 1)
                            dve.tensor_tensor(y[j % 2][:, :], m.ps[4 + j % 2][:P, 0:D], w.b2[i][:, :], ALU.add
                                              ).then_inc(read, 1)
                            dve.drain()
                            if gate is None:
                                dve.tensor_tensor(x, y[j % 2][:, :], x, ALU.add).then_inc(added, 1)
                            else:
                                dve.scalar_tensor_tensor(x, y[j % 2][:, :], gate(c * 4 + (lo * 4 + j)), x,
                                                         ALU.mult, ALU.add).then_inc(added, 1)
                            if after_tile is not None and e == 0:
                                after_tile(dve, c, j)
                    some_chunks(dve, body)


FF = 1024
SHARED_FIRST = 3
TS = 256


class Routes:

    def __init__(self, m, tag, E):
        self.tag, self.E = tag, E
        self.tiles = (2 * N + E * (TS - 1)) // TS
        self.x = m.dram(tag + "_x", [self.tiles * TS, D])
        self.y = m.dram(tag + "_y", [self.tiles * TS, D])
        self.zeros = m.zero16[:, :].bitcast(FP32)
        self.cleared = Loads(m, tag + "_cleared")

    def hold(self, m):
        self.slot = m.sb(self.tag + "_slot", [P, 2, NT], I32)
        self.gate = m.sb(self.tag + "_gate", [P, 2, NT])
        self.rows = m.sb(self.tag + "_rows", [128, self.tiles], I32)

    def clear(self, sp):
        x = self.x.rearrange("(p s) d -> p s d", p=128)
        self.cleared(sp, x, self.zeros.unsqueeze(1).broadcast_to((128, self.tiles * TS // 128, D)))


def find_routes(m, r, sel, gate):
    nc, E, tag, TL = m.nc, r.E, r.tag, r.tiles
    TOP = float(1 << 15)
    with Stage(m):
        count, before, pos, pick = (m.sb(tag + x, [128, NT, E]) for x in ("_count", "_before", "_pos", "_pick"))
        need, num, rest, end = (m.sb(tag + x, [128, E]) for x in ("_need", "_num", "_rest", "_end"))
        slot = m.sb(tag + "_slot_f", [P, 2, NT])
        line = m.sb(tag + "_line", [128, 1])
        row = m.sb(tag + "_row", [128, TL])
        counted, lined = (m.sem(tag + x) for x in ("_counted", "_lined"))
        with nc.Block() as block:
            @block.gpsimd
            def _(pool):
                pool.iota(line[:, :], [[1, 1]], base=0, channel_multiplier=1,
                          allow_small_or_imprecise_dtypes=True).then_inc(lined, 1)

            @block.tensor
            def _(pe):
                s = sel.rearrange("p t e -> p (t e)")
                pe.matmul(m.ps[0][:, 0:NT * E], m.low[:P, :], s, start=True, stop=True)
                pe.matmul(m.ps[1][:, 0:NT * E], m.ones[:P, 0:128], s, start=True, stop=True).then_inc(counted, 1)

            @block.vector
            def _(dve):
                dve.wait_ge(counted, 1)
                dve.tensor_copy(count[:, :, :], m.ps[1][:, 0:NT * E].rearrange("p (t e) -> p t e", e=E))
                dve.drain()
                for e in range(E):
                    dve.tensor_tensor_scan(before[:, :, e], m.ones[:, 0:NT], count[:, :, e], 0.0, ALU.mult, ALU.add)
                dve.drain()
                dve.tensor_scalar(need[:, :], before[:, NT - 1, :], float(TS - 1), None, ALU.add)
                dve.drain()
                dve.tensor_tensor(before[:, :, :], before[:, :, :], count[:, :, :], ALU.subtract)
                dve.drain()
                floor_div(dve, num[:, :], rest[:, :], need[:, :], TS)
                dve.tensor_tensor_scan(end[:, :], m.ones[:, 0:E], num[:, :], 0.0, ALU.mult, ALU.add)
                dve.drain()
                dve.tensor_tensor(rest[:, :], end[:, :], num[:, :], ALU.subtract)
                dve.tensor_tensor(pos[:, :, :], before[:, :, :],
                                  m.ps[0][:, 0:NT * E].rearrange("p (t e) -> p t e", e=E), ALU.add)
                dve.drain()
                dve.tensor_scalar(rest[:, :], rest[:, :], float(TS), None, ALU.mult)
                dve.drain()
                dve.tensor_tensor(pos[:, :, :], pos[:, :, :], rest[:, :].unsqueeze(1).broadcast_to((128, NT, E)), ALU.add)
                dve.drain()
                p = pos[:P, :, :]
                dve.tensor_tensor(pick[:P, :, :], p, sel, ALU.mult)
                dve.tensor_scalar(before[:P, :, :], p, -1.0, TOP, ALU.mult, ALU.add)
                dve.drain()
                dve.tensor_tensor(before[:P, :, :], before[:P, :, :], sel, ALU.mult)
                dve.tensor_reduce(slot[:, 1, :], pick[:P, :, :], AX.X, ALU.max)
                dve.drain()
                dve.tensor_reduce(slot[:, 0, :], before[:P, :, :], AX.X, ALU.max)
                dve.drain()
                dve.tensor_scalar(slot[:, 0, :], slot[:, 0, :], -1.0, TOP, ALU.mult, ALU.add)
                dve.drain()
                dve.tensor_copy(r.slot[:, :, :], slot[:, :, :])
                for i in range(2):
                    dve.tensor_tensor(pick[:P, :, :], p, slot[:, i, :].unsqueeze(2).broadcast_to((P, NT, E)), ALU.is_equal)
                    dve.drain()
                    dve.tensor_tensor(pick[:P, :, :], pick[:P, :, :], gate, ALU.mult)
                    dve.drain()
                    dve.tensor_reduce(r.gate[:, i, :], pick[:P, :, :], AX.X, ALU.add)
                    dve.drain()
                dve.tensor_scalar(row[:, :], m.row16[:, 0:TL], end[:, 0:1], None, ALU.is_ge)
                dve.drain()
                for e in range(1, E - 1):
                    dve.scalar_tensor_tensor(row[:, :], m.row16[:, 0:TL], end[:, e:e + 1], row[:, :], ALU.is_ge, ALU.add)
                    dve.drain()
                dve.wait_ge(lined, 1)
                dve.tensor_scalar(row[:, :], row[:, :], 128.0, line[:, 0:1], ALU.mult, ALU.add)
                dve.drain()
                dve.tensor_copy(r.rows[:, :], row[:, :])


def scatter_nodes(m, r, pool, placed):
    pool.wait_ge(r.cleared.sem, r.cleared.all)
    for t in range(NT):
        for i in range(2):
            pool.indirect_dma_start(out=r.x, out_offset=bass.IndirectOffsetOnAxis(ap=r.slot[:, i, t:t + 1], axis=0),
                                    in_=m.XN[:, t * D:(t + 1) * D], in_offset=None,
                                    bounds_check=r.tiles * TS - 1, oob_is_err=False).then_inc(placed, 16)


def routed_experts(m, r, packed, F):
    nc, tag, TL = m.nc, r.tag, r.tiles
    FC, S = F // 128, TS // 128
    O2, OB1, OB2 = K2 * F, K2 * F + FC * D, K2 * F + FC * D + FC
    assert TL % 2 == 0
    with Stage(m):
        w = [m.sb(f"{tag}_w{i}", [128, OB2 + D]) for i in range(2)]
        w1 = [x[:, 0:O2].rearrange("p (k f) -> p k f", k=K2) for x in w]
        w2 = [x[:, O2:OB1].rearrange("p (f d) -> p f d", d=D) for x in w]
        xs = [m.sb(f"{tag}_xs{i}", [128, S, D]) for i in range(2)]
        xT = [m.sb(f"{tag}_xT{i}", [128, K2, TS]) for i in range(2)]
        hT = [m.sb(f"{tag}_hT{i}", [128, FC, TS]) for i in range(2)]
        y = [m.sb(f"{tag}_ys{i}", [128, S, D]) for i in range(2)]
        w_loaded, x_loaded, y_stored = ([m.sem(f"{tag}_{x}{i}") for i in range(2)]
                                        for x in ("w_loaded", "x_loaded", "y_stored"))
        turned, x_ready, up, acted, down, y_read, y_made = (
            m.sem(f"{tag}_{x}") for x in ("turned", "x_ready", "up", "acted", "down", "y_read", "y_made"))

        def all_tiles(eng, body):
            with eng.Fori(0, TL // 2 - 1) as i:
                for j in range(2):
                    body(i * 2 + j, j, True, True)
            body(TL - 2, 0, True, False)
            body(TL - 1, 1, False, False)

        with nc.Block() as block:
            @block.gpsimd
            def _(pool):
                for i in range(TL):
                    if i >= 2:
                        pool.wait_ge(y_made, i - 1)
                    pool.indirect_dma_start(out=w[i % 2][:, :], out_offset=None, in_=packed,
                                            in_offset=bass.IndirectOffsetOnAxis(ap=r.rows[:, i:i + 1], axis=0)
                                            ).then_inc(w_loaded[i % 2], 16)

            @block.sync
            def _(sp):
                slots = lambda table, i: table[at(i, TS), :].rearrange("(s p) d -> p s d", p=128)
                load = lambda i, j: sp.dma_start(xs[j][:, :, :], slots(r.x, i)).then_inc(x_loaded[j], 16)
                load(0, 0)
                load(1, 1)

                def body(i, j, follows, follow2):
                    if follow2:
                        sp.wait_ge(turned, i + 1)
                        load(i + 2, j)
                    sp.wait_ge(y_made, i + 1)
                    sp.dma_start(slots(r.y, i), y[j][:, :, :]).then_inc(y_stored[j], 16)
                all_tiles(sp, body)
                for j in range(2):
                    sp.wait_ge(y_stored[j], 16 + 8 * TL)

            @block.tensor
            def _(pe):
                def turn(i, j):
                    pe.wait_ge(x_loaded[j], (i - j) * 8 + 16)
                    for k in range(K2):
                        for s in range(S):
                            c = (k * S + s) * 128
                            last = pe.transpose(m.ps[6][:, c:c + 128], xs[j][:, s, k * 128:(k + 1) * 128], m.ident[:, :])
                    last.then_inc(turned, 1)
                turn(0, 0)

                def body(i, j, follows, follow2):
                    pe.wait_ge(w_loaded[j], (i - j) * 8 + 16)
                    pe.wait_ge(x_ready, i + 1)
                    for f in range(FC):
                        pe.wait_ge(acted, i * FC + f + 1)
                        for k in range(K2):
                            last = pe.matmul(m.ps[f % 4][:, 0:TS], w1[j][:, k, f * 128:(f + 1) * 128], xT[j][:, k, :],
                                             start=k == 0, stop=k == K2 - 1)
                        last.then_inc(up, 1)
                    if follows:
                        turn(i + 1, 1 - j)
                    pe.wait_ge(acted, i * FC + FC + 4)
                    for s in range(S):
                        pe.wait_ge(y_read, i * S + s + 1)
                        for f in range(FC):
                            last = pe.matmul(m.ps[4 + s][:, 0:D], hT[j][:, f, s * 128:(s + 1) * 128], w2[j][:, f, :],
                                             start=f == 0, stop=f == FC - 1)
                        last.then_inc(down, 1)
                all_tiles(pe, body)

            @block.scalar
            def _(act):
                act.sem_inc(acted, 4)

                def body(i, j, follows, follow2):
                    act.wait_ge(y_read, i * S + 1)
                    for f in range(FC):
                        act.wait_ge(up, i * FC + f + 1)
                        act.activation(hT[j][:, f, :], m.ps[f % 4][:, 0:TS], ACT.Gelu,
                                       bias=w[j][:, OB1 + f:OB1 + f + 1]).then_inc(acted, 1)
                all_tiles(act, body)

            @block.vector
            def _(dve):
                dve.sem_inc(y_read, S)
                for j in range(2):
                    dve.sem_inc(y_stored[j], 16)

                def take(i, j):
                    dve.wait_ge(turned, i + 1)
                    dve.tensor_copy(xT[j][:, :, :], m.ps[6][:, :].rearrange("p (k c) -> p k c", k=K2)).then_inc(x_ready, 1)
                take(0, 0)

                def body(i, j, follows, follow2):
                    if follows:
                        take(i + 1, 1 - j)
                    dve.wait_ge(y_stored[j], (i - j) * 8 + 16)
                    for s in range(S):
                        dve.wait_ge(down, i * S + s + 1)
                        last = dve.tensor_tensor(y[j][:, s, :], m.ps[4 + s][:, 0:D], w[j][:, OB2:OB2 + D], ALU.add)
                        last.then_inc(y_read, 1)
                    dve.drain().then_inc(y_made, 1)
                all_tiles(dve, body)


class Combine:

    R = 8

    def __init__(self, m, r):
        self.m, self.r = m, r
        self.near = [m.sb(f"{r.tag}_near{j}", [P, 2, D]) for j in range(self.R)]
        self.rows = [m.sem(f"{r.tag}_rows{j}") for j in range(self.R)]
        self.free = m.sem(r.tag + "_free")

    def gather(self, pool):
        for t in range(NT):
            if t >= self.R:
                pool.wait_ge(self.free, t - self.R + 1)
            for i in range(2):
                pool.indirect_dma_start(out=self.near[t % self.R][:, i, :], out_offset=None, in_=self.r.y,
                                        in_offset=bass.IndirectOffsetOnAxis(ap=self.r.slot[:, i, t:t + 1], axis=0)
                                        ).then_inc(self.rows[t % self.R], 16)

    def add(self, dve, c, j):
        for u in (2 * j, 2 * j + 1):
            if isinstance(c, int) and c * self.R + u >= NT:
                break
            dve.drain()
            dve.wait_ge(self.rows[u], c * 32 + 32)
            for i in range(2):
                if i:
                    dve.drain()
                x = self.m.X[:, bass.ds(c * (self.R * D) + u * D, D)]
                gate = self.r.gate[:, i, :][:, bass.ds(c * self.R + u, 1)]
                last = dve.scalar_tensor_tensor(x, self.near[u][:, i, :], gate, x, ALU.mult, ALU.add)
            last.then_inc(self.free, 1)
        dve.drain()


class Gnn1Nodes(NodeProduct):

    H, F = 2, 128

    def __init__(self, m, s_logits):
        super().__init__(m, "h1", D + 2 * self.H)
        m.wh_dram = m.dram("wh_dram", [N, D + self.H])
        m.s_dram = m.dram("s_dram", [N, self.H])
        self.s_logits = s_logits
        self.bias = m.sb("h1_bias", [128, self.ROW])
        self.att = m.sb("h1_att", [128, 2, D])
        self.prod = m.sb("h1_prod", [128, 2, K2 + 1, D])
        self.row = [m.sb(f"h1_row{i}", [P, self.ROW]) for i in range(4)]
        self.row_stored = [m.sem(f"h1_stored{i}") for i in range(4)]

    def load(self, sp):
        io, F = self.m.io, self.F
        self.loads(sp, self.w[:, :, 0:D], io["L1_gnn_W_w"].rearrange("(k p) d -> p k d", p=128))
        self.loads(sp, self.bias[:, 0:D], io["L1_gnn_W_b"].partition_broadcast(128))
        for i in range(2):
            half = io["L1_gnn_a"][(1 - i) * F:(2 - i) * F].partition_broadcast(128)
            for h in range(self.H):
                self.loads(sp, self.att[:, i, h * F:(h + 1) * F], half)

    def store(self, sp):
        m = self.m

        def body(t, j):
            sp.wait_ge(self.kept, t + 5)
            sp.dma_start(m.wh_dram[t * P:(t + 1) * P, :], self.row[j][:, 0:D + self.H]).then_inc(self.row_stored[j], 16)
        tiles_written_out(NT, 4, body)
        self.stored(sp, m.s_dram.rearrange("(t p) h -> p t h", p=P), self.s_logits[:, :, :])
        sp.wait_ge(self.stored.sem, self.stored.all)
        for i in range(4):
            sp.wait_ge(self.row_stored[i], 16 * len(range(i, NT, 4)))

    def prepare(self, dve):
        w, bias, att, prod, H = self.w, self.bias, self.att, self.prod, self.H
        dve.wait_ge(self.loads.sem, 96)
        for i in range(2):
            for k in range(K2):
                dve.tensor_tensor(prod[:, i, k, :], w[:, k, 0:D], att[:, i, :], ALU.mult)
            dve.tensor_tensor(prod[:, i, K2, :], bias[:, 0:D], att[:, i, :], ALU.mult)
        dve.drain()
        for i in range(2):
            lo = D + H * i
            for k in range(K2):
                dve.tensor_reduce(w[:, k, lo:lo + H], prod[:, i, k, :].rearrange("p (h c) -> p h c", h=H),
                                  AX.X, ALU.add)
            dve.tensor_reduce(bias[:, lo:lo + H], prod[:, i, K2, :].rearrange("p (h c) -> p h c", h=H),
                              AX.X, ALU.add)
        dve.drain().then_inc(self.w_ready, 1)

    def start(self, act):
        pass

    def keep(self, act, t):
        pass

    def after(self, dve):
        dve.sem_inc(self.kept, 4)

        def body(t, j):
            dve.wait_ge(self.made, t + 1)
            if t >= 4:
                dve.wait_ge(self.row_stored[j], 16 * (t // 4))
            dve.tensor_tensor(self.row[j][:, :], self.m.ps[4 + j][:P, 0:self.ROW], self.bias[:P, :], ALU.add)
            dve.drain()
            dve.tensor_copy(self.s_logits[:, t, :], self.row[j][:, D + self.H:])
            dve.drain().then_inc(self.kept, 1)
        tiles_written_out(NT, 4, body)


def gnn1_edges_mix1(m, ed):
    nc, io = m.nc, m.io
    H, F, cols = 2, 128, ed.cols
    HF, W = D, D + 2 * H
    with Stage(m):
        spread = Spread(m, "he", ed, H)
        result = m.dram("he_result", [128 * cols, W])
        carry = m.dram("he_carry", [128, W + 1])
        last = m.sb("he_last", [128, W])
        with Stage(m):
            mix = Mix1(m)
            with Stage(m):
                mix1_keys(m, mix, SpreadLogits(m, "hs", ed, spread, m.s_dram, m.s_logits))
            sums_and_mix1(m, mix, ed, spread, result, last)
        carry_rows(m, "hc", ed, H, F, last, carry)
        agg = m.sb("he_agg", [P, NT, HF])
        den = m.sb("he_den", [P, NT, H])
        merge_nodes(m, "hm", ed, spread, H, F, result, carry, agg, den)
        own = m.sb("he_own", [P, NT, HF])
        none = m.sb("he_none", [P, NT])
        own_loaded = m.sem("he_own_loaded")
        with nc.Block() as block:
            @block.sync
            def _(sp):
                sp.dma_start(own[:, :, :], m.wh_dram.rearrange("(t p) c -> p t c", p=P)[:, :, 0:HF]).then_inc(own_loaded, 16)

            @block.vector
            def _(dve):
                has = spread.has
                dve.tensor_scalar(none[:, :], has[:, :], -1.0, 1.0, ALU.mult, ALU.add)
                dve.drain()
                dve.tensor_tensor(den[:, :, :], den[:, :, :], none[:, :].unsqueeze(2).broadcast_to((P, NT, H)), ALU.add)
                dve.drain()
                dve.reciprocal(den[:, :, :], den[:, :, :])
                dve.drain()
                for t in range(NT):
                    for h in range(H):
                        lo = t * D + h * F
                        x = m.X[:, lo:lo + F]
                        dve.scalar_tensor_tensor(x, agg[:, t, h * F:(h + 1) * F], den[:, t, h:h + 1], x, ALU.mult, ALU.add)
                dve.wait_ge(own_loaded, 16)
                dve.drain()
                for t in range(NT):
                    x = m.X[:, t * D:(t + 1) * D]
                    dve.scalar_tensor_tensor(x, own[:, t, :], none[:, t:t + 1], x, ALU.mult, ALU.add)


class Mix1:

    def __init__(self, m):
        self.wq, self.wo = (m.sb("m1_w" + x, [128, K2, D]) for x in "qo")
        self.w1 = m.sb("m1_w1", [128, K2, FF])
        self.w2 = m.sb("m1_w2", [128, FF // 128, D])
        self.bq = m.sb("m1_bq", [128, K2])
        self.b1 = m.sb("m1_b1", [128, FF // 128])
        self.rowb = m.sb("m1_rows", [P, 6, D])
        self.kv = m.sb("m1_kv", [128, K2, 128])
        self.ks = m.sb("m1_ks", [128, K2, 128])


def mix1_keys(m, x, edges):
    nc, io = m.nc, m.io
    HD = 32
    with Stage(m):
        wk, wv = (m.sb("m1_w" + x, [128, K2, D]) for x in "kv")
        bkv = m.sb("m1_bkv", [P, 2, D])
        k_raw = [m.sb(f"m1_kraw{i}", [P, D]) for i in range(2)]
        k_low = [m.sb(f"m1_klow{i}", [P, D]) for i in range(2)]
        kp = [m.sb(f"m1_kp{i}", [P, D]) for i in range(2)]
        v1 = [m.sb(f"m1_v1{i}", [P, K2, 129]) for i in range(2)]
        bmask = m.sb("m1_bmask", [128, 128])
        loads_kv, loads = Loads(m, "m1_kv_loaded"), Loads(m, "m1_loaded")
        made, kv_in, kv_used, kx, kexp, mask_ready = (
            m.sem("m1_" + x) for x in ("made", "kv_in", "kv_used", "kx", "kexp", "mask_ready"))
        with nc.Block() as block:
            @block.sync
            def _(sp):
                for t, name in ((wk, "Wk"), (wv, "Wv")):
                    loads_kv(sp, t[:, :, :], io["L1_mix_" + name].rearrange("(k p) d -> p k d", p=128))
                for i, name in enumerate(("bk", "bv")):
                    loads_kv(sp, bkv[:, i, :], io["L1_mix_" + name].partition_broadcast(P))
                edges.bounds(sp)
                for i, name in enumerate(("bo", "b2", "ln1_g", "ln1_b", "ln2_g", "ln2_b")):
                    loads(sp, x.rowb[:, i, :], io["L1_mix_" + name].partition_broadcast(P))
                for t, name in ((x.wq, "Wq"), (x.wo, "Wo"), (x.w1, "W1"), (x.w2, "W2")):
                    loads(sp, t[:, :, :], io["L1_mix_" + name].rearrange("(k p) d -> p k d", p=128))
                loads(sp, x.bq[:, :], io["L1_mix_bq_cols"])
                loads(sp, x.b1[:, :], io["L1_mix_b1_cols"])
                edges.sync(sp)
                sp.wait_ge(loads.sem, loads.all)

            @block.gpsimd
            def _(pool):
                pool.memset(bmask[:, :], 1.0)
                pool.drain()
                blocks = bmask[:, :].rearrange("p (h c) -> p h c", c=HD)
                pool.affine_select(out=blocks, in_=blocks, compare_op=ALU.is_ge, fill=0.0, base=0,
                                   pattern=[[-HD, 4], [0, HD]], channel_multiplier=1)
                pool.drain()
                pool.affine_select(out=blocks, in_=blocks, compare_op=ALU.is_ge, fill=0.0, base=HD - 1,
                                   pattern=[[HD, 4], [0, HD]], channel_multiplier=-1)
                pool.drain().then_inc(mask_ready, 1)
                edges.gpsimd(pool)

            @block.tensor
            def _(pe):
                pe.wait_ge(loads_kv.sem, 16 * 4)
                for k in range(K2):
                    pe.matmul(m.ps[4 + k][:, 0:129], m.zero16[:, 0:128], m.zero16[:, 0:129], start=True, stop=False)

                def keys(t):
                    pe.wait_ge(kx, t + 1)
                    for half, w in ((0, wk), (1, wv)):
                        for k in range(K2):
                            last = pe.matmul(m.ps[t % 2][:P, half * D:(half + 1) * D], m.XT[:, bass.ds(t * P + k * N, P)],
                                          w[:, k, :], start=k == 0, stop=k == K2 - 1)
                    last.then_inc(made, 1)

                def outer(t):
                    j = t % 2
                    pe.wait_ge(kv_in, t + 1)
                    for k in range(K2):
                        last = pe.matmul(m.ps[4 + k][:, 0:129], kp[j][:, k * 128:(k + 1) * 128], v1[j][:, k, :],
                                      start=False, stop=t == NT - 1)
                    last.then_inc(kv_used, 1)
                keys(0)
                for t in range(NT):
                    if t + 1 < NT:
                        keys(t + 1)
                    outer(t)

            @block.vector
            def _(dve):
                dve.wait_ge(loads_kv.sem, 16 * 4)
                for j in range(2):
                    dve.memset(v1[j][:, :, 128:129], 1.0)
                dve.sem_inc(kv_used, 2)
                dve.sem_inc(kx, 2)

                def body(t, j):
                    dve.wait_ge(made, t + 1)
                    dve.wait_ge(kv_used, t + 1)
                    dve.tensor_tensor(k_raw[j][:, :], m.ps[j][:P, 0:D], bkv[:, 0, :], ALU.add)
                    dve.tensor_tensor(v1[j][:, :, 0:128], m.ps[j][:P, D:2 * D].rearrange("p (k c) -> p k c", k=K2),
                                      bkv[:, 1, :].rearrange("p (k c) -> p k c", k=K2), ALU.add)
                    dve.drain().then_inc(kx, 1)
                    dve.tensor_scalar(k_low[j][:, :], k_raw[j][:, :], 0.0, None, ALU.min)
                    dve.drain().then_inc(kexp, 1)
                    dve.wait_ge(kexp, 2 * t + 2)
                    dve.scalar_tensor_tensor(kp[j][:, :], k_raw[j][:, :], 0.0, k_low[j][:, :], ALU.max, ALU.add)
                    dve.drain().then_inc(kv_in, 1)
                with dve.Fori(0, 4) as i:
                    for j in range(2):
                        body(i * 2 + j, j)
                edges.positions(dve)
                with dve.Fori(0, (NT - 9) // 2) as i:
                    for j in range(2):
                        body(i * 2 + (8 + j), j)
                body(NT - 1, 0)
                dve.wait_ge(kv_used, NT + 2)
                dve.wait_ge(mask_ready, 1)
                for k in range(K2):
                    dve.tensor_tensor(x.kv[:, k, :], m.ps[4 + k][:, 0:128], bmask[:, :], ALU.mult)
                    dve.tensor_scalar(x.ks[:, k, :], bmask[:, :], m.ps[4 + k][:, 128:129], None, ALU.mult)
                edges.spread(dve)

            @block.scalar
            def _(act):
                def body(t, j):
                    act.wait_ge(kexp, 2 * t + 1)
                    act.activation(k_low[j][:, :], k_low[j][:, :], ACT.Exp).then_inc(kexp, 1)
                tiles(act, NT, 2, body)


def sums_and_mix1(m, x, ed, spread, result, last):
    nc = m.nc
    H, F, cols = 2, 128, ed.cols
    HF, W = D, D + 2 * H
    FC = FF // 128
    nb = cols // BC
    R = 4
    assert nb == NCH * R + 1
    with Stage(m):
        idx = [m.sb(f"he_idx{i}", [128, BC], I32) for i in range(R)]
        buf = [m.sb(f"he_buf{i}", [128, BC, W]) for i in range(R)]
        e = [m.sb(f"he_e{i}", [128, BC, H]) for i in range(R)]
        dec = [m.sb(f"he_dec{i}", [128, BC, H]) for i in range(R)]
        con_b = [m.sb(f"he_con_b{i}", [128, BC]) for i in range(R)]
        pen_b = m.sb("he_pen_b", [128, BC])
        top = m.sb("he_top", [128, H])
        hT = m.sb("m1_hT", [128, FC, CH])
        qr, ql = hT[:, 0:K2, :], hT[:, K2:2 * K2, :]
        oT = hT[:, 2 * K2:3 * K2, :]
        xt = m.XT[:, :].rearrange("p (k n) -> p k n", k=K2)
        yT = lambda c, w: xt[:, :, bass.ds(c * CH, w)]
        y = m.sb("m1_y", [P, 4, D])
        st = m.sb("m1_st", [P, 2, 4, 6])
        mv = m.sb("m1_mv", [P, 2, 4, 2])
        rs = m.sb("m1_rs", [P, 2, 4])
        rows, stored = ([m.sem(f"he_{k}{i}") for i in range(R)] for k in ("rows", "stored"))
        e_ready, e_exp, weighted, summed = (m.sem("he_" + k) for k in ("e_ready", "e_exp", "weighted", "summed"))
        names = ("q_made", "q_low", "q_exp", "q_phi", "o_made", "o_ready", "o_made2", "var1", "std1",
                 "y_ready", "y_turned", "y_moved", "up", "acted", "f_made", "var2", "std2")
        S = {k: m.sem("m2_" + k) for k in names}
        with nc.Block() as block:
            @block.gpsimd
            def _(pool):
                for j in range(R):
                    pool.sem_inc(stored[j], 16)

                def body(t, j):
                    pool.wait_ge(stored[j], (t - j) * (16 // R) + 16)
                    pool.tensor_copy(idx[j][:, :], ed.other[:, at(t, BC)])
                    pool.drain()
                    for c in range(BC):
                        pool.indirect_dma_start(out=buf[j][:, c, 0:HF + H], out_offset=None, in_=m.wh_dram,
                                                in_offset=bass.IndirectOffsetOnAxis(ap=idx[j][:, c:c + 1], axis=0)
                                                ).then_inc(rows[j], 16)
                tiles(pool, nb, R, body)

            @block.sync
            def _(sp):
                def body(t, j):
                    sp.wait_ge(summed, t + 1)
                    sp.sem_inc(m.spare, 1)
                    sp.dma_start(result.rearrange("(p t) w -> p t w", p=128)[:, at(t, BC), :], buf[j][:, :, :]
                                 ).then_inc(stored[j], 16)
                tiles(sp, nb, R, body)
                for j in range(R):
                    sp.wait_ge(stored[j], 16 + 16 * len(range(j, nb, R)))

            @block.tensor
            def _(pe):
                def body(c, nt):
                    w = nt * P
                    for o in range(K2):
                        for k in range(K2):
                            last = pe.matmul(m.ps[o][:, 0:w], x.wq[:, k, o * 128:(o + 1) * 128],
                                          m.XT[:, bass.ds(c * CH + k * N, w)], start=k == 0, stop=k == K2 - 1)
                    last.then_inc(S["q_made"], 1)
                    pe.wait_ge(S["q_phi"], c + 1)
                    for o in range(K2):
                        pe.matmul(m.ps[2 + o][:, 0:w], x.kv[:, o, :], qr[:, o, 0:w], start=True, stop=True)
                        last = pe.matmul(m.ps[o][:, 0:w], x.ks[:, o, :], qr[:, o, 0:w], start=True, stop=True)
                    last.then_inc(S["o_made"], 1)
                    pe.wait_ge(S["o_ready"], c + 1)
                    for j in range(nt):
                        for k in range(K2):
                            last = pe.matmul(m.ps[4 + j][:P, 0:D], oT[:, k, j * P:(j + 1) * P], x.wo[:, k, :],
                                          start=k == 0, stop=k == K2 - 1)
                    last.then_inc(S["o_made2"], 1)
                    pe.wait_ge(S["y_ready"], c + 1)
                    for k in range(K2):
                        for j in range(nt):
                            last = pe.transpose(m.ps[k][:, j * P:(j + 1) * P], y[:, j, k * 128:(k + 1) * 128], m.ident[:P, :P])
                    last.then_inc(S["y_turned"], 1)
                    pe.wait_ge(S["y_moved"], c + 1)
                    for f in range(FC):
                        pe.wait_ge(S["acted"], c * FC + f + 1)
                        for k in range(K2):
                            last = pe.matmul(m.ps[f % 4][:, 0:w], x.w1[:, k, f * 128:(f + 1) * 128], yT(c, w)[:, k, :],
                                          start=k == 0, stop=k == K2 - 1)
                        last.then_inc(S["up"], 1)
                    pe.wait_ge(S["acted"], c * FC + FC + 4)
                    for j in range(nt):
                        for f in range(FC):
                            last = pe.matmul(m.ps[4 + j][:P, 0:D], hT[:, f, j * P:(j + 1) * P], x.w2[:, f, :],
                                          start=f == 0, stop=f == FC - 1)
                        last.then_inc(S["f_made"], 1)
                chunks(pe, body)

            @block.scalar
            def _(act):
                act.sem_inc(S["acted"], 4)

                def weights(t, j):
                    act.wait_ge(e_ready, t + 1)
                    act.activation(e[j][:, :, :], e[j][:, :, :], ACT.Exp)
                    act.activation(dec[j][:, :, :], dec[j][:, :, :], ACT.Exp)
                    act.drain().then_inc(e_exp, 1)

                def weigh(j, columns):
                    for c in columns:
                        for h in range(H):
                            f = buf[j][:, c, h * F:(h + 1) * F]
                            done = act.activation(f, f, ACT.Copy, scale=e[j][:, c, h:h + 1])
                        done.then_inc(weighted, 1)

                def hidden(c, w, fs):
                    for f in fs:
                        act.wait_ge(S["up"], c * FC + f + 1)
                        act.activation(hT[:, f, 0:w], m.ps[f % 4][:, 0:w], ACT.Relu, bias=x.b1[:, f:f + 1]
                                       ).then_inc(S["acted"], 1)

                def body(c, nt):
                    w, more = nt * P, nt == 4
                    act.wait_ge(S["q_low"], c + 1)
                    act.activation(ql[:, :, 0:w], ql[:, :, 0:w], ACT.Exp).then_inc(S["q_exp"], 1)
                    if more:
                        weights(c * R + 1, 1)
                        weigh(1, range(BC))
                    act.wait_ge(S["var1"], c + 1)
                    act.sqrt(rs[:, 0, 0:nt], rs[:, 0, 0:nt]).then_inc(S["std1"], 1)
                    if more:
                        weights(c * R + 2, 2)
                        weigh(2, range(BC))
                    act.wait_ge(S["y_turned"], c + 1)
                    for k in range(K2):
                        act.copy(yT(c, w)[:, k, :], m.ps[k][:, 0:w])
                    act.drain().then_inc(S["y_moved"], 1)
                    if more:
                        hidden(c, w, range(0, 2))
                        weights(c * R + 3, 3)
                        for i in range(4):
                            weigh(3, range(4 * i, 4 * i + 4))
                            if i < 3:
                                hidden(c, w, range(2 * i + 2, 2 * i + 4))
                        weights(c * R + R, 0)
                        weigh(0, range(BC))
                    else:
                        hidden(c, w, range(FC))
                    act.wait_ge(S["var2"], c + 1)
                    act.sqrt(rs[:, 1, 0:nt], rs[:, 1, 0:nt]).then_inc(S["std2"], 1)
                weights(0, 0)
                weigh(0, range(BC))
                chunks(act, body)

            @block.vector
            def _(dve):
                dve.memset(last[:, 0:HF + H], 0.0)
                dve.memset(top[:, :], -BIG)
                dve.drain()

                def logits(t, j):
                    v = buf[j]
                    dve.wait_ge(rows[j], (t - j) * (16 * BC // R) + 16 * BC)
                    dve.tensor_tensor(e[j][:, :, :], v[:, :, HF:HF + H], spread.ke[:, at(t, BC), :], ALU.add)
                    dve.tensor_scalar(pen_b[:, :], spread.pen[:, at(t, BC)], 0.0, None, ALU.add)
                    dve.tensor_scalar(con_b[j][:, :], spread.cont[:, at(t, BC)], 0.0, None, ALU.add)
                    dve.drain()
                    dve.scalar_tensor_tensor(e[j][:, :, :], e[j][:, :, :], 0.2, e[j][:, :, :], ALU.mult, ALU.max)
                    dve.drain()
                    mx = v[:, :, HF + H:]
                    for h in range(H):
                        dve.tensor_tensor_scan(mx[:, :, h], pen_b[:, :], e[j][:, :, h], top[:, h:h + 1], ALU.add, ALU.max)
                    dve.drain()
                    wide = con_b[j][:, :].unsqueeze(2).broadcast_to((128, BC, H))
                    dve.tensor_tensor(dec[j][:, 0, :], top[:, :], mx[:, 0, :], ALU.subtract)
                    dve.tensor_tensor(dec[j][:, 1:, :], mx[:, 0:BC - 1, :], mx[:, 1:, :], ALU.subtract)
                    dve.tensor_tensor(e[j][:, :, :], e[j][:, :, :], mx, ALU.subtract)
                    dve.drain()
                    dve.tensor_copy(top[:, :], mx[:, BC - 1, :])
                    dve.tensor_tensor(dec[j][:, :, :], dec[j][:, :, :], wide, ALU.mult)
                    dve.drain().then_inc(e_ready, 1)

                def sums(t, j):
                    first_sums(t, j)
                    last_sums(t, j)

                def first_sums(t, j):
                    v = buf[j]
                    wide = con_b[j][:, :].unsqueeze(2).broadcast_to((128, BC, H))
                    dve.wait_ge(e_exp, t + 1)
                    dve.tensor_tensor(dec[j][:, :, :], dec[j][:, :, :], wide, ALU.mult)
                    dve.drain()
                    for h in range(H):
                        dve.tensor_tensor_scan(v[:, :, HF + h], dec[j][:, :, h], e[j][:, :, h],
                                               last[:, HF + h:HF + h + 1], ALU.mult, ALU.add)
                    rows_sums(t, j, range(0, BC // 2))

                def rows_sums(t, j, columns):
                    v = buf[j]
                    for c in columns:
                        dve.wait_ge(weighted, t * BC + c + 1)
                        prev = last if c == 0 else v[:, c - 1, :]
                        for h in range(H):
                            f = slice(h * F, (h + 1) * F)
                            dve.scalar_tensor_tensor(v[:, c, f], prev[:, f], dec[j][:, c, h:h + 1], v[:, c, f],
                                                     ALU.mult, ALU.add)
                        dve.drain()

                def last_sums(t, j):
                    rows_sums(t, j, range(BC // 2, BC))
                    dve.tensor_copy(last[:, 0:HF + H], buf[j][:, BC - 1, 0:HF + H])
                    dve.drain().then_inc(summed, 1)

                def normal_sums(nt, i):
                    dve.drain()
                    for j in range(nt):
                        dve.bn_stats(st[:, i, j, :], y[:, j, :])
                    dve.drain()
                    for j in range(nt):
                        dve.bn_aggr(mv[:, i, j, :], st[:, i, j, :])
                    dve.drain()
                    dve.tensor_scalar(rs[:, i, 0:nt], mv[:, i, 0:nt, 1], 1e-5, None, ALU.add)
                    dve.drain().then_inc(S[f"var{i + 1}"], 1)

                def normalize(c, nt, i):
                    dve.wait_ge(S[f"std{i + 1}"], c + 1)
                    dve.reciprocal(rs[:, i, 0:nt], rs[:, i, 0:nt])
                    dve.drain()
                    for j in range(nt):
                        dve.tensor_scalar(y[:, j, :], y[:, j, :], mv[:, i, j, 0:1], rs[:, i, j:j + 1],
                                          ALU.subtract, ALU.mult)
                    for b, op in ((2 + 2 * i, ALU.mult), (3 + 2 * i, ALU.add)):
                        dve.drain()
                        dve.tensor_tensor(y[:, 0:nt, :], y[:, 0:nt, :],
                                          x.rowb[:, b, :].unsqueeze(1).broadcast_to((P, nt, D)), op)
                    dve.drain()

                def queries(c, w):
                    dve.wait_ge(S["q_made"], c + 1)
                    for o in range(K2):
                        dve.tensor_scalar(ql[:, o, 0:w], m.ps[o][:, 0:w], x.bq[:, o:o + 1], 0.0, ALU.add, ALU.min)
                        dve.tensor_scalar(qr[:, o, 0:w], m.ps[o][:, 0:w], x.bq[:, o:o + 1], 0.0, ALU.add, ALU.max)
                    dve.drain().then_inc(S["q_low"], 1)
                    dve.wait_ge(S["q_exp"], c + 1)
                    dve.tensor_tensor(qr[:, :, 0:w], qr[:, :, 0:w], ql[:, :, 0:w], ALU.add)
                    dve.drain().then_inc(S["q_phi"], 1)

                def attention(c, w):
                    dve.wait_ge(S["o_made"], c + 1)
                    for o in range(K2):
                        dve.tensor_scalar(ql[:, o, 0:w], m.ps[o][:, 0:w], 1e-6, None, ALU.add)
                    dve.drain()
                    dve.reciprocal(ql[:, :, 0:w], ql[:, :, 0:w])
                    dve.drain()
                    for o in range(K2):
                        dve.tensor_tensor(oT[:, o, 0:w], m.ps[2 + o][:, 0:w], ql[:, o, 0:w], ALU.mult)
                    dve.drain().then_inc(S["o_ready"], 1)

                def after_attention(c, nt):
                    dve.wait_ge(S["o_made2"], c + 1)
                    for j in range(nt):
                        dve.tensor_tensor(y[:, j, :], m.ps[4 + j][:P, 0:D], x.rowb[:, 0, :], ALU.add)
                    dve.drain()
                    for j in range(nt):
                        dve.tensor_tensor(y[:, j, :], y[:, j, :], m.XN[:, bass.ds(c * (4 * D) + j * D, D)], ALU.add)
                    normal_sums(nt, 0)
                    normalize(c, nt, 0)
                    dve.sem_inc(S["y_ready"], 1)

                def after_feed_forward(c, nt):
                    for j in range(nt):
                        dve.wait_ge(S["f_made"], c * 4 + j + 1)
                        if j == 0:
                            dve.wait_ge(S["y_moved"], c + 1)
                        dve.tensor_tensor(y[:, j, :], y[:, j, :], m.ps[4 + j][:P, 0:D], ALU.add)
                    dve.drain()
                    dve.tensor_tensor(y[:, 0:nt, :], y[:, 0:nt, :],
                                      x.rowb[:, 1, :].unsqueeze(1).broadcast_to((P, nt, D)), ALU.add)
                    normal_sums(nt, 1)
                    normalize(c, nt, 1)
                    for j in range(nt):
                        xx = m.X[:, bass.ds(c * (4 * D) + j * D, D)]
                        dve.tensor_tensor(xx, y[:, j, :], xx, ALU.add)
                    dve.drain()

                def body(c, nt):
                    w, more = nt * P, nt == 4
                    queries(c, w)
                    if more:
                        logits(c * R + 1, 1)
                    sums(c * R, 0)
                    attention(c, w)
                    if more:
                        logits(c * R + 2, 2)
                        first_sums(c * R + 1, 1)
                    after_attention(c, nt)
                    if more:
                        last_sums(c * R + 1, 1)
                        logits(c * R + 3, 3)
                        sums(c * R + 2, 2)
                        logits(c * R + R, 0)
                        sums(c * R + 3, 3)
                    after_feed_forward(c, nt)
                logits(0, 0)
                chunks(dve, body)
                dve.tensor_copy(last[:, HF + H:], top[:, :])


def gates1(m, load_next):
    nc, io = m.nc, m.io
    E = 8
    with Stage(m):
        wr = m.sb("r1_wr", [128, K2, E])
        s = m.sb("r1_s", [P, NT, E])
        tmp = m.sb("r1_tmp", [P, NT])
        gt = m.sb("r1_gt", [P, NT, E, E])
        eq = m.sb("r1_eq", [P, NT, E, E])
        low = m.sb("r1_low", [P, E, E])
        sel = m.sel1
        loads = Loads(m, "r1_loaded")
        low_ready, made, s_ready, s_exp = (m.sem("r1_" + x) for x in ("low_ready", "made", "s_ready", "s_exp"))
        with nc.Block() as block:
            @block.sync
            def _(sp):
                loads(sp, wr[:, :, :], io["L1_ffn_Wr"].rearrange("(k p) e -> p k e", p=128))
                load_next(sp)

            @block.gpsimd
            def _(pool):
                pool.memset(low[:, :, :], 1.0)
                pool.drain()
                pool.affine_select(out=low[:, :, :], in_=low[:, :, :], compare_op=ALU.is_gt, fill=0.0,
                                   base=0, pattern=[[1, E], [-1, E]], channel_multiplier=0)
                pool.drain().then_inc(low_ready, 1)

            @block.tensor
            def _(pe):
                pe.wait_ge(loads.sem, 16)

                def body(t, j):
                    for k in range(K2):
                        x = pe.matmul(m.ps[0][:P, t * E:(t + 1) * E], m.XT[:, bass.ds(t * P + k * N, P)], wr[:, k, :],
                                      start=k == 0, stop=k == K2 - 1)
                    x.then_inc(made, 1)
                tiles_written_out(NT, 1, body)

            @block.vector
            def _(dve):
                wide = tmp[:, :].unsqueeze(2).broadcast_to((P, NT, E))
                dve.wait_ge(made, NT)
                dve.tensor_copy(s[:, :, :], m.ps[0][:P, 0:NT * E].rearrange("p (t e) -> p t e", e=E))
                dve.drain()
                dve.tensor_reduce(tmp[:, :], s[:, :, :], AX.X, ALU.max)
                dve.drain()
                dve.tensor_tensor(s[:, :, :], s[:, :, :], wide, ALU.subtract)
                dve.drain().then_inc(s_ready, 1)
                dve.wait_ge(s_exp, 1)
                dve.tensor_reduce(tmp[:, :], s[:, :, :], AX.X, ALU.add)
                dve.drain()
                dve.reciprocal(tmp[:, :], tmp[:, :])
                dve.drain()
                dve.tensor_tensor(s[:, :, :], s[:, :, :], wide, ALU.mult)
                dve.drain()
                dve.wait_ge(low_ready, 1)
                top_two(dve, s, E, gt[:, :, :, :], eq[:, :, :, :], low[:, :, :], sel[:, :, :])
                dve.tensor_tensor(s[:, :, :], s[:, :, :], sel[:, :, :], ALU.mult)
                dve.drain()
                dve.tensor_reduce(tmp[:, :], s[:, :, :], AX.X, ALU.add)
                dve.drain()
                dve.reciprocal(tmp[:, :], tmp[:, :])
                dve.drain()
                dve.tensor_tensor(m.gate1[:, :, :], s[:, :, :], wide, ALU.mult)

            @block.scalar
            def _(act):
                act.wait_ge(s_ready, 1)
                act.activation(s[:, :, :], s[:, :, :], ACT.Exp).then_inc(s_exp, 1)


def store(m):
    out_stored = m.sem("out_stored")
    with m.nc.Block() as block:
        @block.sync
        def _(sp):
            sp.dma_start(m.io["out"].rearrange("(t p) d -> p t d", p=P),
                         m.X[:, :].rearrange("p (t d) -> p t d", d=D)).then_inc(out_stored, 16)
            sp.wait_ge(out_stored, 16)


def program(nc, io, stop=99):
    m = Net(nc, io)
    with m.keep:
        constants(m)
        sort_constants(m)
        m.scratch = m.sb("XN", [128, NT * D])
        m.XN = m.scratch[:P, :]
        ed1 = Edges(m, "s1", COLS1)
        m.XT = m.sb("XT", [128, K2 * N])
        routes = Routes(m, "x1", 8)
        with Stage(m):
            if stop >= 3:
                ed0 = Edges(m, "s0", COLS0)
                sort_edges(m, ed0, io["key0"], io["other0"])
            with Stage(m):
                layer_norm(m, "ln0", Gnn0Nodes(m))
            if stop >= 2:
                mix0_log(m)
                with Stage(m):
                    m.QT = m.sb("QT", [128, OC * N])
                    with Stage(m):
                        mix0_qkv(m, Gnn0Edges(m))
                    mix0_attention(m, routes)
            if stop >= 3:
                m.hg = m.sb("hg", [P, NT, 24])
                with Stage(m):
                    layer_norm(m, "ln1", GatNodes(m, m.hg))
                arena = Arena(m, "arena", (COLS1 + 1) * KB)
                w = ExpertWeights(m, "x0", 512, 2, arena.take)
                load0 = lambda sp, e: w.load(sp, e, io["L0_ffn_W1"][e], io["L0_ffn_b1_cols"][e], io["L0_ffn_W2"][e],
                                             io["L0_ffn_b2"][e])
                b2 = arena.take("x0_b2_early", [P, 2, D])
                b2_loaded = m.sem("x0_b2_early_loaded")

                def load_early(sp, count):
                    for e in range(count):
                        load0(sp, e)
                        sp.dma_start(b2[:, e, :], io["L0_ffn_b2"][e].partition_broadcast(P)).then_inc(b2_loaded, 16)
                near = m.sb("ge_near", [128, COLS0 * 20])
                y_early = [m.XN, near[:P, 0:NT * D]]
                hT = arena.take("x0_hT_early", [128, 4, CH])
                early = lambda: EarlyExperts(m, "xe", w, 512, hT, y_early)
                gat_edges(m, ed0, ed1, (io["key1"], io["other1"]), w, near, early, load_early, arena)
                gates0(m)
                gates = [lambda t, e=e: m.gate0[:, :, e][:, bass.ds(t, 1)] for e in range(4)]

                def add_early(dve, c, j):
                    dve.drain()
                    dve.wait_ge(b2_loaded, 48)
                    y = [y_early[e][:, bass.ds(c * (4 * D) + j * D, D)] for e in range(2)]
                    for e in range(2):
                        dve.tensor_tensor(y[e], y[e], b2[:, e, :], ALU.add)
                    for e in range(2):
                        dve.drain()
                        x = m.X[:, bass.ds(c * (4 * D) + j * D, D)]
                        dve.scalar_tensor_tensor(x, y[e], gates[e](c * 4 + j), x, ALU.mult, ALU.add)
                    dve.drain()
                experts(m, "x0", w, gates[2:], 512, load0, first=2, after_tile=add_early)
        if stop >= 4:
            with Stage(m):
                m.s_logits = m.sb("s_logits", [P, NT, 2])
                with Stage(m):
                    layer_norm(m, "ln2", Gnn1Nodes(m, m.s_logits))
                gnn1_edges_mix1(m, ed1)
        if stop >= 5:
            layer_norm(m, "ln3")
            with Stage(m):
                m.gate1 = m.sb("gate1", [P, NT, 8])
                m.sel1 = m.sb("sel1", [P, NT, 8])
                routes.hold(m)
                w = ExpertWeights(m, "xs", FF, 1)
                gates1(m, lambda sp: w.load(sp, 0, io["L1_ffn_W1s"], io["L1_ffn_b1s_cols"], io["L1_ffn_W2s"],
                                            io["L1_ffn_b2s"]))
                find_routes(m, routes, m.sel1[:, :, :], m.gate1[:, :, :])
                placed = Loads(m, "x1_placed")
                placed.all = 16 * 2 * NT

                def beside(pool):
                    scatter_nodes(m, routes, pool, placed.sem)
                    pool.wait_ge(placed.sem, placed.all)
                experts(m, "xs", w, [None], FF, hi=SHARED_FIRST, beside=beside)
                routed_experts(m, routes, io["L1_ffn_packed"], FF)
                with Stage(m):
                    combine = Combine(m, routes)
                    experts(m, "xt", w, [None], FF, lo=SHARED_FIRST, beside=combine.gather, after_tile=combine.add)
        store(m)


def columns(v, cols, pad):
    out = np.full(cols * 128, pad, v.dtype)
    out[:v.size] = v
    return np.ascontiguousarray(out.reshape(cols, 128).T)


def pack_experts(W1, b1, W2, b2):
    E, _, F = W1.shape
    by_line = lambda w: w.reshape(E, -1, 128, w.shape[-1]).transpose(0, 2, 1, 3).reshape(E, 128, -1)
    parts = [by_line(W1), by_line(W2), by_line(b1[:, :, None]), np.repeat(b2[:, None, :], 128, axis=1)]
    return np.ascontiguousarray(np.concatenate(parts, axis=2).reshape(E * 128, -1))


def layouts(inputs):
    f = {k: np.ascontiguousarray(v) for k, v in inputs.items()}
    skip = ("src", "dst", "L0_mix_w_qkv", "L0_mix_w_dw", "L0_mix_w_pw", "L0_mix_w_res", "L0_ffn_edge_index")
    out = {k: v for k, v in f.items() if k not in skip}
    src, dst = f["src"], f["dst"]
    out["first_dst"] = np.ascontiguousarray(dst[:N].reshape(NT, P).T)
    out["first_src"] = np.ascontiguousarray(src[:N].reshape(NT, P).T)
    ei = f["L0_ffn_edge_index"]
    out["key0"], out["other0"] = columns(ei[1], COLS0, 0), columns(ei[0], COLS0, 0)
    out["key1"], out["other1"] = columns(src, COLS1, KEYS - 1), columns(dst, COLS1, 0)
    out["w_qkv_t"] = np.ascontiguousarray(f["L0_mix_w_qkv"][:, :, 2].T)
    cols = lambda v: np.ascontiguousarray(v.reshape(-1, 128).T)
    out["w_dw_mid_cols"] = cols(f["L0_mix_w_dw"][:, 0, 2])
    for name in ("L0_mix_bn_gamma", "L0_mix_bn_beta", "L1_mix_bq", "L1_mix_b1", "L1_ffn_b1s"):
        out[name + "_cols"] = cols(out.pop(name))
    out["L0_ffn_b1_cols"] = np.ascontiguousarray(np.stack([cols(v) for v in out.pop("L0_ffn_b1")]))
    out["L1_ffn_packed"] = pack_experts(*(out.pop("L1_ffn_" + x) for x in ("W1p", "b1p", "W2p", "b2p")))
    out["w_pw_t"] = np.ascontiguousarray(f["L0_mix_w_pw"][:, :, 0].T)
    out["w_res_t"] = np.ascontiguousarray(f["L0_mix_w_res"][:, :, 0].T)
    return out


def kernel(**inputs):
    import concourse.bacc as bacc
    from concourse.bass_utils import run_bass_kernel_spmd as run

    arrays = layouts({k: np.asarray(v) for k, v in inputs.items()})
    nc = bacc.Bacc("TRN2", target_bir_lowering=False, num_devices=1)
    io = {k: nc.dram_tensor("in_" + k, a.shape, mybir.dt.from_np(a.dtype), kind="ExternalInput").ap()
          for k, a in arrays.items()}
    io["out"] = nc.dram_tensor("out", (N, D), FP32, kind="ExternalOutput").ap()
    program(nc, io)
    r = run(nc, [{"in_" + k: a for k, a in arrays.items()}], core_ids=[0])
    return r.results[0]["out"]
```
